# Optimizing a Trainium2 kernel written in Bass

```python
import numpy as np
import jax
import jax.numpy as jnp

def _softmax(x, axis=-1):
    return jax.nn.softmax(x, axis=axis)

def _gelu(x):
    return jax.nn.gelu(x, approximate=True)

def _silu(x):
    return jax.nn.silu(x)

def _sigmoid(x):
    return jax.nn.sigmoid(x)

def _layernorm(x, axis=-1, eps=1e-05):
    m = jnp.mean(x, axis=axis, keepdims=True)
    v = jnp.var(x, axis=axis, keepdims=True)
    return (x - m) / jnp.sqrt(v + eps)

def _scatter_add(tgt, idx, src, axis=0):
    return tgt.at[idx].add(src)

def _segment_sum(src, seg, n):
    return jax.ops.segment_sum(src, seg, n)
kernel_name = 'mk_decoder_preln_d4_seqx_r4_dac804'

def setup_inputs(seed: int=0):
    np.random.seed(seed)
    _w = jnp.asarray

    def _rec_inputs():
        import jax
        import jax.numpy as jnp
        _rk = jax.random.key(seed)
        x = 7.22e-05 + 1 * jax.random.normal(jax.random.fold_in(_rk, 1), (16, 112, 256), jnp.float32)
        _lenS = 112 - jax.random.randint(jax.random.fold_in(_rk, 7), (16,), 0, max(1, 112 // 4) + 1, jnp.int32)
        _lenS2 = 375 - jax.random.randint(jax.random.fold_in(_rk, 8), (16,), 0, max(1, 375 // 4) + 1, jnp.int32)
        _ctx_1024P = jax.random.normal(jax.random.fold_in(_rk, 11), (16, 16, 256), jnp.float32)
        _ctx_1024c = jax.random.dirichlet(jax.random.fold_in(_rk, 511), 0.3 * jnp.ones((16,), jnp.float32), (16, 375))
        _ctx_1024t = jnp.einsum('bsk,bkd->bsd', _ctx_1024c, _ctx_1024P)
        _ctx_1024t = _ctx_1024t * jax.lax.rsqrt(jnp.mean(jnp.square(_ctx_1024t)) + 1e-12) * 0.953939
        ctx_1024 = 4.13588e-05 + 0.999923 * (_ctx_1024t + 0.3 * jax.random.normal(jax.random.fold_in(_rk, 611), (16, 375, 256), jnp.float32))
        _validS = jnp.arange(112)[None, :] < _lenS[:, None]
        _validS2 = jnp.arange(375)[None, :] < _lenS2[:, None]
        _causal = jnp.tril(jnp.ones((112, 112), dtype=bool))
        mask_BxSxS2_ik0 = jnp.where(jnp.broadcast_to(_validS2[:, None, :], (16, 112, 375)), 0, 1).astype(jnp.int32)
        return (x, ctx_1024, mask_BxSxS2_ik0)
    x, ctx_1024, mask_BxSxS2_ik0 = _rec_inputs()

    def _L0_attn_setup():
        import jax, jax.numpy as jnp
        import numpy as np
        import math
        _OFFSETS = list(range(41)) + [128, 96, 384]
        key = jax.random.key(seed)
        B, T, C, H = (1, 512, 256, 16)
        HD = C // H
        J = len(_OFFSETS)
        k0, k1, k2, k3 = jax.random.split(key, 4)
        x = jax.random.normal(k0, (B, T, C), jnp.float32)
        w_qkv = jax.random.normal(k1, (C, 3 * C), jnp.float32) / math.sqrt(C)
        w_out = jax.random.normal(k2, (C, C), jnp.float32) / math.sqrt(C)
        delta_vals = jnp.log1p(jnp.asarray(_OFFSETS, jnp.float32))
        alphas = jnp.concatenate([jnp.linspace(0.2, 2.0, H - 1) * 1.5, jnp.array([1.0], jnp.float32)])
        pos_bias = -delta_vals[:, None] * alphas[None, :]
        scale_embed = 0.05 * jax.random.normal(k3, (J, HD), jnp.float32)
        if_gain = jnp.ones((H,), jnp.float32)
        return {'x': x, 'w_qkv': w_qkv, 'w_out': w_out, 'pos_bias': pos_bias, 'scale_embed': scale_embed, 'if_gain': if_gain}
    _L0_attn_all = _L0_attn_setup()
    _L0_attn_in = {k: v for k, v in _L0_attn_all.items() if k in ('w_qkv', 'w_out', 'pos_bias', 'scale_embed', 'if_gain')}
    del _L0_attn_all

    def _L0_xattn_setup():
        import jax, jax.numpy as jnp
        import numpy as np
        DIM = 256
        HEADS = 16
        DIM_HEAD = 64
        INNER = HEADS * DIM_HEAD
        MLP = 1024
        EPS = 1e-05

        def _layernorm(x, g, b):
            mu = jnp.mean(x, axis=-1, keepdims=True)
            var = jnp.mean(jnp.square(x - mu), axis=-1, keepdims=True)
            return (x - mu) * jax.lax.rsqrt(var + EPS) * g + b

        def _l2norm(x):
            n = jnp.sqrt(jnp.sum(jnp.square(x), axis=-1, keepdims=True))
            return x / jnp.maximum(n, 1e-12)

        def _split_heads(x, B, N):
            return x.reshape(B, N, HEADS, DIM_HEAD).transpose(0, 2, 1, 3)
        key = jax.random.key(seed)
        ks = jax.random.split(key, 16)
        B, N = (4, 512)
        s = 0.02
        return {'Q': jax.random.normal(ks[0], (B, N, DIM), jnp.float32), 'K': jax.random.normal(ks[1], (B, N, DIM), jnp.float32), 'V': jax.random.normal(ks[2], (B, N, DIM), jnp.float32), 'wq': jax.random.normal(ks[3], (DIM, INNER), jnp.float32) * s, 'wk': jax.random.normal(ks[4], (DIM, INNER), jnp.float32) * s, 'wv': jax.random.normal(ks[5], (DIM, INNER), jnp.float32) * s, 'wo': jax.random.normal(ks[6], (INNER, DIM), jnp.float32) * s, 'bo': jnp.zeros((DIM,), jnp.float32), 'w1': jax.random.normal(ks[7], (DIM, MLP), jnp.float32) * s, 'b1': jnp.zeros((MLP,), jnp.float32), 'w2': jax.random.normal(ks[8], (MLP, DIM), jnp.float32) * s, 'b2': jnp.zeros((DIM,), jnp.float32), 'ln1_g': jnp.ones((DIM,), jnp.float32), 'ln1_b': jnp.zeros((DIM,), jnp.float32), 'ln2_g': jnp.ones((DIM,), jnp.float32), 'ln2_b': jnp.zeros((DIM,), jnp.float32)}
    _L0_xattn_all = _L0_xattn_setup()
    _L0_xattn_in = {k: v for k, v in _L0_xattn_all.items() if k in ('wq', 'wk', 'wv', 'wo', 'bo', 'w1', 'b1', 'w2', 'b2', 'ln1_g', 'ln1_b', 'ln2_g', 'ln2_b')}
    del _L0_xattn_all

    def _L0_ffn_setup():
        import jax, jax.numpy as jnp
        import numpy as np
        D_MODEL = 256
        D1, D2 = (32, 32)
        F1, F2 = (64, 64)
        E = 64
        TOP_K = 2

        def kmoe(x_flat, W_router, A, B, scale, bias, d_in1, d_in2, d_out1, d_out2, top_k):
            logits = x_flat @ W_router.T
            vals, idx = jax.lax.top_k(logits, top_k)
            probs = jax.nn.softmax(vals, axis=-1)
            xs = x_flat.reshape(-1, d_in1, d_in2)
            Ag = A[idx]
            Bg = B[idx]
            Y = jnp.einsum('nkoi,nij,nkpj->nkop', Ag, xs, Bg)
            out = jnp.einsum('nkop,nk->nop', Y, probs).reshape(-1, d_out1 * d_out2)
            return out * scale + bias
        key = jax.random.key(seed)
        ks = jax.random.split(key, 12)
        s = 0.02
        return {'x': jax.random.normal(ks[0], (4, 512, D_MODEL), dtype=jnp.float32), 'W_up': jax.random.normal(ks[1], (E, D1 * D2), dtype=jnp.float32) * s, 'A_up': jax.random.normal(ks[2], (E, F1, D1), dtype=jnp.float32) * s, 'B_up': jax.random.normal(ks[3], (E, F2, D2), dtype=jnp.float32) * s, 'scale_up': jnp.ones((1,), dtype=jnp.float32), 'bias_up': jnp.zeros((F1 * F2,), dtype=jnp.float32), 'W_down': jax.random.normal(ks[4], (E, F1 * F2), dtype=jnp.float32) * s, 'A_down': jax.random.normal(ks[5], (E, D1, F1), dtype=jnp.float32) * s, 'B_down': jax.random.normal(ks[6], (E, D2, F2), dtype=jnp.float32) * s, 'scale_down': jnp.ones((1,), dtype=jnp.float32), 'bias_down': jnp.zeros((D1 * D2,), dtype=jnp.float32)}
    _L0_ffn_all = _L0_ffn_setup()
    _L0_ffn_in = {k: v for k, v in _L0_ffn_all.items() if k in ('W_up', 'A_up', 'B_up', 'scale_up', 'bias_up', 'W_down', 'A_down', 'B_down', 'scale_down', 'bias_down')}
    del _L0_ffn_all

    def _L1_attn_setup():
        import jax, jax.numpy as jnp
        import numpy as np
        D_MODEL = 256
        D_STATE = 128
        key = jax.random.key(seed)
        ks = jax.random.split(key, 16)
        dm, ds = (D_MODEL, D_STATE)

        def lin(kw, kb, out_f, in_f):
            bound = 1.0 / np.sqrt(in_f)
            W = jax.random.uniform(kw, (out_f, in_f), jnp.float32, -bound, bound)
            b = jax.random.uniform(kb, (out_f,), jnp.float32, -bound, bound)
            return (W, b)
        x = jax.random.normal(ks[0], (8, 512, dm), jnp.float32)
        A = jax.random.normal(ks[1], (ds, ds), jnp.float32) * 0.05
        B_w, B_b = lin(ks[2], ks[3], ds, dm)
        C_w, C_b = lin(ks[4], ks[5], dm, ds)
        D_w, D_b = lin(ks[6], ks[7], dm, dm)
        s_w1, s_b1 = lin(ks[8], ks[9], dm // 2, dm)
        s_w2, s_b2 = lin(ks[10], ks[11], ds, dm // 2)
        g_w, g_b = lin(ks[12], ks[13], dm, dm)
        return {'x': x, 'A': A, 'B_w': B_w, 'B_b': B_b, 'C_w': C_w, 'C_b': C_b, 'D_w': D_w, 'D_b': D_b, 's_w1': s_w1, 's_b1': s_b1, 's_w2': s_w2, 's_b2': s_b2, 'g_w': g_w, 'g_b': g_b}
    _L1_attn_all = _L1_attn_setup()
    _L1_attn_in = {k: v for k, v in _L1_attn_all.items() if k in ('A', 'B_w', 'B_b', 'C_w', 'C_b', 'D_w', 'D_b', 's_w1', 's_b1', 's_w2', 's_b2', 'g_w', 'g_b')}
    del _L1_attn_all

    def _L1_xattn_setup():
        import jax, jax.numpy as jnp
        import numpy as np
        import math
        B, N, M, D, HID, OUT = (8, 512, 512, 256, 256, 256)
        key = jax.random.key(seed)
        k1, k2, k3, k4, k5, k6 = jax.random.split(key, 6)
        h1 = jax.random.normal(k1, (B, N, D), dtype=jnp.float32)
        h2 = jax.random.normal(k2, (B, M, D), dtype=jnp.float32)
        mask = jax.random.randint(k3, (B, N, M), 0, 2, dtype=jnp.int32)
        Wq = jax.random.normal(k4, (HID, D), dtype=jnp.float32) / math.sqrt(D)
        Wk = jax.random.normal(k5, (HID, D), dtype=jnp.float32) / math.sqrt(D)
        Wv = jax.random.normal(k6, (OUT, D), dtype=jnp.float32) / math.sqrt(D)
        return {'h1': h1, 'h2': h2, 'mask': mask, 'Wq': Wq, 'Wk': Wk, 'Wv': Wv}
    _L1_xattn_all = _L1_xattn_setup()
    _L1_xattn_in = {k: v for k, v in _L1_xattn_all.items() if k in ('Wq', 'Wk', 'Wv')}
    del _L1_xattn_all

    def _L1_ffn_setup():
        import jax, jax.numpy as jnp
        import numpy as np
        DIM = 256
        MOE_HID = 128
        SHARED_HID = 512
        N_EXPERTS = 16
        TOP_K = 2
        NORM_TOPK_PROB = True
        key = jax.random.key(seed)
        ks = jax.random.split(key, 9)
        s = 0.02
        x = jax.random.normal(ks[0], (2, 256, DIM), dtype=jnp.float32)
        Wg = jax.random.normal(ks[1], (N_EXPERTS, DIM), dtype=jnp.float32) * s
        We_gate = jax.random.normal(ks[2], (N_EXPERTS, MOE_HID, DIM), dtype=jnp.float32) * s
        We_up = jax.random.normal(ks[3], (N_EXPERTS, MOE_HID, DIM), dtype=jnp.float32) * s
        We_down = jax.random.normal(ks[4], (N_EXPERTS, DIM, MOE_HID), dtype=jnp.float32) * s
        Ws_gate = jax.random.normal(ks[5], (SHARED_HID, DIM), dtype=jnp.float32) * s
        Ws_up = jax.random.normal(ks[6], (SHARED_HID, DIM), dtype=jnp.float32) * s
        Ws_down = jax.random.normal(ks[7], (DIM, SHARED_HID), dtype=jnp.float32) * s
        Wsg = jax.random.normal(ks[8], (1, DIM), dtype=jnp.float32) * s
        return {'x': x, 'Wg': Wg, 'We_gate': We_gate, 'We_up': We_up, 'We_down': We_down, 'Ws_gate': Ws_gate, 'Ws_up': Ws_up, 'Ws_down': Ws_down, 'Wsg': Wsg}
    _L1_ffn_all = _L1_ffn_setup()
    _L1_ffn_in = {k: v for k, v in _L1_ffn_all.items() if k in ('Wg', 'We_gate', 'We_up', 'We_down', 'Ws_gate', 'Ws_up', 'Ws_down', 'Wsg')}
    del _L1_ffn_all

    def _L2_attn_setup():
        import jax, jax.numpy as jnp
        import numpy as np
        B, N, D, H = (4, 512, 256, 8)
        HD = D // H
        TEMPER = 1.0
        LN_EPS = 1e-05

        def _leaky(x):
            return jnp.where(x > 0, x, 0.01 * x)
        key = jax.random.key(seed)
        ks = jax.random.split(key, 6)
        return {'h': jax.random.normal(ks[0], (B, N, D), dtype=jnp.float32), 'Wl': jax.random.normal(ks[1], (D, D), dtype=jnp.float32) * D ** (-0.5), 'Wr': jax.random.normal(ks[2], (D, D), dtype=jnp.float32) * D ** (-0.5), 'att_l': jax.random.normal(ks[3], (1, HD), dtype=jnp.float32) * HD ** (-0.5), 'att_r': jax.random.normal(ks[4], (1, HD), dtype=jnp.float32) * HD ** (-0.5), 'Wf': jax.random.normal(ks[5], (D, D), dtype=jnp.float32) * D ** (-0.5), 'ln_gamma': jnp.ones((D,), dtype=jnp.float32), 'ln_beta': jnp.zeros((D,), dtype=jnp.float32)}
    _L2_attn_all = _L2_attn_setup()
    _L2_attn_in = {k: v for k, v in _L2_attn_all.items() if k in ('Wl', 'Wr', 'att_l', 'att_r', 'Wf', 'ln_gamma', 'ln_beta')}
    del _L2_attn_all

    def _L2_xattn_setup():
        import jax, jax.numpy as jnp
        import numpy as np
        D_MODEL = 256
        HEADS = 16
        D_K = D_MODEL // HEADS
        LN_EPS = 1e-06
        NEG_INF = -1000000000.0

        def _layernorm(x, scale, bias):
            mu = jnp.mean(x, axis=-1, keepdims=True)
            var = jnp.var(x, axis=-1, keepdims=True)
            return (x - mu) * jax.lax.rsqrt(var + LN_EPS) * scale + bias
        key = jax.random.key(seed)
        ks = jax.random.split(key, 8)
        bs, sq, skv = (4, 512, 512)
        init = 1.0 / np.sqrt(D_MODEL)
        return {'kv': jax.random.normal(ks[0], (bs, skv, D_MODEL), jnp.float32), 'q': jax.random.normal(ks[1], (bs, sq, D_MODEL), jnp.float32), 'mask': jax.random.randint(ks[2], (bs, sq, skv), 0, 2, jnp.int32), 'Wq': jax.random.normal(ks[3], (D_MODEL, D_MODEL), jnp.float32) * init, 'bq': jnp.zeros((D_MODEL,), jnp.float32), 'Wk': jax.random.normal(ks[4], (D_MODEL, D_MODEL), jnp.float32) * init, 'bk': jnp.zeros((D_MODEL,), jnp.float32), 'Wv': jax.random.normal(ks[5], (D_MODEL, D_MODEL), jnp.float32) * init, 'bv': jnp.zeros((D_MODEL,), jnp.float32), 'qn_scale': jnp.ones((D_MODEL,), jnp.float32), 'qn_bias': jnp.zeros((D_MODEL,), jnp.float32), 'kn_scale': jnp.ones((D_MODEL,), jnp.float32), 'kn_bias': jnp.zeros((D_MODEL,), jnp.float32), 'vn_scale': jnp.ones((D_MODEL,), jnp.float32), 'vn_bias': jnp.zeros((D_MODEL,), jnp.float32), 'Wo': jax.random.normal(ks[6], (D_MODEL, D_MODEL), jnp.float32) * init, 'bo': jnp.zeros((D_MODEL,), jnp.float32)}
    _L2_xattn_all = _L2_xattn_setup()
    _L2_xattn_in = {k: v for k, v in _L2_xattn_all.items() if k in ('Wq', 'bq', 'Wk', 'bk', 'Wv', 'bv', 'qn_scale', 'qn_bias', 'kn_scale', 'kn_bias', 'vn_scale', 'vn_bias', 'Wo', 'bo')}
    del _L2_xattn_all

    def _L2_ffn_setup():
        import jax, jax.numpy as jnp
        import numpy as np
        DIM = 256
        HIDDEN = 1024
        N_EXPERTS = 8
        K = 2
        TEMP = 1.0

        def _expert_ffn(xf, wa, ba, wb, bb):
            h = xf @ wa.T + ba
            h1, h2 = jnp.split(h, 2, axis=-1)
            h = jax.nn.silu(h1) * h2
            return h @ wb.T + bb
        key = jax.random.key(seed)
        ks = jax.random.split(key, 7)
        s = 0.02
        x = jax.random.normal(ks[0], (4, 512, DIM), dtype=jnp.float32)
        router_w = jax.random.normal(ks[1], (N_EXPERTS, DIM), dtype=jnp.float32) * s
        router_b = jnp.zeros((N_EXPERTS,), dtype=jnp.float32)
        w1 = jax.random.normal(ks[2], (N_EXPERTS, 2 * HIDDEN, DIM), dtype=jnp.float32) * s
        b1 = jnp.zeros((N_EXPERTS, 2 * HIDDEN), dtype=jnp.float32)
        w2 = jax.random.normal(ks[3], (N_EXPERTS, DIM, HIDDEN), dtype=jnp.float32) * s
        b2 = jnp.zeros((N_EXPERTS, DIM), dtype=jnp.float32)
        return {'x': x, 'router_w': router_w, 'router_b': router_b, 'w1': w1, 'b1': b1, 'w2': w2, 'b2': b2}
    _L2_ffn_all = _L2_ffn_setup()
    _L2_ffn_in = {k: v for k, v in _L2_ffn_all.items() if k in ('router_w', 'router_b', 'w1', 'b1', 'w2', 'b2')}
    del _L2_ffn_all

    def _L3_attn_setup():
        import jax, jax.numpy as jnp
        import numpy as np
        B, S, D, H, I, A = (2, 512, 256, 16, 1024, 2)
        HD = D // H

        def _gen_param(sub, Wl, W, Bp):
            p = jnp.einsum('a...,a->...', sub, Wl[0])
            return jnp.tanh(p) * W + Bp

        def _student_linear(x, sub_w, Wl_w, W_w, B_w, sub_b, Wl_b, W_b, B_b):
            w = _gen_param(sub_w, Wl_w, W_w, B_w)
            b = _gen_param(sub_b, Wl_b, W_b, B_b)
            return x @ w.T + b

        def _layernorm(x, g, b, eps=1e-05):
            m = jnp.mean(x, axis=-1, keepdims=True)
            v = jnp.mean((x - m) ** 2, axis=-1, keepdims=True)
            return (x - m) * jax.lax.rsqrt(v + eps) * g + b

        def _gelu_new(x):
            c = 0.7978845608028654
            return 0.5 * x * (1.0 + jnp.tanh(c * (x + 0.044715 * x ** 3)))

        def _block(hs, ln1_g, ln1_b, ln2_g, ln2_b, *p):
            ca, cp, cf, cm = (p[0:8], p[8:16], p[16:24], p[24:32])
            b_, s_, d_ = hs.shape
            h = _layernorm(hs, ln1_g, ln1_b)
            qkv = _student_linear(h, *ca)
            q, k, v = jnp.split(qkv, 3, axis=-1)
            split = lambda t: t.reshape(b_, s_, H, HD).transpose(0, 2, 1, 3)
            q, k, v = (split(q), split(k), split(v))
            scores = jnp.einsum('bhqd,bhkd->bhqk', q, k) / float(HD) ** 0.5
            causal = jnp.tril(jnp.ones((s_, s_), dtype=bool))
            scores = jnp.where(causal, scores, jnp.asarray(-10000.0, scores.dtype))
            attn = jax.nn.softmax(scores, axis=-1)
            o = jnp.einsum('bhqk,bhkd->bhqd', attn, v)
            o = o.transpose(0, 2, 1, 3).reshape(b_, s_, d_)
            o = _student_linear(o, *cp)
            hs = hs + o
            h2 = _layernorm(hs, ln2_g, ln2_b)
            m = _student_linear(h2, *cf)
            m = _gelu_new(m)
            m = _student_linear(m, *cm)
            return hs + m
        key = jax.random.key(seed)
        ks = iter(jax.random.split(key, 32))

        def lin(out_f, in_f):
            return {'sub_w': jax.random.normal(next(ks), (A, out_f, in_f), jnp.float32) * 0.02, 'Wl_w': jax.random.normal(next(ks), (1, A), jnp.float32) * 0.5, 'W_w': jnp.ones((out_f, in_f), jnp.float32), 'B_w': jnp.zeros((out_f, in_f), jnp.float32), 'sub_b': jax.random.normal(next(ks), (A, out_f), jnp.float32) * 0.02, 'Wl_b': jax.random.normal(next(ks), (1, A), jnp.float32) * 0.5, 'W_b': jnp.ones((out_f,), jnp.float32), 'B_b': jnp.zeros((out_f,), jnp.float32)}
        inp = {'hs': jax.random.normal(next(ks), (B, S, D), jnp.float32)}
        for name, (o, i) in (('ca', (3 * D, D)), ('cp', (D, D)), ('cf', (I, D)), ('cm', (D, I))):
            for k2, v in lin(o, i).items():
                inp[name + '_' + k2] = v
        inp['ln1_g'] = jnp.ones((D,), jnp.float32)
        inp['ln1_b'] = jnp.zeros((D,), jnp.float32)
        inp['ln2_g'] = jnp.ones((D,), jnp.float32)
        inp['ln2_b'] = jnp.zeros((D,), jnp.float32)
        return inp
    _L3_attn_all = _L3_attn_setup()
    _L3_attn_in = {k: v for k, v in _L3_attn_all.items() if k in ('ln1_g', 'ln1_b', 'ln2_g', 'ln2_b', 'ca_sub_w', 'ca_Wl_w', 'ca_W_w', 'ca_B_w', 'ca_sub_b', 'ca_Wl_b', 'ca_W_b', 'ca_B_b', 'cp_sub_w', 'cp_Wl_w', 'cp_W_w', 'cp_B_w', 'cp_sub_b', 'cp_Wl_b', 'cp_W_b', 'cp_B_b', 'cf_sub_w', 'cf_Wl_w', 'cf_W_w', 'cf_B_w', 'cf_sub_b', 'cf_Wl_b', 'cf_W_b', 'cf_B_b', 'cm_sub_w', 'cm_Wl_w', 'cm_W_w', 'cm_B_w', 'cm_sub_b', 'cm_Wl_b', 'cm_W_b', 'cm_B_b')}
    del _L3_attn_all

    def _L3_xattn_setup():
        import jax, jax.numpy as jnp
        import numpy as np
        D_MODEL = 256
        NUM_HEADS = 16
        HEAD_DIM = D_MODEL // NUM_HEADS
        B, S = (4, 512)
        key = jax.random.key(seed)
        ks = jax.random.split(key, 11)
        scale = 1.0 / np.sqrt(D_MODEL)
        return {'query': jax.random.normal(ks[0], (B, S, D_MODEL), jnp.float32), 'key': jax.random.normal(ks[1], (B, S, D_MODEL), jnp.float32), 'value': jax.random.normal(ks[2], (B, S, D_MODEL), jnp.float32), 'Wq': jax.random.normal(ks[3], (D_MODEL, D_MODEL), jnp.float32) * scale, 'bq': jnp.zeros((D_MODEL,), jnp.float32), 'Wk': jax.random.normal(ks[4], (D_MODEL, D_MODEL), jnp.float32) * scale, 'bk': jnp.zeros((D_MODEL,), jnp.float32), 'Wv': jax.random.normal(ks[5], (D_MODEL, D_MODEL), jnp.float32) * scale, 'bv': jnp.zeros((D_MODEL,), jnp.float32), 'Wo': jax.random.normal(ks[6], (D_MODEL, D_MODEL), jnp.float32) * scale, 'bo': jnp.zeros((D_MODEL,), jnp.float32)}
    _L3_xattn_all = _L3_xattn_setup()
    _L3_xattn_in = {k: v for k, v in _L3_xattn_all.items() if k in ('Wq', 'bq', 'Wk', 'bk', 'Wv', 'bv', 'Wo', 'bo')}
    del _L3_xattn_all

    def _L3_ffn_setup():
        import jax, jax.numpy as jnp
        import numpy as np
        EPS = 1e-06
        LN_EPS = 1e-05

        def _absmean_core(W):
            gamma = jnp.mean(jnp.abs(W)) + EPS
            Ws = W / gamma
            Wq = jnp.sign(Ws) * jnp.minimum(jnp.round(jnp.abs(Ws)), 1.0)
            return (Wq, gamma)

        @jax.custom_vjp
        def absmean(W):
            return _absmean_core(W)[0]

        def _absmean_fwd(W):
            Wq, gamma = _absmean_core(W)
            return (Wq, gamma)

        def _absmean_bwd(gamma, g):
            return (g / gamma,)
        absmean.defvjp(_absmean_fwd, _absmean_bwd)

        def layernorm(x, w, b, eps=LN_EPS):
            mu = jnp.mean(x, axis=-1, keepdims=True)
            var = jnp.mean((x - mu) ** 2, axis=-1, keepdims=True)
            return (x - mu) * jax.lax.rsqrt(var + eps) * w + b
        key = jax.random.key(seed)
        k1, k2, k3 = jax.random.split(key, 3)
        d, h = (256, 1024)
        B, T = (8, 512)
        return {'x': jax.random.normal(k1, (B, T, d), jnp.float32), 'W_fc': jax.random.normal(k2, (h, d), jnp.float32), 'ln_w': jnp.ones((h,), jnp.float32), 'ln_b': jnp.zeros((h,), jnp.float32), 'W_proj': jax.random.normal(k3, (d, h), jnp.float32)}
    _L3_ffn_all = _L3_ffn_setup()
    _L3_ffn_in = {k: v for k, v in _L3_ffn_all.items() if k in ('W_fc', 'ln_w', 'ln_b', 'W_proj')}
    del _L3_ffn_all
    return {'x': x, 'ctx_1024': ctx_1024, 'mask_BxSxS2_ik0': mask_BxSxS2_ik0, 'L0_attn_w_qkv': _L0_attn_in['w_qkv'], 'L0_attn_w_out': _L0_attn_in['w_out'], 'L0_attn_pos_bias': _L0_attn_in['pos_bias'], 'L0_attn_scale_embed': _L0_attn_in['scale_embed'], 'L0_attn_if_gain': _L0_attn_in['if_gain'], 'L0_xattn_wq': _L0_xattn_in['wq'], 'L0_xattn_wk': _L0_xattn_in['wk'], 'L0_xattn_wv': _L0_xattn_in['wv'], 'L0_xattn_wo': _L0_xattn_in['wo'], 'L0_xattn_bo': _L0_xattn_in['bo'], 'L0_xattn_w1': _L0_xattn_in['w1'], 'L0_xattn_b1': _L0_xattn_in['b1'], 'L0_xattn_w2': _L0_xattn_in['w2'], 'L0_xattn_b2': _L0_xattn_in['b2'], 'L0_xattn_ln1_g': _L0_xattn_in['ln1_g'], 'L0_xattn_ln1_b': _L0_xattn_in['ln1_b'], 'L0_xattn_ln2_g': _L0_xattn_in['ln2_g'], 'L0_xattn_ln2_b': _L0_xattn_in['ln2_b'], 'L0_ffn_W_up': _L0_ffn_in['W_up'], 'L0_ffn_A_up': _L0_ffn_in['A_up'], 'L0_ffn_B_up': _L0_ffn_in['B_up'], 'L0_ffn_scale_up': _L0_ffn_in['scale_up'], 'L0_ffn_bias_up': _L0_ffn_in['bias_up'], 'L0_ffn_W_down': _L0_ffn_in['W_down'], 'L0_ffn_A_down': _L0_ffn_in['A_down'], 'L0_ffn_B_down': _L0_ffn_in['B_down'], 'L0_ffn_scale_down': _L0_ffn_in['scale_down'], 'L0_ffn_bias_down': _L0_ffn_in['bias_down'], 'L1_attn_A': _L1_attn_in['A'], 'L1_attn_B_w': _L1_attn_in['B_w'], 'L1_attn_B_b': _L1_attn_in['B_b'], 'L1_attn_C_w': _L1_attn_in['C_w'], 'L1_attn_C_b': _L1_attn_in['C_b'], 'L1_attn_D_w': _L1_attn_in['D_w'], 'L1_attn_D_b': _L1_attn_in['D_b'], 'L1_attn_s_w1': _L1_attn_in['s_w1'], 'L1_attn_s_b1': _L1_attn_in['s_b1'], 'L1_attn_s_w2': _L1_attn_in['s_w2'], 'L1_attn_s_b2': _L1_attn_in['s_b2'], 'L1_attn_g_w': _L1_attn_in['g_w'], 'L1_attn_g_b': _L1_attn_in['g_b'], 'L1_xattn_Wq': _L1_xattn_in['Wq'], 'L1_xattn_Wk': _L1_xattn_in['Wk'], 'L1_xattn_Wv': _L1_xattn_in['Wv'], 'L1_ffn_Wg': _L1_ffn_in['Wg'], 'L1_ffn_We_gate': _L1_ffn_in['We_gate'], 'L1_ffn_We_up': _L1_ffn_in['We_up'], 'L1_ffn_We_down': _L1_ffn_in['We_down'], 'L1_ffn_Ws_gate': _L1_ffn_in['Ws_gate'], 'L1_ffn_Ws_up': _L1_ffn_in['Ws_up'], 'L1_ffn_Ws_down': _L1_ffn_in['Ws_down'], 'L1_ffn_Wsg': _L1_ffn_in['Wsg'], 'L2_attn_Wl': _L2_attn_in['Wl'], 'L2_attn_Wr': _L2_attn_in['Wr'], 'L2_attn_att_l': _L2_attn_in['att_l'], 'L2_attn_att_r': _L2_attn_in['att_r'], 'L2_attn_Wf': _L2_attn_in['Wf'], 'L2_attn_ln_gamma': _L2_attn_in['ln_gamma'], 'L2_attn_ln_beta': _L2_attn_in['ln_beta'], 'L2_xattn_Wq': _L2_xattn_in['Wq'], 'L2_xattn_bq': _L2_xattn_in['bq'], 'L2_xattn_Wk': _L2_xattn_in['Wk'], 'L2_xattn_bk': _L2_xattn_in['bk'], 'L2_xattn_Wv': _L2_xattn_in['Wv'], 'L2_xattn_bv': _L2_xattn_in['bv'], 'L2_xattn_qn_scale': _L2_xattn_in['qn_scale'], 'L2_xattn_qn_bias': _L2_xattn_in['qn_bias'], 'L2_xattn_kn_scale': _L2_xattn_in['kn_scale'], 'L2_xattn_kn_bias': _L2_xattn_in['kn_bias'], 'L2_xattn_vn_scale': _L2_xattn_in['vn_scale'], 'L2_xattn_vn_bias': _L2_xattn_in['vn_bias'], 'L2_xattn_Wo': _L2_xattn_in['Wo'], 'L2_xattn_bo': _L2_xattn_in['bo'], 'L2_ffn_router_w': _L2_ffn_in['router_w'], 'L2_ffn_router_b': _L2_ffn_in['router_b'], 'L2_ffn_w1': _L2_ffn_in['w1'], 'L2_ffn_b1': _L2_ffn_in['b1'], 'L2_ffn_w2': _L2_ffn_in['w2'], 'L2_ffn_b2': _L2_ffn_in['b2'], 'L3_attn_ln1_g': _L3_attn_in['ln1_g'], 'L3_attn_ln1_b': _L3_attn_in['ln1_b'], 'L3_attn_ln2_g': _L3_attn_in['ln2_g'], 'L3_attn_ln2_b': _L3_attn_in['ln2_b'], 'L3_attn_ca_sub_w': _L3_attn_in['ca_sub_w'], 'L3_attn_ca_Wl_w': _L3_attn_in['ca_Wl_w'], 'L3_attn_ca_W_w': _L3_attn_in['ca_W_w'], 'L3_attn_ca_B_w': _L3_attn_in['ca_B_w'], 'L3_attn_ca_sub_b': _L3_attn_in['ca_sub_b'], 'L3_attn_ca_Wl_b': _L3_attn_in['ca_Wl_b'], 'L3_attn_ca_W_b': _L3_attn_in['ca_W_b'], 'L3_attn_ca_B_b': _L3_attn_in['ca_B_b'], 'L3_attn_cp_sub_w': _L3_attn_in['cp_sub_w'], 'L3_attn_cp_Wl_w': _L3_attn_in['cp_Wl_w'], 'L3_attn_cp_W_w': _L3_attn_in['cp_W_w'], 'L3_attn_cp_B_w': _L3_attn_in['cp_B_w'], 'L3_attn_cp_sub_b': _L3_attn_in['cp_sub_b'], 'L3_attn_cp_Wl_b': _L3_attn_in['cp_Wl_b'], 'L3_attn_cp_W_b': _L3_attn_in['cp_W_b'], 'L3_attn_cp_B_b': _L3_attn_in['cp_B_b'], 'L3_attn_cf_sub_w': _L3_attn_in['cf_sub_w'], 'L3_attn_cf_Wl_w': _L3_attn_in['cf_Wl_w'], 'L3_attn_cf_W_w': _L3_attn_in['cf_W_w'], 'L3_attn_cf_B_w': _L3_attn_in['cf_B_w'], 'L3_attn_cf_sub_b': _L3_attn_in['cf_sub_b'], 'L3_attn_cf_Wl_b': _L3_attn_in['cf_Wl_b'], 'L3_attn_cf_W_b': _L3_attn_in['cf_W_b'], 'L3_attn_cf_B_b': _L3_attn_in['cf_B_b'], 'L3_attn_cm_sub_w': _L3_attn_in['cm_sub_w'], 'L3_attn_cm_Wl_w': _L3_attn_in['cm_Wl_w'], 'L3_attn_cm_W_w': _L3_attn_in['cm_W_w'], 'L3_attn_cm_B_w': _L3_attn_in['cm_B_w'], 'L3_attn_cm_sub_b': _L3_attn_in['cm_sub_b'], 'L3_attn_cm_Wl_b': _L3_attn_in['cm_Wl_b'], 'L3_attn_cm_W_b': _L3_attn_in['cm_W_b'], 'L3_attn_cm_B_b': _L3_attn_in['cm_B_b'], 'L3_xattn_Wq': _L3_xattn_in['Wq'], 'L3_xattn_bq': _L3_xattn_in['bq'], 'L3_xattn_Wk': _L3_xattn_in['Wk'], 'L3_xattn_bk': _L3_xattn_in['bk'], 'L3_xattn_Wv': _L3_xattn_in['Wv'], 'L3_xattn_bv': _L3_xattn_in['bv'], 'L3_xattn_Wo': _L3_xattn_in['Wo'], 'L3_xattn_bo': _L3_xattn_in['bo'], 'L3_ffn_W_fc': _L3_ffn_in['W_fc'], 'L3_ffn_ln_w': _L3_ffn_in['ln_w'], 'L3_ffn_ln_b': _L3_ffn_in['ln_b'], 'L3_ffn_W_proj': _L3_ffn_in['W_proj']}

def reference(x, ctx_1024, mask_BxSxS2_ik0, L0_attn_w_qkv, L0_attn_w_out, L0_attn_pos_bias, L0_attn_scale_embed, L0_attn_if_gain, L0_xattn_wq, L0_xattn_wk, L0_xattn_wv, L0_xattn_wo, L0_xattn_bo, L0_xattn_w1, L0_xattn_b1, L0_xattn_w2, L0_xattn_b2, L0_xattn_ln1_g, L0_xattn_ln1_b, L0_xattn_ln2_g, L0_xattn_ln2_b, L0_ffn_W_up, L0_ffn_A_up, L0_ffn_B_up, L0_ffn_scale_up, L0_ffn_bias_up, L0_ffn_W_down, L0_ffn_A_down, L0_ffn_B_down, L0_ffn_scale_down, L0_ffn_bias_down, L1_attn_A, L1_attn_B_w, L1_attn_B_b, L1_attn_C_w, L1_attn_C_b, L1_attn_D_w, L1_attn_D_b, L1_attn_s_w1, L1_attn_s_b1, L1_attn_s_w2, L1_attn_s_b2, L1_attn_g_w, L1_attn_g_b, L1_xattn_Wq, L1_xattn_Wk, L1_xattn_Wv, L1_ffn_Wg, L1_ffn_We_gate, L1_ffn_We_up, L1_ffn_We_down, L1_ffn_Ws_gate, L1_ffn_Ws_up, L1_ffn_Ws_down, L1_ffn_Wsg, L2_attn_Wl, L2_attn_Wr, L2_attn_att_l, L2_attn_att_r, L2_attn_Wf, L2_attn_ln_gamma, L2_attn_ln_beta, L2_xattn_Wq, L2_xattn_bq, L2_xattn_Wk, L2_xattn_bk, L2_xattn_Wv, L2_xattn_bv, L2_xattn_qn_scale, L2_xattn_qn_bias, L2_xattn_kn_scale, L2_xattn_kn_bias, L2_xattn_vn_scale, L2_xattn_vn_bias, L2_xattn_Wo, L2_xattn_bo, L2_ffn_router_w, L2_ffn_router_b, L2_ffn_w1, L2_ffn_b1, L2_ffn_w2, L2_ffn_b2, L3_attn_ln1_g, L3_attn_ln1_b, L3_attn_ln2_g, L3_attn_ln2_b, L3_attn_ca_sub_w, L3_attn_ca_Wl_w, L3_attn_ca_W_w, L3_attn_ca_B_w, L3_attn_ca_sub_b, L3_attn_ca_Wl_b, L3_attn_ca_W_b, L3_attn_ca_B_b, L3_attn_cp_sub_w, L3_attn_cp_Wl_w, L3_attn_cp_W_w, L3_attn_cp_B_w, L3_attn_cp_sub_b, L3_attn_cp_Wl_b, L3_attn_cp_W_b, L3_attn_cp_B_b, L3_attn_cf_sub_w, L3_attn_cf_Wl_w, L3_attn_cf_W_w, L3_attn_cf_B_w, L3_attn_cf_sub_b, L3_attn_cf_Wl_b, L3_attn_cf_W_b, L3_attn_cf_B_b, L3_attn_cm_sub_w, L3_attn_cm_Wl_w, L3_attn_cm_W_w, L3_attn_cm_B_w, L3_attn_cm_sub_b, L3_attn_cm_Wl_b, L3_attn_cm_W_b, L3_attn_cm_B_b, L3_xattn_Wq, L3_xattn_bq, L3_xattn_Wk, L3_xattn_bk, L3_xattn_Wv, L3_xattn_bv, L3_xattn_Wo, L3_xattn_bo, L3_ffn_W_fc, L3_ffn_ln_w, L3_ffn_ln_b, L3_ffn_W_proj):
    import jax
    import jax.numpy as jnp

    def _L0_attn_ref(x, w_qkv, w_out, pos_bias, scale_embed, if_gain):
        import jax, jax.numpy as jnp
        import numpy as np
        import math
        _OFFSETS = list(range(41)) + [128, 96, 384]
        B, T, C = x.shape
        H = if_gain.shape[0]
        HD = C // H
        deltas = jnp.asarray(_OFFSETS)
        qkv = x @ w_qkv
        q, k, v = jnp.split(qkv, 3, axis=-1)
        q = q.reshape(B, T, H, HD).transpose(0, 2, 1, 3)
        k = k.reshape(B, T, H, HD).transpose(0, 2, 1, 3)
        v = v.reshape(B, T, H, HD).transpose(0, 2, 1, 3)
        idx = jnp.arange(T)[:, None] - deltas[None, :]
        valid = idx >= 0
        idxc = jnp.maximum(idx, 0)
        k_g = k[:, :, idxc]
        v_g = v[:, :, idxc]
        k_mod = k_g * (1.0 + scale_embed)
        scale = 1.0 / math.sqrt(HD)
        scores = jnp.einsum('bhtd,bhtjd->bhtj', q, k_mod) * scale
        scores = scores + pos_bias.T[None, :, None, :]
        scores = jnp.where(valid[None, None], scores, jnp.finfo(scores.dtype).min)
        attn = jax.nn.softmax(scores, axis=-1)
        out = jnp.einsum('bhtj,bhtjd->bhtd', attn, v_g)
        out = out * if_gain[None, :, None, None]
        out = out.transpose(0, 2, 1, 3).reshape(B, T, C)
        return out @ w_out

    def _L0_xattn_ref(Q, K, V, wq, wk, wv, wo, bo, w1, b1, w2, b2, ln1_g, ln1_b, ln2_g, ln2_b):
        import jax, jax.numpy as jnp
        import numpy as np
        DIM = 256
        HEADS = 16
        DIM_HEAD = 64
        INNER = HEADS * DIM_HEAD
        MLP = 1024
        EPS = 1e-05

        def _layernorm(x, g, b):
            mu = jnp.mean(x, axis=-1, keepdims=True)
            var = jnp.mean(jnp.square(x - mu), axis=-1, keepdims=True)
            return (x - mu) * jax.lax.rsqrt(var + EPS) * g + b

        def _l2norm(x):
            n = jnp.sqrt(jnp.sum(jnp.square(x), axis=-1, keepdims=True))
            return x / jnp.maximum(n, 1e-12)

        def _split_heads(x, B, N):
            return x.reshape(B, N, HEADS, DIM_HEAD).transpose(0, 2, 1, 3)
        B, Nq, _ = Q.shape
        Nk = K.shape[1]
        Qn = _layernorm(Q, ln1_g, ln1_b)
        Kn = _layernorm(K, ln1_g, ln1_b)
        Vn = _layernorm(V, ln1_g, ln1_b)
        q = _split_heads(Qn @ wq, B, Nq)
        k = _split_heads(Kn @ wk, B, Nk)
        v = _split_heads(Vn @ wv, B, Nk)
        qn = _l2norm(q)
        kn = _l2norm(k)
        attn = jnp.einsum('bhqd,bhkd->bhqk', qn, kn)
        out = jnp.einsum('bhqk,bhkd->bhqd', attn, v)
        out = out.transpose(0, 2, 1, 3).reshape(B, Nq, INNER)
        x = Q + out @ wo + bo
        xn = _layernorm(x, ln2_g, ln2_b)
        h = jax.nn.gelu(xn @ w1 + b1, approximate=False)
        return x + h @ w2 + b2

    def _L0_ffn_ref(x, W_up, A_up, B_up, scale_up, bias_up, W_down, A_down, B_down, scale_down, bias_down):
        import jax, jax.numpy as jnp
        import numpy as np
        D_MODEL = 256
        D1, D2 = (32, 32)
        F1, F2 = (64, 64)
        E = 64
        TOP_K = 2

        def kmoe(x_flat, W_router, A, B, scale, bias, d_in1, d_in2, d_out1, d_out2, top_k):
            logits = x_flat @ W_router.T
            vals, idx = jax.lax.top_k(logits, top_k)
            probs = jax.nn.softmax(vals, axis=-1)
            xs = x_flat.reshape(-1, d_in1, d_in2)
            Ag = A[idx]
            Bg = B[idx]
            Y = jnp.einsum('nkoi,nij,nkpj->nkop', Ag, xs, Bg)
            out = jnp.einsum('nkop,nk->nop', Y, probs).reshape(-1, d_out1 * d_out2)
            return out * scale + bias
        orig_shape = x.shape
        x_flat = x.reshape(-1, D1 * D2)
        h = kmoe(x_flat, W_up, A_up, B_up, scale_up, bias_up, D1, D2, F1, F2, TOP_K)
        h = jax.nn.gelu(h, approximate=False)
        y = kmoe(h, W_down, A_down, B_down, scale_down, bias_down, F1, F2, D1, D2, TOP_K)
        return y.reshape(*orig_shape[:-1], D_MODEL)

    def _L1_attn_ref(x, A, B_w, B_b, C_w, C_b, D_w, D_b, s_w1, s_b1, s_w2, s_b2, g_w, g_b):
        import jax, jax.numpy as jnp
        import numpy as np
        D_MODEL = 256
        D_STATE = 128
        s = jax.nn.sigmoid(jax.nn.silu(jnp.einsum('btd,hd->bth', x, s_w1) + s_b1) @ s_w2.T + s_b2)
        Bt = jnp.einsum('btd,sd->bts', x, B_w) + B_b
        u = Bt * s
        h0 = jnp.zeros((x.shape[0], A.shape[0]), x.dtype)

        def step(h, u_t):
            h = h @ A.T + u_t
            return (h, h)
        _, hs = jax.lax.scan(step, h0, jnp.swapaxes(u, 0, 1))
        hs = jnp.swapaxes(hs, 0, 1)
        y = jnp.einsum('bts,ds->btd', hs, C_w) + C_b + jnp.einsum('btd,ed->bte', x, D_w) + D_b
        gate = jax.nn.sigmoid(jnp.einsum('btd,ed->bte', x, g_w) + g_b)
        return y * gate

    def _L1_xattn_ref(h1, h2, mask, Wq, Wk, Wv):
        import jax, jax.numpy as jnp
        import numpy as np
        import math
        B, N, M, D, HID, OUT = (8, 512, 512, 256, 256, 256)
        Q = jnp.einsum('bnd,hd->bnh', h1, Wq)
        K = jnp.einsum('bmd,hd->bmh', h2, Wk)
        V = jnp.einsum('bmd,od->bmo', h2, Wv)
        E = jnp.einsum('bnh,bmh->bnm', Q, K)
        E = jnp.where(mask == 0, jnp.float32(-10000000000.0), E)
        A = jax.nn.softmax(E / math.sqrt(HID), axis=2)
        return jnp.einsum('bnm,bmo->bno', A, V)

    def _L1_ffn_ref(x, Wg, We_gate, We_up, We_down, Ws_gate, Ws_up, Ws_down, Wsg):
        import jax, jax.numpy as jnp
        import numpy as np
        DIM = 256
        MOE_HID = 128
        SHARED_HID = 512
        N_EXPERTS = 16
        TOP_K = 2
        NORM_TOPK_PROB = True
        B, S, D = x.shape
        xt = x.reshape(-1, D)
        gates = jax.nn.softmax(xt @ Wg.T, axis=-1)
        scores, inds = jax.lax.top_k(gates, TOP_K)
        if NORM_TOPK_PROB:
            scores = scores / jnp.sum(scores, axis=-1, keepdims=True)
        g = jnp.einsum('td,ehd->teh', xt, We_gate)
        u = jnp.einsum('td,ehd->teh', xt, We_up)
        h = jax.nn.silu(g) * u
        y_all = jnp.einsum('teh,edh->ted', h, We_down)
        y_sel = jnp.take_along_axis(y_all, inds[:, :, None], axis=1)
        y = jnp.sum(y_sel * scores[:, :, None], axis=1)
        shared = jax.nn.silu(xt @ Ws_gate.T) * (xt @ Ws_up.T) @ Ws_down.T
        y = y + jax.nn.sigmoid(xt @ Wsg.T) * shared
        return y.reshape(B, S, D)

    def _L2_attn_ref(h, Wl, Wr, att_l, att_r, Wf, ln_gamma, ln_beta):
        import jax, jax.numpy as jnp
        import numpy as np
        B, N, D, H = (4, 512, 256, 8)
        HD = D // H
        TEMPER = 1.0
        LN_EPS = 1e-05

        def _leaky(x):
            return jnp.where(x > 0, x, 0.01 * x)
        b, n, d = h.shape
        fl = (h @ Wl.T).reshape(b, n, H, HD).transpose(0, 2, 1, 3)
        fr = (h @ Wr.T).reshape(b, n, H, HD).transpose(0, 2, 1, 3)
        sl = jnp.einsum('bhnd,d->bhn', _leaky(fl), att_l[0])
        sr = jnp.einsum('bhnd,d->bhn', _leaky(fr), att_r[0])
        score = (sl[:, :, :, None] + sr[:, :, None, :]) / TEMPER
        p = jax.nn.softmax(score, axis=-1)
        ctx = jnp.einsum('bhnm,bhmd->bhnd', p, fr)
        h_sa = ctx.transpose(0, 2, 1, 3).reshape(b, n, d)
        fh = h_sa @ Wf.T
        y = h + fh
        mu = jnp.mean(y, axis=-1, keepdims=True)
        var = jnp.mean(jnp.square(y - mu), axis=-1, keepdims=True)
        return (y - mu) * jax.lax.rsqrt(var + LN_EPS) * ln_gamma + ln_beta

    def _L2_xattn_ref(kv, q, mask, Wq, bq, Wk, bk, Wv, bv, qn_scale, qn_bias, kn_scale, kn_bias, vn_scale, vn_bias, Wo, bo):
        import jax, jax.numpy as jnp
        import numpy as np
        D_MODEL = 256
        HEADS = 16
        D_K = D_MODEL // HEADS
        LN_EPS = 1e-06
        NEG_INF = -1000000000.0

        def _layernorm(x, scale, bias):
            mu = jnp.mean(x, axis=-1, keepdims=True)
            var = jnp.var(x, axis=-1, keepdims=True)
            return (x - mu) * jax.lax.rsqrt(var + LN_EPS) * scale + bias
        bs = q.shape[0]
        query = _layernorm(q @ Wq + bq, qn_scale, qn_bias)
        key = _layernorm(kv @ Wk + bk, kn_scale, kn_bias)
        value = _layernorm(kv @ Wv + bv, vn_scale, vn_bias)
        query = query.reshape(bs, -1, HEADS, D_K).transpose(0, 2, 1, 3)
        key = key.reshape(bs, -1, HEADS, D_K).transpose(0, 2, 1, 3)
        value = value.reshape(bs, -1, HEADS, D_K).transpose(0, 2, 1, 3)
        scores = jnp.einsum('bhqd,bhkd->bhqk', query, key) / jnp.sqrt(jnp.asarray(D_K, query.dtype))
        m = mask[:, None, :, :]
        scores = jnp.where(m == 0, NEG_INF, scores)
        probs = jax.nn.softmax(scores, axis=-1)
        out = jnp.einsum('bhqk,bhkd->bhqd', probs, value)
        out = out.transpose(0, 2, 1, 3).reshape(bs, -1, D_MODEL)
        return out @ Wo + bo

    def _L2_ffn_ref(x, router_w, router_b, w1, b1, w2, b2):
        import jax, jax.numpy as jnp
        import numpy as np
        DIM = 256
        HIDDEN = 1024
        N_EXPERTS = 8
        K = 2
        TEMP = 1.0

        def _expert_ffn(xf, wa, ba, wb, bb):
            h = xf @ wa.T + ba
            h1, h2 = jnp.split(h, 2, axis=-1)
            h = jax.nn.silu(h1) * h2
            return h @ wb.T + bb
        b, t, d = x.shape
        logits = (x @ router_w.T + router_b) / TEMP
        topk_val, topk_idx = jax.lax.top_k(logits, K)
        weights = jax.nn.softmax(topk_val, axis=-1)
        xf = x.reshape(-1, d)
        outs = jax.vmap(_expert_ffn, in_axes=(None, 0, 0, 0, 0))(xf, w1, b1, w2, b2)
        outs = jnp.transpose(outs, (1, 0, 2))
        idx = topk_idx.reshape(-1, K)
        gathered = jnp.take_along_axis(outs, idx[:, :, None], axis=1)
        combined = (gathered * weights.reshape(-1, K, 1)).sum(axis=1)
        return combined.reshape(b, t, d)

    def _L3_attn_ref(hs, ln1_g, ln1_b, ln2_g, ln2_b, ca_sub_w, ca_Wl_w, ca_W_w, ca_B_w, ca_sub_b, ca_Wl_b, ca_W_b, ca_B_b, cp_sub_w, cp_Wl_w, cp_W_w, cp_B_w, cp_sub_b, cp_Wl_b, cp_W_b, cp_B_b, cf_sub_w, cf_Wl_w, cf_W_w, cf_B_w, cf_sub_b, cf_Wl_b, cf_W_b, cf_B_b, cm_sub_w, cm_Wl_w, cm_W_w, cm_B_w, cm_sub_b, cm_Wl_b, cm_W_b, cm_B_b):
        import jax, jax.numpy as jnp
        import numpy as np
        B, S, D, H, I, A = (2, 512, 256, 16, 1024, 2)
        HD = D // H

        def _gen_param(sub, Wl, W, Bp):
            p = jnp.einsum('a...,a->...', sub, Wl[0])
            return jnp.tanh(p) * W + Bp

        def _student_linear(x, sub_w, Wl_w, W_w, B_w, sub_b, Wl_b, W_b, B_b):
            w = _gen_param(sub_w, Wl_w, W_w, B_w)
            b = _gen_param(sub_b, Wl_b, W_b, B_b)
            return x @ w.T + b

        def _layernorm(x, g, b, eps=1e-05):
            m = jnp.mean(x, axis=-1, keepdims=True)
            v = jnp.mean((x - m) ** 2, axis=-1, keepdims=True)
            return (x - m) * jax.lax.rsqrt(v + eps) * g + b

        def _gelu_new(x):
            c = 0.7978845608028654
            return 0.5 * x * (1.0 + jnp.tanh(c * (x + 0.044715 * x ** 3)))

        def _block(hs, ln1_g, ln1_b, ln2_g, ln2_b, *p):
            ca, cp, cf, cm = (p[0:8], p[8:16], p[16:24], p[24:32])
            b_, s_, d_ = hs.shape
            h = _layernorm(hs, ln1_g, ln1_b)
            qkv = _student_linear(h, *ca)
            q, k, v = jnp.split(qkv, 3, axis=-1)
            split = lambda t: t.reshape(b_, s_, H, HD).transpose(0, 2, 1, 3)
            q, k, v = (split(q), split(k), split(v))
            scores = jnp.einsum('bhqd,bhkd->bhqk', q, k) / float(HD) ** 0.5
            causal = jnp.tril(jnp.ones((s_, s_), dtype=bool))
            scores = jnp.where(causal, scores, jnp.asarray(-10000.0, scores.dtype))
            attn = jax.nn.softmax(scores, axis=-1)
            o = jnp.einsum('bhqk,bhkd->bhqd', attn, v)
            o = o.transpose(0, 2, 1, 3).reshape(b_, s_, d_)
            o = _student_linear(o, *cp)
            hs = hs + o
            h2 = _layernorm(hs, ln2_g, ln2_b)
            m = _student_linear(h2, *cf)
            m = _gelu_new(m)
            m = _student_linear(m, *cm)
            return hs + m
        return _block(hs, ln1_g, ln1_b, ln2_g, ln2_b, ca_sub_w, ca_Wl_w, ca_W_w, ca_B_w, ca_sub_b, ca_Wl_b, ca_W_b, ca_B_b, cp_sub_w, cp_Wl_w, cp_W_w, cp_B_w, cp_sub_b, cp_Wl_b, cp_W_b, cp_B_b, cf_sub_w, cf_Wl_w, cf_W_w, cf_B_w, cf_sub_b, cf_Wl_b, cf_W_b, cf_B_b, cm_sub_w, cm_Wl_w, cm_W_w, cm_B_w, cm_sub_b, cm_Wl_b, cm_W_b, cm_B_b)

    def _L3_xattn_ref(query, key, value, Wq, bq, Wk, bk, Wv, bv, Wo, bo):
        import jax, jax.numpy as jnp
        import numpy as np
        D_MODEL = 256
        NUM_HEADS = 16
        HEAD_DIM = D_MODEL // NUM_HEADS
        B, S = (4, 512)
        b = query.shape[0]

        def split_heads(x):
            return x.reshape(b, -1, NUM_HEADS, HEAD_DIM).transpose(0, 2, 1, 3)
        q = split_heads(query @ Wq.T + bq)
        k = split_heads(key @ Wk.T + bk)
        v = split_heads(value @ Wv.T + bv)
        scores = jnp.einsum('bhqd,bhkd->bhqk', q, k) / np.sqrt(HEAD_DIM)
        weights = jax.nn.softmax(scores, axis=-1)
        out = jnp.einsum('bhqk,bhkd->bhqd', weights, v)
        out = out.transpose(0, 2, 1, 3).reshape(b, -1, D_MODEL)
        return out @ Wo.T + bo

    def _L3_ffn_ref(x, W_fc, ln_w, ln_b, W_proj):
        import jax, jax.numpy as jnp
        import numpy as np
        EPS = 1e-06
        LN_EPS = 1e-05

        def _absmean_core(W):
            gamma = jnp.mean(jnp.abs(W)) + EPS
            Ws = W / gamma
            Wq = jnp.sign(Ws) * jnp.minimum(jnp.round(jnp.abs(Ws)), 1.0)
            return (Wq, gamma)

        @jax.custom_vjp
        def absmean(W):
            return _absmean_core(W)[0]

        def _absmean_fwd(W):
            Wq, gamma = _absmean_core(W)
            return (Wq, gamma)

        def _absmean_bwd(gamma, g):
            return (g / gamma,)
        absmean.defvjp(_absmean_fwd, _absmean_bwd)

        def layernorm(x, w, b, eps=LN_EPS):
            mu = jnp.mean(x, axis=-1, keepdims=True)
            var = jnp.mean((x - mu) ** 2, axis=-1, keepdims=True)
            return (x - mu) * jax.lax.rsqrt(var + eps) * w + b
        h = jnp.einsum('btd,hd->bth', x, absmean(W_fc))
        h = jax.nn.gelu(h, approximate=False)
        h = layernorm(h, ln_w, ln_b)
        return jnp.einsum('bth,dh->btd', h, absmean(W_proj))
    x = x + _L0_attn_ref(_layernorm(x, axis=-1), L0_attn_w_qkv, L0_attn_w_out, L0_attn_pos_bias, L0_attn_scale_embed, L0_attn_if_gain)
    x = x + _L0_xattn_ref(_layernorm(x, axis=-1), ctx_1024, ctx_1024, L0_xattn_wq, L0_xattn_wk, L0_xattn_wv, L0_xattn_wo, L0_xattn_bo, L0_xattn_w1, L0_xattn_b1, L0_xattn_w2, L0_xattn_b2, L0_xattn_ln1_g, L0_xattn_ln1_b, L0_xattn_ln2_g, L0_xattn_ln2_b)
    x = x + _L0_ffn_ref(_layernorm(x, axis=-1), L0_ffn_W_up, L0_ffn_A_up, L0_ffn_B_up, L0_ffn_scale_up, L0_ffn_bias_up, L0_ffn_W_down, L0_ffn_A_down, L0_ffn_B_down, L0_ffn_scale_down, L0_ffn_bias_down)
    x = x + _L1_attn_ref(_layernorm(x, axis=-1), L1_attn_A, L1_attn_B_w, L1_attn_B_b, L1_attn_C_w, L1_attn_C_b, L1_attn_D_w, L1_attn_D_b, L1_attn_s_w1, L1_attn_s_b1, L1_attn_s_w2, L1_attn_s_b2, L1_attn_g_w, L1_attn_g_b)
    x = x + _L1_xattn_ref(_layernorm(x, axis=-1), ctx_1024, mask_BxSxS2_ik0, L1_xattn_Wq, L1_xattn_Wk, L1_xattn_Wv)
    x = x + _L1_ffn_ref(_layernorm(x, axis=-1), L1_ffn_Wg, L1_ffn_We_gate, L1_ffn_We_up, L1_ffn_We_down, L1_ffn_Ws_gate, L1_ffn_Ws_up, L1_ffn_Ws_down, L1_ffn_Wsg)
    x = x + _L2_attn_ref(_layernorm(x, axis=-1), L2_attn_Wl, L2_attn_Wr, L2_attn_att_l, L2_attn_att_r, L2_attn_Wf, L2_attn_ln_gamma, L2_attn_ln_beta)
    x = x + _L2_xattn_ref(ctx_1024, _layernorm(x, axis=-1), mask_BxSxS2_ik0, L2_xattn_Wq, L2_xattn_bq, L2_xattn_Wk, L2_xattn_bk, L2_xattn_Wv, L2_xattn_bv, L2_xattn_qn_scale, L2_xattn_qn_bias, L2_xattn_kn_scale, L2_xattn_kn_bias, L2_xattn_vn_scale, L2_xattn_vn_bias, L2_xattn_Wo, L2_xattn_bo)
    x = x + _L2_ffn_ref(_layernorm(x, axis=-1), L2_ffn_router_w, L2_ffn_router_b, L2_ffn_w1, L2_ffn_b1, L2_ffn_w2, L2_ffn_b2)
    x = x + _L3_attn_ref(_layernorm(x, axis=-1), L3_attn_ln1_g, L3_attn_ln1_b, L3_attn_ln2_g, L3_attn_ln2_b, L3_attn_ca_sub_w, L3_attn_ca_Wl_w, L3_attn_ca_W_w, L3_attn_ca_B_w, L3_attn_ca_sub_b, L3_attn_ca_Wl_b, L3_attn_ca_W_b, L3_attn_ca_B_b, L3_attn_cp_sub_w, L3_attn_cp_Wl_w, L3_attn_cp_W_w, L3_attn_cp_B_w, L3_attn_cp_sub_b, L3_attn_cp_Wl_b, L3_attn_cp_W_b, L3_attn_cp_B_b, L3_attn_cf_sub_w, L3_attn_cf_Wl_w, L3_attn_cf_W_w, L3_attn_cf_B_w, L3_attn_cf_sub_b, L3_attn_cf_Wl_b, L3_attn_cf_W_b, L3_attn_cf_B_b, L3_attn_cm_sub_w, L3_attn_cm_Wl_w, L3_attn_cm_W_w, L3_attn_cm_B_w, L3_attn_cm_sub_b, L3_attn_cm_Wl_b, L3_attn_cm_W_b, L3_attn_cm_B_b)
    x = x + _L3_xattn_ref(_layernorm(x, axis=-1), ctx_1024, ctx_1024, L3_xattn_Wq, L3_xattn_bq, L3_xattn_Wk, L3_xattn_bk, L3_xattn_Wv, L3_xattn_bv, L3_xattn_Wo, L3_xattn_bo)
    x = x + _L3_ffn_ref(_layernorm(x, axis=-1), L3_ffn_W_fc, L3_ffn_ln_w, L3_ffn_ln_b, L3_ffn_W_proj)
    return x

_drawn_inputs = setup_inputs


def setup_inputs(seed=0):
    import zlib

    import numpy as np

    out = dict(_drawn_inputs(seed))
    spreads = {'L0_attn_if_gain': (1.0, 0.2),
     'L0_xattn_bo': (0.0, 0.1),
     'L0_xattn_b1': (0.0, 0.625),
     'L0_xattn_b2': (0.0, 0.1),
     'L0_xattn_ln1_g': (1.0, 0.2),
     'L0_xattn_ln1_b': (0.0, 0.1),
     'L0_xattn_ln2_g': (1.0, 0.6),
     'L0_xattn_ln2_b': (0.0, 0.8),
     'L0_ffn_bias_up': (0.0, 0.8),
     'L0_ffn_bias_down': (0.0, 0.1),
     'L2_attn_ln_gamma': (1.0, 0.2),
     'L2_attn_ln_beta': (0.0, 0.1),
     'L2_xattn_bq': (0.0, 0.8),
     'L2_xattn_bk': (0.0, 0.8),
     'L2_xattn_bv': (0.0, 0.1),
     'L2_xattn_qn_scale': (1.0, 0.6),
     'L2_xattn_qn_bias': (0.0, 0.8),
     'L2_xattn_kn_scale': (1.0, 0.6),
     'L2_xattn_kn_bias': (0.0, 2.0),
     'L2_xattn_vn_scale': (1.0, 0.2),
     'L2_xattn_vn_bias': (0.0, 0.1),
     'L2_xattn_bo': (0.0, 0.1),
     'L2_ffn_router_b': (0.0, 0.706),
     'L2_ffn_b1': (0.0, 0.8),
     'L2_ffn_b2': (0.0, 1.18),
     'L3_attn_ln1_g': (1.0, 0.2),
     'L3_attn_ln1_b': (0.0, 0.1),
     'L3_attn_ln2_g': (1.0, 0.2),
     'L3_attn_ln2_b': (0.0, 0.315),
     'L3_attn_ca_W_w': (1.0, 0.2),
     'L3_attn_ca_B_w': (0.0, 0.1),
     'L3_attn_ca_W_b': (1.0, 0.6),
     'L3_attn_ca_B_b': (0.0, 0.271),
     'L3_attn_cp_W_w': (1.0, 0.6),
     'L3_attn_cp_B_w': (0.0, 0.1),
     'L3_attn_cp_W_b': (1.0, 0.6),
     'L3_attn_cp_B_b': (0.0, 0.8),
     'L3_attn_cf_W_w': (1.0, 0.6),
     'L3_attn_cf_B_w': (0.0, 0.1),
     'L3_attn_cf_W_b': (1.0, 0.6),
     'L3_attn_cf_B_b': (0.0, 0.619),
     'L3_attn_cm_W_w': (1.0, 0.599),
     'L3_attn_cm_B_w': (0.0, 0.1),
     'L3_attn_cm_W_b': (1.0, 0.6),
     'L3_attn_cm_B_b': (0.0, 1.415),
     'L3_xattn_bq': (0.0, 2.0),
     'L3_xattn_bk': (0.0, 2.0),
     'L3_xattn_bv': (0.0, 1.592),
     'L3_xattn_bo': (0.0, 1.35),
     'L3_ffn_ln_w': (1.0, 0.2),
     'L3_ffn_ln_b': (0.0, 0.1)}
    factors = {'L0_ffn_W_up': 8.0,
     'L0_ffn_A_up': 8.0,
     'L0_ffn_B_up': 8.0,
     'L0_ffn_W_down': 8.0,
     'L0_ffn_A_down': 8.0,
     'L0_ffn_B_down': 8.0,
     'L1_attn_B_b': 8.0,
     'L1_attn_C_b': 4.795,
     'L1_attn_D_b': 7.086,
     'L1_attn_s_w1': 8.0,
     'L1_attn_s_b1': 8.0,
     'L1_attn_s_w2': 8.0,
     'L1_attn_s_b2': 8.0,
     'L1_attn_g_b': 8.0,
     'L1_ffn_Wg': 8.0,
     'L1_ffn_We_gate': 8.0,
     'L1_ffn_We_up': 8.0,
     'L1_ffn_We_down': 8.0,
     'L1_ffn_Ws_gate': 8.0,
     'L1_ffn_Ws_up': 8.0,
     'L1_ffn_Ws_down': 8.0,
     'L1_ffn_Wsg': 8.0,
     'L2_attn_Wl': 200.0,
     'L2_attn_att_l': 200.0,
     'L2_ffn_router_w': 2.727,
     'L2_ffn_w1': 6.707,
     'L2_ffn_w2': 6.692,
     'L3_attn_ca_Wl_w': 7.265,
     'L3_attn_ca_sub_b': 6.491,
     'L3_attn_ca_Wl_b': 4.608,
     'L3_attn_cp_sub_b': 8.0,
     'L3_attn_cp_Wl_b': 8.0,
     'L3_attn_cf_Wl_w': 4.283,
     'L3_attn_cf_sub_b': 8.0,
     'L3_attn_cf_Wl_b': 8.0,
     'L3_attn_cm_sub_b': 8.0,
     'L3_attn_cm_Wl_b': 33.766,
     'L3_xattn_Wq': 4.135,
     'L3_xattn_Wk': 3.409}
    for name, (base, spread) in spreads.items():
        noise = np.random.default_rng([zlib.crc32(name.encode()), seed]).standard_normal(out[name].shape)
        drawn = base * np.exp(spread * noise) if base else spread * noise
        out[name] = jnp.asarray(drawn.astype(out[name].dtype))
    for name, factor in factors.items():
        out[name] = (out[name] * factor).astype(out[name].dtype)
    return out
```

```python
from contextlib import ExitStack

import concourse.bass as bass
from concourse import mybir
from concourse.alu_op_type import AluOpType as ALU

F32 = mybir.dt.float32
I32 = mybir.dt.int32
U32 = mybir.dt.uint32
ACT = mybir.ActivationFunctionType
AX = mybir.AxisListType

NB, T, D = 16, 112, 256
S = 375
ST, SP_ = 3, 125
U = 4
NCH = NB // U
N4 = U * T
KD = D // 128
DMA = 16


class Progress:

    def __init__(self, core, name, *steps):
        self.sem = core.semaphore(name)
        self.offset, self.per = {}, 0
        for s in steps:
            s, count = s if isinstance(s, tuple) else (s, U)
            self.offset[s] = (self.per, count)
            self.per += count
        self.raised = 0

    def step(self, step, u=0):
        at, count = self.offset[step]
        assert u < count and self.raised % self.per == at + u, (step, u, self.raised)
        self.raised += 1
        return self.sem

    def at(self, c, step, u=0):
        at, count = self.offset[step]
        assert u < count
        return c * self.per + (at + u + 1)


class Core:

    def __init__(self, nc, dram, stack):
        self.nc, self.dram = nc, dram
        self.stack, self.whole, self.stage, self.open = stack, stack, "core", []
        self.passed = {e: stack.enter_context(nc.semaphore(f"passed{i}")) for i, e in enumerate(
            (nc.sync, nc.scalar, nc.vector, nc.gpsimd, nc.tensor))}
        sb = lambda name, shape, dt=F32: stack.enter_context(nc.sbuf_tensor(name, shape, dt))
        self.x = sb("x", [T, NB, D])
        self.y = sb("y", [T, NB, D])
        self.ident = sb("ident", [128, 128])
        self.stats = sb("stats", [T, NB, 6])
        self.mean = sb("mean", [T, NB])
        self.rstd = sb("rstd", [T, NB])
        self.nsc = sb("nsc", [T, 5, NB])
        self.ones = sb("ones", [128, 128])
        self.mhalf = sb("mhalf", [128, 64])
        self.phalf = sb("phalf", [128, 64])
        self.arena = [sb(f"arena{i}", [128, ARENA]) for i in range(2)]
        self.ps = stack.enter_context(nc.psum_tensor("ps", [128, 8, 512], F32))
        self.constants = stack.enter_context(nc.semaphore("constants"))

    def semaphore(self, name):
        s = self.stack.enter_context(self.nc.semaphore(f"{self.stage}_{name}"))
        self.open.append(s.num)
        return s

    def pool_dma_semaphore(self, name):
        return self.whole.enter_context(self.nc.semaphore(f"{self.stage}_{name}"))

    def scratch(self, name, shape):
        return self.nc.dram_tensor(f"{self.stage}_{name}", shape, F32).ap()

    def stand(self, eng):
        eng.sem_inc(self.passed[eng], 1)


ARENA = 12800
EPS = 1e-5


class Arena:

    def __init__(self, core, i):
        self.t, self.at, self.loads = core.arena[i], 0, []

    def take(self, parts, *free):
        n = 1
        for f in free:
            n *= f
        v = self.t[0:parts, self.at:self.at + n]
        self.at += n
        assert self.at <= ARENA, self.at
        if len(free) == 2:
            v = v.rearrange("p (a b) -> p a b", a=free[0])
        if len(free) == 3:
            v = v.rearrange("p (a b c) -> p a b c", a=free[0], b=free[1])
        return v

    def load(self, src, parts, *free):
        v = self.take(parts, *free)
        self.loads.append((v, src))
        return v


def rows(ap, p=128):
    return ap.rearrange("(k p) n -> p k n", p=p)


def col(ap, p=128):
    return ap.rearrange("(k p) -> p k", p=p)


def every(ap, parts):
    n = 1
    for d in ap.shape:
        n *= d
    return bass.AP(ap.tensor, ap.offset, [[0, parts], [1, n]])


def norm_vector(core, dve, first, norm):
    nc, st, sc = core.nc, core.stats, core.nsc
    me, qe, mo, qo = (st[:, :, i] for i in (1, 2, 4, 5))
    nc.vector.tensor_tensor(sc[:, 0, :], me, mo, ALU.add).then_inc(norm, 1)
    nc.vector.tensor_tensor(sc[:, 1, :], me, mo, ALU.subtract).then_inc(norm, 1)
    nc.vector.tensor_tensor(sc[:, 2, :], qe, qo, ALU.add).then_inc(norm, 1)
    dve.wait_ge(norm, 3)
    nc.vector.tensor_scalar(core.mean[:, :], sc[:, 0, :], 0.5, None, ALU.mult).then_inc(norm, 1)
    nc.vector.tensor_tensor(sc[:, 3, :], sc[:, 1, :], sc[:, 1, :], ALU.mult).then_inc(norm, 1)
    nc.vector.tensor_scalar(sc[:, 4, :], sc[:, 2, :], 1.0 / D, EPS, ALU.mult, ALU.add).then_inc(norm, 1)
    dve.wait_ge(norm, 6)
    nc.vector.scalar_tensor_tensor(out=sc[:, 0, :], in0=sc[:, 3, :], scalar=0.25, in1=sc[:, 4, :],
                                   op0=ALU.mult, op1=ALU.add).then_inc(norm, 1)
    dve.wait_ge(norm, 8)


def norm_pool(core, norm):
    core.nc.gpsimd.wait_ge(norm, 7)
    core.nc.gpsimd.tensor_tensor(core.rstd[:, :], core.nsc[:, 0, :], core.mhalf[0:T, 0:NB],
                                 ALU.pow).then_inc(norm, 1)


def normed(core, out, n):
    return core.nc.vector.tensor_scalar(out, core.x[:, n, :], core.mean[:, bass.ds(n, 1)],
                                        core.rstd[:, bass.ds(n, 1)], ALU.subtract, ALU.mult)


def row_stats(core, dve, n):
    core.stand(dve)
    return core.nc.vector.bn_stats(core.stats[:, n, :], core.x[:, n, :])


def transposes(core, ps, src, rows_, parts):
    for k in range(parts):
        ins = core.nc.tensor.transpose(ps[:, k * rows_:(k + 1) * rows_], src[:, k * 128:(k + 1) * 128],
                                       core.ident[0:rows_, 0:rows_])
    return ins


class Norm:

    STEPS = ("st", "ag", ("eps", 1))

    def __init__(self, core, run, name, rows_=T, eps=EPS, parts=1, units=U):
        self.core, self.rows, self.eps, self.parts, self.units = core, rows_, eps, parts, units
        self.st = run.sbuf(name + "_st", [rows_, units, 6 * parts])
        self.mv = run.sbuf(name + "_mv", [rows_, units, 2])
        self.ve = run.sbuf(name + "_ve", [rows_, units])
        self.rs = run.sbuf(name + "_rs", [rows_, units])
        self.tag = name

    def steps(self, unit_count=None):
        n = self.units
        return ((self.tag + "st", n * self.parts), (self.tag + "ag", n), (self.tag + "eps", 1))

    def vector(self, dve, ve, c, src, ready):
        nc = self.core.nc
        for u in range(self.units):
            ready(u)
            for q in range(self.parts):
                nc.vector.bn_stats(self.st[:, u, 6 * q:6 * q + 6], src(u, q)).then_inc(ve.step(self.tag + "st", u * self.parts + q), 1)
        for u in range(self.units):
            dve.wait_ge(ve.sem, ve.at(c, self.tag + "st", u * self.parts + self.parts - 1))
            self.core.stand(dve)
            nc.vector.bn_aggr(self.mv[:, u, :], self.st[:, u, :]).then_inc(ve.step(self.tag + "ag", u), 1)
        dve.wait_ge(ve.sem, ve.at(c, self.tag + "ag", self.units - 1))
        nc.vector.tensor_scalar(self.ve[:, :], self.mv[:, :, 1], self.eps, None, ALU.add).then_inc(ve.step(self.tag + "eps"), 1)

    def pool(self, pool, ve, po, c):
        pool.wait_ge(ve.sem, ve.at(c, self.tag + "eps"))
        self.core.nc.gpsimd.tensor_tensor(self.rs[:, :], self.ve[:, :], self.core.mhalf[0:self.rows, 0:self.units],
                                                  ALU.pow).then_inc(po.step(self.tag + "rs"), 1)

    def apply(self, out, src, u):
        return self.core.nc.vector.tensor_scalar(out, src, self.mv[:, u, 0:1], self.rs[:, u:u + 1],
                                                 ALU.subtract, ALU.mult)


class L0Banded:

    name = "L0_attn"
    H = 16
    HD = D // H
    HK = H // KD
    NEAR = 41
    FAR = 96
    J = NEAR + 1
    DIST = (*range(NEAR - 1, -1, -1), FAR)
    ROWS = (*range(NEAR - 1, -1, -1), NEAR + 1)
    PAD = NEAR - 1
    GD = 128 // H
    NG = -(-J // GD)
    LEFT = 128 - HK

    def weights(self, a, d):
        n = self.name + "_"
        self.wqkv = a.load(rows(d[n + "w_qkv"]), 128, KD, 3 * D)
        self.wo = a.load(rows(d[n + "w_out"]), 128, KD, D)
        self.bias = a.load(every(d[n + "bias"], T), T, self.J * self.H)
        self.se = a.load(d[n + "scales"], 128, self.J)
        self.gain = a.load(every(d[n + "if_gain"], T), T, self.H)
        self.heads = a.load(d["heads"], 128, self.HK)
        self.scale = a.take(128, self.LEFT + 128 * self.J)
        self.e = a.take(T, U, self.J * self.H)
        self.q = a.take(128, KD, N4)

    def build(self, core, run):
        nc, ps, H, HD, HK, J, NEAR, PAD, GD, NG = core.nc, core.ps, self.H, self.HD, self.HK, self.J, self.NEAR, self.PAD, self.GD, self.NG
        sb, e, q = run.sbuf, self.e, self.q
        NI, RING = J * KD, 4
        xn, xT = sb("xn", [T, U, D]), sb("xT", [128, KD, N4])
        k = sb("k", [128, KD, U, PAD + T])
        v = sb("v", [T, U, (2 * H + 1) * HD])
        prod = sb("prod", [128, RING, U, T])
        sT = sb("sT", [128, 2, N4])
        mx, den, rden = sb("mx", [T, U, H]), sb("den", [T, U, H]), sb("rden", [T, U, H])
        a, aT = sb("a", [T, 2, T * H]), sb("aT", [T, 2, H * T])
        oT = sb("oT", [128, 2, KD * T])
        LEAD = (NEAR - 1) * H
        P = LEAD + T * H
        skew = core.scratch("skew", [U, T * P])
        norm, ready, cleared = core.semaphore("norm"), core.semaphore("ready"), core.semaphore("cleared")
        zeroed = core.semaphore("zeroed")
        written = [core.semaphore(f"written{u}") for u in range(U)]
        got = [core.semaphore(f"got{u}") for u in range(U)]
        one = lambda eng, n, c: Progress(core, eng + "_" + n, (n, c))
        pe_x, pe_q, pe_v, pe_i = one("tensor", "xT", KD), one("tensor", "qk", 2 * KD), one("tensor", "v", U), one("tensor", "used", NI)
        pe_g, pe_a, pe_o, pe_w = one("tensor", "turned", NG), one("tensor", "aT", 4 * U), one("tensor", "oT", U), one("tensor", "out", U)
        ac_x, ac_q, ac_v, ac_e = one("scalar", "xT", KD), one("scalar", "qk", 2 * KD), one("scalar", "v", U), one("scalar", "exp", U)
        ac_g, ac_a, ac_o = one("scalar", "scores", NG), one("scalar", "aT", 4 * U), one("scalar", "oT", U)
        ve_x, ve_i, ve_g = one("vector", "xn", U), one("vector", "prod", NI), one("vector", "biased", NG)
        ve_m = Progress(core, "vector_max", ("max", U), ("sub", U))
        ve_n = [Progress(core, f"vector_norm{u}", ("den", 1), ("rden", 1), ("gain", 1), ("e", 1)) for u in range(U)]
        ve_w = [Progress(core, f"vector_x{u}", ("out", 1), ("stats", 1)) for u in range(U)]
        block = run.block
        by_head = lambda t: t.rearrange("p (j h) -> p h j", h=H)
        by_batch = lambda t: t.rearrange("p (b t) -> p b t", b=U)
        size = lambda g: min(GD, J - GD * g) * H
        last_of = lambda g: min(16 * g + 15, NI - 1)
        DIVIDE = {2 + 2 * u: u for u in range(U)}
        TURN = {16 + 3 * n: n for n in range(4 * U)}
        ATTEND = {27 + 12 * u: u for u in range(U)}
        PROJECT = {31 + 12 * u: u for u in range(U)}
        UPDATE = {36 + 12 * u: u for u in range(U)}
        VALUES = {70 + 2 * u: u for u in range(U)}
        XN, XT = 66, 80
        BACK = {last_of(g) + 5: g for g in range(NG) if last_of(g) + 5 < NI}
        BIAS = {last_of(g) + 11: g for g in range(NG) if last_of(g) + 11 < NI}

        def passes(eng, body):
            body(0, True, False)
            with eng.Fori(1, NCH - 1) as c:
                body(c, False, False)
            body(NCH - 1, False, True)

        def start(i):
            return 0 if i % 16 == 0 else self.DIST[i // KD]

        @block.sync
        def _(sp):
            sp.wait_ge(cleared, 1)
            for u in range(U):
                rows_ = skew[u].rearrange("(t n) -> t n", t=T)
                sp.dma_start(rows_[:, 0:T * H], aT[:, 0, :]).then_inc(zeroed, DMA)
                sp.dma_start(rows_[:, T * H:P], aT[:, 0, 0:LEAD]).then_inc(zeroed, DMA)
            sp.wait_ge(zeroed, 2 * U * DMA)

            def body(c, first, last):
                def write(u):
                    if not first:
                        sp.wait_ge(got[u], c * DMA)
                        core.stand(sp)
                    sp.wait_ge(ve_n[u].sem, ve_n[u].at(c, "e"))
                    near = bass.AP(skew.tensor, u * T * P, [[P + H, T], [1, NEAR * H]])
                    far = bass.AP(skew.tensor, u * T * P + self.FAR * P + LEAD, [[P + H, T - self.FAR], [1, H]])
                    sp.dma_start(near, e[:, u, 0:NEAR * H]).then_inc(written[u], DMA)
                    sp.dma_start(far, e[self.FAR:T, u, NEAR * H:J * H]).then_inc(written[u], DMA)

                def read(u):
                    if u >= 2:
                        sp.wait_ge(pe_a.sem, pe_a.at(c, "aT", 4 * (u - 2) + 3))
                        core.stand(sp)
                    elif not first:
                        sp.wait_ge(pe_a.sem, pe_a.at(c - 1, "aT", 4 * (u + 2) + 3))
                        core.stand(sp)
                    sp.wait_ge(written[u], (c + 1) * 2 * DMA)
                    sp.dma_start(a[:, u % 2, :], skew[u].rearrange("(t n) -> t n", t=T)[:, LEAD:P]).then_inc(got[u], DMA)
                write(0)
                write(1)
                read(0)
                write(2)
                write(3)
                for u in range(1, U):
                    read(u)
            passes(sp, body)

        @block.gpsimd
        def _(pool):
            nc.gpsimd.memset(aT[:, 0, :], 0.0).then_inc(cleared, 1)
            norm_pool(core, norm)
            nc.gpsimd.memset(self.scale, 0.0).then_inc(ready, 1)
            nc.gpsimd.memset(k[:, :, :, :], 0.0).then_inc(ready, 1)
            nc.gpsimd.memset(v[:, :, :], 0.0).then_inc(ready, 1)
            pool.wait_ge(run.arrived, run.loads)
            near = self.bias[:, 0:NEAR * H].rearrange("p (j h) -> p j h", h=H)
            nc.gpsimd.affine_select(near, near, pattern=[[1, NEAR], [0, H]], compare_op=ALU.is_ge, fill=-1e30, base=1 - NEAR,
                                    channel_multiplier=1).then_inc(ready, 1)
            far = self.bias[:, NEAR * H:J * H]
            nc.gpsimd.affine_select(far, far, pattern=[[0, H]], compare_op=ALU.is_ge, fill=-1e30, base=-self.FAR,
                                    channel_multiplier=1).then_inc(ready, 1)

        @block.vector
        def _(dve):
            norm_vector(core, dve, None, norm)
            dve.wait_ge(run.arrived, run.loads)
            nc.vector.tensor_scalar(self.se, self.se, 1.0, HD ** -0.5, ALU.add, ALU.mult).then_inc(norm, 1)
            dve.wait_ge(ready, 5)
            dve.wait_ge(norm, 9)
            nc.vector.tensor_tensor(self.scale[:, self.LEFT:].rearrange("p (j n) -> p j n", j=J)[:, :, 0:HK],
                                    self.heads.unsqueeze(1).to_broadcast([128, J, HK]),
                                    self.se.unsqueeze(2).to_broadcast([128, J, HK]), ALU.mult).then_inc(norm, 1)

            def front(c):
                for u in range(U):
                    normed(core, xn[:, u], U * c + u).then_inc(ve_x.step("xn", u), 1)

            def biased(c, g, first):
                n = size(g)
                if g == 0 and not first:
                    for u in range(U):
                        dve.wait_ge(written[u], c * 2 * DMA)
                        core.stand(dve)
                dve.wait_ge(pe_g.sem, pe_g.at(c, "turned", g))
                nc.vector.tensor_tensor(e[:, :, g * 128:g * 128 + n], ps[0:T, 2 + g % 2, 0:U * n].rearrange("p (b n) -> p b n", b=U),
                                        self.bias[:, g * 128:g * 128 + n].unsqueeze(1).to_broadcast([T, U, n]), ALU.add).then_inc(ve_g.step("biased", g), 1)

            def divide(c, u):
                ve = ve_n[u]
                dve.wait_ge(ac_e.sem, ac_e.at(c, "exp", u))
                nc.vector.tensor_reduce(den[:, u, :], by_head(e[:, u]), AX.X, ALU.add).then_inc(ve.step("den"), 1)
                dve.wait_ge(ve.sem, ve.at(c, "den"))
                nc.vector.reciprocal(rden[:, u, :], den[:, u, :]).then_inc(ve.step("rden"), 1)
                dve.wait_ge(ve.sem, ve.at(c, "rden"))
                nc.vector.tensor_tensor(rden[:, u, :], rden[:, u, :], self.gain, ALU.mult).then_inc(ve.step("gain"), 1)
                dve.wait_ge(ve.sem, ve.at(c, "gain"))
                by_dist = e[:, u].rearrange("p (j h) -> p j h", h=H)
                nc.vector.tensor_tensor(by_dist, by_dist, rden[:, u, :].unsqueeze(1).to_broadcast([T, J, H]), ALU.mult).then_inc(ve.step("e"), 1)

            def update(c, u):
                ve = ve_w[u]
                dve.wait_ge(pe_w.sem, pe_w.at(c, "out", u))
                core.stand(dve)
                x = core.x[:, U * c + u, :]
                nc.vector.tensor_tensor(x, x, ps[0:T, 7, 0:D], ALU.add).then_inc(ve.step("out"), 1)
                dve.wait_ge(ve.sem, ve.at(c, "out"))
                row_stats(core, dve, U * c + u).then_inc(ve.step("stats"), 1)

            def body(c, first, last):
                for i in range(NI):
                    if not first and i in DIVIDE:
                        divide(c - 1, DIVIDE[i])
                    if not first and i in UPDATE:
                        update(c - 1, UPDATE[i])
                    if not last and i == XN:
                        dve.wait_ge(pe_x.sem, pe_x.at(c, "xT", KD - 1))
                        core.stand(dve)
                        front(c + 1)
                    if i in BIAS:
                        biased(c, BIAS[i], first)
                    if i < KD:
                        dve.wait_ge(ac_q.sem, ac_q.at(c, "qk", KD + i))
                    if i >= RING:
                        dve.wait_ge(pe_i.sem, pe_i.at(c, "used", i - RING))
                    j, b, t0 = self.DIST[i // KD], i % KD, start(i)
                    nc.vector.tensor_tensor(prod[:, i % RING, :, t0:T], by_batch(q[:, b])[:, :, t0:T], k[:, b, :, PAD + t0 - j:PAD + T - j],
                                            ALU.mult).then_inc(ve_i.step("prod", i), 1)
                for g in range(NG):
                    if g not in BIAS.values():
                        biased(c, g, first)
                dve.wait_ge(ve_g.sem, ve_g.at(c, "biased", NG - 1))
                for u in range(U):
                    nc.vector.tensor_reduce(mx[:, u, :], by_head(e[:, u]), AX.X, ALU.max).then_inc(ve_m.step("max", u), 1)
                for u in range(U):
                    dve.wait_ge(ve_m.sem, ve_m.at(c, "max", u))
                    nc.vector.tensor_tensor(by_head(e[:, u]), by_head(e[:, u]), mx[:, u, :].unsqueeze(2).to_broadcast([T, H, J]),
                                            ALU.subtract).then_inc(ve_m.step("sub", u), 1)
            front(0)
            passes(dve, body)
            for u in range(U):
                divide(NCH - 1, u)
            for u in range(U):
                update(NCH - 1, u)

        @block.scalar
        def _(act):
            run.prefetch(act)
            act.wait_ge(ready, 5)

            def turned(c):
                for b in range(KD):
                    act.wait_ge(pe_x.sem, pe_x.at(c, "xT", b))
                    nc.scalar.copy(xT[:, b], ps[:, 6 + b, 0:N4]).then_inc(ac_x.step("xT", b), 1)

            def qk(c, m):
                act.wait_ge(pe_q.sem, pe_q.at(c, "qk", m))
                if m < KD:
                    nc.scalar.copy(q[:, m], ps[:, 6 + m % 2, 0:N4]).then_inc(ac_q.step("qk", m), 1)
                else:
                    nc.scalar.copy(k[:, m - KD, :, PAD:PAD + T], by_batch(ps[:, 6 + m % 2, 0:N4])).then_inc(ac_q.step("qk", m), 1)

            def values(c, u):
                act.wait_ge(pe_v.sem, pe_v.at(c, "v", u))
                nc.scalar.copy(v[:, u, HD:].rearrange("p (h e) -> p h e", h=H)[:, :, 0:HD],
                               ps[0:T, 6 + u % 2, 0:D].rearrange("p (h e) -> p h e", h=H)).then_inc(ac_v.step("v", u), 1)

            def scores(c, g):
                act.wait_ge(pe_i.sem, pe_i.at(c, "used", last_of(g)))
                nc.scalar.copy(sT[0:size(g), g % 2], ps[0:size(g), g % 2, 0:N4]).then_inc(ac_g.step("scores", g), 1)

            def weights_turned(c, n):
                act.wait_ge(pe_a.sem, pe_a.at(c, "aT", n))
                w = H // 4 * T
                nc.scalar.copy(aT[:, n // 4 % 2, n % 4 * w:(n % 4 + 1) * w], ps[0:T, 4 + n % 2, 0:w]).then_inc(ac_a.step("aT", n), 1)

            def results(c, u):
                act.wait_ge(pe_o.sem, pe_o.at(c, "oT", u))
                nc.scalar.copy(oT[:, u % 2], ps[:, 6, 0:KD * T]).then_inc(ac_o.step("oT", u), 1)

            def body(c, first, last):
                for i in range(NI):
                    if not first and i in TURN:
                        weights_turned(c - 1, TURN[i])
                    if not first and i in ATTEND:
                        results(c - 1, ATTEND[i])
                    if i in VALUES:
                        values(c, VALUES[i])
                    if not last and i == XT:
                        turned(c + 1)
                    if i % 16 == 15:
                        scores(c, i // 16)
                scores(c, NG - 1)
                if not last:
                    for m in range(2 * KD):
                        qk(c + 1, m)
                for u in range(U):
                    act.wait_ge(ve_m.sem, ve_m.at(c, "sub", u))
                    nc.scalar.activation(e[:, u], e[:, u], ACT.Exp).then_inc(ac_e.step("exp", u), 1)
            turned(0)
            for m in range(2 * KD):
                qk(0, m)
            passes(act, body)
            for u in range(U):
                for n in range(4 * u, 4 * u + 4):
                    weights_turned(NCH - 1, n)
                results(NCH - 1, u)

        @block.tensor
        def _(ten):
            ten.wait_ge(run.arrived, run.loads)

            def turn(c):
                for b in range(KD):
                    for u in range(U):
                        if b == 0:
                            ten.wait_ge(ve_x.sem, ve_x.at(c, "xn", u))
                        ins = nc.tensor.transpose(ps[:, 6 + b, u * T:(u + 1) * T], xn[:, u, b * 128:(b + 1) * 128], core.ident[0:T, 0:T])
                    ins.then_inc(pe_x.step("xT", b), 1)

            def qk(c, m):
                if m < KD:
                    ten.wait_ge(ac_x.sem, ac_x.at(c, "xT", KD - 1))
                else:
                    ten.wait_ge(ac_q.sem, ac_q.at(c, "qk", m - KD))
                for b in range(KD):
                    ins = nc.tensor.matmul(ps[:, 6 + m % 2, 0:N4], self.wqkv[:, b, m * 128:(m + 1) * 128], xT[:, b], start=(b == 0), stop=(b == KD - 1))
                ins.then_inc(pe_q.step("qk", m), 1)

            def values(c, first, u):
                if u >= 2:
                    ten.wait_ge(ac_v.sem, ac_v.at(c, "v", u - 2))
                elif u == 1 and not first:
                    ten.wait_ge(ve_w[U - 1].sem, ve_w[U - 1].at(c - 1, "out"))
                for b in range(KD):
                    ins = nc.tensor.matmul(ps[0:T, 6 + u % 2, 0:D], xT[:, b, u * T:(u + 1) * T], self.wqkv[:, b, 2 * D:3 * D],
                                           start=(b == 0), stop=(b == KD - 1))
                ins.then_inc(pe_v.step("v", u), 1)

            def back(c, g):
                n = size(g)
                ten.wait_ge(ac_g.sem, ac_g.at(c, "scores", g))
                if g >= 2:
                    ten.wait_ge(ve_g.sem, ve_g.at(c, "biased", g - 2))
                core.stand(ten)
                for u in range(U):
                    ins = nc.tensor.transpose(ps[0:T, 2 + g % 2, u * n:(u + 1) * n], sT[0:n, g % 2, u * T:(u + 1) * T], core.ident[0:n, 0:n])
                ins.then_inc(pe_g.step("turned", g), 1)

            def weights_turned(c, n):
                u = n // 4
                if n % 4 == 0:
                    ten.wait_ge(got[u], (c + 1) * DMA)
                if n >= 2:
                    ten.wait_ge(ac_a.sem, ac_a.at(c, "aT", n - 2))
                for i in range(H // 4):
                    h = n % 4 * (H // 4) + i
                    ins = nc.tensor.transpose(ps[0:T, 4 + n % 2, i * T:(i + 1) * T], a[:, u % 2].rearrange("p (s h) -> p h s", h=H)[:, h, :],
                                              core.ident[0:T, 0:T])
                ins.then_inc(pe_a.step("aT", n), 1)

            def attend(c, u):
                ten.wait_ge(ac_a.sem, ac_a.at(c, "aT", 4 * u + 3))
                if u >= 1:
                    ten.wait_ge(ac_o.sem, ac_o.at(c, "oT", u - 1))
                for h in range(H):
                    odd, r = h % 2, h % HK // 2 * 2 * HD
                    at = (2 * h + 1 - odd) * HD
                    ins = nc.tensor.matmul(ps[r:r + 2 * HD, 6, h // HK * T:(h // HK + 1) * T], v[:, u, at:at + 2 * HD], aT[:, u % 2, h * T:(h + 1) * T],
                                           start=(odd == 0), stop=(odd == 1))
                ins.then_inc(pe_o.step("oT", u), 1)

            def project(c, u):
                ten.wait_ge(ac_o.sem, ac_o.at(c, "oT", u))
                if u >= 1:
                    ten.wait_ge(ve_w[u - 1].sem, ve_w[u - 1].at(c, "out"))
                for b in range(KD):
                    ins = nc.tensor.matmul(ps[0:T, 7, 0:D], oT[:, u % 2, b * T:(b + 1) * T], self.wo[:, b, :], start=(b == 0), stop=(b == KD - 1))
                ins.then_inc(pe_w.step("out", u), 1)

            def body(c, first, last):
                for i in range(NI):
                    if not first and i in TURN:
                        weights_turned(c - 1, TURN[i])
                    if not first and i in ATTEND:
                        attend(c - 1, ATTEND[i])
                    if not first and i in PROJECT:
                        project(c - 1, PROJECT[i])
                    if i in VALUES:
                        values(c, first, VALUES[i])
                    if not last and i == XT:
                        ten.wait_ge(ac_v.sem, ac_v.at(c, "v", U - 1))
                        turn(c + 1)
                    if i in BACK:
                        back(c, BACK[i])
                    p, b, g, t0 = i // KD, i % KD, i // 16, start(i)
                    n = size(g)
                    if i % 16 == 0 and g >= 2:
                        ten.wait_ge(ac_g.sem, ac_g.at(c, "scores", g - 2))
                    ten.wait_ge(ve_i.sem, ve_i.at(c, "prod", i))
                    w = self.LEFT + 128 * p - p % GD * H - b * HK
                    nc.tensor.matmul(by_batch(ps[0:n, g % 2, 0:N4])[:, :, t0:T], self.scale[:, w:w + n], prod[:, i % RING, :, t0:T],
                                     start=(i % 16 == 0), stop=(i == last_of(g))).then_inc(pe_i.step("used", i), 1)
                rest = [g for g in range(NG) if g not in BACK.values()]
                for g in rest[:-1]:
                    back(c, g)
                if not last:
                    qk(c + 1, 0)
                    qk(c + 1, 1)
                back(c, rest[-1])
                if not last:
                    qk(c + 1, 2)
                    qk(c + 1, 3)
            turn(0)
            for m in range(2 * KD):
                qk(0, m)
            ten.wait_ge(norm, 10)
            passes(ten, body)
            for u in range(U):
                for n in range(4 * u, 4 * u + 4):
                    weights_turned(NCH - 1, n)
                attend(NCH - 1, u)
                project(NCH - 1, u)


class L0Cross:

    name = "L0_xattn"
    H, E = 16, 64
    I = H * E
    W = 2
    UNIT = 1e-24

    def weights(self, a, d):
        n = self.name + "_"
        self.wq, self.wk, self.wv = (a.load(rows(d[n + "w" + k]), 128, KD, self.I) for k in "qkv")
        self.wo = a.load(rows(d[n + "wo"]), 128, self.I // 128, D)
        self.bo = a.load(every(d[n + "bo"], 1), 1, D)
        self.gain_c, self.shift_c = (a.load(d[n + "ln1_" + k + "_c"], 128, KD) for k in "gb")
        self.gain, self.shift = (a.load(every(d[n + "ln1_" + k], SP_), SP_, D) for k in "gb")
        self.g = a.take(128, KD, self.I)
        self.kv0 = a.take(128, self.I)

    def build(self, core, run):
        nc, d, ps, H, E, I, W = core.nc, core.dram, core.ps, self.H, self.E, self.I, self.W
        sb, g = run.sbuf, self.g
        C, HP, G = NB // W, H // 2, W * ST
        N = W + G
        ctx, cn = sb("ctx", [SP_, G, D]), sb("cn", [SP_, G, D])
        cT = sb("cT", [128, W, KD * S])
        xn, h, hT = sb("xn", [T, W, D]), sb("h", [T, W, D]), sb("hT", [128, W, KD * T])
        unit = sb("unit", [SP_, N, I])
        sq = sb("sq", [SP_, I])
        ss, rn = sb("ss", [SP_, N, H]), sb("rn", [SP_, N, H])
        qT = sb("qT", [128, W, HP * T])
        kv = [self.kv0, sb("kv1", [128, I])]
        norm, zeroed = core.semaphore("norm"), core.semaphore("zeroed")
        loaded = [core.semaphore(f"ctx{u}") for u in range(W)]
        lnc, lnx = Norm(core, run, "lnc", rows_=SP_, units=G), Norm(core, run, "lnx", units=W)
        pe = Progress(core, "tensor", ("cT", W * KD), ("hT", W), ("wide", N), ("qT", W * 2), ("g0", KD), ("g1a", 1), ("kv0", 1),
                      ("g1b", 1), ("oT0", 2), ("kv1", 1), ("out0", 1), ("oT1", 2), ("out1", 1))
        ac = Progress(core, "scalar", ("cT", W * KD), ("hT", W), ("sq", N), ("qT", W * 2), ("g0", KD), ("g1a", 1), ("kv0", 1),
                      ("g1b", 1), ("oT0", 2), ("kv1", 1), ("oT1", 2))
        ve = Progress(core, "vector", ("xn", W), *lnx.steps(), *lnc.steps(), ("h", W), ("cn", G), ("gain", G), ("shift", G))
        ve_s, ve_m = Progress(core, "vector_sum", ("sum", N), ), Progress(core, "vector_unit", ("unit", N))
        ve_c, ve_y = Progress(core, "vector_least", ("least", N)), Progress(core, "vector_y", ("y", W))
        po = Progress(core, "pool", ("lnxrs", 1), ("lncrs", 1), ("root", N))
        block = run.block
        height = lambda i: T if i < W else SP_
        bank = lambda i: 2 * ((i + 2) % 4)
        wide = lambda i: ps[0:height(i), bank(i):bank(i) + 2, :].rearrange("p a b -> p (a b)")
        by_head = lambda t: t.rearrange("p (h e) -> p h e", h=H)

        @block.sync
        def _(sp):
            def load(n, u):
                sp.dma_start(ctx[:, u * ST:(u + 1) * ST, :], d["ctx"][n].rearrange("(s p) c -> p s c", p=SP_)).then_inc(loaded[u], DMA)
            for u in range(W):
                load(u, u)
            with sp.Fori(1, C) as c:
                for u in range(W):
                    sp.wait_ge(ve.sem, ve.at(c - 1, "cn", ST * u + ST - 1))
                    core.stand(sp)
                    load(W * c + u, u)

        @block.gpsimd
        def _(pool):
            norm_pool(core, norm)
            for u in range(W):
                nc.gpsimd.memset(kv[u][:, :], 0.0).then_inc(zeroed, 1)
            with pool.Fori(0, C) as c:
                lnx.pool(pool, ve, po, c)
                lnc.pool(pool, ve, po, c)
                for i in range(N):
                    pool.wait_ge(ve_c.sem, ve_c.at(c, "least", i))
                    r = height(i)
                    nc.gpsimd.tensor_tensor(rn[0:r, i], ss[0:r, i], core.mhalf[0:r, 0:H], ALU.pow).then_inc(po.step("root", i), 1)

        @block.vector
        def _(dve):
            norm_vector(core, dve, None, norm)
            dve.wait_ge(run.arrived, run.loads)
            with dve.Fori(0, C) as c:
                for u in range(W):
                    normed(core, xn[:, u], W * c + u).then_inc(ve.step("xn", u), 1)
                lnx.vector(dve, ve, c, lambda u, q: xn[:, u], lambda u: dve.wait_ge(ve.sem, ve.at(c, "xn", u)))
                lnc.vector(dve, ve, c, lambda t, q: ctx[:, t, :],
                           lambda t: dve.wait_ge(loaded[t // ST], (c + 1) * DMA))
                dve.wait_ge(po.sem, po.at(c, "lnxrs"))
                core.stand(dve)
                for u in range(W):
                    lnx.apply(h[:, u], xn[:, u], u).then_inc(ve.step("h", u), 1)
                dve.wait_ge(po.sem, po.at(c, "lncrs"))
                core.stand(dve)
                for t in range(G):
                    lnc.apply(cn[:, t, :], ctx[:, t, :], t).then_inc(ve.step("cn", t), 1)
                for t in range(G):
                    dve.wait_ge(ve.sem, ve.at(c, "cn", t))
                    nc.vector.tensor_tensor(cn[:, t, :], cn[:, t, :], self.gain, ALU.mult).then_inc(ve.step("gain", t), 1)
                for t in range(G):
                    dve.wait_ge(ve.sem, ve.at(c, "gain", t))
                    nc.vector.tensor_tensor(cn[:, t, :], cn[:, t, :], self.shift, ALU.add).then_inc(ve.step("shift", t), 1)

                def unit_length(i):
                    r = height(i)
                    dve.wait_ge(po.sem, po.at(c, "root", i))
                    nc.vector.tensor_tensor(by_head(unit[0:r, i]), by_head(wide(i)),
                                                      rn[0:r, i].unsqueeze(2).to_broadcast([r, H, E]), ALU.mult).then_inc(ve_m.step("unit", i), 1)
                for i in range(N):
                    r = height(i)
                    dve.wait_ge(ac.sem, ac.at(c, "sq", i))
                    nc.vector.tensor_reduce(ss[0:r, i], by_head(sq[0:r, :]), AX.X, ALU.add).then_inc(ve_s.step("sum", i), 1)
                    dve.wait_ge(ve_s.sem, ve_s.at(c, "sum", i))
                    nc.vector.tensor_scalar(ss[0:r, i], ss[0:r, i], self.UNIT, None, ALU.max).then_inc(ve_c.step("least", i), 1)
                    if i >= 2:
                        unit_length(i - 2)
                unit_length(N - 2)
                unit_length(N - 1)
                for u in range(W):
                    dve.wait_ge(pe.sem, pe.at(c, f"out{u}"))
                    core.stand(dve)
                    nc.vector.tensor_tensor(core.y[:, W * c + u, :], xn[:, u], ps[0:T, 6 + u, 0:D], ALU.add).then_inc(ve_y.step("y", u), 1)
                dve.wait_ge(ve_y.sem, ve_y.at(c, "y", W - 1))
                core.stand(dve)

        @block.scalar
        def _(act):
            run.prefetch(act)
            act.wait_ge(run.arrived, run.loads)
            act.wait_ge(zeroed, W)
            with act.Fori(0, C) as c:
                for u in range(W):
                    for k in range(KD):
                        act.wait_ge(pe.sem, pe.at(c, "cT", KD * u + k))
                        nc.scalar.copy(cT[:, u, k * S:(k + 1) * S], ps[:, 4 + KD * u + k, 0:S]).then_inc(ac.step("cT", KD * u + k), 1)
                for u in range(W):
                    act.wait_ge(pe.sem, pe.at(c, "hT", u))
                    for k in range(KD):
                        w = slice(k * T, (k + 1) * T)
                        ins = nc.scalar.activation(hT[:, u, w], ps[:, u, w], ACT.Identity, bias=self.shift_c[:, k:k + 1],
                                                   scale=self.gain_c[:, k:k + 1])
                    ins.then_inc(ac.step("hT", u), 1)
                for i in range(N):
                    if i >= 1:
                        act.wait_ge(ve_s.sem, ve_s.at(c, "sum", i - 1))
                    act.wait_ge(pe.sem, pe.at(c, "wide", i))
                    nc.scalar.activation(sq[0:height(i), :], wide(i), ACT.Square).then_inc(ac.step("sq", i), 1)
                for u in range(W):
                    for b in range(2):
                        act.wait_ge(pe.sem, pe.at(c, "qT", 2 * u + b))
                        w = HP // 2 * T
                        nc.scalar.copy(qT[:, u, b * w:(b + 1) * w], ps[:, 2 * u + b, 0:w]).then_inc(ac.step("qT", 2 * u + b), 1)

                def keep_g(step, m, at=0):
                    act.wait_ge(pe.sem, pe.at(c, step, at))
                    nc.scalar.copy(g[:, m, :], ps[:, 4 + 2 * m:6 + 2 * m, :].rearrange("p a b -> p (a b)")).then_inc(ac.step(step, at), 1)

                def keep_kv(u):
                    act.wait_ge(pe.sem, pe.at(c, f"kv{u}"))
                    for j in range(2):
                        r = slice(j * E, (j + 1) * E)
                        ins = nc.scalar.copy(kv[u][r, :].rearrange("p (h e) -> p h e", h=HP)[:, :, j * E:(j + 1) * E],
                                             ps[r, u, :].rearrange("p (h e) -> p h e", h=HP))
                    ins.then_inc(ac.step(f"kv{u}"), 1)

                def keep_o(u):
                    for b in range(2):
                        act.wait_ge(pe.sem, pe.at(c, f"oT{u}", b))
                        w = HP // 2 * T
                        nc.scalar.copy(qT[:, u, b * w:(b + 1) * w], ps[:, 2 + 2 * u + b, 0:w]).then_inc(ac.step(f"oT{u}", b), 1)
                keep_g("g0", 0, 0)
                keep_g("g0", 1, 1)
                act.wait_ge(pe.sem, pe.at(c, "kv0"))
                keep_g("g1a", 0)
                keep_kv(0)
                keep_g("g1b", 1)
                keep_o(0)
                keep_kv(1)
                keep_o(1)

        @block.tensor
        def _(ten):
            ten.wait_ge(run.arrived, run.loads)
            with ten.Fori(0, C) as c:
                for u in range(W):
                    for k in range(KD):
                        for s in range(ST):
                            ten.wait_ge(ve.sem, ve.at(c, "shift", ST * u + s))
                            ins = nc.tensor.transpose(ps[:, 4 + KD * u + k, s * SP_:(s + 1) * SP_], cn[:, ST * u + s, k * 128:(k + 1) * 128],
                                                      core.ident[0:SP_, 0:SP_])
                        ins.then_inc(pe.step("cT", KD * u + k), 1)
                for u in range(W):
                    ten.wait_ge(ve.sem, ve.at(c, "h", u))
                    transposes(core, ps[:, u], h[:, u], T, KD).then_inc(pe.step("hT", u), 1)
                for i in range(N):
                    if i >= 4:
                        ten.wait_ge(ve_m.sem, ve_m.at(c, "unit", i - 4))
                    for b in range(2):
                        for k in range(KD):
                            cols = slice(b * 512, (b + 1) * 512)
                            if i < W:
                                if b == 0 and k == 0:
                                    ten.wait_ge(ac.sem, ac.at(c, "hT", i))
                                lhs, w = hT[:, i, k * T:(k + 1) * T], self.wq
                            else:
                                t = i - W
                                lhs, w = cT[:, t // ST, k * S + (t % ST) * SP_:k * S + (t % ST + 1) * SP_], self.wk
                            ins = nc.tensor.matmul(ps[0:height(i), bank(i) + b, :], lhs, w[:, k, cols], start=(k == 0), stop=(k == KD - 1))
                    ins.then_inc(pe.step("wide", i), 1)
                for u in range(W):
                    ten.wait_ge(ve_m.sem, ve_m.at(c, "unit", N - 2 + u))
                    for b in range(2):
                        for j in range(HP // 2):
                            k = HP // 2 * b + j
                            ins = nc.tensor.transpose(ps[:, 2 * u + b, j * T:(j + 1) * T], unit[0:T, u, k * 128:(k + 1) * 128],
                                                      core.ident[0:T, 0:T])
                        ins.then_inc(pe.step("qT", 2 * u + b), 1)

                def make_g(u, m):
                    for b in range(2):
                        for s in range(ST):
                            t = ST * u + s
                            ins = nc.tensor.matmul(ps[:, 4 + 2 * m + b, :], cn[:, t, m * 128:(m + 1) * 128], unit[:, W + t, b * 512:(b + 1) * 512],
                                                   start=(s == 0), stop=(s == ST - 1))
                    return ins

                def make_kv(u):
                    for j in range(H):
                        e = slice(j * E, (j + 1) * E)
                        for k in range(KD):
                            ins = nc.tensor.matmul(ps[j % 2 * E:(j % 2 + 1) * E, u, j // 2 * E:(j // 2 + 1) * E], g[:, k, e], self.wv[:, k, e],
                                                   start=(k == 0), stop=(k == KD - 1))
                    return ins

                def make_o(u):
                    ten.wait_ge(ac.sem, ac.at(c, f"kv{u}"))
                    for b in range(2):
                        for j in range(HP // 2):
                            k = HP // 2 * b + j
                            ins = nc.tensor.matmul(ps[:, 2 + 2 * u + b, j * T:(j + 1) * T], kv[u][:, k * 128:(k + 1) * 128],
                                                   qT[:, u, k * T:(k + 1) * T], start=True, stop=True)
                        ins.then_inc(pe.step(f"oT{u}", b), 1)

                def project(u):
                    ten.wait_ge(ac.sem, ac.at(c, f"oT{u}", 1))
                    for k in range(HP):
                        nc.tensor.matmul(ps[0:T, 6 + u, 0:D], qT[:, u, k * T:(k + 1) * T], self.wo[:, k, :], start=(k == 0), stop=False)
                    nc.tensor.matmul(ps[0:T, 6 + u, 0:D], core.ones[0:1, 0:T], self.bo, start=False, stop=True).then_inc(pe.step(f"out{u}"), 1)
                for m in range(KD):
                    make_g(0, m).then_inc(pe.step("g0", m), 1)
                ten.wait_ge(ac.sem, ac.at(c, "g0", 0))
                make_g(1, 0).then_inc(pe.step("g1a"), 1)
                ten.wait_ge(ac.sem, ac.at(c, "g0", 1))
                make_kv(0).then_inc(pe.step("kv0"), 1)
                make_g(1, 1).then_inc(pe.step("g1b"), 1)
                make_o(0)
                ten.wait_ge(ac.sem, ac.at(c, "g1b"))
                make_kv(1).then_inc(pe.step("kv1"), 1)
                project(0)
                make_o(1)
                project(1)


class Picked:

    def __init__(self, core, run, name, lanes, by_expert, first_row, work):
        self.core, self.lanes, self.by_expert, self.first_row = core, lanes, by_expert, first_row
        K, G = L0Kron.K, L0Kron.G
        self.P, self.C = P, C = G // NCH, 2 * NCH
        sb = lambda n, shape, dt=F32: run.sbuf(name + n, shape, dt)
        self.top, self.which = sb("top", [P, C, 8]), sb("which", [P, C, 8], U32)
        self.at, self.s = sb("at", [P, K, C]), sb("s", [P, K, C])
        self.e2, self.den = sb("e2", [P, C]), sb("den", [P, C])
        self.sheets = 1 if by_expert else K
        self.wide = work
        self.index = sb("index", [128, self.sheets, G], U32)
        self.weight = sb("weight", [128, G, self.sheets])
        self.ve = Progress(core, "vector_" + name, ("top", C), ("which", C), ("at", 1), ("gap", 1), ("den", 1), ("s1", 1), ("s2", 1),
                           ("wide", 2 * K), ("index", self.sheets), ("weight", 1))
        self.ac = Progress(core, "scalar_" + name, ("e2", 1))
        self.pe = Progress(core, "tensor_" + name, ("index", 1), ("weight", 1))

    def vector(self, dve, lg):
        nc, ps, ve, K, P, C = self.core.nc, self.core.ps, self.ve, L0Kron.K, self.P, self.C
        for n in range(C):
            nc.vector.max(self.top[:, n, :], lg[:, n, :]).then_inc(ve.step("top", n), 1)
        for n in range(C):
            dve.wait_ge(ve.sem, ve.at(0, "top", n))
            nc.vector.max_index(self.which[:, n, :], self.top[:, n, :], lg[:, n, :]).then_inc(ve.step("which", n), 1)
        dve.wait_ge(ve.sem, ve.at(0, "which", C - 1))
        nc.vector.tensor_copy(self.at[:, :, :].rearrange("p k n -> p n k"), self.which[:, :, 0:K]).then_inc(ve.step("at"), 1)
        nc.vector.tensor_tensor(self.e2[:, :], self.top[:, :, 1], self.top[:, :, 0], ALU.subtract).then_inc(ve.step("gap"), 1)
        dve.wait_ge(self.ac.sem, self.ac.at(0, "e2"))
        nc.vector.tensor_scalar(self.den[:, :], self.e2[:, :], 1.0, None, ALU.add).then_inc(ve.step("den"), 1)
        dve.wait_ge(ve.sem, ve.at(0, "den"))
        nc.vector.reciprocal(self.s[:, 0, :], self.den[:, :]).then_inc(ve.step("s1"), 1)
        dve.wait_ge(ve.sem, ve.at(0, "s1"))
        nc.vector.tensor_tensor(self.s[:, 1, :], self.s[:, 0, :], self.e2[:, :], ALU.mult).then_inc(ve.step("s2"), 1)
        dve.wait_ge(ve.sem, ve.at(0, "s2"))
        L, G = self.lanes, L0Kron.G
        for i, v in enumerate((self.at, self.s)):
            for k in range(K):
                if self.by_expert:
                    out = self.wide[i].rearrange("p (c r k l) -> p c r k l", r=2, k=K, l=L)[:, :, :, k, :]
                else:
                    out = self.wide[i].rearrange("p (c k r l) -> p c k r l", r=2, k=K, l=L)[:, :, k, :, :]
                nc.vector.tensor_copy(out, v[:, k, :].rearrange("p (c r) -> p c r", r=2).unsqueeze(3).to_broadcast([P, NCH, 2, L])).then_inc(ve.step("wide", K * i + k), 1)
        dve.wait_ge(self.pe.sem, self.pe.at(0, "index"))
        for t in range(self.sheets):
            nc.vector.tensor_scalar(self.index[:, t, :], ps[:, 0, t * G:(t + 1) * G], float(L), self.first_row, ALU.mult, ALU.add).then_inc(ve.step("index", t), 1)
        dve.wait_ge(self.pe.sem, self.pe.at(0, "weight"))
        nc.vector.tensor_copy(self.weight[:, :, :].rearrange("p g t -> p t g"),
                                      ps[:, 1, 0:self.sheets * G].rearrange("p (t g) -> p t g", t=self.sheets)).then_inc(ve.step("weight"), 1)

    def scalar(self, act):
        act.wait_ge(self.ve.sem, self.ve.at(0, "gap"))
        self.core.nc.scalar.activation(self.e2[:, :], self.e2[:, :], ACT.Exp).then_inc(self.ac.step("e2"), 1)

    def tensor(self, ten):
        nc, ps, G, P = self.core.nc, self.core.ps, L0Kron.G, self.P
        ten.wait_ge(self.ve.sem, self.ve.at(0, "wide", 2 * L0Kron.K - 1))
        for i, step in enumerate(("index", "weight")):
            for t in range(self.sheets):
                for c in range(NCH):
                    col = (c * self.sheets + t) * 128
                    ins = nc.tensor.transpose(ps[:, i, t * G + c * P:t * G + (c + 1) * P], self.wide[i][:, col:col + 128], self.core.ident[0:P, 0:P])
            ins.then_inc(self.pe.step(step), 1)


class L0Kron:

    name = "L0_ffn"
    E, K = 64, 2
    R = NB * T // 4
    G = R // 2
    I, F = 32, 64
    B = 8
    PASSES = G // (2 * B)
    BY_SP, BY_ACT = {"up": (), "dn": (2, 3, 4)}, {"up": (7,), "dn": (5, 6, 7)}

    def weights(self, a, d):
        n, E, I, F, B = self.name + "_", self.E, self.I, self.F, self.B
        self.wup = a.load(rows(d[n + "W_upT"]), 128, 8, E)
        self.wdn = a.take(128, F, E)
        self.bias_up, self.bias_dn = a.take(128, F), a.take(128, I)
        for r in range(2):
            half = slice(r * F, (r + 1) * F)
            a.loads.append((self.wdn[half], d[n + "W_downP"]))
            a.loads.append((self.bias_up[half], d[n + "bias_up"].rearrange("(o p) -> o p", o=F)))
            a.loads.append((self.bias_dn[r * F:r * F + I], d[n + "bias_down"].rearrange("(o p) -> o p", o=I)))
        self.scale_up, self.scale_dn = (a.load(every(d[n + "scale_" + k], 128), 128, 1) for k in ("up", "down"))
        self.row32, self.row64 = a.load(d["row32"], 128, 1), a.load(d["row64"], 128, 1)
        self.xs = a.take(128, 2, B * I)
        self.ab = a.take(128, 2, B * 2 * F)
        self.u = a.take(128, 2, B * F)
        self.pre = a.take(128, 2, B * F)
        self.out = a.take(128, 2, B * I)

    def build(self, core, run):
        nc, d, ps, sb = core.nc, core.dram, core.ps, run.sbuf
        G, E, K, I, F, B, PASSES, R = self.G, self.E, self.K, self.I, self.F, self.B, self.PASSES, self.R
        x_rows, y_rows = core.scratch("x_rows", [R, 4 * D]), core.scratch("y_rows", [R, 4 * D])
        h = sb("h", [128, G, F])
        flat = h[:, :, :].rearrange("p g f -> p (g f)")
        P = G // NCH
        lg = sb("lg", [P, 2 * NCH, E])
        lgT = sb("lgT", [128, G])
        now = sb("now", [128, K, 2, B], U32)
        xn = flat[0:T, 0:U * D].rearrange("p (u d) -> p u d", u=U)
        xT = flat[:, U * D:U * D + KD * N4].rearrange("p (k n) -> p k n", k=KD)
        at = U * D + KD * N4
        up = Picked(core, run, "up", I, True, self.row32, [flat[0:P, at + i * NCH * 128:at + (i + 1) * NCH * 128] for i in range(2)])
        ab = self.ab.rearrange("p b n -> p (b n)")
        dn = Picked(core, run, "dn", F, False, self.row64, [ab[0:P, i * 2 * NCH * 128:(i + 1) * 2 * NCH * 128] for i in range(2)])
        names = ("norm", "rows_out", "back")
        norm, rows_out, back = (core.semaphore(n) for n in names)
        rows_in = [core.semaphore(f"rows_in{b}") for b in range(2)]
        table_up = [core.pool_dma_semaphore(f"table_up{b}") for b in range(2)]
        table_dn = [core.pool_dma_semaphore(f"table_dn{b}") for b in range(2)]
        by_pool = lambda part: [g for g in range(B) if g not in self.BY_SP[part] + self.BY_ACT[part]]
        others = lambda part: len(self.BY_SP[part] + self.BY_ACT[part])
        taken_up = [core.semaphore(f"taken_up{b}") for b in range(2)]
        taken_dn = [core.semaphore(f"taken_dn{b}") for b in range(2)]
        stored = [core.semaphore(f"stored{b}") for b in range(2)]
        ve, po = Progress(core, "vector", "xn"), Progress(core, "pool", "kept")
        pe, ac = Progress(core, "tensor", ("xT", KD), ("lg", 1)), Progress(core, "scalar", ("xT", KD), ("lg", 1))
        by_block = lambda *names: (Progress(core, n, ("block", 2)) for n in names)
        po_up, pe_u, ve_u, pe_y, ve_y, ac_y = by_block("pool_up", "tensor_u", "vector_u", "tensor_y", "vector_y", "scalar_gelu")
        po_dn, ac_h, pe_v, ve_v, pe_z, ve_z = by_block("pool_dn", "scalar_h", "tensor_v", "vector_v", "tensor_z", "vector_z")
        pe_r, ac_r = Progress(core, "tensor_route", ("sums", 2), ("lg", 1)), Progress(core, "scalar_route", ("sums", 2))
        ve_r, ve_e = Progress(core, "vector_route", ("lg", 1)), Progress(core, "vector_end", "out", "stats")
        block = run.block
        by_group = lambda t: t.rearrange("p (g n) -> p g n", g=B)
        groups = lambda j, b: bass.ds(2 * B * j + B * b, B)

        def take_up(eng, j, b, mine):
            core.stand(eng)
            for g in mine:
                for p in range(0, 128, I):
                    at = eng.value_load(up.index[p:p + 1, 0, bass.ds(2 * B * j + B * b + g, 1)], min_val=0, max_val=(E - 1) * I)
                    eng.dma_start(self.ab[p:p + I, b, g * 2 * F:(g + 1) * 2 * F], d["L0_ffn_up"][bass.ds(at, I), :]).then_inc(taken_up[b], DMA)

        def take_dn(eng, j, b, mine):
            core.stand(eng)
            for g in mine:
                for p in range(0, 128, F):
                    at = eng.value_load(dn.index[p:p + 1, 1, bass.ds(2 * B * j + B * b + g, 1)], min_val=0, max_val=(E - 1) * F)
                    eng.dma_start(self.ab[p:p + F, b, (g * K + 1) * F:(g * K + 2) * F], d["L0_ffn_down"][bass.ds(at, F), :]).then_inc(taken_dn[b], DMA)

        def passes(eng, body):
            body(0, True)
            with eng.Fori(1, PASSES) as j:
                body(j, False)

        @block.sync
        def _(sp):
            sp.wait_ge(po.sem, po.at(NCH - 1, "kept", U - 1))
            sp.dma_start(x_rows.rearrange("n (q c) -> (n q) c", q=4).rearrange("(b t) c -> t b c", t=T), core.y[:, :, :]).then_inc(rows_out, DMA)
            sp.wait_ge(rows_out, DMA)

            def load(j, first):
                src = x_rows.rearrange("(g r) (i n) -> r i g n", r=2, n=I)
                for b in range(2):
                    if not first:
                        sp.wait_ge(pe_u.sem, pe_u.at(j - 1, "block", b))
                        core.stand(sp)
                    for r in range(2):
                        for k in range(K):
                            p = slice((r * K + k) * I, (r * K + k + 1) * I)
                            sp.dma_start(by_group(self.xs[p, b]), src[r][:, groups(j, b), :]).then_inc(rows_in[b], DMA)
            passes(sp, load)
            sp.wait_ge(dn.ve.sem, dn.ve.at(0, "weight"))

            def store(j, b):
                dst = y_rows.rearrange("(g r) (o n) -> r o g n", r=2, n=I)
                sp.wait_ge(ve_z.sem, ve_z.at(j, "block", b))
                core.stand(sp)
                for r in range(2):
                    sp.dma_start(dst[r][:, groups(j, b), :], by_group(self.out[r * F:r * F + I, b])).then_inc(stored[b], DMA)

            def downward(j, first):
                for b in range(2):
                    if not first:
                        sp.wait_ge(pe_z.sem, pe_z.at(j - 1, "block", b))
                    take_dn(sp, j, b, self.BY_SP["dn"])
                    if not first:
                        store(j - 1, b)
            passes(sp, downward)
            for b in range(2):
                store(PASSES - 1, b)
            for b in range(2):
                sp.wait_ge(stored[b], 2 * DMA * PASSES)
            sp.dma_start(core.y[:, :, :], y_rows.rearrange("n (q c) -> (n q) c", q=4).rearrange("(b t) c -> t b c", t=T)).then_inc(back, DMA)

        @block.gpsimd
        def _(pool):
            norm_pool(core, norm)
            with pool.Fori(0, NCH) as c:
                for u in range(U):
                    pool.wait_ge(ve.sem, ve.at(c, "xn", u))
                    core.stand(pool)
                    nc.gpsimd.tensor_copy(core.y[:, bass.ds(U * c + u, 1), :], xn[:, u:u + 1, :]).then_inc(po.step("kept", u), 1)
            pool.wait_ge(up.ve.sem, up.ve.at(0, "weight"))

            def fetch(picked, copied, used, source, dst, arrived):
                def body(j, first):
                    for b in range(2):
                        if not first:
                            pool.wait_ge(used.sem, used.at(j - 1, "block", b))
                            core.stand(pool)
                        nc.gpsimd.tensor_copy(now[:, 0:picked.sheets, b, :], picked.index[:, :, groups(j, b)]).then_inc(copied.step("block", b), 1)
                        pool.wait_ge(copied.sem, copied.at(j, "block", b))
                        core.stand(pool)
                        for t, g, place in dst(b):
                            at = bass.IndirectOffsetOnAxis(ap=now[:, t, b, g:g + 1], axis=0)
                            nc.gpsimd.indirect_dma_start(out=place, out_offset=None, in_=source[:, :], in_offset=at).then_inc(arrived[b], DMA)
                passes(pool, body)
            fetch(up, po_up, pe_y, d["L0_ffn_up"], lambda b: [(0, g, self.ab[:, b, g * 2 * F:(g + 1) * 2 * F]) for g in by_pool("up")], table_up)
            pool.wait_ge(dn.ve.sem, dn.ve.at(0, "weight"))
            fetch(dn, po_dn, pe_z, d["L0_ffn_down"], lambda b: [(k, g, self.ab[:, b, (g * K + k) * F:(g * K + k + 1) * F])
                                                                for k in range(K) for g in (by_pool("dn") if k else range(B))], table_dn)

        @block.vector
        def _(dve):
            norm_vector(core, dve, None, norm)
            dve.wait_ge(run.arrived, run.loads)
            with dve.Fori(0, NCH) as c:
                for u in range(U):
                    normed(core, xn[:, u], U * c + u).then_inc(ve.step("xn", u), 1)
                dve.wait_ge(po.sem, po.at(c, "kept", U - 1))
                dve.wait_ge(pe.sem, pe.at(c, "xT", KD - 1))
                core.stand(dve)
            dve.wait_ge(ac.sem, ac.at(NCH - 1, "lg"))
            up.vector(dve, lg)
            dve.wait_ge(up.ve.sem, up.ve.at(0, "weight"))

            def weighted(j, b, made, used, picked, inner):
                dve.wait_ge(used.sem, used.at(j, "block", b))
                n = B * picked.sheets
                view = lambda t: t.rearrange("p (g n) -> p g n", g=n)
                w = picked.weight[:, groups(j, b), :].rearrange("p g t -> p (g t)").unsqueeze(2).to_broadcast([128, n, inner])
                nc.vector.tensor_tensor(view(self.u[:, b]), view(ps[:, b, 0:B * F]), w, ALU.mult).then_inc(made.step("block", b), 1)

            def upward(j, first):
                for b in range(2):
                    weighted(j, b, ve_u, pe_u, up, F)
                    if not first:
                        dve.wait_ge(ac_y.sem, ac_y.at(j - 1, "block", b))
                    dve.wait_ge(pe_y.sem, pe_y.at(j, "block", b))
                    nc.vector.scalar_tensor_tensor(out=by_group(self.pre[:, b]), in0=by_group(ps[:, 2 + b, 0:B * F]), scalar=self.scale_up,
                                                             in1=self.bias_up.unsqueeze(1).to_broadcast([128, B, F]), op0=ALU.mult, op1=ALU.add).then_inc(ve_y.step("block", b), 1)
            passes(dve, upward)
            dve.wait_ge(pe_r.sem, pe_r.at(0, "lg"))
            nc.vector.tensor_copy(lg[:, :, :].rearrange("p c e -> p (c e)"), ps[0:P, 4, :]).then_inc(ve_r.step("lg"), 1)
            dve.wait_ge(ve_r.sem, ve_r.at(0, "lg"))
            dn.vector(dve, lg)
            dve.wait_ge(dn.ve.sem, dn.ve.at(0, "weight"))
            def downward(j, first):
                for b in range(2):
                    weighted(j, b, ve_v, pe_v, dn, I)
                    if not first:
                        dve.wait_ge(stored[b], j * 2 * DMA)
                    dve.wait_ge(pe_z.sem, pe_z.at(j, "block", b))
                    for r in range(2):
                        p = slice(r * F, r * F + I)
                        ins = nc.vector.scalar_tensor_tensor(out=by_group(self.out[p, b]), in0=by_group(ps[p, 2 + b, 0:B * I]), scalar=self.scale_dn[p],
                                                             in1=self.bias_dn[p].unsqueeze(1).to_broadcast([I, B, I]), op0=ALU.mult, op1=ALU.add)
                    ins.then_inc(ve_z.step("block", b), 1)
            passes(dve, downward)
            dve.wait_ge(back, DMA)
            with dve.Fori(0, NCH) as c:
                for u in range(U):
                    x = core.x[:, U * c + u, :]
                    nc.vector.tensor_tensor(x, x, core.y[:, U * c + u, :], ALU.add).then_inc(ve_e.step("out", u), 1)
                for u in range(U):
                    dve.wait_ge(ve_e.sem, ve_e.at(c, "out", u))
                    row_stats(core, dve, U * c + u).then_inc(ve_e.step("stats", u), 1)

        @block.scalar
        def _(act):
            run.prefetch(act)
            with act.Fori(0, NCH) as c:
                for k in range(KD):
                    act.wait_ge(pe.sem, pe.at(c, "xT", k))
                    nc.scalar.copy(xT[:, k], ps[:, k, 0:N4]).then_inc(ac.step("xT", k), 1)
                act.wait_ge(pe.sem, pe.at(c, "lg"))
                nc.scalar.copy(lg[:, bass.ds(2 * c, 2), :].rearrange("p c e -> p (c e)"), ps[0:P, 2, 0:2 * E]).then_inc(ac.step("lg"), 1)
            up.scalar(act)
            act.wait_ge(up.ve.sem, up.ve.at(0, "weight"))
            def gelu(j, b):
                act.wait_ge(ve_y.sem, ve_y.at(j, "block", b))
                nc.scalar.activation(h[:, groups(j, b), :].rearrange("p g f -> p (g f)"), self.pre[:, b], ACT.Gelu).then_inc(ac_y.step("block", b), 1)

            def upward(j, first):
                for b in range(2):
                    if not first:
                        act.wait_ge(pe_y.sem, pe_y.at(j - 1, "block", b))
                    take_up(act, j, b, self.BY_ACT["up"])
                    if not first:
                        gelu(j - 1, b)
            passes(act, upward)
            for b in range(2):
                gelu(PASSES - 1, b)
            for r in range(2):
                act.wait_ge(pe_r.sem, pe_r.at(0, "sums", r))
                p = slice(r * F, (r + 1) * F)
                nc.scalar.copy(lgT[p, :], ps[p, 6 + r, 0:G]).then_inc(ac_r.step("sums", r), 1)
            dn.scalar(act)

            act.wait_ge(dn.ve.sem, dn.ve.at(0, "weight"))

            def downward(j, first):
                for b in range(2):
                    if not first:
                        act.wait_ge(pe_v.sem, pe_v.at(j - 1, "block", b))
                    nc.scalar.copy(self.pre[:, b], h[:, groups(j, b), :].rearrange("p g f -> p (g f)")).then_inc(ac_h.step("block", b), 1)
                    if not first:
                        act.wait_ge(pe_z.sem, pe_z.at(j - 1, "block", b))
                    take_dn(act, j, b, self.BY_ACT["dn"])
            passes(act, downward)

        @block.tensor
        def _(ten):
            ten.wait_ge(run.arrived, run.loads)
            with ten.Fori(0, NCH) as c:
                for k in range(KD):
                    for u in range(U):
                        if k == 0:
                            ten.wait_ge(ve.sem, ve.at(c, "xn", u))
                        ins = nc.tensor.transpose(ps[:, k, u * T:(u + 1) * T], xn[:, u, k * 128:(k + 1) * 128], core.ident[0:T, 0:T])
                    ins.then_inc(pe.step("xT", k), 1)
                ten.wait_ge(ac.sem, ac.at(c, "xT", KD - 1))
                for r in range(2):
                    for q in range(4):
                        for k in range(KD):
                            ins = nc.tensor.matmul(ps[0:P, 2, r * E:(r + 1) * E], xT[:, k, 4 * r + q:N4:8], self.wup[:, KD * q + k, :],
                                                   start=(q == 0 and k == 0), stop=(q == 3 and k == KD - 1))
                ins.then_inc(pe.step("lg"), 1)
            up.tensor(ten)
            ten.wait_ge(up.ve.sem, up.ve.at(0, "weight"))
            with ten.Fori(0, PASSES) as j:
                for b in range(2):
                    ten.wait_ge(rows_in[b], (j + 1) * 2 * K * DMA)
                    ten.wait_ge(table_up[b], (j + 1) * len(by_pool("up")) * DMA)
                    core.stand(ten)
                    ten.wait_ge(taken_up[b], (j + 1) * 2 * K * others("up") * DMA)
                    core.stand(ten)
                    for g in range(B):
                        for r in range(2 * K):
                            p = slice(r * I, (r + 1) * I)
                            ins = nc.tensor.matmul(ps[p, b, g * F:(g + 1) * F], self.xs[p, b, g * I:(g + 1) * I], self.ab[p, b, g * 2 * F:g * 2 * F + F],
                                                   start=True, stop=True)
                    ins.then_inc(pe_u.step("block", b), 1)
                    ten.wait_ge(ve_u.sem, ve_u.at(j, "block", b))
                    core.stand(ten)
                    for g in range(B):
                        for r in range(2):
                            p = slice(r * F, (r + 1) * F)
                            ins = nc.tensor.matmul(ps[p, 2 + b, g * F:(g + 1) * F], self.u[p, b, g * F:(g + 1) * F],
                                                   self.ab[p, b, g * 2 * F + F:(g + 1) * 2 * F], start=True, stop=True)
                    ins.then_inc(pe_y.step("block", b), 1)
            ten.wait_ge(ac_y.sem, ac_y.at(PASSES - 1, "block", 1))
            for r in range(2):
                p = slice(r * F, (r + 1) * F)
                for f in range(F):
                    ins = nc.tensor.matmul(ps[p, 6 + r, 0:G], self.wdn[p, f, :], h[p, :, f], start=(f == 0), stop=(f == F - 1))
                ins.then_inc(pe_r.step("sums", r), 1)
            ten.wait_ge(ac_r.sem, ac_r.at(0, "sums", 1))
            for c in range(NCH):
                ins = nc.tensor.transpose(ps[0:P, 4, c * 128:(c + 1) * 128], lgT[:, c * P:(c + 1) * P], core.ident[:, :])
            ins.then_inc(pe_r.step("lg"), 1)
            dn.tensor(ten)
            ten.wait_ge(dn.ve.sem, dn.ve.at(0, "weight"))
            with ten.Fori(0, PASSES) as j:
                for b in range(2):
                    ten.wait_ge(ac_h.sem, ac_h.at(j, "block", b))
                    ten.wait_ge(table_dn[b], (j + 1) * (B + len(by_pool("dn"))) * DMA)
                    core.stand(ten)
                    ten.wait_ge(taken_dn[b], (j + 1) * 2 * others("dn") * DMA)
                    core.stand(ten)
                    for g in range(B):
                        for r in range(2):
                            p = slice(r * F, (r + 1) * F)
                            a = self.ab[p, b, g * K * F:(g + 1) * K * F].rearrange("p (k n) -> p k n", k=K)[:, :, 0:I]
                            ins = nc.tensor.matmul(ps[p, b, g * F:(g + 1) * F], self.pre[p, b, g * F:(g + 1) * F], a, start=True, stop=True)
                    ins.then_inc(pe_v.step("block", b), 1)
                    ten.wait_ge(ve_v.sem, ve_v.at(j, "block", b))
                    core.stand(ten)
                    for g in range(B):
                        for r in range(2):
                            p = slice(r * F, (r + 1) * F)
                            for k in range(K):
                                n = (g * K + k) * F
                                ins = nc.tensor.matmul(ps[r * F:r * F + I, 2 + b, g * I:(g + 1) * I], self.u[p, b, (g * K + k) * I:(g * K + k + 1) * I],
                                                       self.ab[p, b, n + I:n + F], start=(k == 0), stop=(k == K - 1))
                    ins.then_inc(pe_z.step("block", b), 1)


class Mlp:

    H = 1024
    HK = H // 128

    def build(self, core, run):
        nc, ps, HK = core.nc, core.ps, self.HK
        sb = run.sbuf
        self.prepare(core, run)
        yn, yT, hT = sb("yn", [T, U, D]), sb("yT", [128, KD, N4]), sb("hT", [128, HK, N4])
        ln = Norm(core, run, "ln")
        pe = Progress(core, "tensor", ("yT", KD), ("up", HK), "out")
        ac = Progress(core, "scalar", ("yT", KD), ("act", HK))
        ve = Progress(core, "vector", *ln.steps(), "yn", "inner", "out", "stats")
        po = Progress(core, "pool", ("lnrs", 1))
        block = run.block

        @block.gpsimd
        def _(pool):
            self.prepare_pool(core, run, pool)
            with pool.Fori(0, NCH) as c:
                ln.pool(pool, ve, po, c)

        @block.vector
        def _(dve):
            self.prepare_vector(core, run, dve)
            with dve.Fori(0, NCH) as c:
                ln.vector(dve, ve, c, lambda u, q: core.y[:, U * c + u, :], lambda u: None)
                dve.wait_ge(po.sem, po.at(c, "lnrs"))
                core.stand(dve)
                for u in range(U):
                    ln.apply(yn[:, u], core.y[:, U * c + u, :], u).then_inc(ve.step("yn", u), 1)
                for u in range(U):
                    x = core.x[:, U * c + u, :]
                    nc.vector.tensor_tensor(x, x, core.y[:, U * c + u, :], ALU.add).then_inc(ve.step("inner", u), 1)
                for u in range(U):
                    dve.wait_ge(pe.sem, pe.at(c, "out", u))
                    core.stand(dve)
                    dve.wait_ge(ve.sem, ve.at(c, "inner", u))
                    x = core.x[:, U * c + u, :]
                    nc.vector.tensor_tensor(x, x, ps[0:T, 4 + u, 0:D], ALU.add).then_inc(ve.step("out", u), 1)
                for u in range(U):
                    dve.wait_ge(ve.sem, ve.at(c, "out", u))
                    row_stats(core, dve, U * c + u).then_inc(ve.step("stats", u), 1)

        @block.scalar
        def _(act):
            self.prepare_scalar(core, run, act)
            with act.Fori(0, NCH) as c:
                for k in range(KD):
                    act.wait_ge(pe.sem, pe.at(c, "yT", k))
                    nc.scalar.activation(yT[:, k], ps[:, k, 0:N4], ACT.Identity, bias=self.shift[:, k:k + 1],
                                                 scale=self.gain[:, k:k + 1]).then_inc(ac.step("yT", k), 1)
                for i in range(HK):
                    act.wait_ge(pe.sem, pe.at(c, "up", i))
                    nc.scalar.activation(hT[:, i], ps[:, i % 4, 0:N4], self.act, bias=self.b1[:, i:i + 1]).then_inc(ac.step("act", i), 1)

        @block.tensor
        def _(ten):
            ten.wait_ge(run.arrived, run.loads)
            self.prepare_tensor(core, run, ten)
            with ten.Fori(0, NCH) as c:
                for k in range(KD):
                    for u in range(U):
                        if k == 0:
                            ten.wait_ge(ve.sem, ve.at(c, "yn", u))
                        ins = nc.tensor.transpose(ps[:, k, u * T:(u + 1) * T], yn[:, u, k * 128:(k + 1) * 128],
                                                  core.ident[0:T, 0:T])
                    ins.then_inc(pe.step("yT", k), 1)
                for i in range(HK):
                    if i >= 4:
                        ten.wait_ge(ac.sem, ac.at(c, "act", i - 4))
                    for k in range(KD):
                        if i == 0:
                            ten.wait_ge(ac.sem, ac.at(c, "yT", 1 if k else 0))
                        ins = nc.tensor.matmul(ps[:, i % 4, 0:N4], self.w1[:, k, i * 128:(i + 1) * 128], yT[:, k],
                                               start=(k == 0), stop=(k == KD - 1))
                    ins.then_inc(pe.step("up", i), 1)
                for u in range(U):
                    for i in range(HK):
                        if u == 0:
                            ten.wait_ge(ac.sem, ac.at(c, "act", i))
                        nc.tensor.matmul(ps[0:T, 4 + u, 0:D], hT[:, i, u * T:(u + 1) * T], self.w2[:, i, :],
                                         start=(i == 0), stop=False)
                    nc.tensor.matmul(ps[0:T, 4 + u, 0:D], core.ones[0:1, 0:T], self.b2, start=False, stop=True).then_inc(pe.step("out", u), 1)

    def prepare(self, core, run):
        pass

    def prepare_vector(self, core, run, dve):
        pass

    def prepare_pool(self, core, run, pool):
        pass

    def prepare_scalar(self, core, run, act):
        run.prefetch(act)
        act.wait_ge(run.arrived, run.loads)

    def prepare_tensor(self, core, run, ten):
        pass


class L0Mlp(Mlp):
    name = "L0_mlp"
    act = ACT.Gelu

    def weights(self, a, d):
        self.w1 = a.load(rows(d["L0_xattn_w1"]), 128, KD, self.H)
        self.w2 = a.load(rows(d["L0_xattn_w2"]), 128, self.HK, D)
        self.b1 = a.load(d["L0_xattn_b1_c"], 128, self.HK)
        self.b2 = a.load(every(d["L0_xattn_b2"], 1), 1, D)
        self.gain = a.load(d["L0_xattn_ln2_g_c"], 128, KD)
        self.shift = a.load(d["L0_xattn_ln2_b_c"], 128, KD)


class L1State:

    name = "L1_attn"
    DIST = (1, 2, 4, 8, 16, 32, 64)

    def weights(self, a, d):
        self.bw = a.load(rows(d["L1_attn_B_wT"]), 128, KD, 128)
        self.dw = a.load(rows(d["L1_attn_D_wT"]), 128, KD, D)
        self.s1 = a.load(rows(d["L1_attn_s_w1T"]), 128, KD, 128)
        self.gw = a.load(rows(d["L1_attn_g_wT"]), 128, KD, D)
        self.cw = a.load(d["L1_attn_C_wT"], 128, D)
        self.s2 = a.load(d["L1_attn_s_w2T"], 128, 128)
        self.sb1 = a.load(d["L1_attn_s_b1_c"], 128, 1)
        self.sb2 = a.load(d["L1_attn_s_b2_c"], 128, 1)
        self.bb = a.load(d["L1_attn_B_b_c"], 128, 1)
        self.cb = a.load(d["L1_attn_C_b_c"], 128, KD)
        self.db = a.load(d["L1_attn_D_b_c"], 128, KD)
        self.gb = a.load(d["L1_attn_g_b_c"], 128, KD)
        n = len(self.DIST)
        self.pow = a.take(128, n, 128)
        self.powT = a.take(128, n, 128)
        a.loads.append((self.pow[:, 0, :], d["L1_attn_A"]))
        a.loads.append((self.powT[:, 0, :], d["L1_attn_AT"]))

    def build(self, core, run):
        nc, ps, DIST = core.nc, core.ps, self.DIST
        sb = run.sbuf
        xn, xT = sb("xn", [T, U, D]), sb("xT", [128, KD, NB * T])
        s1, s2, h = sb("s1", [128, N4]), sb("s2", [128, N4]), sb("h", [128, NB, T])
        gate, z, ydb = sb("gate", [128, KD, N4]), sb("z", [128, KD, N4]), sb("ydb", [128, KD])
        norm, squared, squares = core.semaphore("norm"), core.semaphore("squared"), core.semaphore("squares")
        grown, added = core.semaphore("grown"), core.semaphore("added")
        pe = Progress(core, "tensor", ("xT", KD), ("s1", 1), ("s2", 1), ("b", 1))
        ac = Progress(core, "scalar", ("xT", KD), ("s1", 1), ("s2", 1))
        ve = Progress(core, "vector", "xn", ("u", 1))
        pe2 = Progress(core, "tensor2", ("g", KD), ("y", KD), "back")
        ac2 = Progress(core, "scalar2", ("gate", KD))
        ve2 = Progress(core, "vector2", ("z", KD), "out", "stats")
        block = run.block
        tok = lambda c: bass.ds(c * N4, N4)

        @block.gpsimd
        def _(pool):
            norm_pool(core, norm)

        @block.vector
        def _(dve):
            norm_vector(core, dve, None, norm)
            dve.wait_ge(run.arrived, run.loads)
            nc.vector.tensor_tensor(ydb[:, :], self.cb, self.db, ALU.add).then_inc(norm, 1)
            with dve.Fori(0, NCH) as c:
                for u in range(U):
                    normed(core, xn[:, u], U * c + u).then_inc(ve.step("xn", u), 1)
                dve.wait_ge(pe.sem, pe.at(c, "b"))
                dve.wait_ge(ac.sem, ac.at(c, "s2"))
                nc.vector.scalar_tensor_tensor(out=h[:, bass.ds(U * c, U), :].rearrange("p b t -> p (b t)"),
                                                       in0=ps[:, 4, 0:N4], scalar=self.bb, in1=s2[:, :],
                                                       op0=ALU.add, op1=ALU.mult).then_inc(ve.step("u"), 1)
            for i, dist in enumerate(DIST):
                for g in range(NCH):
                    dve.wait_ge(grown, NCH * i + g + 1)
                    hg = h[:, U * g:U * g + U, dist:T]
                    nc.vector.tensor_tensor(hg, hg, ps[:, g, 0:U * (T - dist)].rearrange("p (b t) -> p b t", b=U),
                                            ALU.add).then_inc(added, 1)
            dve.wait_ge(norm, 9)
            with dve.Fori(0, NCH) as c:
                for m in range(KD):
                    dve.wait_ge(pe2.sem, pe2.at(c, "y", m))
                    dve.wait_ge(ac2.sem, ac2.at(c, "gate", m))
                    nc.vector.scalar_tensor_tensor(out=z[:, m], in0=ps[:, 2 + m, 0:N4], scalar=ydb[:, m:m + 1],
                                                            in1=gate[:, m], op0=ALU.add, op1=ALU.mult).then_inc(ve2.step("z", m), 1)
                for u in range(U):
                    dve.wait_ge(pe2.sem, pe2.at(c, "back", u))
                    x = core.x[:, U * c + u, :]
                    nc.vector.tensor_tensor(x, x, ps[0:T, 4 + u, 0:D], ALU.add).then_inc(ve2.step("out", u), 1)
                for u in range(U):
                    dve.wait_ge(ve2.sem, ve2.at(c, "out", u))
                    row_stats(core, dve, U * c + u).then_inc(ve2.step("stats", u), 1)

        @block.scalar
        def _(act):
            run.prefetch(act)
            act.wait_ge(run.arrived, run.loads)
            for i in range(1, len(DIST)):
                act.wait_ge(squares, i)
                nc.scalar.copy(self.pow[:, i, :], ps[:, 6, 0:128]).then_inc(squared, 1)
                nc.scalar.copy(self.powT[:, i, :], ps[:, 6, 128:256]).then_inc(squared, 1)
            with act.Fori(0, NCH) as c:
                for k in range(KD):
                    act.wait_ge(pe.sem, pe.at(c, "xT", k))
                    nc.scalar.copy(xT[:, k, tok(c)], ps[:, k, 0:N4]).then_inc(ac.step("xT", k), 1)
                act.wait_ge(pe.sem, pe.at(c, "s1"))
                nc.scalar.activation(s1[:, :], ps[:, 2, 0:N4], ACT.Silu, bias=self.sb1).then_inc(ac.step("s1"), 1)
                act.wait_ge(pe.sem, pe.at(c, "s2"))
                nc.scalar.activation(s2[:, :], ps[:, 3, 0:N4], ACT.Sigmoid, bias=self.sb2).then_inc(ac.step("s2"), 1)
            with act.Fori(0, NCH) as c:
                for m in range(KD):
                    act.wait_ge(pe2.sem, pe2.at(c, "g", m))
                    nc.scalar.activation(gate[:, m], ps[:, m, 0:N4], ACT.Sigmoid, bias=self.gb[:, m:m + 1]).then_inc(ac2.step("gate", m), 1)

        @block.tensor
        def _(ten):
            ten.wait_ge(run.arrived, run.loads)
            for i in range(1, len(DIST)):
                if i > 1:
                    ten.wait_ge(squared, 2 * (i - 1))
                nc.tensor.matmul(ps[:, 6, 0:128], self.powT[:, i - 1, :], self.pow[:, i - 1, :], start=True, stop=True)
                nc.tensor.matmul(ps[:, 6, 128:256], self.pow[:, i - 1, :], self.powT[:, i - 1, :],
                                 start=True, stop=True).then_inc(squares, 1)
            ten.wait_ge(squared, 2 * (len(DIST) - 1))
            with ten.Fori(0, NCH) as c:
                for k in range(KD):
                    for u in range(U):
                        if k == 0:
                            ten.wait_ge(ve.sem, ve.at(c, "xn", u))
                        ins = nc.tensor.transpose(ps[:, k, u * T:(u + 1) * T], xn[:, u, k * 128:(k + 1) * 128],
                                                  core.ident[0:T, 0:T])
                    ins.then_inc(pe.step("xT", k), 1)
                for k in range(KD):
                    ten.wait_ge(ac.sem, ac.at(c, "xT", k))
                    ins = nc.tensor.matmul(ps[:, 2, 0:N4], self.s1[:, k, :], xT[:, k, tok(c)], start=(k == 0), stop=(k == KD - 1))
                ins.then_inc(pe.step("s1"), 1)
                ten.wait_ge(ac.sem, ac.at(c, "s1"))
                nc.tensor.matmul(ps[:, 3, 0:N4], self.s2, s1[:, :], start=True, stop=True).then_inc(pe.step("s2"), 1)
                for k in range(KD):
                    ins = nc.tensor.matmul(ps[:, 4, 0:N4], self.bw[:, k, :], xT[:, k, tok(c)], start=(k == 0), stop=(k == KD - 1))
                ins.then_inc(pe.step("b"), 1)
            for i, dist in enumerate(DIST):
                for g in range(NCH):
                    if i == 0:
                        ten.wait_ge(ve.sem, ve.at(g, "u"))
                    else:
                        ten.wait_ge(added, NCH * (i - 1) + g + 1)
                    nc.tensor.matmul(ps[:, g, 0:U * (T - dist)], self.powT[:, i, :], h[:, U * g:U * g + U, 0:T - dist],
                                     start=True, stop=True).then_inc(grown, 1)
            ten.wait_ge(added, NCH * len(DIST))
            with ten.Fori(0, NCH) as c:
                for m in range(KD):
                    for k in range(KD):
                        ins = nc.tensor.matmul(ps[:, m, 0:N4], self.gw[:, k, m * 128:(m + 1) * 128], xT[:, k, tok(c)],
                                               start=(k == 0), stop=(k == KD - 1))
                    ins.then_inc(pe2.step("g", m), 1)
                for m in range(KD):
                    for k in range(KD):
                        nc.tensor.matmul(ps[:, 2 + m, 0:N4], self.dw[:, k, m * 128:(m + 1) * 128], xT[:, k, tok(c)],
                                         start=(k == 0), stop=False)
                    nc.tensor.matmul(ps[:, 2 + m, 0:N4], self.cw[:, m * 128:(m + 1) * 128],
                                              h[:, bass.ds(U * c, U), :].rearrange("p b t -> p (b t)"),
                                              start=False, stop=True).then_inc(pe2.step("y", m), 1)
                for u in range(U):
                    for m in range(KD):
                        ten.wait_ge(ve2.sem, ve2.at(c, "z", m))
                        ins = nc.tensor.transpose(ps[0:T, 4 + u, m * 128:(m + 1) * 128], z[:, m, u * T:(u + 1) * T], core.ident[:, :])
                    ins.then_inc(pe2.step("back", u), 1)


class L1Cross:

    name = "L1_xattn"

    def weights(self, a, d):
        self.wq = a.load(rows(d["L1_xattn_Wq"]), 128, KD, D)
        self.wk = a.load(rows(d["L1_xattn_Wk"]), 128, KD, D)
        self.wvT = a.load(rows(d["L1_xattn_WvT"]), 128, KD, D)
        self.wqk = a.take(128, KD, D)

    def build(self, core, run):
        nc, d, ps = core.nc, core.dram, core.ps
        sb = run.sbuf
        xn, xT, qT = sb("xn", [T, U, D]), sb("xT", [128, U, KD * T]), sb("qT", [128, U, KD * T])
        ctx, ctxT = sb("ctx", [SP_, U, ST, D]), sb("ctxT", [128, U, KD, S])
        mask, keep, low = sb("mask", [T, U, S], I32), sb("keep", [T, U, S]), sb("low", [T, U, S])
        e = sb("e", [T, U, S])
        pT, acT = sb("pT", [SP_, U, ST * T]), sb("acT", [128, U, KD * T])
        mx, nmx, den, rden = (sb(n, [T, U]) for n in ("mx", "nmx", "den", "rden"))
        norm = core.semaphore("norm")
        wqk_ready = core.semaphore("wqk")
        loaded = [core.semaphore(f"ctx{u}") for u in range(U)]
        pe = Progress(core, "tensor", "xT", "qT", "e", "pT", "ac", "out")
        ac = Progress(core, "scalar", "xT", "qT", "exp", "pT", "acT")
        ve = Progress(core, "vector", "xn", "kept", "masked", "max", "negmax", "rden", "out", "stats")
        po = Progress(core, "pool", "gone", "low", "keep")
        LOADS = 3 * DMA
        SCALE = D ** -0.5
        block = run.block

        @block.sync
        def _(sp):
            def load(n, u):
                sp.dma_start(ctx[:, u], d["ctx"][n].rearrange("(s p) c -> p s c", p=SP_)).then_inc(loaded[u], DMA)
                sp.dma_start(ctxT[:, u], d["ctxT"][n].rearrange("(k p) s -> p k s", p=128)).then_inc(loaded[u], DMA)
                sp.dma_start(mask[:, u], d["mask"][n]).then_inc(loaded[u], DMA)
            for u in range(U):
                load(u, u)
            with sp.Fori(1, NCH) as c:
                for u in range(U):
                    sp.wait_ge(pe.sem, pe.at(c - 1, "ac", u))
                    core.stand(sp)
                    sp.wait_ge(po.sem, po.at(c - 1, "keep", u))
                    core.stand(sp)
                    load(U * c + u, u)

        @block.gpsimd
        def _(pool):
            norm_pool(core, norm)
            with pool.Fori(0, NCH) as c:
                for u in range(U):
                    pool.wait_ge(loaded[u], (c + 1) * LOADS)
                    core.stand(pool)
                    pool.wait_ge(pe.sem, pe.at(c, "xT", u))
                    core.stand(pool)
                    nc.gpsimd.tensor_scalar(keep[:, u], mask[:, u], 0.0, None, ALU.is_equal).then_inc(po.step("gone", u), 1)
                for u in range(U):
                    pool.wait_ge(po.sem, po.at(c, "gone", u))
                    core.stand(pool)
                    nc.gpsimd.tensor_scalar(low[:, u], keep[:, u], -1e10, None, ALU.mult).then_inc(po.step("low", u), 1)
                for u in range(U):
                    pool.wait_ge(po.sem, po.at(c, "low", u))
                    core.stand(pool)
                    nc.gpsimd.tensor_scalar(keep[:, u], keep[:, u], -1.0, 1.0, ALU.mult, ALU.add).then_inc(po.step("keep", u), 1)

        @block.vector
        def _(dve):
            norm_vector(core, dve, None, norm)
            with dve.Fori(0, NCH) as c:
                for u in range(U):
                    normed(core, xn[:, u], U * c + u).then_inc(ve.step("xn", u), 1)
                for u in range(U):
                    dve.wait_ge(pe.sem, pe.at(c, "e", u))
                    dve.wait_ge(po.sem, po.at(c, "keep", u))
                    nc.vector.tensor_tensor(e[:, u], ps[0:T, u, 0:S], keep[:, u], ALU.mult).then_inc(ve.step("kept", u), 1)
                for u in range(U):
                    dve.wait_ge(ve.sem, ve.at(c, "kept", u))
                    nc.vector.tensor_tensor(e[:, u], e[:, u], low[:, u], ALU.add).then_inc(ve.step("masked", u), 1)
                for u in range(U):
                    dve.wait_ge(ve.sem, ve.at(c, "masked", u))
                    nc.vector.tensor_reduce(mx[:, u:u + 1], e[:, u], AX.X, ALU.max).then_inc(ve.step("max", u), 1)
                for u in range(U):
                    dve.wait_ge(ve.sem, ve.at(c, "max", u))
                    nc.vector.tensor_scalar(nmx[:, u:u + 1], mx[:, u:u + 1], -SCALE, None, ALU.mult).then_inc(ve.step("negmax", u), 1)
                for u in range(U):
                    dve.wait_ge(ac.sem, ac.at(c, "exp", u))
                    nc.vector.reciprocal(rden[:, u:u + 1], den[:, u:u + 1]).then_inc(ve.step("rden", u), 1)
                for u in range(U):
                    dve.wait_ge(pe.sem, pe.at(c, "out", u))
                    dve.wait_ge(ve.sem, ve.at(c, "rden", u))
                    x = core.x[:, U * c + u, :]
                    nc.vector.scalar_tensor_tensor(out=x, in0=ps[0:T, 4 + u, 0:D], scalar=rden[:, u:u + 1],
                                                           in1=x, op0=ALU.mult, op1=ALU.add).then_inc(ve.step("out", u), 1)
                for u in range(U):
                    dve.wait_ge(ve.sem, ve.at(c, "out", u))
                    row_stats(core, dve, U * c + u).then_inc(ve.step("stats", u), 1)

        @block.scalar
        def _(act):
            run.prefetch(act)
            act.wait_ge(wqk_ready, 1)
            nc.scalar.copy(self.wqk, ps[:, 6:8, 0:D]).then_inc(wqk_ready, 1)
            with act.Fori(0, NCH) as c:
                for u in range(U):
                    act.wait_ge(pe.sem, pe.at(c, "xT", u))
                    nc.scalar.copy(xT[:, u], ps[:, u, 0:KD * T]).then_inc(ac.step("xT", u), 1)
                for u in range(U):
                    act.wait_ge(pe.sem, pe.at(c, "qT", u))
                    nc.scalar.copy(qT[:, u], ps[:, 4 + u, 0:KD * T]).then_inc(ac.step("qT", u), 1)
                for u in range(U):
                    act.wait_ge(ve.sem, ve.at(c, "negmax", u))
                    nc.scalar.activation(e[:, u], e[:, u], ACT.Exp, bias=nmx[:, u:u + 1], scale=SCALE,
                                                 accum_out=den[:, u:u + 1]).then_inc(ac.step("exp", u), 1)
                for u in range(U):
                    act.wait_ge(pe.sem, pe.at(c, "pT", u))
                    nc.scalar.copy(pT[:, u], ps[0:SP_, 4 + u, 0:ST * T]).then_inc(ac.step("pT", u), 1)
                for u in range(U):
                    act.wait_ge(pe.sem, pe.at(c, "ac", u))
                    nc.scalar.copy(acT[:, u], ps[:, u, 0:KD * T]).then_inc(ac.step("acT", u), 1)

        @block.tensor
        def _(ten):
            ten.wait_ge(run.arrived, run.loads)
            for k in range(KD):
                for h in range(KD):
                    ins = nc.tensor.matmul(ps[:, 6 + k, 0:D], self.wq[:, h, k * 128:(k + 1) * 128], self.wk[:, h, :],
                                           start=(h == 0), stop=(h == KD - 1))
            ins.then_inc(wqk_ready, 1)
            ten.wait_ge(wqk_ready, 2)
            with ten.Fori(0, NCH) as c:
                for u in range(U):
                    ten.wait_ge(ve.sem, ve.at(c, "xn", u))
                    transposes(core, ps[:, u], xn[:, u], T, KD).then_inc(pe.step("xT", u), 1)
                for u in range(U):
                    ten.wait_ge(ac.sem, ac.at(c, "xT", u))
                    for m in range(KD):
                        for k in range(KD):
                            ins = nc.tensor.matmul(ps[:, 4 + u, m * T:(m + 1) * T], self.wqk[:, k, m * 128:(m + 1) * 128],
                                                   xT[:, u, k * T:(k + 1) * T], start=(k == 0), stop=(k == KD - 1))
                    ins.then_inc(pe.step("qT", u), 1)
                for u in range(U):
                    ten.wait_ge(ac.sem, ac.at(c, "qT", u))
                    ten.wait_ge(loaded[u], (c + 1) * LOADS)
                    for k in range(KD):
                        ins = nc.tensor.matmul(ps[0:T, u, 0:S], qT[:, u, k * T:(k + 1) * T], ctxT[:, u, k, :],
                                               start=(k == 0), stop=(k == KD - 1))
                    ins.then_inc(pe.step("e", u), 1)
                for u in range(U):
                    ten.wait_ge(ac.sem, ac.at(c, "exp", u))
                    for s in range(ST):
                        ins = nc.tensor.transpose(ps[0:SP_, 4 + u, s * T:(s + 1) * T], e[:, u, s * SP_:(s + 1) * SP_],
                                                  core.ident[0:T, 0:T])
                    ins.then_inc(pe.step("pT", u), 1)
                for u in range(U):
                    ten.wait_ge(ac.sem, ac.at(c, "pT", u))
                    for m in range(KD):
                        for s in range(ST):
                            ins = nc.tensor.matmul(ps[:, u, m * T:(m + 1) * T], ctx[:, u, s, m * 128:(m + 1) * 128],
                                                   pT[:, u, s * T:(s + 1) * T], start=(s == 0), stop=(s == ST - 1))
                    ins.then_inc(pe.step("ac", u), 1)
                for u in range(U):
                    ten.wait_ge(ac.sem, ac.at(c, "acT", u))
                    for k in range(KD):
                        ins = nc.tensor.matmul(ps[0:T, 4 + u, 0:D], acT[:, u, k * T:(k + 1) * T], self.wvT[:, k, :],
                                               start=(k == 0), stop=(k == KD - 1))
                    ins.then_inc(pe.step("out", u), 1)


class Experts:

    K = 2

    def build(self, core, run):
        nc, d, ps, E, K, TS, HM, W, NT = core.nc, core.dram, core.ps, self.E, self.K, self.TS, self.HM, self.W, self.NT
        sb, R = run.sbuf, self.R
        slots = NT * TS
        Q = TS // 128
        J = -(-NB * T // TS)
        rows_in = core.scratch("rows_in", [slots, D])
        rows_out = core.scratch("rows_out", [slots, D])
        zero = sb("zero", [128, D])
        xn, xT = sb("xn", [T, U, D]), sb("xT", [128, KD, N4])
        lg = sb("lg", [T, NB, R])
        top, which = sb("top", [T, NB, 8]), sb("which", [T, NB, 8], U32)
        at = sb("at", [T, K, NB])
        hot = sb("hot", [T, K + 1, NB, E])
        place = sb("place", [T, NB, E])
        tmp = sb("tmp", [T, K, NB, E])
        slot, slot_i = sb("slot", [T, K, NB]), sb("slot_i", [T, K * NB], U32)
        s, e2, rden = sb("s", [T, K, NB]), sb("e2", [T, NB]), sb("rden", [T, NB])
        more, tiles = sb("more", [E, J]), sb("tiles", [E, 1])
        tiles_w, base = sb("tiles_w", [E, 128]), sb("base", [T, E])
        ended, table_f, table = sb("ended", [E, NT]), sb("table_f", [1, NT]), sb("table", [1, NT], I32)
        xs, xsT = sb("xs", [128, W, Q, D]), sb("xsT", [128, W, KD, TS])
        silu, hT = sb("silu", [128, 2, TS]), sb("hT", [128, W, HM, TS])
        ys, back = sb("ys", [128, W, Q, D]), sb("back", [T, NB, D])
        norm, zeroed, cleared = (core.semaphore(n) for n in ("norm", "zeroed", "cleared"))
        sent = core.pool_dma_semaphore("sent")
        loaded = [core.semaphore(f"loaded{w}") for w in range(W)]
        stored = [core.pool_dma_semaphore(f"stored{w}") for w in range(W)]
        fetched = [core.pool_dma_semaphore(f"fetched{g}") for g in range(NCH)]
        pe, ac = Progress(core, "tensor", ("xT", KD), ("lg", 1)), Progress(core, "scalar", ("xT", KD), ("lg", 1))
        ve, po = Progress(core, "vector", "xn"), Progress(core, "pool", "kept")
        ve_p = Progress(core, "vector_place", ("top", NB), ("which", NB), ("at", 1), ("hot", K), ("either", 1), ("gap", 1), ("more", 1), ("tiles", 1),
                        ("wide", 1), ("ended", 1), ("table_f", 1), ("table", 1), ("base", 1), ("place", 1), ("tmp", K), ("slot", K), ("slot_i", 1),
                        ("den", 1), ("s1", 1), ("s2", 1))
        pe_p = Progress(core, "tensor_place", ("place", 1), ("count", 1), ("base", 1), ("end", 1), ("table", 1))
        ac_p = Progress(core, "scalar_place", ("e2", 1))
        pe_t, pe_u, pe_d = (Progress(core, "tensor_" + n, (n, c)) for n, c in (("xsT", W), ("up", W * HM), ("down", W)))
        ac_s, ac_y = (Progress(core, "scalar_" + n, (n, c)) for n, c in (("silu", W * HM), ("ys", W)))
        ve_t, ve_h = (Progress(core, "vector_" + n, (n, c)) for n, c in (("xsT", W), ("h", W * HM)))
        ve_e = Progress(core, "vector_end", *(("first", U), ("second", U), ("stats", U)) * 1)
        block = run.block
        passes, LAG = NT // W, self.LAG
        ve_a = Progress(core, "vector_xT", ("xTa", KD))

        @block.sync
        def _(sp):
            sp.wait_ge(cleared, 1)
            sp.dma_start(rows_in.rearrange("(p r) c -> p r c", p=128), zero[:, :].unsqueeze(1).to_broadcast([128, slots // 128, D])).then_inc(zeroed, DMA)
            sp.wait_ge(ve_p.sem, ve_p.at(0, "table"))

            def weights(j, w):
                i = W * j + w
                e = sp.value_load(table[0:1, bass.ds(i, 1)], min_val=0, max_val=E - 1)
                for dst, src in self.of_expert(w, d, e):
                    sp.dma_start(dst, src).then_inc(loaded[w], DMA)

            def tile(j, w):
                i = W * j + w
                sp.dma_start(xs[:, w], rows_in[bass.ds(i * TS, TS), :].rearrange("(q p) c -> p q c", p=128)).then_inc(loaded[w], DMA)
            for w in range(W):
                weights(0, w)
            sp.wait_ge(sent, DMA * K * NB)
            for w in range(W):
                tile(0, w)
            with sp.Fori(1, passes) as j:
                for w in range(W):
                    sp.wait_ge(pe_d.sem, pe_d.at(j - 1, "down", w))
                    core.stand(sp)
                    weights(j, w)
                    tile(j, w)

        LOADS = DMA * (self.PARTS + 1)

        @block.gpsimd
        def _(pool):
            nc.gpsimd.memset(zero[:, :], 0.0).then_inc(cleared, 1)
            norm_pool(core, norm)
            with pool.Fori(0, NCH) as c:
                for u in range(U):
                    pool.wait_ge(ve.sem, ve.at(c, "xn", u))
                    core.stand(pool)
                    nc.gpsimd.tensor_copy(core.y[:, bass.ds(U * c + u, 1), :], xn[:, u:u + 1, :]).then_inc(po.step("kept", u), 1)
            pool.wait_ge(zeroed, DMA)
            pool.wait_ge(ve_p.sem, ve_p.at(0, "slot_i"))
            pool.wait_ge(po.sem, po.at(NCH - 1, "kept", U - 1))
            for k in range(K):
                for n in range(NB):
                    nc.gpsimd.indirect_dma_start(out=rows_in[:, :], out_offset=bass.IndirectOffsetOnAxis(ap=slot_i[:, k * NB + n:k * NB + n + 1], axis=0),
                                                 in_=core.y[:, n, :], in_offset=None).then_inc(sent, DMA)
            with pool.Fori(0, passes) as j:
                for w in range(W):
                    pool.wait_ge(ac_y.sem, ac_y.at(j, "ys", w))
                    core.stand(pool)
                    pool.dma_start(rows_out[bass.ds((W * j + w) * TS, TS), :].rearrange("(q p) c -> p q c", p=128), ys[:, w]).then_inc(stored[w], DMA)
            for w in range(W):
                pool.wait_ge(stored[w], DMA * passes)
            for n in range(NB):
                for k in range(K):
                    dst = core.y if k == 0 else back
                    nc.gpsimd.indirect_dma_start(out=dst[:, n, :], out_offset=None, in_=rows_out[:, :],
                                                 in_offset=bass.IndirectOffsetOnAxis(ap=slot_i[:, k * NB + n:k * NB + n + 1], axis=0)).then_inc(fetched[n // U], DMA)

        @block.vector
        def _(dve):
            norm_vector(core, dve, None, norm)
            dve.wait_ge(run.arrived, run.loads)
            with dve.Fori(0, NCH) as c:
                for u in range(U):
                    normed(core, xn[:, u], U * c + u).then_inc(ve.step("xn", u), 1)
                if self.shared:
                    for k in range(KD):
                        dve.wait_ge(ac.sem, ac.at(c, "xT", k))
                        nc.vector.tensor_copy(self.xTa[:, k, bass.ds(c * N4, N4)], xT[:, k]).then_inc(ve_a.step("xTa", k), 1)
                dve.wait_ge(po.sem, po.at(c, "kept", U - 1))
                dve.wait_ge(pe.sem, pe.at(c, "xT", KD - 1))
                core.stand(dve)
            dve.wait_ge(ac.sem, ac.at(NCH - 1, "lg"))
            for n in range(NB):
                nc.vector.max(top[:, n, :], lg[:, n, 0:E]).then_inc(ve_p.step("top", n), 1)
            for n in range(NB):
                dve.wait_ge(ve_p.sem, ve_p.at(0, "top", n))
                nc.vector.max_index(which[:, n, :], top[:, n, :], lg[:, n, 0:E]).then_inc(ve_p.step("which", n), 1)
            dve.wait_ge(ve_p.sem, ve_p.at(0, "which", NB - 1))
            nc.vector.tensor_copy(at[:, :, :].rearrange("p k n -> p n k"), which[:, :, 0:K]).then_inc(ve_p.step("at"), 1)
            dve.wait_ge(ve_p.sem, ve_p.at(0, "at"))
            for k in range(K):
                nc.vector.tensor_tensor(hot[:, k], self.iota[0:T, 0:E].unsqueeze(1).to_broadcast([T, NB, E]),
                                                  at[:, k, :].unsqueeze(2).to_broadcast([T, NB, E]), ALU.is_equal).then_inc(ve_p.step("hot", k), 1)
            dve.wait_ge(ve_p.sem, ve_p.at(0, "hot", K - 1))
            nc.vector.tensor_tensor(hot[:, K], hot[:, 0], hot[:, 1], ALU.add).then_inc(ve_p.step("either"), 1)
            nc.vector.tensor_tensor(e2[:, :], top[:, :, 1], top[:, :, 0], ALU.subtract).then_inc(ve_p.step("gap"), 1)
            dve.wait_ge(pe_p.sem, pe_p.at(0, "count"))
            nc.vector.tensor_scalar(more[:, :], self.steps, ps[0:E, 3, 0:1], None, ALU.is_lt).then_inc(ve_p.step("more"), 1)
            dve.wait_ge(ve_p.sem, ve_p.at(0, "more"))
            nc.vector.tensor_reduce(tiles[:, :], more[:, :], AX.X, ALU.add).then_inc(ve_p.step("tiles"), 1)
            dve.wait_ge(ve_p.sem, ve_p.at(0, "tiles"))
            nc.vector.tensor_scalar(tiles_w[:, :], core.ones[0:E, :], tiles[:, 0:1], None, ALU.mult).then_inc(ve_p.step("wide"), 1)
            dve.wait_ge(pe_p.sem, pe_p.at(0, "end"))
            nc.vector.tensor_scalar(ended[:, :], self.iota[0:E, 0:NT], ps[0:E, 5, 0:1], None, ALU.is_ge).then_inc(ve_p.step("ended"), 1)
            dve.wait_ge(pe_p.sem, pe_p.at(0, "table"))
            nc.vector.tensor_scalar(table_f[:, :], ps[0:1, 6, 0:NT], float(E - 1), None, ALU.min).then_inc(ve_p.step("table_f"), 1)
            dve.wait_ge(ve_p.sem, ve_p.at(0, "table_f"))
            nc.vector.tensor_copy(table[:, :], table_f[:, :]).then_inc(ve_p.step("table"), 1)
            nc.vector.tensor_scalar(base[:, :], ps[0:T, 4, 0:E], float(TS), None, ALU.mult).then_inc(ve_p.step("base"), 1)
            dve.wait_ge(ve_p.sem, ve_p.at(0, "base"))
            nc.vector.tensor_tensor(place[:, :, :], ps[0:T, 2, 0:NB * E].rearrange("p (n e) -> p n e", n=NB),
                                              base[:, :].unsqueeze(1).to_broadcast([T, NB, E]), ALU.add).then_inc(ve_p.step("place"), 1)
            dve.wait_ge(ve_p.sem, ve_p.at(0, "place"))
            for k in range(K):
                nc.vector.tensor_tensor(tmp[:, k], hot[:, k], place[:, :, :], ALU.mult).then_inc(ve_p.step("tmp", k), 1)
            for k in range(K):
                dve.wait_ge(ve_p.sem, ve_p.at(0, "tmp", k))
                nc.vector.tensor_reduce(slot[:, k, :], tmp[:, k], AX.X, ALU.add).then_inc(ve_p.step("slot", k), 1)
            dve.wait_ge(ve_p.sem, ve_p.at(0, "slot", K - 1))
            nc.vector.tensor_copy(slot_i[:, :], slot[:, :, :].rearrange("p k n -> p (k n)")).then_inc(ve_p.step("slot_i"), 1)
            dve.wait_ge(ac_p.sem, ac_p.at(0, "e2"))
            nc.vector.tensor_scalar(rden[:, :], e2[:, :], 1.0, None, ALU.add).then_inc(ve_p.step("den"), 1)
            dve.wait_ge(ve_p.sem, ve_p.at(0, "den"))
            nc.vector.reciprocal(s[:, 0, :], rden[:, :]).then_inc(ve_p.step("s1"), 1)
            dve.wait_ge(ve_p.sem, ve_p.at(0, "s1"))
            nc.vector.tensor_tensor(s[:, 1, :], s[:, 0, :], e2[:, :], ALU.mult).then_inc(ve_p.step("s2"), 1)
            if self.shared:
                self.shared_vector(core, dve)
            with dve.Fori(0, passes) as j:
                def turned(w):
                    dve.wait_ge(pe_t.sem, pe_t.at(j, "xsT", w))
                    nc.vector.tensor_copy(xsT[:, w].rearrange("p k s -> p (k s)"), ps[:, w % 2, 0:KD * TS]).then_inc(ve_t.step("xsT", w), 1)
                turned(0)
                for w in range(W):
                    for m in range(HM):
                        i = w * HM + m
                        dve.wait_ge(ac_s.sem, ac_s.at(j, "silu", i))
                        up = ps[:, 2 + i % 4, TS:2 * TS]
                        h = hT[:, w, m]
                        if self.biased:
                            ins = nc.vector.scalar_tensor_tensor(out=h, in0=up, scalar=self.bias(w, HM + m), in1=silu[:, i % 2], op0=ALU.add, op1=ALU.mult)
                        else:
                            ins = nc.vector.tensor_tensor(h, up, silu[:, i % 2], ALU.mult)
                        ins.then_inc(ve_h.step("h", i), 1)
                    if w + 1 < W:
                        turned(w + 1)
            dve.wait_ge(ve_p.sem, ve_p.at(0, "s2"))
            for g in range(NCH):
                dve.wait_ge(fetched[g], DMA * K * U)
                for k in range(K):
                    for u in range(U):
                        n = U * g + u
                        if k:
                            dve.wait_ge(ve_e.sem, ve_e.at(g, "first", u))
                        x = core.x[:, n, :]
                        ins = nc.vector.scalar_tensor_tensor(out=x, in0=(back if k else core.y)[:, n, :], scalar=s[:, k, n:n + 1], in1=x, op0=ALU.mult, op1=ALU.add)
                        ins.then_inc(ve_e.step("second" if k else "first", u), 1)
                for u in range(U):
                    dve.wait_ge(ve_e.sem, ve_e.at(g, "second", u))
                    row_stats(core, dve, U * g + u).then_inc(ve_e.step("stats", u), 1)

        @block.scalar
        def _(act):
            run.prefetch(act)
            act.wait_ge(run.arrived, run.loads)
            with act.Fori(0, NCH) as c:
                for k in range(KD):
                    act.wait_ge(pe.sem, pe.at(c, "xT", k))
                    nc.scalar.copy(xT[:, k], ps[:, k, 0:N4]).then_inc(ac.step("xT", k), 1)
                act.wait_ge(pe.sem, pe.at(c, "lg"))
                nc.scalar.copy(lg[:, bass.ds(U * c, U), :], ps[0:T, 2, 0:U * R].rearrange("p (u r) -> p u r", u=U)).then_inc(ac.step("lg"), 1)
            act.wait_ge(ve_p.sem, ve_p.at(0, "gap"))
            nc.scalar.activation(e2[:, :], e2[:, :], ACT.Exp).then_inc(ac_p.step("e2"), 1)
            if self.shared:
                self.shared_scalar(core, act, lg)
            def body(j, first):
                def hidden(w):
                    for m in range(HM):
                        i = w * HM + m
                        if i >= 2:
                            act.wait_ge(ve_h.sem, ve_h.at(j, "h", i - 2))
                        act.wait_ge(pe_u.sem, pe_u.at(j, "up", i))
                        src = ps[:, 2 + i % 4, 0:TS]
                        if self.biased:
                            ins = nc.scalar.activation(silu[:, i % 2], src, ACT.Silu, bias=self.bias(w, m))
                        else:
                            ins = nc.scalar.activation(silu[:, i % 2], src, ACT.Silu)
                        ins.then_inc(ac_s.step("silu", i), 1)

                def result(w):
                    if not first:
                        act.wait_ge(stored[w], j * DMA)
                    act.wait_ge(pe_d.sem, pe_d.at(j, "down", w))
                    nc.scalar.copy(ys[:, w].rearrange("p q c -> p (q c)"), ps[:, 6 + w % 2, 0:Q * D]).then_inc(ac_y.step("ys", w), 1)
                for w in range(W + LAG):
                    if w < W:
                        hidden(w)
                    if w >= LAG:
                        result(w - LAG)
            body(0, True)
            with act.Fori(1, passes) as j:
                body(j, False)

        @block.tensor
        def _(ten):
            ten.wait_ge(run.arrived, run.loads)
            with ten.Fori(0, NCH) as c:
                for k in range(KD):
                    for u in range(U):
                        if k == 0:
                            ten.wait_ge(ve.sem, ve.at(c, "xn", u))
                        ins = nc.tensor.transpose(ps[:, k, u * T:(u + 1) * T], xn[:, u, k * 128:(k + 1) * 128], core.ident[0:T, 0:T])
                    ins.then_inc(pe.step("xT", k), 1)
                for u in range(U):
                    for k in range(KD):
                        if u == 0:
                            ten.wait_ge(ac.sem, ac.at(c, "xT", k))
                        ins = nc.tensor.matmul(ps[0:T, 2, u * R:(u + 1) * R], xT[:, k, u * T:(u + 1) * T], self.wr[:, k, :],
                                               start=(k == 0), stop=(k == KD - 1 and not self.biased))
                    if self.biased:
                        ins = nc.tensor.matmul(ps[0:T, 2, u * R:(u + 1) * R], core.ones[0:1, 0:T], self.br, start=False, stop=True)
                ins.then_inc(pe.step("lg"), 1)
            ten.wait_ge(ve_p.sem, ve_p.at(0, "either"))
            ten.wait_ge(ac.sem, ac.at(NCH - 1, "lg"))
            either = hot[:, K]
            by_batch = ps[0:T, 2, 0:NB * E].rearrange("p (n e) -> p n e", n=NB)
            nc.tensor.matmul(by_batch, self.before[0:T, 0:T], either, start=True, stop=False)
            for n in range(NB - 1):
                ins = nc.tensor.matmul(by_batch[:, n + 1:NB, :], core.ones[0:T, 0:T], either[:, n:n + 1, :].to_broadcast([T, NB - 1 - n, E]),
                                       start=False, stop=(n == NB - 2))
            ins.then_inc(pe_p.step("place"), 1)
            for n in range(NB):
                ins = nc.tensor.matmul(ps[0:E, 3, 0:1], either[:, n, :], core.ones[0:T, 0:1], start=(n == 0), stop=(n == NB - 1))
            ins.then_inc(pe_p.step("count"), 1)
            ten.wait_ge(ve_p.sem, ve_p.at(0, "wide"))
            nc.tensor.matmul(ps[0:T, 4, 0:E], tiles_w[:, 0:T], self.before[0:E, 0:E], start=True, stop=True).then_inc(pe_p.step("base"), 1)
            nc.tensor.matmul(ps[0:E, 5, 0:1], self.upto[0:E, 0:E], tiles[:, 0:1], start=True, stop=True).then_inc(pe_p.step("end"), 1)
            ten.wait_ge(ve_p.sem, ve_p.at(0, "ended"))
            nc.tensor.matmul(ps[0:1, 6, 0:NT], core.ones[0:E, 0:1], ended[:, :], start=True, stop=True).then_inc(pe_p.step("table"), 1)
            ten.wait_ge(ve_p.sem, ve_p.at(0, "place"))
            if self.shared:
                self.shared_tensor(core, ten)
            with ten.Fori(0, passes) as j:
                def turn(w):
                    if w >= 2:
                        ten.wait_ge(ve_t.sem, ve_t.at(j, "xsT", w - 2))
                    ten.wait_ge(loaded[w], (j + 1) * LOADS)
                    for q in range(Q):
                        for k in range(KD):
                            ins = nc.tensor.transpose(ps[:, w % 2, k * TS + q * 128:k * TS + (q + 1) * 128], xs[:, w, q, k * 128:(k + 1) * 128], core.ident[:, :])
                    ins.then_inc(pe_t.step("xsT", w), 1)

                def hidden(w):
                    ten.wait_ge(ve_t.sem, ve_t.at(j, "xsT", w))
                    for m in range(HM):
                        i = w * HM + m
                        if i >= 4:
                            ten.wait_ge(ve_h.sem, ve_h.at(j, "h", i - 4))
                        for b in range(2):
                            for k in range(KD):
                                ins = nc.tensor.matmul(ps[:, 2 + i % 4, b * TS:(b + 1) * TS], self.up(w, k, b * HM + m), xsT[:, w, k],
                                                       start=(k == 0), stop=(k == KD - 1))
                        ins.then_inc(pe_u.step("up", i), 1)

                def result(w):
                    if w >= 2:
                        ten.wait_ge(ac_y.sem, ac_y.at(j, "ys", w - 2))
                    ten.wait_ge(ve_h.sem, ve_h.at(j, "h", w * HM + HM - 1))
                    for q in range(Q):
                        for m in range(HM):
                            ins = nc.tensor.matmul(ps[:, 6 + w % 2, q * D:(q + 1) * D], hT[:, w, m, q * 128:(q + 1) * 128], self.down(w, m),
                                                   start=(m == 0), stop=(m == HM - 1 and not self.biased))
                        if self.biased:
                            ins = nc.tensor.matmul(ps[:, 6 + w % 2, q * D:(q + 1) * D], core.ones[0:1, 0:128], self.bias_down(w), start=False, stop=True)
                    ins.then_inc(pe_d.step("down", w), 1)
                turn(0)
                for w in range(W + LAG):
                    if w < W:
                        hidden(w)
                    if w + 1 < W:
                        turn(w + 1)
                    if w >= LAG:
                        result(w - LAG)


def tiles_for_any(experts, size, w):
    return -(-((Experts.K * NB * T + experts * (size - 1)) // size) // w) * w


class L1Experts(Experts):

    name = "L1_ffn"
    E, TS, W = 16, 128, 4
    HM = 1
    R = E + 1
    NT = tiles_for_any(E, TS, W)
    LAG = 1
    shared, biased = True, False
    PARTS = 1
    UP, DOWN = KD * 2 * 128, D
    SM = 512 // 128

    def weights(self, a, d):
        n = self.name + "_"
        self.packed = a.take(128, self.W, self.UP + self.DOWN)
        self.xTa = a.take(128, KD, NB * T)
        self.wr = a.load(rows(d[n + "routerT"]), 128, KD, self.R)
        self.sg, self.su = (a.load(rows(d[n + k + "T"]), 128, KD, 128 * self.SM) for k in ("Ws_gate", "Ws_up"))
        self.sd = a.load(rows(d[n + "Ws_downT"]), 128, self.SM, D)
        self.iota = a.load(every(d["iota"], 128), 128, 64)
        self.before = a.load(d["before"], 128, 128)
        self.upto = a.load(d["upto"][0:self.E, 0:self.E], self.E, self.E)
        self.steps = a.load(every(d["L1_ffn_steps"], self.E), self.E, -(-NB * T // self.TS))

    @staticmethod
    def pack(np, a):
        part = lambda m: m.swapaxes(-1, -2).reshape(m.shape[0], -1, 128, m.shape[1]).swapaxes(1, 2)
        up = np.concatenate([part(a.pop("L1_ffn_We_gate")), part(a.pop("L1_ffn_We_up"))], axis=3)
        down = part(a.pop("L1_ffn_We_down"))
        return np.concatenate([m.reshape(m.shape[0], 128, -1) for m in (up, down)], axis=2)

    def of_expert(self, w, d, e):
        yield self.packed[:, w, :], d["L1_ffn_packed"][bass.ds(e, 1)].rearrange("a p n -> p (a n)")

    def up(self, w, k, m):
        return self.packed[:, w, k * 256 + m * 128:k * 256 + (m + 1) * 128]

    def down(self, w, m):
        return self.packed[:, w, self.UP:self.UP + D]

    def build(self, core, run):
        sb, SM = run.sbuf, self.SM
        self.gate = sb("gate", [T, NB])
        self.ssilu, self.sh = sb("ssilu", [128, 2, N4]), sb("sh", [128, SM, N4])
        self.pe_s = Progress(core, "tensor_shared", ("up", SM), "down")
        self.ac_g = Progress(core, "scalar_gate", ("gate", 1))
        self.ac_sh, self.ve_sh = Progress(core, "scalar_shared", ("silu", SM)), Progress(core, "vector_shared", ("h", SM), "add")
        super().build(core, run)

    def shared_vector(self, core, dve):
        nc, ps, SM = core.nc, core.ps, self.SM
        dve.wait_ge(self.ac_g.sem, self.ac_g.at(0, "gate"))
        with dve.Fori(0, NCH) as c:
            for m in range(SM):
                dve.wait_ge(self.ac_sh.sem, self.ac_sh.at(c, "silu", m))
                nc.vector.tensor_tensor(self.sh[:, m], ps[:, 2 + m % 2, 0:N4], self.ssilu[:, m % 2], ALU.mult).then_inc(self.ve_sh.step("h", m), 1)
            for u in range(U):
                dve.wait_ge(self.pe_s.sem, self.pe_s.at(c, "down", u))
                x = core.x[:, U * c + u, :]
                nc.vector.scalar_tensor_tensor(out=x, in0=ps[0:T, 4 + u, 0:D], scalar=self.gate[:, bass.ds(U * c + u, 1)], in1=x,
                                                               op0=ALU.mult, op1=ALU.add).then_inc(self.ve_sh.step("add", u), 1)
        dve.wait_ge(self.ve_sh.sem, self.ve_sh.at(NCH - 1, "add", U - 1))

    def shared_scalar(self, core, act, lg):
        nc, ps, SM = core.nc, core.ps, self.SM
        nc.scalar.activation(self.gate[:, :], lg[:, :, self.E], ACT.Sigmoid).then_inc(self.ac_g.step("gate"), 1)
        with act.Fori(0, NCH) as c:
            for m in range(SM):
                if m >= 2:
                    act.wait_ge(self.ve_sh.sem, self.ve_sh.at(c, "h", m - 2))
                act.wait_ge(self.pe_s.sem, self.pe_s.at(c, "up", m))
                nc.scalar.activation(self.ssilu[:, m % 2], ps[:, m % 2, 0:N4], ACT.Silu).then_inc(self.ac_sh.step("silu", m), 1)

    def shared_tensor(self, core, ten):
        nc, ps, SM = core.nc, core.ps, self.SM
        with ten.Fori(0, NCH) as c:
            for m in range(SM):
                if m >= 2:
                    ten.wait_ge(self.ve_sh.sem, self.ve_sh.at(c, "h", m - 2))
                for b, w in enumerate((self.sg, self.su)):
                    for k in range(KD):
                        ins = nc.tensor.matmul(ps[:, 2 * b + m % 2, 0:N4], w[:, k, m * 128:(m + 1) * 128], self.xTa[:, k, bass.ds(c * N4, N4)],
                                               start=(k == 0), stop=(k == KD - 1))
                ins.then_inc(self.pe_s.step("up", m), 1)
            for u in range(U):
                for m in range(SM):
                    if u == 0:
                        ten.wait_ge(self.ve_sh.sem, self.ve_sh.at(c, "h", m))
                    ins = nc.tensor.matmul(ps[0:T, 4 + u, 0:D], self.sh[:, m, u * T:(u + 1) * T], self.sd[:, m, :], start=(m == 0), stop=(m == SM - 1))
                ins.then_inc(self.pe_s.step("down", u), 1)


class L2Experts(Experts):

    name = "L2_ffn"
    E, TS, W = 8, 256, 2
    HM = 1024 // 128
    R = E
    NT = tiles_for_any(E, TS, W)
    LAG = 0
    shared, biased = False, True
    PARTS = 2
    UP, DOWN = KD * 2 * 1024, HM * D

    def weights(self, a, d):
        self.packed = a.take(128, self.W, self.UP + self.DOWN + 2 * self.HM)
        self.wr = a.load(rows(d["L2_ffn_router_wT"]), 128, KD, self.E)
        self.br = a.load(every(d["L2_ffn_router_b"], 1), 1, self.E)
        self.iota = a.load(every(d["iota"], 128), 128, 64)
        self.before = a.load(d["before"], 128, 128)
        self.upto = a.load(d["upto"][0:self.E, 0:self.E], self.E, self.E)
        self.steps = a.load(every(d["L2_ffn_steps"], self.E), self.E, -(-NB * T // self.TS))

    @staticmethod
    def pack(np, a):
        part = lambda m: m.swapaxes(-1, -2).reshape(m.shape[0], -1, 128, m.shape[1]).swapaxes(1, 2).reshape(m.shape[0], 128, -1)
        return np.concatenate([part(a.pop("L2_ffn_w1")), part(a.pop("L2_ffn_w2")),
                               a.pop("L2_ffn_b1").reshape(8, -1, 128).swapaxes(1, 2)], axis=2)

    def of_expert(self, w, d, e):
        yield self.packed[:, w, :], d["L2_ffn_packed"][bass.ds(e, 1)].rearrange("a p n -> p (a n)")
        yield self.bdown[:, w, :], d["L2_ffn_b2"][bass.ds(e, 1), :]

    def build(self, core, run):
        self.bdown = run.sbuf("bdown", [1, self.W, D])
        super().build(core, run)

    def up(self, w, k, m):
        return self.packed[:, w, k * 2048 + m * 128:k * 2048 + (m + 1) * 128]

    def down(self, w, m):
        return self.packed[:, w, self.UP + m * D:self.UP + (m + 1) * D]

    def bias(self, w, m):
        return self.packed[:, w, self.UP + self.DOWN + m:self.UP + self.DOWN + m + 1]

    def bias_down(self, w):
        return self.bdown[:, w, :]


class L2Graph:

    name = "L2_attn"
    H = 8
    HD = D // H
    HQ = 128 // HD

    def weights(self, a, d):
        self.wl = a.load(rows(d["L2_attn_WlT"]), 128, KD, D)
        self.wr = a.load(rows(d["L2_attn_WrT"]), 128, KD, D)
        self.wf = a.load(rows(d["L2_attn_WfT"]), 128, KD, D)
        self.gam = a.load(every(d["L2_attn_ln_gamma"], T), T, D)
        self.bet = a.load(every(d["L2_attn_ln_beta"], T), T, D)
        self.att = a.take(128, 2)
        for q in range(self.HQ):
            for i, k in enumerate(("att_l", "att_r")):
                a.loads.append((self.att[q * self.HD:(q + 1) * self.HD, i:i + 1],
                                d["L2_attn_" + k].rearrange("a d -> d a")))
        self.attl = a.take(128, T)
        self.attr = a.take(128, T)

    def build(self, core, run):
        nc, ps, H, HD, HQ = core.nc, core.ps, self.H, self.HD, self.HQ
        sb = run.sbuf
        xn, xT = sb("xn", [T, U, D]), sb("xT", [128, U, KD * T])
        f, lk = sb("f", [128, U, 2 * KD * T]), sb("lk", [128, U, 2 * KD * T])
        fr = sb("fr", [T, U, D])
        p, pT = sb("p", [T, U, H * T]), sb("pT", [T, U, H * T])
        ctxT = sb("ctxT", [128, U, KD * T])
        mx, den, rden = sb("mx", [T, U, H]), sb("den", [T, U, H]), sb("rden", [T, U, H])
        y = sb("y", [T, U, D])
        norm, spread = core.semaphore("norm"), core.semaphore("spread")
        ln = Norm(core, run, "ln")
        pe = Progress(core, "tensor", "xT", "f", "fr", "e", ("pT", 2 * U), "ctx", "out")
        ac = Progress(core, "scalar", "xT", "f", "fr", "exp", ("pT", 2 * U), "ctx")
        ve = Progress(core, "vector", "xn", "leaky", "max", "sub", "den", "rden", "p", "y", *ln.steps(),
                      "yn", "gain", "shift", "out", "stats")
        po = Progress(core, "pool", ("lnrs", 1))
        block = run.block
        heads = lambda v: v.rearrange("p (h s) -> p h s", s=T)
        HB = H // 2 * T

        def scores(u):
            return ps[0:T, 4 * (u // 2):4 * (u // 2) + HQ, (u % 2) * KD * T:(u % 2 + 1) * KD * T].rearrange(
                "p q (b s) -> p q b s", b=KD)

        @block.gpsimd
        def _(pool):
            norm_pool(core, norm)
            with pool.Fori(0, NCH) as c:
                ln.pool(pool, ve, po, c)

        @block.vector
        def _(dve):
            dve.wait_ge(run.arrived, run.loads)
            nc.vector.tensor_scalar(self.attl, core.ones[:, 0:T], self.att[:, 0:1], None, ALU.mult).then_inc(spread, 1)
            nc.vector.tensor_scalar(self.attr, core.ones[:, 0:T], self.att[:, 1:2], None, ALU.mult).then_inc(spread, 1)
            norm_vector(core, dve, None, norm)
            with dve.Fori(0, NCH) as c:
                for u in range(U):
                    normed(core, xn[:, u], U * c + u).then_inc(ve.step("xn", u), 1)
                for u in range(U):
                    dve.wait_ge(ac.sem, ac.at(c, "f", u))
                    nc.vector.scalar_tensor_tensor(out=lk[:, u], in0=f[:, u], scalar=0.01, in1=f[:, u],
                                                           op0=ALU.mult, op1=ALU.max).then_inc(ve.step("leaky", u), 1)
                for u in range(U):
                    dve.wait_ge(pe.sem, pe.at(c, "e", u | 1))
                    nc.vector.tensor_reduce(mx[:, u], scores(u), AX.X, ALU.max).then_inc(ve.step("max", u), 1)
                for u in range(U):
                    dve.wait_ge(ve.sem, ve.at(c, "max", u))
                    nc.vector.tensor_tensor(p[:, u].rearrange("p (q b s) -> p q b s", q=HQ, b=KD), scores(u),
                                                    mx[:, u].rearrange("p (q b) -> p q b", q=HQ).unsqueeze(3).to_broadcast([T, HQ, KD, T]),
                                                    ALU.subtract).then_inc(ve.step("sub", u), 1)
                for u in range(U):
                    dve.wait_ge(ac.sem, ac.at(c, "exp", u))
                    nc.vector.tensor_reduce(den[:, u, :], heads(p[:, u]), AX.X, ALU.add).then_inc(ve.step("den", u), 1)
                for u in range(U):
                    dve.wait_ge(ve.sem, ve.at(c, "den", u))
                    nc.vector.reciprocal(rden[:, u, :], den[:, u, :]).then_inc(ve.step("rden", u), 1)
                for u in range(U):
                    dve.wait_ge(ve.sem, ve.at(c, "rden", u))
                    nc.vector.tensor_tensor(heads(p[:, u]), heads(p[:, u]),
                                                    rden[:, u, :].unsqueeze(2).to_broadcast([T, H, T]), ALU.mult).then_inc(ve.step("p", u), 1)
                for u in range(U):
                    dve.wait_ge(pe.sem, pe.at(c, "out", u))
                    nc.vector.tensor_tensor(y[:, u], xn[:, u], ps[0:T, 4 + u, 0:D], ALU.add).then_inc(ve.step("y", u), 1)
                ln.vector(dve, ve, c, lambda u, q: y[:, u], lambda u: dve.wait_ge(ve.sem, ve.at(c, "y", u)))
                dve.wait_ge(po.sem, po.at(c, "lnrs"))
                core.stand(dve)
                for u in range(U):
                    ln.apply(y[:, u], y[:, u], u).then_inc(ve.step("yn", u), 1)
                for u in range(U):
                    dve.wait_ge(ve.sem, ve.at(c, "yn", u))
                    nc.vector.tensor_tensor(y[:, u], y[:, u], self.gam, ALU.mult).then_inc(ve.step("gain", u), 1)
                for u in range(U):
                    dve.wait_ge(ve.sem, ve.at(c, "gain", u))
                    nc.vector.tensor_tensor(y[:, u], y[:, u], self.bet, ALU.add).then_inc(ve.step("shift", u), 1)
                for u in range(U):
                    dve.wait_ge(ve.sem, ve.at(c, "shift", u))
                    x = core.x[:, U * c + u, :]
                    nc.vector.tensor_tensor(x, x, y[:, u], ALU.add).then_inc(ve.step("out", u), 1)
                for u in range(U):
                    dve.wait_ge(ve.sem, ve.at(c, "out", u))
                    row_stats(core, dve, U * c + u).then_inc(ve.step("stats", u), 1)

        @block.scalar
        def _(act):
            run.prefetch(act)
            with act.Fori(0, NCH) as c:
                for u in range(U):
                    act.wait_ge(pe.sem, pe.at(c, "xT", u))
                    nc.scalar.copy(xT[:, u], ps[:, u, 0:KD * T]).then_inc(ac.step("xT", u), 1)
                for u in range(U):
                    act.wait_ge(pe.sem, pe.at(c, "f", u))
                    nc.scalar.copy(f[:, u], ps[:, 4 + u, 0:2 * KD * T]).then_inc(ac.step("f", u), 1)
                for u in range(U):
                    act.wait_ge(pe.sem, pe.at(c, "fr", u))
                    nc.scalar.copy(fr[:, u], ps[0:T, u, 0:D]).then_inc(ac.step("fr", u), 1)
                for u in range(U):
                    act.wait_ge(ve.sem, ve.at(c, "sub", u))
                    nc.scalar.activation(p[:, u], p[:, u], ACT.Exp).then_inc(ac.step("exp", u), 1)
                for u in range(U):
                    for b in range(2):
                        act.wait_ge(pe.sem, pe.at(c, "pT", 2 * u + b))
                        nc.scalar.copy(pT[:, u, b * HB:(b + 1) * HB], ps[0:T, (2 * u + b) % 8, 0:HB]).then_inc(ac.step("pT", 2 * u + b), 1)
                for u in range(U):
                    act.wait_ge(pe.sem, pe.at(c, "ctx", u))
                    nc.scalar.copy(ctxT[:, u], ps[:, u, 0:KD * T]).then_inc(ac.step("ctx", u), 1)

        @block.tensor
        def _(ten):
            ten.wait_ge(run.arrived, run.loads)
            ten.wait_ge(spread, 2)
            with ten.Fori(0, NCH) as c:
                for u in range(U):
                    ten.wait_ge(ve.sem, ve.at(c, "xn", u))
                    transposes(core, ps[:, u], xn[:, u], T, KD).then_inc(pe.step("xT", u), 1)
                for u in range(U):
                    ten.wait_ge(ac.sem, ac.at(c, "xT", u))
                    for i, w in enumerate((self.wl, self.wr)):
                        for m in range(KD):
                            o = (i * KD + m) * T
                            for k in range(KD):
                                ins = nc.tensor.matmul(ps[:, 4 + u, o:o + T], w[:, k, m * 128:(m + 1) * 128],
                                                       xT[:, u, k * T:(k + 1) * T], start=(k == 0), stop=(k == KD - 1))
                    ins.then_inc(pe.step("f", u), 1)
                for u in range(U):
                    for k in range(KD):
                        ins = nc.tensor.matmul(ps[0:T, u, 0:D], xT[:, u, k * T:(k + 1) * T], self.wr[:, k, :],
                                               start=(k == 0), stop=(k == KD - 1))
                    ins.then_inc(pe.step("fr", u), 1)
                for u in range(U):
                    ten.wait_ge(ve.sem, ve.at(c, "leaky", u))
                    if u == 0:
                        ten.wait_ge(ac.sem, ac.at(c, "fr", U - 1))
                    for b in range(KD):
                        for q in range(HQ):
                            r = slice(q * HD, (q + 1) * HD)
                            lr = lambda i: lk[r, u, (i * KD + b) * T:(i * KD + b + 1) * T]
                            o = scores(u)[:, q, b, :]
                            nc.tensor.matmul(o, self.attr[r, :], lr(1), start=True, stop=False)
                            ins = nc.tensor.matmul(o, lr(0), self.attl[r, :], start=False, stop=True)
                    ins.then_inc(pe.step("e", u), 1)
                for u in range(U):
                    ten.wait_ge(ve.sem, ve.at(c, "p", u))
                    for b in range(2):
                        for q in range(HQ):
                            h = HQ * b + q
                            ins = nc.tensor.transpose(ps[0:T, (2 * u + b) % 8, q * T:(q + 1) * T],
                                                      p[:, u, (q * KD + b) * T:(q * KD + b + 1) * T], core.ident[0:T, 0:T])
                        ins.then_inc(pe.step("pT", 2 * u + b), 1)
                for u in range(U):
                    ten.wait_ge(ac.sem, ac.at(c, "pT", 2 * u + 1))
                    if u < U - 1:
                        ten.wait_ge(ac.sem, ac.at(c, "pT", U - 1))
                    for b in range(KD):
                        for q in range(HQ):
                            h = HQ * b + q
                            ins = nc.tensor.matmul(ps[q * HD:(q + 1) * HD, u, b * T:(b + 1) * T], fr[:, u, h * HD:(h + 1) * HD],
                                                   pT[:, u, h * T:(h + 1) * T], start=True, stop=True)
                    ins.then_inc(pe.step("ctx", u), 1)
                for u in range(U):
                    ten.wait_ge(ac.sem, ac.at(c, "ctx", u))
                    if u == 0:
                        ten.wait_ge(ac.sem, ac.at(c, "pT", 2 * U - 1))
                    for k in range(KD):
                        ins = nc.tensor.matmul(ps[0:T, 4 + u, 0:D], ctxT[:, u, k * T:(k + 1) * T], self.wf[:, k, :],
                                               start=(k == 0), stop=(k == KD - 1))
                    ins.then_inc(pe.step("out", u), 1)


class Cross:

    H = 16
    HD = D // H
    HK = H // KD
    HU = H * U

    def build(self, core, run):
        nc, d, ps, H, HD, HK, HU = core.nc, core.dram, core.ps, self.H, self.HD, self.HK, self.HU
        full, sb = self.full, run.sbuf
        xn, xT = sb("xn", [T, U, D]), sb("xT", [128, U, KD * T])
        ctxT = sb("ctxT", [128, U, KD * S])
        q = sb("q", [128, U, KD * T])
        mq = sb("mq", [128, 2, HK * T])
        kT, v = ctxT if full else sb("kT", [128, U, KD * S]), sb("v", [SP_, U, ST * D])
        p, pT = sb("p", [T, 4, S]), sb("pT", [SP_, 2, ST * T])
        mx, nmx, den, rden = (sb(n, [T, HU]) for n in ("mx", "nmx", "den", "rden"))
        o, oT = xn, xT
        norm, gains = core.semaphore("norm"), core.semaphore("gains")
        loaded = [core.semaphore(f"ctx{u}") for u in range(U)]
        block = run.block
        G = U * ST
        if full:
            mask = sb("mask", [T, U, S], I32)
            es = core.y[:, :, :].rearrange("p b c -> p (b c)")[:, 0:8 * S].rearrange("p (a i s) -> p a i s", a=2, i=4)
            kn, qn = sb("kn", [SP_, G, D]), xn
            lnq = Norm(core, run, "lnq", eps=1e-6)
            lnk = Norm(core, run, "lnk", rows_=SP_, eps=1e-6, units=G)
            lnv = Norm(core, run, "lnv", rows_=SP_, eps=1e-6, units=G)
            kv = lambda w, g: v[:, g // ST, (g % ST) * D:(g % ST + 1) * D] if w else kn[:, g]
            pe = Progress(core, "tensor", "xT", "qp", ("kv", G), "qT", ("kT", KD * U))
            ac = Progress(core, "scalar", "xT", "qp", ("kv", G), ("kT", KD * U))
            ve = Progress(core, "vector", "xn", *lnq.steps(), "qn", *lnk.steps(), *lnv.steps(), ("kn", G), ("vn", G), "q")
            po = Progress(core, "pool", ("lnqrs", 1), ("lnkrs", 1), ("lnvrs", 1))
            po_f = Progress(core, "pool_fill", "fill")
            ve_k = Progress(core, "vector_kept", ("kept", HU))
            ve_o = Progress(core, "vector_o", "mul", "gain", "o")
        else:
            pe = Progress(core, "tensor", "xT", "qT", ("kT", KD * U), ("v", 2 * U))
            ac = Progress(core, "scalar", "xT", ("kT", KD * U), ("v", 2 * U))
            ve = Progress(core, "vector", "xn", "q")
            ve_o = Progress(core, "vector_o", "mul", "o")
        pe_e, pe_t, pe_o = (Progress(core, "tensor_" + n, (n, HU)) for n in ("e", "pT", "pv"))
        pe2 = Progress(core, "tensor2", "oT", "out")
        ac_p, ac2 = Progress(core, "scalar_p", ("exp", HU)), Progress(core, "scalar2", "oT")
        ve_m, ve_n = Progress(core, "vector_max", ("max", HU)), Progress(core, "vector_neg", ("neg", HU))
        turned = Progress(core, "pT", ("pT", HU))
        po_m = Progress(core, "pool_mq", ("mq", KD * U))
        ve_r, ve2 = Progress(core, "vector_rden", "rden"), Progress(core, "vector2", "out", "stats")
        LAG = 3
        LOADS = (2 if full else 1) * DMA
        @block.sync
        def _(sp):
            def load(n, u):
                sp.dma_start(ctxT[:, u].rearrange("p (k s) -> p k s", k=KD), d["ctxT"][n].rearrange("(k p) s -> p k s", p=128)).then_inc(loaded[u], DMA)
                if full:
                    sp.dma_start(mask[:, u], d["mask"][n]).then_inc(loaded[u], DMA)
            for u in range(U):
                load(u, u)
            with sp.Fori(1, NCH) as c:
                for u in range(U):
                    if full:
                        sp.wait_ge(pe_e.sem, pe_e.at(c - 1, "e", H * u + H - 1))
                        core.stand(sp)
                        sp.wait_ge(ve_k.sem, ve_k.at(c - 1, "kept", H * u + H - 1))
                    else:
                        sp.wait_ge(pe.sem, pe.at(c - 1, "v", 2 * u + 1))
                    core.stand(sp)
                    load(U * c + u, u)

        @block.gpsimd
        def _(pool):
            norm_pool(core, norm)
            pool.wait_ge(run.arrived, run.loads)
            with pool.Fori(0, NCH) as c:
                if full:
                    for ln in (lnq, lnk, lnv):
                        ln.pool(pool, ve, po, c)
                for u in range(U):
                    if full:
                        if u >= 2:
                            pool.wait_ge(ac_p.sem, ac_p.at(c, "exp", H * (u - 1) - 1))
                            core.stand(pool)
                        nc.gpsimd.memset(es[:, u % 2], -1e9).then_inc(po_f.step("fill", u), 1)
                    for b in range(KD):
                        g = KD * u + b
                        pool.wait_ge(ve.sem, ve.at(c, "q", u))
                        if g >= 2:
                            pool.wait_ge(pe_e.sem, pe_e.at(c, "e", HK * (g - 1) - 1))
                        nc.gpsimd.tensor_tensor(mq[:, g % 2].rearrange("p (h t) -> p h t", h=HK),
                                                          q[:, u, b * T:(b + 1) * T].unsqueeze(1).to_broadcast([128, HK, T]),
                                                          self.heads.unsqueeze(2).to_broadcast([128, HK, T]), ALU.mult).then_inc(po_m.step("mq", g), 1)

        @block.vector
        def _(dve):
            norm_vector(core, dve, None, norm)
            dve.wait_ge(run.arrived, run.loads)
            if full:
                nc.vector.tensor_scalar(self.gain_q, self.gain_q, HD ** -0.5, None, ALU.mult).then_inc(gains, 1)
                nc.vector.tensor_scalar(self.shift_q, self.shift_q, HD ** -0.5, None, ALU.mult).then_inc(gains, 1)
                dve.wait_ge(gains, 2)

            def scores(c, n):
                u, i = n // H, n % H
                src = ps[0:T, i % 4, 0:S]
                if full:
                    if i == 0:
                        dve.wait_ge(po_f.sem, po_f.at(c, "fill", u))
                        core.stand(dve)
                        dve.wait_ge(loaded[u], (c + 1) * LOADS)
                        core.stand(dve)
                    if i >= 4:
                        dve.wait_ge(ac_p.sem, ac_p.at(c, "exp", n - 4))
                        core.stand(dve)
                    dve.wait_ge(pe_e.sem, pe_e.at(c, "e", n))
                    core.stand(dve)
                    nc.vector.copy_predicated(es[:, u % 2, i % 4], mask[:, u], src).then_inc(ve_k.step("kept", n), 1)
                    src = es[:, u % 2, i % 4]
                    dve.wait_ge(ve_k.sem, ve_k.at(c, "kept", n))
                else:
                    dve.wait_ge(pe_e.sem, pe_e.at(c, "e", n))
                nc.vector.tensor_reduce(mx[:, n:n + 1], src, AX.X, ALU.max).then_inc(ve_m.step("max", n), 1)
                dve.wait_ge(ve_m.sem, ve_m.at(c, "max", n))
                nc.vector.tensor_scalar(nmx[:, n:n + 1], mx[:, n:n + 1], -1.0, None, ALU.mult).then_inc(ve_n.step("neg", n), 1)

            def turn(c, n):
                if n >= 2:
                    dve.wait_ge(pe_o.sem, pe_o.at(c, "pv", n - 2))
                dve.wait_ge(pe_t.sem, pe_t.at(c, "pT", n))
                nc.vector.tensor_copy(pT[:, n % 2], ps[0:SP_, 4 + n % 2, 0:ST * T]).then_inc(turned.step("pT", n), 1)

            def divide(c, u):
                h = slice(H * u, H * u + H)
                dve.wait_ge(ac_p.sem, ac_p.at(c, "exp", H * u + H - 1))
                nc.vector.reciprocal(rden[:, h], den[:, h]).then_inc(ve_r.step("rden", u), 1)
                dve.wait_ge(ve_r.sem, ve_r.at(c, "rden", u))
                core.stand(dve)
                dve.wait_ge(pe_o.sem, pe_o.at(c, "pv", H * u + H - 1))
                heads = lambda t: t.rearrange("p (h e) -> p h e", h=H)
                ins = nc.vector.tensor_tensor(heads(o[:, u]), heads(ps[0:T, 6 + u % 2, 0:D]),
                                              rden[:, h].unsqueeze(2).to_broadcast([T, H, HD]), ALU.mult)
                ins.then_inc(ve_o.step("mul", u), 1)

            with dve.Fori(0, NCH) as c:
                for u in range(U):
                    normed(core, xn[:, u], U * c + u).then_inc(ve.step("xn", u), 1)
                if full:
                    lnq.vector(dve, ve, c, lambda u, q: qn[:, u], lambda u: dve.wait_ge(ac.sem, ac.at(c, "qp", u)))
                    dve.wait_ge(po.sem, po.at(c, "lnqrs"))
                    for u in range(U):
                        lnq.apply(qn[:, u], qn[:, u], u).then_inc(ve.step("qn", u), 1)
                    lnk.vector(dve, ve, c, lambda g, q: kv(0, g), lambda g: dve.wait_ge(ac.sem, ac.at(c, "kv", g)))
                    lnv.vector(dve, ve, c, lambda g, q: kv(1, g), lambda g: None)
                    for w, (ln, step) in enumerate(((lnk, "kn"), (lnv, "vn"))):
                        dve.wait_ge(po.sem, po.at(c, ln.tag + "rs"))
                        for g in range(G):
                            ln.apply(kv(w, g), kv(w, g), g).then_inc(ve.step(step, g), 1)
                for u in range(U):
                    dve.wait_ge(pe.sem, pe.at(c, "qT", u))
                    for m in range(KD):
                        t = slice(m * T, (m + 1) * T)
                        if full:
                            ins = nc.vector.tensor_scalar(q[:, u, t], ps[:, 4 + u, t], self.gain_q[:, m:m + 1],
                                                          self.shift_q[:, m:m + 1], ALU.mult, ALU.add)
                        else:
                            ins = nc.vector.tensor_scalar(q[:, u, t], ps[:, 4 + u, t], self.bq[:, m:m + 1], HD ** -0.5, ALU.add, ALU.mult)
                    ins.then_inc(ve.step("q", u), 1)
                for n in range(HU):
                    scores(c, n)
                    if not full and n >= LAG:
                        turn(c, n - LAG)
                    if n >= H and n % H == 6:
                        divide(c, n // H - 1)
                if not full:
                    for n in range(HU - LAG, HU):
                        turn(c, n)
                divide(c, U - 1)
                if full:
                    for u in range(U):
                        dve.wait_ge(ve_o.sem, ve_o.at(c, "mul", u))
                        nc.vector.tensor_tensor(o[:, u], o[:, u], self.gain_v, ALU.mult).then_inc(ve_o.step("gain", u), 1)
                for u in range(U):
                    dve.wait_ge(ve_o.sem, ve_o.at(c, "gain" if full else "mul", u))
                    nc.vector.tensor_tensor(o[:, u], o[:, u], self.shift_v, ALU.add).then_inc(ve_o.step("o", u), 1)
                for u in range(U):
                    dve.wait_ge(pe2.sem, pe2.at(c, "out", u))
                    x = core.x[:, U * c + u, :]
                    nc.vector.tensor_tensor(x, x, ps[0:T, 4 + u, 0:D], ALU.add).then_inc(ve2.step("out", u), 1)
                for u in range(U):
                    dve.wait_ge(ve2.sem, ve2.at(c, "out", u))
                    row_stats(core, dve, U * c + u).then_inc(ve2.step("stats", u), 1)

        @block.scalar
        def _(act):
            run.prefetch(act)
            act.wait_ge(run.arrived, run.loads)

            def turn(c, n):
                if n >= 2:
                    act.wait_ge(pe_o.sem, pe_o.at(c, "pv", n - 2))
                act.wait_ge(pe_t.sem, pe_t.at(c, "pT", n))
                nc.scalar.copy(pT[:, n % 2], ps[0:SP_, 4 + n % 2, 0:ST * T]).then_inc(turned.step("pT", n), 1)

            with act.Fori(0, NCH) as c:
                for u in range(U):
                    act.wait_ge(pe.sem, pe.at(c, "xT", u))
                    nc.scalar.copy(xT[:, u], ps[:, u, 0:KD * T]).then_inc(ac.step("xT", u), 1)
                if full:
                    for u in range(U):
                        act.wait_ge(pe.sem, pe.at(c, "qp", u))
                        nc.scalar.copy(qn[:, u], ps[0:T, 4 + u, 0:D]).then_inc(ac.step("qp", u), 1)
                    for g in range(G):
                        act.wait_ge(pe.sem, pe.at(c, "kv", g))
                        nc.scalar.copy(kv(0, g), ps[0:SP_, g % 4, 0:D])
                        nc.scalar.copy(kv(1, g), ps[0:SP_, g % 4, D:2 * D]).then_inc(ac.step("kv", g), 1)
                for u in range(U):
                    for m in range(KD):
                        act.wait_ge(pe.sem, pe.at(c, "kT", KD * u + m))
                        k = kT[:, u, m * S:(m + 1) * S]
                        src = ps[:, (KD * u + m) % 4, 0:S]
                        if full:
                            ins = nc.scalar.activation(k, src, ACT.Identity, bias=self.shift_k[:, m:m + 1], scale=self.gain_k[:, m:m + 1])
                        else:
                            ins = nc.scalar.activation(k, src, ACT.Identity, bias=self.bk[:, m:m + 1])
                        ins.then_inc(ac.step("kT", KD * u + m), 1)
                if not full:
                    for u in range(U):
                        for i in range(2):
                            w = (2 - i) * D
                            act.wait_ge(pe.sem, pe.at(c, "v", 2 * u + i))
                            nc.scalar.copy(v[:, u, 2 * i * D:2 * i * D + w], ps[0:SP_, (2 * u + i) % 4, 0:w]).then_inc(ac.step("v", 2 * u + i), 1)
                for n in range(HU):
                    u, i = n // H, n % H
                    if full and n >= LAG:
                        turn(c, n - LAG)
                    if n >= 4:
                        act.wait_ge(pe_t.sem, pe_t.at(c, "pT", n - 4))
                    act.wait_ge(ve_n.sem, ve_n.at(c, "neg", n))
                    nc.scalar.activation(p[:, n % 4], es[:, u % 2, i % 4] if full else ps[0:T, i % 4, 0:S], ACT.Exp,
                                                   bias=nmx[:, n:n + 1], accum_out=den[:, n:n + 1]).then_inc(ac_p.step("exp", n), 1)
                if full:
                    for n in range(HU - LAG, HU):
                        turn(c, n)
                for u in range(U):
                    act.wait_ge(pe2.sem, pe2.at(c, "oT", u))
                    nc.scalar.copy(oT[:, u], ps[:, u, 0:KD * T]).then_inc(ac2.step("oT", u), 1)

        @block.tensor
        def _(ten):
            ten.wait_ge(run.arrived, run.loads)

            def qk(c, n):
                u, i = n // H, n % H
                b = i // HK
                if n >= 4:
                    if full:
                        ten.wait_ge(ve_k.sem, ve_k.at(c, "kept", n - 4))
                    else:
                        ten.wait_ge(ac_p.sem, ac_p.at(c, "exp", n - 4))
                if i % HK == 0:
                    ten.wait_ge(po_m.sem, po_m.at(c, "mq", KD * u + b))
                nc.tensor.matmul(ps[0:T, i % 4, 0:S], mq[:, b, i % HK * T:(i % HK + 1) * T], kT[:, u, b * S:(b + 1) * S],
                                           start=True, stop=True).then_inc(pe_e.step("e", n), 1)

            def turn(c, n):
                ten.wait_ge(ac_p.sem, ac_p.at(c, "exp", n))
                if n >= 2:
                    ten.wait_ge(turned.sem, turned.at(c, "pT", n - 2))
                for s in range(ST):
                    ins = nc.tensor.transpose(ps[0:SP_, 4 + n % 2, s * T:(s + 1) * T], p[:, n % 4, s * SP_:(s + 1) * SP_],
                                              core.ident[0:T, 0:T])
                ins.then_inc(pe_t.step("pT", n), 1)

            def pv(c, n):
                u, i = n // H, n % H
                if i == 0 and u >= 2:
                    ten.wait_ge(ve_o.sem, ve_o.at(c, "mul", u - 2))
                ten.wait_ge(turned.sem, turned.at(c, "pT", n))
                e = slice(i * HD, (i + 1) * HD)
                for s in range(ST):
                    ins = nc.tensor.matmul(ps[0:T, 6 + u % 2, e], pT[:, n % 2, s * T:(s + 1) * T],
                                           v[:, u, s * D + i * HD:s * D + (i + 1) * HD], start=(s == 0), stop=(s == ST - 1))
                ins.then_inc(pe_o.step("pv", n), 1)

            with ten.Fori(0, NCH) as c:
                for u in range(U):
                    ten.wait_ge(ve.sem, ve.at(c, "xn", u))
                    transposes(core, ps[:, u], xn[:, u], T, KD).then_inc(pe.step("xT", u), 1)
                if full:
                    for u in range(U):
                        ten.wait_ge(ac.sem, ac.at(c, "xT", u))
                        for k in range(KD):
                            nc.tensor.matmul(ps[0:T, 4 + u, 0:D], xT[:, u, k * T:(k + 1) * T], self.wq[:, k, :], start=(k == 0), stop=False)
                        nc.tensor.matmul(ps[0:T, 4 + u, 0:D], core.ones[0:1, 0:T], self.bq, start=False, stop=True).then_inc(pe.step("qp", u), 1)
                    for g in range(G):
                        u, s = g // ST, g % ST
                        if s == 0:
                            ten.wait_ge(loaded[u], (c + 1) * LOADS)
                        if g >= 4:
                            ten.wait_ge(ac.sem, ac.at(c, "kv", g - 4))
                        for k in range(KD):
                            nc.tensor.matmul(ps[0:SP_, g % 4, :], ctxT[:, u, k * S + s * SP_:k * S + (s + 1) * SP_], self.wkv[:, k, :],
                                             start=(k == 0), stop=False)
                        nc.tensor.matmul(ps[0:SP_, g % 4, :], core.ones[0:1, 0:SP_], self.bkv, start=False, stop=True).then_inc(pe.step("kv", g), 1)
                    for u in range(U):
                        ten.wait_ge(ve.sem, ve.at(c, "qn", u))
                        transposes(core, ps[:, 4 + u], qn[:, u], T, KD).then_inc(pe.step("qT", u), 1)
                    for u in range(U):
                        for m in range(KD):
                            if KD * u + m >= 4:
                                ten.wait_ge(ac.sem, ac.at(c, "kT", KD * u + m - 4))
                            else:
                                ten.wait_ge(ac.sem, ac.at(c, "kv", G - 1))
                            for s in range(ST):
                                ten.wait_ge(ve.sem, ve.at(c, "kn", ST * u + s))
                                ins = nc.tensor.transpose(ps[:, (KD * u + m) % 4, s * SP_:(s + 1) * SP_],
                                                          kn[:, ST * u + s, m * 128:(m + 1) * 128], core.ident[0:SP_, 0:SP_])
                            ins.then_inc(pe.step("kT", KD * u + m), 1)
                    ten.wait_ge(ve.sem, ve.at(c, "vn", G - 1))
                else:
                    for u in range(U):
                        ten.wait_ge(ac.sem, ac.at(c, "xT", u))
                        for m in range(KD):
                            for k in range(KD):
                                ins = nc.tensor.matmul(ps[:, 4 + u, m * T:(m + 1) * T], self.wq[:, k, m * 128:(m + 1) * 128],
                                                       xT[:, u, k * T:(k + 1) * T], start=(k == 0), stop=(k == KD - 1))
                        ins.then_inc(pe.step("qT", u), 1)
                    for u in range(U):
                        ten.wait_ge(loaded[u], (c + 1) * LOADS)
                        for m in range(KD):
                            if KD * u + m >= 4:
                                ten.wait_ge(ac.sem, ac.at(c, "kT", KD * u + m - 4))
                            for k in range(KD):
                                ins = nc.tensor.matmul(ps[:, (KD * u + m) % 4, 0:S], self.wk[:, k, m * 128:(m + 1) * 128], ctxT[:, u, k * S:(k + 1) * S],
                                                       start=(k == 0), stop=(k == KD - 1))
                            ins.then_inc(pe.step("kT", KD * u + m), 1)
                    for u in range(U):
                        for i in range(2):
                            if 2 * u + i >= 4:
                                ten.wait_ge(ac.sem, ac.at(c, "v", 2 * u + i - 4))
                            else:
                                ten.wait_ge(ac.sem, ac.at(c, "kT", KD * U - 4 + 2 * u + i))
                            for s in range(2 * i, min(2 * i + 2, ST)):
                                for k in range(KD):
                                    ins = nc.tensor.matmul(ps[0:SP_, (2 * u + i) % 4, (s % 2) * D:(s % 2 + 1) * D],
                                                           ctxT[:, u, k * S + s * SP_:k * S + (s + 1) * SP_], self.wv[:, k, :],
                                                           start=(k == 0), stop=(k == KD - 1))
                            ins.then_inc(pe.step("v", 2 * u + i), 1)
                ten.wait_ge(ve.sem, ve.at(c, "q", U - 1))
                ten.wait_ge(ac.sem, ac.at(c, *(("kT", KD * U - 1) if full else ("v", 2 * U - 1))))
                for n in range(HU + LAG + 1):
                    if n < HU:
                        qk(c, n)
                    if LAG <= n < HU + LAG:
                        turn(c, n - LAG)
                    if n > LAG:
                        pv(c, n - LAG - 1)
                for u in range(U):
                    ten.wait_ge(ve_o.sem, ve_o.at(c, "o", u))
                    transposes(core, ps[:, u], o[:, u], T, KD).then_inc(pe2.step("oT", u), 1)
                for u in range(U):
                    ten.wait_ge(ac2.sem, ac2.at(c, "oT", u))
                    for k in range(KD):
                        nc.tensor.matmul(ps[0:T, 4 + u, 0:D], oT[:, u, k * T:(k + 1) * T], self.wo[:, k, :], start=(k == 0), stop=False)
                    nc.tensor.matmul(ps[0:T, 4 + u, 0:D], core.ones[0:1, 0:T], self.bo, start=False, stop=True).then_inc(pe2.step("out", u), 1)


class L2Cross(Cross):

    name, full = "L2_xattn", True

    def weights(self, a, d):
        n = self.name + "_"
        self.wq = a.load(rows(d[n + "Wq"]), 128, KD, D)
        self.wkv = a.take(128, KD, 2 * D)
        self.bkv = a.take(1, 2 * D)
        for i, k in enumerate("kv"):
            a.loads.append((self.wkv[:, :, i * D:(i + 1) * D], rows(d[n + "W" + k])))
            a.loads.append((self.bkv[:, i * D:(i + 1) * D], every(d[n + "b" + k], 1)))
        self.wo = a.load(rows(d[n + "Wo"]), 128, KD, D)
        self.bq = a.load(every(d[n + "bq"], 1), 1, D)
        self.bo = a.load(every(d[n + "bo"], 1), 1, D)
        self.gain_q, self.shift_q = (a.load(d[n + "qn_" + k + "_c"], 128, KD) for k in ("scale", "bias"))
        self.gain_k, self.shift_k = (a.load(d[n + "kn_" + k + "_c"], 128, KD) for k in ("scale", "bias"))
        self.gain_v, self.shift_v = (a.load(every(d[n + "vn_" + k], T), T, D) for k in ("scale", "bias"))
        self.heads = a.load(d["heads"], 128, self.HK)


class L3Cross(Cross):
    name, full = "L3_xattn", False

    def weights(self, a, d):
        n = self.name + "_"
        self.wq, self.wk, self.wv, self.wo = (a.load(rows(d[n + "W" + k + "T"]), 128, KD, D) for k in "qkvo")
        self.bq, self.bk = (a.load(d[n + "b" + k + "_c"], 128, KD) for k in "qk")
        self.shift_v = a.load(every(d[n + "bv"], T), T, D)
        self.bo = a.load(every(d[n + "bo"], 1), 1, D)
        self.heads = a.load(d["heads"], 128, self.HK)


class Generated:

    def __init__(self, s0, s1, w, b, mix):
        self.s0, self.s1, self.w, self.b, self.mix = s0, s1, w, b, mix

    @staticmethod
    def vector(core, dve, items, mixed, bent):
        nc, n = core.nc, len(items)
        for i in items:
            nc.vector.tensor_scalar(i.s0, i.s0, i.mix[:, 0:1], None, ALU.mult).then_inc(mixed, 1)
        for k, i in enumerate(items):
            dve.wait_ge(mixed, k + 1)
            nc.vector.scalar_tensor_tensor(out=i.s0, in0=i.s1, scalar=i.mix[:, 1:2], in1=i.s0,
                                           op0=ALU.mult, op1=ALU.add).then_inc(mixed, 1)
        for k, i in enumerate(items):
            dve.wait_ge(bent, k + 1)
            nc.vector.tensor_tensor(i.s0, i.s0, i.w, ALU.mult).then_inc(mixed, 1)
        for k, i in enumerate(items):
            dve.wait_ge(mixed, 2 * n + k + 1)
            nc.vector.tensor_tensor(i.s0, i.s0, i.b, ALU.add).then_inc(mixed, 1)

    @staticmethod
    def scalar(core, act, items, mixed, bent):
        n = len(items)
        for k, i in enumerate(items):
            act.wait_ge(mixed, n + k + 1)
            core.nc.scalar.activation(i.s0, i.s0, ACT.Tanh).then_inc(bent, 1)


def generated(load, d, name, pick, w, mix, late=None):
    kind = "w" if w else "b"
    turned = "T" if w else ""
    sub = d[f"{name}_sub_{kind}{turned}"]
    return Generated(load(pick(sub[0])), load(pick(sub[1])), load(pick(d[f"{name}_W_{kind}{turned}"])),
                     (late or load)(pick(d[f"{name}_B_{kind}{turned}"])), mix)


class L3Self:

    name = "L3_attn"
    H = 16
    HD = D // H
    HG = 8
    NG = U * H // HG

    def weights(self, a, d):
        n = self.name + "_"

        def flat(src, parts, k):
            cols = 1
            for s in src.shape[1:]:
                cols *= s
            v = a.take(parts, cols)
            a.loads.append((v.rearrange("p (k n) -> p k n", k=k) if k else v, src))
            return v
        mat = lambda s: flat(rows(s), 128, KD)
        row = lambda s: flat(s.rearrange("(a n) -> a n", a=1), 1, 0)
        mix = {(p, k): a.load(every(d[n + p + "_Wl_" + k], 128), 128, 2) for p in ("ca", "cp") for k in "wb"}
        self.ca = generated(mat, d, n + "ca", lambda s: s, True, mix["ca", "w"])
        self.cp = generated(mat, d, n + "cp", lambda s: s, True, mix["cp", "w"])
        col_d = {k: d[k + "_cols"] for k in (n + "ca_sub_b", n + "ca_W_b", n + "ca_B_b")}
        self.bqk = generated(lambda s: flat(s, 128, 0), col_d_named(col_d, n + "ca"), n + "ca", lambda s: s[:, 0:2 * KD], False, mix["ca", "b"])
        self.bv = generated(row, d, n + "ca", lambda s: s[2 * D:3 * D], False, mix["ca", "b"][0:1, :])
        self.bp = generated(row, d, n + "cp", lambda s: s, False, mix["cp", "b"][0:1, :])
        self.gain, self.shift = (a.load(d[n + "ln1_" + k + "_c"], 128, KD) for k in "gb")
        self.heads = a.load(d["heads"], 128, self.HG)

    def build(self, core, run):
        nc, ps, H, HD, HG, NG = core.nc, core.ps, self.H, self.HD, self.HG, self.NG
        sb = run.sbuf
        xn, h, hT = sb("xn", [T, U, D]), sb("h", [T, U, D]), sb("hT", [128, KD, N4])
        qk = sb("qk", [128, 2 * KD, N4])
        v = sb("v", [T, U, H, HD + 1])
        mq = sb("mq", [128, 3, HG * T])
        p, pT = sb("p", [T, 4, HG * T]), sb("pT", [T, 2, HG * T])
        mx, rden = sb("mx", [T, NG, HG]), sb("rden", [T, U, H])
        o, oT = h, hT
        ca = self.ca.s0.rearrange("p (k n) -> p k n", k=KD)
        cp = self.cp.s0.rearrange("p (k n) -> p k n", k=KD)
        items = [self.ca, self.bqk, self.bv, self.cp, self.bp]
        norm, mixed, bent = core.semaphore("norm"), core.semaphore("mixed"), core.semaphore("bent")
        quarter, filled = core.semaphore("quarter"), core.semaphore("filled")
        ln = Norm(core, run, "ln")
        pe = Progress(core, "tensor", ("hT", KD), ("qk", 2 * KD), "v")
        ac = Progress(core, "scalar", ("hT", KD), ("qk", 2 * KD), "v")
        ve = Progress(core, "vector", "xn", *ln.steps(), "hn")
        po = Progress(core, "pool", ("lnrs", 1))
        pe_e, pe_t, pe_o = Progress(core, "tensor_e", ("e", NG)), Progress(core, "tensor_pT", ("pT", 2 * NG)), Progress(core, "tensor_pv", ("pv", NG))
        po_q, po_c = Progress(core, "pool_mq", ("mq", NG)), Progress(core, "pool_causal", ("causal", NG))
        ve_m, ve_s = Progress(core, "vector_max", ("max", NG)), Progress(core, "vector_sub", ("sub", NG))
        ac_s = Progress(core, "scalar_e", ("scores", NG))
        ac_e, ac_t = Progress(core, "scalar_exp", ("exp", NG)), Progress(core, "scalar_pT", ("pT", 2 * NG))
        ve_r, ve_o = Progress(core, "vector_rden", "rden"), Progress(core, "vector_o", "o", "y")
        pe2, ac2 = Progress(core, "tensor2", "oT", "out"), Progress(core, "scalar2", "oT")
        block = run.block
        by_head = lambda t: t.rearrange("p (h s) -> p h s", s=T)
        HB = HG // 2 * T

        def group(n):
            return ps[0:T, 2 * (n % 2):2 * (n % 2) + 2, 0:HB]

        @block.gpsimd
        def _(pool):
            norm_pool(core, norm)
            nc.gpsimd.memset(v[:, :, :, HD:HD + 1], 1.0).then_inc(filled, 1)
            pool.wait_ge(run.arrived, run.loads)
            with pool.Fori(0, NCH) as c:
                ln.pool(pool, ve, po, c)

                def heads_of(n):
                    u, b = n // KD, n % KD
                    if n >= 3:
                        pool.wait_ge(pe_e.sem, pe_e.at(c, "e", n - 3))
                    pool.wait_ge(ac.sem, ac.at(c, "qk", b))
                    nc.gpsimd.tensor_tensor(by_head(mq[:, n % 3]), qk[:, b, u * T:(u + 1) * T].unsqueeze(1).to_broadcast([128, HG, T]),
                                                      self.heads.unsqueeze(2).to_broadcast([128, HG, T]), ALU.mult).then_inc(po_q.step("mq", n), 1)

                def causal(n):
                    pool.wait_ge(ac_s.sem, ac_s.at(c, "scores", n))
                    core.stand(pool)
                    nc.gpsimd.affine_select(p[:, n % 4], p[:, n % 4], pattern=[[0, HG], [-1, T]],
                                                      compare_op=ALU.is_ge, fill=-1e4, base=0, channel_multiplier=1).then_inc(po_c.step("causal", n), 1)
                for n in range(NG):
                    heads_of(n)
                    if n >= 1:
                        causal(n - 1)
                causal(NG - 1)

        @block.vector
        def _(dve):
            norm_vector(core, dve, None, norm)
            dve.wait_ge(run.arrived, run.loads)
            Generated.vector(core, dve, items, mixed, bent)
            dve.wait_ge(mixed, 4 * len(items))
            nc.vector.tensor_scalar(self.bqk.s0[:, 0:KD], self.bqk.s0[:, 0:KD], HD ** -0.5, None, ALU.mult).then_inc(quarter, 1)
            with dve.Fori(0, NCH) as c:
                for u in range(U):
                    normed(core, xn[:, u], U * c + u).then_inc(ve.step("xn", u), 1)
                ln.vector(dve, ve, c, lambda u, q: xn[:, u], lambda u: dve.wait_ge(ve.sem, ve.at(c, "xn", u)))
                dve.wait_ge(po.sem, po.at(c, "lnrs"))
                core.stand(dve)
                for u in range(U):
                    ln.apply(h[:, u], xn[:, u], u).then_inc(ve.step("hn", u), 1)

                def divide(u):
                    dve.wait_ge(pe_o.sem, pe_o.at(c, "pv", KD * u + KD - 1))
                    heads = ps[0:T, 6 + u % 2, 0:H * (HD + 1)].rearrange("p (h e) -> p h e", h=H)
                    nc.vector.reciprocal(rden[:, u, :], heads[:, :, HD]).then_inc(ve_r.step("rden", u), 1)
                    dve.wait_ge(ve_r.sem, ve_r.at(c, "rden", u))
                    nc.vector.tensor_tensor(o[:, u].rearrange("p (h e) -> p h e", h=H), heads[:, :, 0:HD],
                                                      rden[:, u, :].unsqueeze(2).to_broadcast([T, H, HD]), ALU.mult).then_inc(ve_o.step("o", u), 1)
                for n in range(NG):
                    dve.wait_ge(po_c.sem, po_c.at(c, "causal", n))
                    nc.vector.tensor_reduce(mx[:, n, :], by_head(p[:, n % 4]), AX.X, ALU.max).then_inc(ve_m.step("max", n), 1)
                    dve.wait_ge(ve_m.sem, ve_m.at(c, "max", n))
                    nc.vector.tensor_tensor(by_head(p[:, n % 4]), by_head(p[:, n % 4]),
                                                      mx[:, n, :].unsqueeze(2).to_broadcast([T, HG, T]), ALU.subtract).then_inc(ve_s.step("sub", n), 1)
                    if n % KD == 1 and n >= 5:
                        divide((n - 5) // KD)
                for u in range((NG - 5) // KD + 1, U):
                    divide(u)
                for u in range(U):
                    dve.wait_ge(pe2.sem, pe2.at(c, "out", u))
                    core.stand(dve)
                    nc.vector.tensor_tensor(core.y[:, U * c + u, :], xn[:, u], ps[0:T, 4 + u % 2, 0:D] if u < 2 else ps[0:T, u % 2, 0:D], ALU.add).then_inc(ve_o.step("y", u), 1)
                dve.wait_ge(ve_o.sem, ve_o.at(c, "y", U - 1))
                core.stand(dve)

        @block.scalar
        def _(act):
            run.prefetch(act)
            act.wait_ge(run.arrived, run.loads)
            Generated.scalar(core, act, items, mixed, bent)
            act.wait_ge(quarter, 1)
            act.wait_ge(filled, 1)
            with act.Fori(0, NCH) as c:
                for k in range(KD):
                    act.wait_ge(pe.sem, pe.at(c, "hT", k))
                    nc.scalar.activation(hT[:, k], ps[:, k, 0:N4], ACT.Identity, bias=self.shift[:, k:k + 1],
                                                 scale=self.gain[:, k:k + 1]).then_inc(ac.step("hT", k), 1)
                for m in range(2 * KD):
                    act.wait_ge(pe.sem, pe.at(c, "qk", m))
                    nc.scalar.activation(qk[:, m], ps[:, 2 + m, 0:N4], ACT.Identity, bias=self.bqk.s0[:, m:m + 1],
                                                 scale=HD ** -0.5 if m < KD else 1.0).then_inc(ac.step("qk", m), 1)
                for u in range(U):
                    act.wait_ge(pe.sem, pe.at(c, "v", u))
                    nc.scalar.copy(v[:, u, :, 0:HD], ps[0:T, (6 + u) % 8, 0:D].rearrange("p (h e) -> p h e", h=H)).then_inc(ac.step("v", u), 1)

                def turn(n):
                    if n >= 2:
                        act.wait_ge(pe_o.sem, pe_o.at(c, "pv", n - 2))
                    for b in range(2):
                        act.wait_ge(pe_t.sem, pe_t.at(c, "pT", 2 * n + b))
                        nc.scalar.copy(pT[:, n % 2, b * HB:(b + 1) * HB], ps[0:T, 4 + b, 0:HB]).then_inc(ac_t.step("pT", 2 * n + b), 1)
                def scores(n):
                    if n >= 4:
                        act.wait_ge(pe_t.sem, pe_t.at(c, "pT", 2 * (n - 4) + 1))
                    act.wait_ge(pe_e.sem, pe_e.at(c, "e", n))
                    nc.scalar.copy(p[:, n % 4].rearrange("p (b s) -> p b s", b=2), group(n)).then_inc(ac_s.step("scores", n), 1)

                def exp(n):
                    act.wait_ge(ve_s.sem, ve_s.at(c, "sub", n))
                    nc.scalar.activation(p[:, n % 4], p[:, n % 4], ACT.Exp).then_inc(ac_e.step("exp", n), 1)
                for n in range(NG + 3):
                    if n < NG:
                        scores(n)
                    if 2 <= n < NG + 2:
                        exp(n - 2)
                    if n >= 3:
                        turn(n - 3)
                for u in range(U):
                    act.wait_ge(pe2.sem, pe2.at(c, "oT", u))
                    nc.scalar.copy(oT[:, :, u * T:(u + 1) * T], ps[:, 2 + u % 2, 0:KD * T].rearrange("p (k t) -> p k t", k=KD)).then_inc(ac2.step("oT", u), 1)

        @block.tensor
        def _(ten):
            ten.wait_ge(run.arrived, run.loads)
            ten.wait_ge(mixed, 4 * len(items))
            with ten.Fori(0, NCH) as c:
                for k in range(KD):
                    for u in range(U):
                        if k == 0:
                            ten.wait_ge(ve.sem, ve.at(c, "hn", u))
                        ins = nc.tensor.transpose(ps[:, k, u * T:(u + 1) * T], h[:, u, k * 128:(k + 1) * 128], core.ident[0:T, 0:T])
                    ins.then_inc(pe.step("hT", k), 1)
                for m in range(2 * KD):
                    for k in range(KD):
                        if m == 0:
                            ten.wait_ge(ac.sem, ac.at(c, "hT", k))
                        ins = nc.tensor.matmul(ps[:, 2 + m, 0:N4], ca[:, k, m * 128:(m + 1) * 128], hT[:, k], start=(k == 0), stop=(k == KD - 1))
                    ins.then_inc(pe.step("qk", m), 1)
                for u in range(U):
                    for k in range(KD):
                        nc.tensor.matmul(ps[0:T, (6 + u) % 8, 0:D], hT[:, k, u * T:(u + 1) * T], ca[:, k, 2 * D:3 * D], start=(k == 0), stop=False)
                    nc.tensor.matmul(ps[0:T, (6 + u) % 8, 0:D], core.ones[0:1, 0:T], self.bv.s0, start=False, stop=True).then_inc(pe.step("v", u), 1)

                def scores(n):
                    u, b = n // KD, n % KD
                    if n >= 2:
                        ten.wait_ge(ac_s.sem, ac_s.at(c, "scores", n - 2))
                    if n < 2:
                        ten.wait_ge(ac.sem, ac.at(c, "v", U - 1))
                    ten.wait_ge(po_q.sem, po_q.at(c, "mq", n))
                    for i in range(HG):
                        ins = nc.tensor.matmul(ps[0:T, 2 * (n % 2) + 2 * i // HG, i % (HG // 2) * T:(i % (HG // 2) + 1) * T], mq[:, n % 3, i * T:(i + 1) * T],
                                               qk[:, KD + b, u * T:(u + 1) * T], start=True, stop=True)
                    ins.then_inc(pe_e.step("e", n), 1)

                def turn(n):
                    ten.wait_ge(ac_e.sem, ac_e.at(c, "exp", n))
                    for b in range(2):
                        if n >= 1:
                            ten.wait_ge(ac_t.sem, ac_t.at(c, "pT", 2 * n + b - 2))
                        for i in range(HG // 2):
                            k = HG // 2 * b + i
                            ins = nc.tensor.transpose(ps[0:T, 4 + b, i * T:(i + 1) * T], p[:, n % 4, k * T:(k + 1) * T], core.ident[0:T, 0:T])
                        ins.then_inc(pe_t.step("pT", 2 * n + b), 1)

                def pv(n):
                    u, b = n // KD, n % KD
                    ten.wait_ge(ac_t.sem, ac_t.at(c, "pT", 2 * n + 1))
                    if b == 0 and u >= 2:
                        ten.wait_ge(ve_o.sem, ve_o.at(c, "o", u - 2))
                    for i in range(HG):
                        k = HG * b + i
                        ins = nc.tensor.matmul(ps[0:T, 6 + u % 2, k * (HD + 1):(k + 1) * (HD + 1)], pT[:, n % 2, i * T:(i + 1) * T], v[:, u, k, :],
                                               start=True, stop=True)
                    ins.then_inc(pe_o.step("pv", n), 1)
                for n in range(NG + 4):
                    if n < NG:
                        scores(n)
                    if 3 <= n < NG + 3:
                        turn(n - 3)
                    if n >= 4:
                        pv(n - 4)
                for u in range(U):
                    ten.wait_ge(ve_o.sem, ve_o.at(c, "o", u))
                    if u >= 2:
                        ten.wait_ge(ac2.sem, ac2.at(c, "oT", u - 2))
                    transposes(core, ps[:, 2 + u % 2], o[:, u], T, KD).then_inc(pe2.step("oT", u), 1)
                for u in range(U):
                    ten.wait_ge(ac2.sem, ac2.at(c, "oT", u))
                    bank = 4 + u if u < 2 else u % 2
                    for k in range(KD):
                        nc.tensor.matmul(ps[0:T, bank, 0:D], oT[:, k, u * T:(u + 1) * T], cp[:, k, :], start=(k == 0), stop=False)
                    nc.tensor.matmul(ps[0:T, bank, 0:D], core.ones[0:1, 0:T], self.bp.s0, start=False, stop=True).then_inc(pe2.step("out", u), 1)


def col_d_named(arrays, name):
    return {f"{name}_sub_b": [arrays[f"{name}_sub_b"][:, i, :] for i in range(2)],
            f"{name}_W_b": arrays[f"{name}_W_b"], f"{name}_B_b": arrays[f"{name}_B_b"]}


class L3Mlp(Mlp):

    name = "L3_mlp"
    act = ACT.Gelu_apprx_tanh

    def weights(self, a, d):
        n = "L3_attn_"
        self.late = []

        def flat(src, parts, k):
            cols = 1
            for s in src.shape[1:]:
                cols *= s
            v = a.take(parts, cols)
            a.loads.append((v.rearrange("p (k n) -> p k n", k=k) if k else v, src))
            return v
        later = lambda src: self.late.append(src)
        mix = {(p, k): a.load(every(d[n + p + "_Wl_" + k], 128), 128, 2) for p in ("cf", "cm") for k in "wb"}
        self.cf = generated(lambda s: flat(rows(s), 128, KD), d, n + "cf", lambda s: s, True, mix["cf", "w"], later)
        self.cm = generated(lambda s: flat(rows(s), 128, self.HK), d, n + "cm", lambda s: s, True, mix["cm", "w"], later)
        col_d = {k: d[k + "_cols"] for k in (n + "cf_sub_b", n + "cf_W_b", n + "cf_B_b")}
        self.bf = generated(lambda s: flat(s, 128, 0), col_d_named(col_d, n + "cf"), n + "cf", lambda s: s, False, mix["cf", "b"])
        self.bm = generated(later, d, n + "cm", lambda s: s, False, mix["cm", "b"][0:1, :])
        self.gain, self.shift = (a.load(d[n + "ln2_" + k + "_c"], 128, KD) for k in "gb")

    def prepare(self, core, run):
        sb, late = run.sbuf, self.late
        self.cf.b, self.cm.b = sb("cf_b", [128, KD * self.H])[:, :], sb("cm_b", [128, self.HK * D])[:, :]
        row = sb("bm", [1, 4, D])
        self.bm.s0, self.bm.s1, self.bm.w, self.bm.b = (row[:, i, :] for i in range(4))
        self.items = [self.cf, self.bf, self.cm, self.bm]
        self.w1 = self.cf.s0.rearrange("p (k n) -> p k n", k=KD)
        self.w2 = self.cm.s0.rearrange("p (k n) -> p k n", k=self.HK)
        self.b1, self.b2 = self.bf.s0, self.bm.s0
        self.mixed, self.bent, arrived = (core.semaphore(n) for n in ("mixed", "bent", "arrived"))
        self.arrived = arrived

        @run.block.sync
        def _(sp):
            sp.dma_start(self.cf.b.rearrange("p (k n) -> p k n", k=KD), rows(late[0])).then_inc(arrived, DMA)
            sp.dma_start(self.cm.b.rearrange("p (k n) -> p k n", k=self.HK), rows(late[1])).then_inc(arrived, DMA)
            for i in range(4):
                sp.dma_start(row[:, i, :], late[2 + i].rearrange("(a n) -> a n", a=1)).then_inc(arrived, DMA)

    def prepare_vector(self, core, run, dve):
        dve.wait_ge(run.arrived, run.loads)
        dve.wait_ge(self.arrived, DMA * len(self.late))
        Generated.vector(core, dve, self.items, self.mixed, self.bent)

    def prepare_scalar(self, core, run, act):
        run.prefetch(act)
        Generated.scalar(core, act, self.items, self.mixed, self.bent)
        act.wait_ge(self.mixed, 4 * len(self.items))

    def prepare_tensor(self, core, run, ten):
        ten.wait_ge(self.mixed, 4 * len(self.items))


class L3Feed:

    name = "L3_ffn"
    H = 1024
    HK = H // 128

    def weights(self, a, d):
        self.fc = a.load(rows(d["L3_ffn_W_fcT"]), 128, KD, self.H)
        self.pr = a.load(rows(d["L3_ffn_W_projT"]), 128, self.HK, D)
        self.lw = a.load(d["L3_ffn_ln_w_c"], 128, self.HK)
        self.lb = a.load(d["L3_ffn_ln_b_c"], 128, self.HK)

    def build(self, core, run):
        nc, ps, H, HK = core.nc, core.ps, self.H, self.HK
        sb = run.sbuf
        mats = [self.fc.rearrange("p k n -> p (k n)"), self.pr.rearrange("p k n -> p (k n)")]
        size = [sb(f"size{i}", [128, KD * H]) for i in range(2)]
        total, high, low = sb("total", [128, 2]), sb("high", [128, 2]), sb("low", [128, 2])
        brow = sb("brow", [1, D])
        xn, xT = sb("xn", [T, U, D]), sb("xT", [128, U, KD * T])
        h, hT = sb("h", [T, U, H]), sb("hT", [128, U, HK * T])
        norm, tern, tern_pe = core.semaphore("norm"), core.semaphore("tern"), core.semaphore("tern_pe")
        sized = core.semaphore("sized")
        ln = Norm(core, run, "ln", parts=2)
        pe = Progress(core, "tensor", "xT", ("up", 2 * U), ("hT", 2 * U), "out")
        ac = Progress(core, "scalar", "xT", ("gelu", 2 * U), ("hT", 2 * U))
        ve = Progress(core, "vector", "xn", *ln.steps(), "hn", "out", "stats")
        po = Progress(core, "pool", ("lnrs", 1))
        block = run.block

        @block.gpsimd
        def _(pool):
            norm_pool(core, norm)
            with pool.Fori(0, NCH) as c:
                ln.pool(pool, ve, po, c)

        @block.vector
        def _(dve):
            dve.wait_ge(run.arrived, run.loads)
            dve.wait_ge(tern_pe, 1)
            nc.vector.tensor_scalar(high[:, :], ps[:, 7, 0:2], 1.0 / (D * H), 1e-6, ALU.mult, ALU.add).then_inc(tern, 1)
            dve.wait_ge(tern, 1)
            nc.vector.tensor_scalar(low[:, :], high[:, :], -0.5, None, ALU.mult).then_inc(tern, 1)
            nc.vector.tensor_scalar(total[:, :], high[:, :], 0.5, None, ALU.mult).then_inc(tern, 1)
            dve.wait_ge(tern, 3)
            for i in range(2):
                nc.vector.tensor_scalar(size[i][:, :], mats[i], low[:, i:i + 1], None, ALU.is_lt).then_inc(tern, 1)
                nc.vector.tensor_scalar(mats[i], mats[i], total[:, i:i + 1], None, ALU.is_gt).then_inc(tern, 1)
                dve.wait_ge(tern, 5 + 3 * i)
                nc.vector.tensor_tensor(mats[i], mats[i], size[i][:, :], ALU.subtract).then_inc(tern, 1)
            dve.wait_ge(tern_pe, 2)
            nc.vector.tensor_copy(brow[:, :], ps[0:1, 6, 0:D]).then_inc(tern, 1)
            for i in range(HK):
                ins = nc.vector.tensor_scalar(self.pr[:, i, :], self.pr[:, i, :], self.lw[:, i:i + 1], None, ALU.mult)
                ins.then_inc(tern, 1)
            norm_vector(core, dve, None, norm)
            with dve.Fori(0, NCH) as c:
                for u in range(U):
                    normed(core, xn[:, u], U * c + u).then_inc(ve.step("xn", u), 1)
                ln.vector(dve, ve, c, lambda u, q: h[:, u, q * 512:(q + 1) * 512], lambda u: dve.wait_ge(ac.sem, ac.at(c, "gelu", 2 * u + 1)))
                for u in range(U):
                    dve.wait_ge(po.sem, po.at(c, "lnrs"))
                    ln.apply(h[:, u], h[:, u], u).then_inc(ve.step("hn", u), 1)
                for u in range(U):
                    dve.wait_ge(pe.sem, pe.at(c, "out", u))
                    x = core.x[:, U * c + u, :]
                    nc.vector.tensor_tensor(x, x, ps[0:T, u, 0:D], ALU.add).then_inc(ve.step("out", u), 1)
                for u in range(U):
                    dve.wait_ge(ve.sem, ve.at(c, "out", u))
                    row_stats(core, dve, U * c + u).then_inc(ve.step("stats", u), 1)

        @block.scalar
        def _(act):
            run.prefetch(act)
            act.wait_ge(run.arrived, run.loads)
            for i in range(2):
                nc.scalar.activation(size[i][:, :], mats[i], ACT.Abs, accum_out=total[:, i:i + 1]).then_inc(sized, 1)
            with act.Fori(0, NCH) as c:
                for u in range(U):
                    act.wait_ge(pe.sem, pe.at(c, "xT", u))
                    nc.scalar.copy(xT[:, u], ps[:, u, 0:KD * T]).then_inc(ac.step("xT", u), 1)
                for u in range(U):
                    for q in range(2):
                        act.wait_ge(pe.sem, pe.at(c, "up", 2 * u + q))
                        nc.scalar.activation(h[:, u, q * 512:(q + 1) * 512], ps[0:T, 4 + (2 * u + q) % 4, :], ACT.Gelu).then_inc(ac.step("gelu", 2 * u + q), 1)
                for u in range(U):
                    for q in range(2):
                        act.wait_ge(pe.sem, pe.at(c, "hT", 2 * u + q))
                        w = HK // 2 * T
                        nc.scalar.copy(hT[:, u, q * w:(q + 1) * w], ps[:, 4 + (2 * u + q) % 4, 0:w]).then_inc(ac.step("hT", 2 * u + q), 1)

        @block.tensor
        def _(ten):
            ten.wait_ge(run.arrived, run.loads)
            ten.wait_ge(sized, 2)
            nc.tensor.matmul(ps[:, 7, 0:2], core.ones[:, :], total[:, :], start=True, stop=True).then_inc(tern_pe, 1)
            ten.wait_ge(tern, 9)
            for i in range(HK):
                ins = nc.tensor.matmul(ps[0:1, 6, 0:D], self.lb[:, i:i + 1], self.pr[:, i, :], start=(i == 0), stop=(i == HK - 1))
            ins.then_inc(tern_pe, 1)
            ten.wait_ge(tern, 10 + HK)
            with ten.Fori(0, NCH) as c:
                for u in range(U):
                    ten.wait_ge(ve.sem, ve.at(c, "xn", u))
                    transposes(core, ps[:, u], xn[:, u], T, KD).then_inc(pe.step("xT", u), 1)
                for u in range(U):
                    ten.wait_ge(ac.sem, ac.at(c, "xT", u))
                    for q in range(2):
                        if u >= 2:
                            ten.wait_ge(ac.sem, ac.at(c, "gelu", 2 * u + q - 4))
                        for k in range(KD):
                            ins = nc.tensor.matmul(ps[0:T, 4 + (2 * u + q) % 4, :], xT[:, u, k * T:(k + 1) * T],
                                                   self.fc[:, k, q * 512:(q + 1) * 512], start=(k == 0), stop=(k == KD - 1))
                        ins.then_inc(pe.step("up", 2 * u + q), 1)

                def turn(u):
                    ten.wait_ge(ve.sem, ve.at(c, "hn", u))
                    for q in range(2):
                        if u >= 2:
                            ten.wait_ge(ac.sem, ac.at(c, "hT", 2 * u + q - 4))
                        transposes(core, ps[:, 4 + (2 * u + q) % 4], h[:, u, q * 512:(q + 1) * 512], T, HK // 2).then_inc(pe.step("hT", 2 * u + q), 1)

                def down(u):
                    ten.wait_ge(ac.sem, ac.at(c, "hT", 2 * u + 1))
                    for i in range(HK):
                        nc.tensor.matmul(ps[0:T, u, 0:D], hT[:, u, i * T:(i + 1) * T], self.pr[:, i, :],
                                         start=(i == 0), stop=False)
                    return nc.tensor.matmul(ps[0:T, u, 0:D], core.ones[0:1, 0:T], brow[:, :], start=False, stop=True)
                for u in range(U):
                    turn(u)
                for u in range(U):
                    down(u).then_inc(pe.step("out", u), 1)


class Run:

    def __init__(self, core, stack, block, own, ahead):
        self.core, self.stack, self.block, self.ahead = core, stack, block, ahead
        self.arrived, self.loads = own[0], DMA * len(own[1].loads)

    def sbuf(self, name, shape, dt=F32):
        return self.stack.enter_context(self.core.nc.sbuf_tensor(f"{self.core.stage}_{name}", shape, dt))

    def prefetch(self, eng):
        if self.ahead:
            sem, arena = self.ahead
            for dst, src in arena.loads:
                eng.dma_start(dst, src).then_inc(sem, DMA)


STAGES = [L0Banded, L0Cross, L0Mlp, L0Kron, L1State, L1Cross, L1Experts, L2Graph, L2Cross, L2Experts, L3Self, L3Mlp, L3Cross, L3Feed]


def runs(numbers):
    out = []
    for n in sorted(numbers):
        if out and out[-1][1] == n:
            out[-1][1] = n + 1
        else:
            out.append([n, n + 1])
    return out


def program(nc, d, out, stages):
    with ExitStack() as stack:
        core = Core(nc, d, stack)
        stages = [s() for s in stages]
        fetched = []
        for i, s in enumerate(stages):
            core.stage = s.name
            arena = Arena(core, i % 2)
            s.weights(arena, d)
            fetched.append((core.semaphore("weights"), arena))
        core.stage = "begin"
        x_in, x_stats = core.semaphore("x_in"), core.semaphore("x_stats")
        first = core.semaphore("ident")
        with nc.Block() as block:
            @block.sync
            def _(sp):
                sp.dma_start(core.x[:, :, :], d["x"].rearrange("b t c -> t b c")).then_inc(x_in, DMA)
                sp.dma_start(core.ident[:, :], d["ident"]).then_inc(first, DMA)
                sem, arena = fetched[0]
                for dst, src in arena.loads:
                    sp.dma_start(dst, src).then_inc(sem, DMA)

            @block.gpsimd
            def _(pool):
                nc.gpsimd.memset(core.mhalf[:, :], -0.5)
                nc.gpsimd.memset(core.ones[:, :], 1.0)
                pool.wait_ge(first, DMA)
                nc.gpsimd.memset(core.phalf[:, :], 0.5).then_inc(core.constants, 1)

            @block.vector
            def _(dve):
                dve.wait_ge(x_in, DMA)
                dve.wait_ge(core.constants, 1)
                for n in range(NB):
                    nc.vector.bn_stats(core.stats[:, n, :], core.x[:, n, :]).then_inc(x_stats, 1)
                dve.wait_ge(x_stats, NB)
        before, used = ExitStack(), []
        for i, s in enumerate(stages):
            core.stage, core.stack, core.open = s.name, ExitStack(), []
            with ExitStack() as own, nc.Block() as block:
                if used:
                    @block.gpsimd
                    def _(pool):
                        for first, stop in runs(used):
                            nc.gpsimd.sem_clear(range(first, stop))
                ahead = fetched[i + 1] if i + 1 < len(stages) else None
                s.build(core, Run(core, own, block, fetched[i], ahead))
            before.close()
            before, used = core.stack, core.open
        stack.push(before)
        core.stack = stack
        core.stage = "end"
        written = core.semaphore("written")
        with nc.Block() as block:
            @block.sync
            def _(sp):
                sp.dma_start(out.rearrange("b t c -> t b c"), core.x[:, :, :]).then_inc(written, DMA)
                sp.wait_ge(written, DMA)


def layout(inputs):
    import numpy as np
    i = {k: np.asarray(v) for k, v in inputs.items()}
    a = {k: v for k, v in i.items() if k not in ("ctx_1024", "mask_BxSxS2_ik0")}
    a["ctx"] = i["ctx_1024"]
    a["ctxT"] = i["ctx_1024"].transpose(0, 2, 1)
    a["mask"] = i["mask_BxSxS2_ik0"]
    a["ident"] = np.eye(128, dtype=np.float32)
    a["L1_attn_AT"] = i["L1_attn_A"].T
    a["heads"] = np.kron(np.eye(8), np.ones((16, 1))).astype(np.float32)
    for k in list(a):
        if a[k].ndim == 1 and a[k].size % 128 == 0:
            a[k + "_c"] = a[k].reshape(-1, 128).T
    bias, scales = a.pop("L0_attn_pos_bias"), a.pop("L0_attn_scale_embed")
    a["L0_attn_bias"] = bias[list(L0Banded.ROWS)].reshape(-1)
    a["L0_attn_scales"] = np.tile(scales[list(L0Banded.ROWS)].T, (L0Banded.HK, 1))
    a["iota"] = np.arange(64, dtype=np.float32)
    a["before"] = np.triu(np.ones((128, 128), np.float32), 1)
    a["upto"] = np.triu(np.ones((128, 128), np.float32))
    a["L1_ffn_router"] = np.concatenate([a.pop("L1_ffn_Wg"), a.pop("L1_ffn_Wsg")])
    turn = lambda v: np.swapaxes(v, -1, -2)
    for k in ("up", "down"):
        a["L0_ffn_" + k] = np.concatenate([turn(a.pop(f"L0_ffn_{m}_{k}")) for m in "AB"], axis=2)
        a["L0_ffn_" + k] = a["L0_ffn_" + k].reshape(-1, a["L0_ffn_" + k].shape[2])
    a["L0_ffn_W_downP"] = a.pop("L0_ffn_W_down").reshape(L0Kron.E, L0Kron.F, L0Kron.F).transpose(1, 2, 0)
    a["row32"], a["row64"] = ((np.arange(128) % n).astype(np.float32).reshape(-1, 1) for n in (32, 64))
    for e in (L1Experts, L2Experts):
        a[e.name + "_packed"] = e.pack(np, a)
        a[e.name + "_steps"] = np.arange(0, NB * T, e.TS, dtype=np.float32)
    for p in ("ca", "cf"):
        for k in ("sub", "W", "B"):
            v = a[f"L3_attn_{p}_{k}_b"]
            a[f"L3_attn_{p}_{k}_b_cols"] = np.moveaxis(v.reshape(v.shape[:-1] + (-1, 128)), -1, 0)
    for k in TURNED:
        a[k + "T"] = np.swapaxes(a.pop(k), -1, -2)
    return {k: np.ascontiguousarray(v) for k, v in a.items()}


TURNED = ["L0_ffn_W_up", "L2_ffn_router_w", "L1_ffn_router", "L1_ffn_Ws_gate", "L1_ffn_Ws_up", "L1_ffn_Ws_down"] + [f"L3_attn_{p}_{k}_w" for p in ("ca", "cp", "cf", "cm") for k in ("sub", "W", "B")] + ["L1_xattn_Wv", "L3_ffn_W_fc", "L3_ffn_W_proj", "L1_attn_B_w", "L1_attn_C_w", "L1_attn_D_w", "L1_attn_s_w1",
          "L1_attn_s_w2", "L1_attn_g_w", "L2_attn_Wl", "L2_attn_Wr", "L2_attn_Wf",
          "L3_xattn_Wq", "L3_xattn_Wk", "L3_xattn_Wv", "L3_xattn_Wo"]



def kernel(**inputs):
    from concourse import bacc
    from concourse.bass_utils import run_bass_kernel_spmd
    nc = bacc.Bacc("TRN2", target_bir_lowering=False, num_devices=1)
    arrays = layout(inputs)
    dram = {k: nc.dram_tensor("in_" + k, v.shape, mybir.dt.from_np(v.dtype), kind="ExternalInput").ap()
            for k, v in arrays.items()}
    out = nc.dram_tensor("out_x", (NB, T, D), F32, kind="ExternalOutput").ap()
    program(nc, dram, out, STAGES)
    r = run_bass_kernel_spmd(nc, [{"in_" + k: v for k, v in arrays.items()}], core_ids=[0])
    return r.results[0]["out_x"]
```

```python
from contextlib import ExitStack

import concourse.bass as bass
from concourse import mybir
from concourse.alu_op_type import AluOpType as ALU

F32 = mybir.dt.float32
I32 = mybir.dt.int32
U32 = mybir.dt.uint32
ACT = mybir.ActivationFunctionType
AX = mybir.AxisListType

NB, T, D = 16, 112, 256
S = 375
ST, SP_ = 3, 125
U = 4
NCH = NB // U
N4 = U * T
KD = D // 128
DMA = 16


class Progress:

    def __init__(self, core, name, *steps):
        self.sem = core.semaphore(name)
        self.offset, self.per = {}, 0
        for s in steps:
            s, count = s if isinstance(s, tuple) else (s, U)
            self.offset[s] = (self.per, count)
            self.per += count
        self.raised = 0

    def step(self, step, u=0):
        at, count = self.offset[step]
        assert u < count and self.raised % self.per == at + u, (step, u, self.raised)
        self.raised += 1
        return self.sem

    def at(self, c, step, u=0):
        at, count = self.offset[step]
        assert u < count
        return c * self.per + (at + u + 1)


class Core:

    def __init__(self, nc, dram, stack):
        self.nc, self.dram = nc, dram
        self.stack, self.whole, self.stage, self.open = stack, stack, "core", []
        self.passed = {e: stack.enter_context(nc.semaphore(f"passed{i}")) for i, e in enumerate(
            (nc.sync, nc.scalar, nc.vector, nc.gpsimd, nc.tensor))}
        sb = lambda name, shape, dt=F32: stack.enter_context(nc.sbuf_tensor(name, shape, dt))
        self.x = sb("x", [T, NB, D])
        self.y = sb("y", [T, NB, D])
        self.ident = sb("ident", [128, 128])
        self.stats = sb("stats", [T, NB, 6])
        self.mean = sb("mean", [T, NB])
        self.rstd = sb("rstd", [T, NB])
        self.nsc = sb("nsc", [T, 5, NB])
        self.ones = sb("ones", [128, 128])
        self.mhalf = sb("mhalf", [128, 16])
        self.arena = [sb(f"arena{i}", [128, ARENA]) for i in range(2)]
        self.ps = stack.enter_context(nc.psum_tensor("ps", [128, 8, 512], F32))
        self.constants = stack.enter_context(nc.semaphore("constants"))

    def semaphore(self, name):
        s = self.stack.enter_context(self.nc.semaphore(f"{self.stage}_{name}"))
        self.open.append(s.num)
        return s

    def pool_dma_semaphore(self, name):
        return self.whole.enter_context(self.nc.semaphore(f"{self.stage}_{name}"))

    def scratch(self, name, shape):
        return self.nc.dram_tensor(f"{self.stage}_{name}", shape, F32).ap()

    def stand(self, eng):
        eng.sem_inc(self.passed[eng], 1)


ARENA = 13412
EPS = 1e-5


class Arena:

    def __init__(self, core, i):
        self.t, self.at, self.loads = core.arena[i], 0, []

    def take(self, parts, *free):
        n = 1
        for f in free:
            n *= f
        v = self.t[0:parts, self.at:self.at + n]
        self.at += n
        assert self.at <= ARENA, self.at
        if len(free) == 2:
            v = v.rearrange("p (a b) -> p a b", a=free[0])
        if len(free) == 3:
            v = v.rearrange("p (a b c) -> p a b c", a=free[0], b=free[1])
        return v

    def load(self, src, parts, *free):
        v = self.take(parts, *free)
        self.loads.append((v, src))
        return v


def rows(ap, p=128):
    return ap.rearrange("(k p) n -> p k n", p=p)


def col(ap, p=128):
    return ap.rearrange("(k p) -> p k", p=p)


def every(ap, parts):
    n = 1
    for d in ap.shape:
        n *= d
    return bass.AP(ap.tensor, ap.offset, [[0, parts], [1, n]])


def norm_vector(core, dve, norm):
    nc, st, sc = core.nc, core.stats, core.nsc
    me, qe, mo, qo = (st[:, :, i] for i in (1, 2, 4, 5))
    nc.vector.tensor_tensor(sc[:, 0, :], me, mo, ALU.add).then_inc(norm, 1)
    nc.vector.tensor_tensor(sc[:, 1, :], me, mo, ALU.subtract).then_inc(norm, 1)
    nc.vector.tensor_tensor(sc[:, 2, :], qe, qo, ALU.add).then_inc(norm, 1)
    dve.wait_ge(norm, 3)
    nc.vector.tensor_scalar(core.mean[:, :], sc[:, 0, :], 0.5, None, ALU.mult).then_inc(norm, 1)
    nc.vector.tensor_tensor(sc[:, 3, :], sc[:, 1, :], sc[:, 1, :], ALU.mult).then_inc(norm, 1)
    nc.vector.tensor_scalar(sc[:, 4, :], sc[:, 2, :], 1.0 / D, EPS, ALU.mult, ALU.add).then_inc(norm, 1)
    dve.wait_ge(norm, 6)
    nc.vector.scalar_tensor_tensor(out=sc[:, 0, :], in0=sc[:, 3, :], scalar=0.25, in1=sc[:, 4, :],
                                   op0=ALU.mult, op1=ALU.add).then_inc(norm, 1)
    dve.wait_ge(norm, 8)


def norm_pool(core, norm):
    core.nc.gpsimd.wait_ge(norm, 7)
    core.nc.gpsimd.tensor_tensor(core.rstd[:, :], core.nsc[:, 0, :], core.mhalf[0:T, 0:NB],
                                 ALU.pow).then_inc(norm, 1)


def normed(core, out, n):
    return core.nc.vector.tensor_scalar(out, core.x[:, n, :], core.mean[:, bass.ds(n, 1)],
                                        core.rstd[:, bass.ds(n, 1)], ALU.subtract, ALU.mult)


def row_stats(core, dve, n):
    core.stand(dve)
    return core.nc.vector.bn_stats(core.stats[:, n, :], core.x[:, n, :])


def transposes(core, ps, src, rows_, parts):
    for k in range(parts):
        ins = core.nc.tensor.transpose(ps[:, k * rows_:(k + 1) * rows_], src[:, k * 128:(k + 1) * 128],
                                       core.ident[0:rows_, 0:rows_])
    return ins


class Norm:

    def __init__(self, core, run, name, rows_=T, eps=EPS, parts=1, units=U):
        self.core, self.rows, self.eps, self.parts, self.units = core, rows_, eps, parts, units
        self.st = run.sbuf(name + "_st", [rows_, units, 6 * parts])
        self.mv = run.sbuf(name + "_mv", [rows_, units, 2])
        self.ve = run.sbuf(name + "_ve", [rows_, units])
        self.rs = run.sbuf(name + "_rs", [rows_, units])
        self.tag = name

    def steps(self):
        n = self.units
        return ((self.tag + "st", n * self.parts), (self.tag + "ag", n), (self.tag + "eps", 1))

    def vector(self, dve, ve, c, src, ready):
        nc = self.core.nc
        for u in range(self.units):
            ready(u)
            for q in range(self.parts):
                nc.vector.bn_stats(self.st[:, u, 6 * q:6 * q + 6], src(u, q)).then_inc(ve.step(self.tag + "st", u * self.parts + q), 1)
        for u in range(self.units):
            dve.wait_ge(ve.sem, ve.at(c, self.tag + "st", u * self.parts + self.parts - 1))
            self.core.stand(dve)
            nc.vector.bn_aggr(self.mv[:, u, :], self.st[:, u, :]).then_inc(ve.step(self.tag + "ag", u), 1)
        dve.wait_ge(ve.sem, ve.at(c, self.tag + "ag", self.units - 1))
        nc.vector.tensor_scalar(self.ve[:, :], self.mv[:, :, 1], self.eps, None, ALU.add).then_inc(ve.step(self.tag + "eps"), 1)

    def pool(self, pool, ve, po, c):
        pool.wait_ge(ve.sem, ve.at(c, self.tag + "eps"))
        self.core.nc.gpsimd.tensor_tensor(self.rs[:, :], self.ve[:, :], self.core.mhalf[0:self.rows, 0:self.units],
                                                  ALU.pow).then_inc(po.step(self.tag + "rs"), 1)

    def apply(self, out, src, u):
        return self.core.nc.vector.tensor_scalar(out, src, self.mv[:, u, 0:1], self.rs[:, u:u + 1],
                                                 ALU.subtract, ALU.mult)


class L0Banded:

    name = "L0_attn"
    H = 16
    HD = D // H
    HK = H // KD
    NEAR = 41
    FAR = 96
    J = NEAR + 1
    DIST = (*range(NEAR - 1, -1, -1), FAR)
    ROWS = (*range(NEAR - 1, -1, -1), NEAR + 1)
    PAD = NEAR - 1
    GD = 128 // H
    NG = -(-J // GD)
    LEFT = 128 - HK

    def weights(self, a, d):
        n = self.name + "_"
        self.wqkv = a.load(rows(d[n + "w_qkv"]), 128, KD, 3 * D)
        self.wo = a.load(rows(d[n + "w_out"]), 128, KD, D)
        self.bias = a.load(every(d[n + "bias"], T), T, self.J * self.H)
        self.se = a.load(d[n + "scales"], 128, self.J)
        self.gain = a.load(every(d[n + "if_gain"], T), T, self.H)
        self.heads = a.load(d["heads"], 128, self.HK)
        self.scale = a.take(128, self.LEFT + 128 * self.J)
        self.e = a.take(T, U, self.J * self.H)
        self.q = a.take(128, KD, N4)

    def build(self, core, run):
        nc, ps, H, HD, HK, J, NEAR, PAD, GD, NG = core.nc, core.ps, self.H, self.HD, self.HK, self.J, self.NEAR, self.PAD, self.GD, self.NG
        sb, e, q = run.sbuf, self.e, self.q
        NI, RING = J * KD, 4
        xn, xT = sb("xn", [T, U, D]), sb("xT", [128, KD, N4])
        k = sb("k", [128, KD, U, PAD + T])
        v = sb("v", [T, U, (2 * H + 1) * HD])
        prod = sb("prod", [128, RING, U, T])
        sT = sb("sT", [128, 2, N4])
        mx, den, rden = sb("mx", [T, U, H]), sb("den", [T, U, H]), sb("rden", [T, U, H])
        a, aT = sb("a", [T, 2, T * H]), sb("aT", [T, 2, H * T])
        oT = sb("oT", [128, 2, KD * T])
        LEAD = (NEAR - 1) * H
        P = LEAD + T * H
        skew = core.scratch("skew", [U, T * P])
        norm, ready, cleared = core.semaphore("norm"), core.semaphore("ready"), core.semaphore("cleared")
        zeroed = core.semaphore("zeroed")
        written = [core.semaphore(f"written{u}") for u in range(U)]
        got = [core.semaphore(f"got{u}") for u in range(U)]
        one = lambda eng, n, c: Progress(core, eng + "_" + n, (n, c))
        pe_x, pe_q, pe_v, pe_i = one("tensor", "xT", KD), one("tensor", "qk", 2 * KD), one("tensor", "v", U), one("tensor", "used", NI)
        pe_g, pe_a, pe_o, pe_w = one("tensor", "turned", NG), one("tensor", "aT", 4 * U), one("tensor", "oT", U), one("tensor", "out", U)
        ac_x, ac_q, ac_v, ac_e = one("scalar", "xT", KD), one("scalar", "qk", 2 * KD), one("scalar", "v", U), one("scalar", "exp", U)
        ac_g, ac_a, ac_o = one("scalar", "scores", NG), one("scalar", "aT", 4 * U), one("scalar", "oT", U)
        ve_x, ve_i, ve_g = one("vector", "xn", U), one("vector", "prod", NI), one("vector", "biased", NG)
        ve_m = Progress(core, "vector_max", ("max", U), ("sub", U))
        ve_n = [Progress(core, f"vector_norm{u}", ("den", 1), ("rden", 1), ("gain", 1), ("e", 1)) for u in range(U)]
        ve_w = [Progress(core, f"vector_x{u}", ("out", 1), ("stats", 1)) for u in range(U)]
        block = run.block
        by_head = lambda t: t.rearrange("p (j h) -> p h j", h=H)
        by_batch = lambda t: t.rearrange("p (b t) -> p b t", b=U)
        size = lambda g: min(GD, J - GD * g) * H
        last_of = lambda g: min(16 * g + 15, NI - 1)
        DIVIDE = {2 + 2 * u: u for u in range(U)}
        TURN = {16 + 3 * n: n for n in range(4 * U)}
        ATTEND = {27 + 12 * u: u for u in range(U)}
        PROJECT = {31 + 12 * u: u for u in range(U)}
        UPDATE = {36 + 12 * u: u for u in range(U)}
        VALUES = {70 + 2 * u: u for u in range(U)}
        XN, XT = 66, 80
        BACK = {last_of(g) + 5: g for g in range(NG) if last_of(g) + 5 < NI}
        BIAS = {last_of(g) + 11: g for g in range(NG) if last_of(g) + 11 < NI}

        def passes(eng, body):
            body(0, True, False)
            with eng.Fori(1, NCH - 1) as c:
                body(c, False, False)
            body(NCH - 1, False, True)

        def start(i):
            return 0 if i % 16 == 0 else self.DIST[i // KD]

        @block.sync
        def _(sp):
            sp.wait_ge(cleared, 1)
            for u in range(U):
                rows_ = skew[u].rearrange("(t n) -> t n", t=T)
                sp.dma_start(rows_[:, 0:T * H], aT[:, 0, :]).then_inc(zeroed, DMA)
                sp.dma_start(rows_[:, T * H:P], aT[:, 0, 0:LEAD]).then_inc(zeroed, DMA)
            sp.wait_ge(zeroed, 2 * U * DMA)

            def body(c, first, last):
                def write(u):
                    if not first:
                        sp.wait_ge(got[u], c * DMA)
                        core.stand(sp)
                    sp.wait_ge(ve_n[u].sem, ve_n[u].at(c, "e"))
                    near = bass.AP(skew.tensor, u * T * P, [[P + H, T], [1, NEAR * H]])
                    far = bass.AP(skew.tensor, u * T * P + self.FAR * P + LEAD, [[P + H, T - self.FAR], [1, H]])
                    sp.dma_start(near, e[:, u, 0:NEAR * H]).then_inc(written[u], DMA)
                    sp.dma_start(far, e[self.FAR:T, u, NEAR * H:J * H]).then_inc(written[u], DMA)

                def read(u):
                    if u >= 2:
                        sp.wait_ge(pe_a.sem, pe_a.at(c, "aT", 4 * (u - 2) + 3))
                        core.stand(sp)
                    elif not first:
                        sp.wait_ge(pe_a.sem, pe_a.at(c - 1, "aT", 4 * (u + 2) + 3))
                        core.stand(sp)
                    sp.wait_ge(written[u], (c + 1) * 2 * DMA)
                    sp.dma_start(a[:, u % 2, :], skew[u].rearrange("(t n) -> t n", t=T)[:, LEAD:P]).then_inc(got[u], DMA)
                write(0)
                write(1)
                read(0)
                write(2)
                write(3)
                for u in range(1, U):
                    read(u)
            passes(sp, body)

        @block.gpsimd
        def _(pool):
            nc.gpsimd.memset(aT[:, 0, :], 0.0).then_inc(cleared, 1)
            norm_pool(core, norm)
            nc.gpsimd.memset(self.scale, 0.0).then_inc(ready, 1)
            nc.gpsimd.memset(k[:, :, :, :], 0.0).then_inc(ready, 1)
            nc.gpsimd.memset(v[:, :, :], 0.0).then_inc(ready, 1)
            pool.wait_ge(run.arrived, run.loads)
            near = self.bias[:, 0:NEAR * H].rearrange("p (j h) -> p j h", h=H)
            nc.gpsimd.affine_select(near, near, pattern=[[1, NEAR], [0, H]], compare_op=ALU.is_ge, fill=-1e30, base=1 - NEAR,
                                    channel_multiplier=1).then_inc(ready, 1)
            far = self.bias[:, NEAR * H:J * H]
            nc.gpsimd.affine_select(far, far, pattern=[[0, H]], compare_op=ALU.is_ge, fill=-1e30, base=-self.FAR,
                                    channel_multiplier=1).then_inc(ready, 1)

        @block.vector
        def _(dve):
            norm_vector(core, dve, norm)
            dve.wait_ge(run.arrived, run.loads)
            nc.vector.tensor_scalar(self.se, self.se, 1.0, HD ** -0.5, ALU.add, ALU.mult).then_inc(norm, 1)
            dve.wait_ge(ready, 5)
            dve.wait_ge(norm, 9)
            nc.vector.tensor_tensor(self.scale[:, self.LEFT:].rearrange("p (j n) -> p j n", j=J)[:, :, 0:HK],
                                    self.heads.unsqueeze(1).to_broadcast([128, J, HK]),
                                    self.se.unsqueeze(2).to_broadcast([128, J, HK]), ALU.mult).then_inc(norm, 1)

            def front(c):
                for u in range(U):
                    normed(core, xn[:, u], U * c + u).then_inc(ve_x.step("xn", u), 1)

            def biased(c, g, first):
                n = size(g)
                if g == 0 and not first:
                    for u in range(U):
                        dve.wait_ge(written[u], c * 2 * DMA)
                        core.stand(dve)
                dve.wait_ge(pe_g.sem, pe_g.at(c, "turned", g))
                nc.vector.tensor_tensor(e[:, :, g * 128:g * 128 + n], ps[0:T, 2 + g % 2, 0:U * n].rearrange("p (b n) -> p b n", b=U),
                                        self.bias[:, g * 128:g * 128 + n].unsqueeze(1).to_broadcast([T, U, n]), ALU.add).then_inc(ve_g.step("biased", g), 1)

            def divide(c, u):
                ve = ve_n[u]
                dve.wait_ge(ac_e.sem, ac_e.at(c, "exp", u))
                nc.vector.tensor_reduce(den[:, u, :], by_head(e[:, u]), AX.X, ALU.add).then_inc(ve.step("den"), 1)
                dve.wait_ge(ve.sem, ve.at(c, "den"))
                nc.vector.reciprocal(rden[:, u, :], den[:, u, :]).then_inc(ve.step("rden"), 1)
                dve.wait_ge(ve.sem, ve.at(c, "rden"))
                nc.vector.tensor_tensor(rden[:, u, :], rden[:, u, :], self.gain, ALU.mult).then_inc(ve.step("gain"), 1)
                dve.wait_ge(ve.sem, ve.at(c, "gain"))
                by_dist = e[:, u].rearrange("p (j h) -> p j h", h=H)
                nc.vector.tensor_tensor(by_dist, by_dist, rden[:, u, :].unsqueeze(1).to_broadcast([T, J, H]), ALU.mult).then_inc(ve.step("e"), 1)

            def update(c, u):
                ve = ve_w[u]
                dve.wait_ge(pe_w.sem, pe_w.at(c, "out", u))
                core.stand(dve)
                x = core.x[:, U * c + u, :]
                nc.vector.tensor_tensor(x, x, ps[0:T, 7, 0:D], ALU.add).then_inc(ve.step("out"), 1)
                dve.wait_ge(ve.sem, ve.at(c, "out"))
                row_stats(core, dve, U * c + u).then_inc(ve.step("stats"), 1)

            def body(c, first, last):
                for i in range(NI):
                    if not first and i in DIVIDE:
                        divide(c - 1, DIVIDE[i])
                    if not first and i in UPDATE:
                        update(c - 1, UPDATE[i])
                    if not last and i == XN:
                        dve.wait_ge(pe_x.sem, pe_x.at(c, "xT", KD - 1))
                        core.stand(dve)
                        front(c + 1)
                    if i in BIAS:
                        biased(c, BIAS[i], first)
                    if i < KD:
                        dve.wait_ge(ac_q.sem, ac_q.at(c, "qk", KD + i))
                    if i >= RING:
                        dve.wait_ge(pe_i.sem, pe_i.at(c, "used", i - RING))
                    j, b, t0 = self.DIST[i // KD], i % KD, start(i)
                    nc.vector.tensor_tensor(prod[:, i % RING, :, t0:T], by_batch(q[:, b])[:, :, t0:T], k[:, b, :, PAD + t0 - j:PAD + T - j],
                                            ALU.mult).then_inc(ve_i.step("prod", i), 1)
                for g in range(NG):
                    if g not in BIAS.values():
                        biased(c, g, first)
                dve.wait_ge(ve_g.sem, ve_g.at(c, "biased", NG - 1))
                for u in range(U):
                    nc.vector.tensor_reduce(mx[:, u, :], by_head(e[:, u]), AX.X, ALU.max).then_inc(ve_m.step("max", u), 1)
                for u in range(U):
                    dve.wait_ge(ve_m.sem, ve_m.at(c, "max", u))
                    nc.vector.tensor_tensor(by_head(e[:, u]), by_head(e[:, u]), mx[:, u, :].unsqueeze(2).to_broadcast([T, H, J]),
                                            ALU.subtract).then_inc(ve_m.step("sub", u), 1)
            front(0)
            passes(dve, body)
            for u in range(U):
                divide(NCH - 1, u)
            for u in range(U):
                update(NCH - 1, u)

        @block.scalar
        def _(act):
            run.prefetch(act)
            act.wait_ge(ready, 5)

            def turned(c):
                for b in range(KD):
                    act.wait_ge(pe_x.sem, pe_x.at(c, "xT", b))
                    nc.scalar.copy(xT[:, b], ps[:, 6 + b, 0:N4]).then_inc(ac_x.step("xT", b), 1)

            def qk(c, m):
                act.wait_ge(pe_q.sem, pe_q.at(c, "qk", m))
                if m < KD:
                    nc.scalar.copy(q[:, m], ps[:, 6 + m % 2, 0:N4]).then_inc(ac_q.step("qk", m), 1)
                else:
                    nc.scalar.copy(k[:, m - KD, :, PAD:PAD + T], by_batch(ps[:, 6 + m % 2, 0:N4])).then_inc(ac_q.step("qk", m), 1)

            def values(c, u):
                act.wait_ge(pe_v.sem, pe_v.at(c, "v", u))
                nc.scalar.copy(v[:, u, HD:].rearrange("p (h e) -> p h e", h=H)[:, :, 0:HD],
                               ps[0:T, 6 + u % 2, 0:D].rearrange("p (h e) -> p h e", h=H)).then_inc(ac_v.step("v", u), 1)

            def scores(c, g):
                act.wait_ge(pe_i.sem, pe_i.at(c, "used", last_of(g)))
                nc.scalar.copy(sT[0:size(g), g % 2], ps[0:size(g), g % 2, 0:N4]).then_inc(ac_g.step("scores", g), 1)

            def weights_turned(c, n):
                act.wait_ge(pe_a.sem, pe_a.at(c, "aT", n))
                w = H // 4 * T
                nc.scalar.copy(aT[:, n // 4 % 2, n % 4 * w:(n % 4 + 1) * w], ps[0:T, 4 + n % 2, 0:w]).then_inc(ac_a.step("aT", n), 1)

            def results(c, u):
                act.wait_ge(pe_o.sem, pe_o.at(c, "oT", u))
                nc.scalar.copy(oT[:, u % 2], ps[:, 6, 0:KD * T]).then_inc(ac_o.step("oT", u), 1)

            def body(c, first, last):
                for i in range(NI):
                    if not first and i in TURN:
                        weights_turned(c - 1, TURN[i])
                    if not first and i in ATTEND:
                        results(c - 1, ATTEND[i])
                    if i in VALUES:
                        values(c, VALUES[i])
                    if not last and i == XT:
                        turned(c + 1)
                    if i % 16 == 15:
                        scores(c, i // 16)
                scores(c, NG - 1)
                if not last:
                    for m in range(2 * KD):
                        qk(c + 1, m)
                for u in range(U):
                    act.wait_ge(ve_m.sem, ve_m.at(c, "sub", u))
                    nc.scalar.activation(e[:, u], e[:, u], ACT.Exp).then_inc(ac_e.step("exp", u), 1)
            turned(0)
            for m in range(2 * KD):
                qk(0, m)
            passes(act, body)
            for u in range(U):
                for n in range(4 * u, 4 * u + 4):
                    weights_turned(NCH - 1, n)
                results(NCH - 1, u)

        @block.tensor
        def _(ten):
            ten.wait_ge(run.arrived, run.loads)

            def turn(c):
                for b in range(KD):
                    for u in range(U):
                        if b == 0:
                            ten.wait_ge(ve_x.sem, ve_x.at(c, "xn", u))
                        ins = nc.tensor.transpose(ps[:, 6 + b, u * T:(u + 1) * T], xn[:, u, b * 128:(b + 1) * 128], core.ident[0:T, 0:T])
                    ins.then_inc(pe_x.step("xT", b), 1)

            def qk(c, m):
                if m < KD:
                    ten.wait_ge(ac_x.sem, ac_x.at(c, "xT", KD - 1))
                else:
                    ten.wait_ge(ac_q.sem, ac_q.at(c, "qk", m - KD))
                for b in range(KD):
                    ins = nc.tensor.matmul(ps[:, 6 + m % 2, 0:N4], self.wqkv[:, b, m * 128:(m + 1) * 128], xT[:, b], start=(b == 0), stop=(b == KD - 1))
                ins.then_inc(pe_q.step("qk", m), 1)

            def values(c, first, u):
                if u >= 2:
                    ten.wait_ge(ac_v.sem, ac_v.at(c, "v", u - 2))
                elif u == 1 and not first:
                    ten.wait_ge(ve_w[U - 1].sem, ve_w[U - 1].at(c - 1, "out"))
                for b in range(KD):
                    ins = nc.tensor.matmul(ps[0:T, 6 + u % 2, 0:D], xT[:, b, u * T:(u + 1) * T], self.wqkv[:, b, 2 * D:3 * D],
                                           start=(b == 0), stop=(b == KD - 1))
                ins.then_inc(pe_v.step("v", u), 1)

            def back(c, g):
                n = size(g)
                ten.wait_ge(ac_g.sem, ac_g.at(c, "scores", g))
                if g >= 2:
                    ten.wait_ge(ve_g.sem, ve_g.at(c, "biased", g - 2))
                core.stand(ten)
                for u in range(U):
                    ins = nc.tensor.transpose(ps[0:T, 2 + g % 2, u * n:(u + 1) * n], sT[0:n, g % 2, u * T:(u + 1) * T], core.ident[0:n, 0:n])
                ins.then_inc(pe_g.step("turned", g), 1)

            def weights_turned(c, n):
                u = n // 4
                if n % 4 == 0:
                    ten.wait_ge(got[u], (c + 1) * DMA)
                if n >= 2:
                    ten.wait_ge(ac_a.sem, ac_a.at(c, "aT", n - 2))
                for i in range(H // 4):
                    h = n % 4 * (H // 4) + i
                    ins = nc.tensor.transpose(ps[0:T, 4 + n % 2, i * T:(i + 1) * T], a[:, u % 2].rearrange("p (s h) -> p h s", h=H)[:, h, :],
                                              core.ident[0:T, 0:T])
                ins.then_inc(pe_a.step("aT", n), 1)

            def attend(c, u):
                ten.wait_ge(ac_a.sem, ac_a.at(c, "aT", 4 * u + 3))
                if u >= 1:
                    ten.wait_ge(ac_o.sem, ac_o.at(c, "oT", u - 1))
                for h in range(H):
                    odd, r = h % 2, h % HK // 2 * 2 * HD
                    at = (2 * h + 1 - odd) * HD
                    ins = nc.tensor.matmul(ps[r:r + 2 * HD, 6, h // HK * T:(h // HK + 1) * T], v[:, u, at:at + 2 * HD], aT[:, u % 2, h * T:(h + 1) * T],
                                           start=(odd == 0), stop=(odd == 1))
                ins.then_inc(pe_o.step("oT", u), 1)

            def project(c, u):
                ten.wait_ge(ac_o.sem, ac_o.at(c, "oT", u))
                if u >= 1:
                    ten.wait_ge(ve_w[u - 1].sem, ve_w[u - 1].at(c, "out"))
                for b in range(KD):
                    ins = nc.tensor.matmul(ps[0:T, 7, 0:D], oT[:, u % 2, b * T:(b + 1) * T], self.wo[:, b, :], start=(b == 0), stop=(b == KD - 1))
                ins.then_inc(pe_w.step("out", u), 1)

            def body(c, first, last):
                for i in range(NI):
                    if not first and i in TURN:
                        weights_turned(c - 1, TURN[i])
                    if not first and i in ATTEND:
                        attend(c - 1, ATTEND[i])
                    if not first and i in PROJECT:
                        project(c - 1, PROJECT[i])
                    if i in VALUES:
                        values(c, first, VALUES[i])
                    if not last and i == XT:
                        ten.wait_ge(ac_v.sem, ac_v.at(c, "v", U - 1))
                        turn(c + 1)
                    if i in BACK:
                        back(c, BACK[i])
                    p, b, g, t0 = i // KD, i % KD, i // 16, start(i)
                    n = size(g)
                    if i % 16 == 0 and g >= 2:
                        ten.wait_ge(ac_g.sem, ac_g.at(c, "scores", g - 2))
                    ten.wait_ge(ve_i.sem, ve_i.at(c, "prod", i))
                    w = self.LEFT + 128 * p - p % GD * H - b * HK
                    nc.tensor.matmul(by_batch(ps[0:n, g % 2, 0:N4])[:, :, t0:T], self.scale[:, w:w + n], prod[:, i % RING, :, t0:T],
                                     start=(i % 16 == 0), stop=(i == last_of(g))).then_inc(pe_i.step("used", i), 1)
                rest = [g for g in range(NG) if g not in BACK.values()]
                for g in rest[:-1]:
                    back(c, g)
                if not last:
                    qk(c + 1, 0)
                    qk(c + 1, 1)
                back(c, rest[-1])
                if not last:
                    qk(c + 1, 2)
                    qk(c + 1, 3)
            turn(0)
            for m in range(2 * KD):
                qk(0, m)
            ten.wait_ge(norm, 10)
            passes(ten, body)
            for u in range(U):
                for n in range(4 * u, 4 * u + 4):
                    weights_turned(NCH - 1, n)
                attend(NCH - 1, u)
                project(NCH - 1, u)


class L0Cross:

    name = "L0_xattn"
    H, E = 16, 64
    I = H * E
    W = 2
    UNIT = 1e-24

    def weights(self, a, d):
        n = self.name + "_"
        self.wq, self.wk, self.wv = (a.load(rows(d[n + "w" + k]), 128, KD, self.I) for k in "qkv")
        self.wo = a.load(rows(d[n + "wo"]), 128, self.I // 128, D)
        self.bo = a.load(every(d[n + "bo"], 1), 1, D)
        self.gain_c, self.shift_c = (a.load(d[n + "ln1_" + k + "_c"], 128, KD) for k in "gb")
        self.gain, self.shift = (a.load(every(d[n + "ln1_" + k], SP_), SP_, D) for k in "gb")
        self.g = a.take(128, KD, self.I)
        self.kv = [a.take(128, self.I) for _ in range(self.W)]

    def build(self, core, run):
        nc, d, ps, H, E, I, W = core.nc, core.dram, core.ps, self.H, self.E, self.I, self.W
        sb, g = run.sbuf, self.g
        C, HP, G = NB // W, H // 2, W * ST
        N = W + G
        ctx, cn = sb("ctx", [SP_, G, D]), sb("cn", [SP_, G, D])
        cT = sb("cT", [128, W, KD * S])
        h, hT = sb("h", [T, W, D]), sb("hT", [128, W, KD * T])
        unit = sb("unit", [SP_, N, I])
        sq = sb("sq", [SP_, I])
        ss, rn = sb("ss", [SP_, N, H]), sb("rn", [SP_, N, H])
        qT = sb("qT", [128, W, HP * T])
        kv = self.kv
        norm, zeroed = core.semaphore("norm"), core.semaphore("zeroed")
        loaded = [core.semaphore(f"ctx{u}") for u in range(W)]
        lnc, lnx = Norm(core, run, "lnc", rows_=SP_, units=G), Norm(core, run, "lnx", units=W)
        pe = Progress(core, "tensor", ("cT0", KD), ("hT", W), ("cT1", KD), ("wide", N), ("qT", W * 2), ("g0", KD), ("g1a", 1), ("kv0", 1),
                      ("g1b", 1), ("oT0", 2), ("kv1", 1), ("out0", 1), ("oT1", 2), ("out1", 1))
        ac = Progress(core, "scalar", ("cT0", KD), ("hT", W), ("cT1", KD), ("sq", N), ("qT", W * 2), ("g0", KD), ("g1a", 1), ("kv0", 1),
                      ("g1b", 1), ("oT0", 2), ("kv1", 1), ("oT1", 2))
        ve = Progress(core, "vector", ("xn", W), *lnx.steps(), *lnc.steps(), ("h", W), ("gain0", ST), ("cn0", ST), ("gain1", ST), ("cn1", ST))
        ve_s, ve_m = Progress(core, "vector_sum", ("sum", N), ), Progress(core, "vector_unit", ("unit", N))
        ve_c, ve_y = Progress(core, "vector_least", ("least", N)), Progress(core, "vector_y", ("y", W))
        po, po_r = Progress(core, "pool", ("lnxrs", 1), ("lncrs", 1)), Progress(core, "pool_root", ("root", N))
        block = run.block
        height = lambda i: T if i < W else SP_
        bank = lambda i: 2 * ((i + 2) % 4)
        wide = lambda i: ps[0:height(i), bank(i):bank(i) + 2, :].rearrange("p a b -> p (a b)")
        by_head = lambda t: t.rearrange("p (h e) -> p h e", h=H)

        @block.sync
        def _(sp):
            def load(n, u):
                sp.dma_start(ctx[:, u * ST:(u + 1) * ST, :], d["ctx"][n].rearrange("(s p) c -> p s c", p=SP_)).then_inc(loaded[u], DMA)
            for u in range(W):
                load(u, u)
            with sp.Fori(1, C) as c:
                for u in range(W):
                    sp.wait_ge(ve.sem, ve.at(c - 1, f"gain{u}", ST - 1))
                    core.stand(sp)
                    load(W * c + u, u)

        @block.gpsimd
        def _(pool):
            norm_pool(core, norm)
            for u in range(W):
                nc.gpsimd.memset(kv[u][:, :], 0.0).then_inc(zeroed, 1)
            def norm_roots(c):
                lnx.pool(pool, ve, po, c)
                lnc.pool(pool, ve, po, c)

            def unit_roots(c):
                for i in range(N):
                    pool.wait_ge(ve_c.sem, ve_c.at(c, "least", i))
                    r = height(i)
                    nc.gpsimd.tensor_tensor(rn[0:r, i], ss[0:r, i], core.mhalf[0:r, 0:H], ALU.pow).then_inc(po_r.step("root", i), 1)
            norm_roots(0)
            with pool.Fori(0, C - 1) as c:
                unit_roots(c)
                norm_roots(c + 1)
            unit_roots(C - 1)

        @block.vector
        def _(dve):
            norm_vector(core, dve, norm)
            dve.wait_ge(run.arrived, run.loads)

            def norms(c, first):
                for u in range(W):
                    normed(core, core.y[:, W * c + u, :], W * c + u).then_inc(ve.step("xn", u), 1)

                def made(u):
                    dve.wait_ge(ve.sem, ve.at(c, "xn", u))
                    core.stand(dve)
                lnx.vector(dve, ve, c, lambda u, q: core.y[:, W * c + u, :], made)
                lnc.vector(dve, ve, c, lambda t, q: ctx[:, t, :], lambda t: dve.wait_ge(loaded[t // ST], (c + 1) * DMA))
                dve.wait_ge(po.sem, po.at(c, "lnxrs"))
                core.stand(dve)
                for u in range(W):
                    lnx.apply(h[:, u], core.y[:, W * c + u, :], u).then_inc(ve.step("h", u), 1)
                dve.wait_ge(po.sem, po.at(c, "lncrs"))
                core.stand(dve)
                if not first:
                    dve.wait_ge(pe.sem, pe.at(c - 1, "g1b"))
                    core.stand(dve)
                for u in range(W):
                    for t in range(ST * u, ST * u + ST):
                        nc.vector.scalar_tensor_tensor(out=cn[:, t, :], in0=ctx[:, t, :], scalar=lnc.mv[:, t, 0:1], in1=self.gain,
                                                       op0=ALU.subtract, op1=ALU.mult).then_inc(ve.step(f"gain{u}", t % ST), 1)
                    for t in range(ST * u, ST * u + ST):
                        dve.wait_ge(ve.sem, ve.at(c, f"gain{u}", t % ST))
                        nc.vector.scalar_tensor_tensor(out=cn[:, t, :], in0=cn[:, t, :], scalar=lnc.rs[:, t:t + 1], in1=self.shift,
                                                       op0=ALU.mult, op1=ALU.add).then_inc(ve.step(f"cn{u}", t % ST), 1)

            def unit_lengths(c):
                def scale(i):
                    r = height(i)
                    dve.wait_ge(po_r.sem, po_r.at(c, "root", i))
                    nc.vector.tensor_tensor(by_head(unit[0:r, i]), by_head(wide(i)),
                                                      rn[0:r, i].unsqueeze(2).to_broadcast([r, H, E]), ALU.mult).then_inc(ve_m.step("unit", i), 1)
                for i in range(N):
                    r = height(i)
                    dve.wait_ge(ac.sem, ac.at(c, "sq", i))
                    nc.vector.tensor_reduce(ss[0:r, i], by_head(sq[0:r, :]), AX.X, ALU.add).then_inc(ve_s.step("sum", i), 1)
                    dve.wait_ge(ve_s.sem, ve_s.at(c, "sum", i))
                    nc.vector.tensor_scalar(ss[0:r, i], ss[0:r, i], self.UNIT, None, ALU.max).then_inc(ve_c.step("least", i), 1)
                    if i >= 2:
                        scale(i - 2)
                scale(N - 2)
                scale(N - 1)

            def outputs(c):
                for u in range(W):
                    dve.wait_ge(pe.sem, pe.at(c, f"out{u}"))
                    core.stand(dve)
                    y = core.y[:, W * c + u, :]
                    nc.vector.tensor_tensor(y, y, ps[0:T, 6 + u, 0:D], ALU.add).then_inc(ve_y.step("y", u), 1)
            norms(0, True)
            with dve.Fori(0, C - 1) as c:
                unit_lengths(c)
                norms(c + 1, False)
                outputs(c)
            unit_lengths(C - 1)
            outputs(C - 1)

        @block.scalar
        def _(act):
            run.prefetch(act)
            act.wait_ge(run.arrived, run.loads)
            act.wait_ge(zeroed, W)
            with act.Fori(0, C) as c:
                def keep_context(u):
                    for k in range(KD):
                        act.wait_ge(pe.sem, pe.at(c, f"cT{u}", k))
                        nc.scalar.copy(cT[:, u, k * S:(k + 1) * S], ps[:, 4 + KD * u + k, 0:S]).then_inc(ac.step(f"cT{u}", k), 1)
                keep_context(0)
                for u in range(W):
                    act.wait_ge(pe.sem, pe.at(c, "hT", u))
                    for k in range(KD):
                        w = slice(k * T, (k + 1) * T)
                        ins = nc.scalar.activation(hT[:, u, w], ps[:, u, w], ACT.Identity, bias=self.shift_c[:, k:k + 1],
                                                   scale=self.gain_c[:, k:k + 1])
                    ins.then_inc(ac.step("hT", u), 1)
                keep_context(1)
                for i in range(N):
                    if i >= 1:
                        act.wait_ge(ve_s.sem, ve_s.at(c, "sum", i - 1))
                    act.wait_ge(pe.sem, pe.at(c, "wide", i))
                    nc.scalar.activation(sq[0:height(i), :], wide(i), ACT.Square).then_inc(ac.step("sq", i), 1)
                for u in range(W):
                    for b in range(2):
                        act.wait_ge(pe.sem, pe.at(c, "qT", 2 * u + b))
                        w = HP // 2 * T
                        nc.scalar.copy(qT[:, u, b * w:(b + 1) * w], ps[:, 4 + 2 * u + b, 0:w]).then_inc(ac.step("qT", 2 * u + b), 1)

                def keep_g(step, m, at=0):
                    act.wait_ge(pe.sem, pe.at(c, step, at))
                    nc.scalar.copy(g[:, m, :], ps[:, 4 + 2 * m:6 + 2 * m, :].rearrange("p a b -> p (a b)")).then_inc(ac.step(step, at), 1)

                def keep_kv(u):
                    act.wait_ge(pe.sem, pe.at(c, f"kv{u}"))
                    for j in range(2):
                        r = slice(j * E, (j + 1) * E)
                        ins = nc.scalar.copy(kv[u][r, :].rearrange("p (h e) -> p h e", h=HP)[:, :, j * E:(j + 1) * E],
                                             ps[r, u, :].rearrange("p (h e) -> p h e", h=HP))
                    ins.then_inc(ac.step(f"kv{u}"), 1)

                def keep_o(u):
                    for b in range(2):
                        act.wait_ge(pe.sem, pe.at(c, f"oT{u}", b))
                        w = HP // 2 * T
                        nc.scalar.copy(qT[:, u, b * w:(b + 1) * w], ps[:, 2 + 2 * u + b, 0:w]).then_inc(ac.step(f"oT{u}", b), 1)
                keep_g("g0", 0, 0)
                keep_g("g0", 1, 1)
                act.wait_ge(pe.sem, pe.at(c, "kv0"))
                keep_g("g1a", 0)
                keep_kv(0)
                keep_g("g1b", 1)
                keep_o(0)
                keep_kv(1)
                keep_o(1)

        @block.tensor
        def _(ten):
            ten.wait_ge(run.arrived, run.loads)

            def attend(c, first):
                def turn_context(u):
                    for k in range(KD):
                        for s in range(ST):
                            ten.wait_ge(ve.sem, ve.at(c, f"cn{u}", s))
                            ins = nc.tensor.transpose(ps[:, 4 + KD * u + k, s * SP_:(s + 1) * SP_], cn[:, ST * u + s, k * 128:(k + 1) * 128],
                                                      core.ident[0:SP_, 0:SP_])
                        ins.then_inc(pe.step(f"cT{u}", k), 1)
                turn_context(0)
                for u in range(W):
                    ten.wait_ge(ve.sem, ve.at(c, "h", u))
                    transposes(core, ps[:, u], h[:, u], T, KD).then_inc(pe.step("hT", u), 1)
                if not first:
                    ten.wait_ge(ve_y.sem, ve_y.at(c - 1, "y", W - 1))
                    core.stand(ten)
                turn_context(1)
                for i in range(N):
                    if i >= 4:
                        ten.wait_ge(ve_m.sem, ve_m.at(c, "unit", i - 4))
                    for b in range(2):
                        for k in range(KD):
                            cols = slice(b * 512, (b + 1) * 512)
                            if i < W:
                                if b == 0 and k == 0:
                                    ten.wait_ge(ac.sem, ac.at(c, "cT1", KD - 1) if i else ac.at(c, "hT"))
                                lhs, w = hT[:, i, k * T:(k + 1) * T], self.wq
                            else:
                                t = i - W
                                lhs, w = cT[:, t // ST, k * S + (t % ST) * SP_:k * S + (t % ST + 1) * SP_], self.wk
                            ins = nc.tensor.matmul(ps[0:height(i), bank(i) + b, :], lhs, w[:, k, cols], start=(k == 0), stop=(k == KD - 1))
                    ins.then_inc(pe.step("wide", i), 1)
                for u in range(W):
                    ten.wait_ge(ve_m.sem, ve_m.at(c, "unit", N - 4 + u))
                    for b in range(2):
                        for j in range(HP // 2):
                            k = HP // 2 * b + j
                            ins = nc.tensor.transpose(ps[:, 4 + 2 * u + b, j * T:(j + 1) * T], unit[0:T, u, k * 128:(k + 1) * 128],
                                                      core.ident[0:T, 0:T])
                        ins.then_inc(pe.step("qT", 2 * u + b), 1)

                def make_g(u, m):
                    for b in range(2):
                        for s in range(ST):
                            t = ST * u + s
                            ins = nc.tensor.matmul(ps[:, 4 + 2 * m + b, :], cn[:, t, m * 128:(m + 1) * 128], unit[:, W + t, b * 512:(b + 1) * 512],
                                                   start=(s == 0), stop=(s == ST - 1))
                    return ins

                def make_kv(u):
                    for j in range(H):
                        e = slice(j * E, (j + 1) * E)
                        for k in range(KD):
                            ins = nc.tensor.matmul(ps[j % 2 * E:(j % 2 + 1) * E, u, j // 2 * E:(j // 2 + 1) * E], g[:, k, e], self.wv[:, k, e],
                                                   start=(k == 0), stop=(k == KD - 1))
                    return ins

                def make_o(u):
                    ten.wait_ge(ac.sem, ac.at(c, f"kv{u}"))
                    for b in range(2):
                        for j in range(HP // 2):
                            k = HP // 2 * b + j
                            ins = nc.tensor.matmul(ps[:, 2 + 2 * u + b, j * T:(j + 1) * T], kv[u][:, k * 128:(k + 1) * 128],
                                                   qT[:, u, k * T:(k + 1) * T], start=True, stop=True)
                        ins.then_inc(pe.step(f"oT{u}", b), 1)

                def project(u):
                    ten.wait_ge(ac.sem, ac.at(c, f"oT{u}", 1))
                    for k in range(HP):
                        nc.tensor.matmul(ps[0:T, 6 + u, 0:D], qT[:, u, k * T:(k + 1) * T], self.wo[:, k, :], start=(k == 0), stop=False)
                    nc.tensor.matmul(ps[0:T, 6 + u, 0:D], core.ones[0:1, 0:T], self.bo, start=False, stop=True).then_inc(pe.step(f"out{u}"), 1)
                for m in range(KD):
                    ten.wait_ge(ac.sem, ac.at(c, "qT", 2 * m + 1))
                    make_g(0, m).then_inc(pe.step("g0", m), 1)
                ten.wait_ge(ve_m.sem, ve_m.at(c, "unit", N - 1))
                ten.wait_ge(ac.sem, ac.at(c, "g0", 0))
                make_g(1, 0).then_inc(pe.step("g1a"), 1)
                ten.wait_ge(ac.sem, ac.at(c, "g0", 1))
                make_kv(0).then_inc(pe.step("kv0"), 1)
                make_g(1, 1).then_inc(pe.step("g1b"), 1)
                make_o(0)
                ten.wait_ge(ac.sem, ac.at(c, "g1b"))
                make_kv(1).then_inc(pe.step("kv1"), 1)
                project(0)
                make_o(1)
                project(1)

            attend(0, True)
            with ten.Fori(1, C) as c:
                attend(c, False)


class Picked:

    def __init__(self, core, run, name, lanes, by_expert, first_row, work):
        self.core, self.lanes, self.by_expert, self.first_row = core, lanes, by_expert, first_row
        K, G = L0Kron.K, L0Kron.G
        self.P, self.C = P, C = G // NCH, 2 * NCH
        sb = lambda n, shape, dt=F32: run.sbuf(name + n, shape, dt)
        self.top, self.which = sb("top", [P, C, 8]), sb("which", [P, C, 8], U32)
        self.at, self.s = sb("at", [P, K, C]), sb("s", [P, K, C])
        self.e2, self.den = sb("e2", [P, C]), sb("den", [P, C])
        self.sheets = 1 if by_expert else K
        self.wide = work
        self.index = sb("index", [128, self.sheets, G], U32)
        self.weight = sb("weight", [128, G, self.sheets])
        self.ve = Progress(core, "vector_" + name, ("top", C), ("which", C), ("at", 1), ("gap", 1), ("den", 1), ("s1", 1), ("s2", 1),
                           ("wide", 2 * K), ("index", self.sheets), ("weight", 1))
        self.ac = Progress(core, "scalar_" + name, ("e2", 1))
        self.pe = Progress(core, "tensor_" + name, ("index", 1), ("weight", 1))

    def vector(self, dve, lg):
        nc, ps, ve, K, P, C = self.core.nc, self.core.ps, self.ve, L0Kron.K, self.P, self.C
        for n in range(C):
            nc.vector.max(self.top[:, n, :], lg[:, n, :]).then_inc(ve.step("top", n), 1)
        for n in range(C):
            dve.wait_ge(ve.sem, ve.at(0, "top", n))
            nc.vector.max_index(self.which[:, n, :], self.top[:, n, :], lg[:, n, :]).then_inc(ve.step("which", n), 1)
        dve.wait_ge(ve.sem, ve.at(0, "which", C - 1))
        nc.vector.tensor_copy(self.at[:, :, :].rearrange("p k n -> p n k"), self.which[:, :, 0:K]).then_inc(ve.step("at"), 1)
        nc.vector.tensor_tensor(self.e2[:, :], self.top[:, :, 1], self.top[:, :, 0], ALU.subtract).then_inc(ve.step("gap"), 1)
        dve.wait_ge(self.ac.sem, self.ac.at(0, "e2"))
        nc.vector.tensor_scalar(self.den[:, :], self.e2[:, :], 1.0, None, ALU.add).then_inc(ve.step("den"), 1)
        dve.wait_ge(ve.sem, ve.at(0, "den"))
        nc.vector.reciprocal(self.s[:, 0, :], self.den[:, :]).then_inc(ve.step("s1"), 1)
        dve.wait_ge(ve.sem, ve.at(0, "s1"))
        nc.vector.tensor_tensor(self.s[:, 1, :], self.s[:, 0, :], self.e2[:, :], ALU.mult).then_inc(ve.step("s2"), 1)
        dve.wait_ge(ve.sem, ve.at(0, "s2"))
        L, G = self.lanes, L0Kron.G
        for i, v in enumerate((self.at, self.s)):
            for k in range(K):
                if self.by_expert:
                    out = self.wide[i].rearrange("p (c r k l) -> p c r k l", r=2, k=K, l=L)[:, :, :, k, :]
                else:
                    out = self.wide[i].rearrange("p (c k r l) -> p c k r l", r=2, k=K, l=L)[:, :, k, :, :]
                nc.vector.tensor_copy(out, v[:, k, :].rearrange("p (c r) -> p c r", r=2).unsqueeze(3).to_broadcast([P, NCH, 2, L])).then_inc(ve.step("wide", K * i + k), 1)
        dve.wait_ge(self.pe.sem, self.pe.at(0, "index"))
        for t in range(self.sheets):
            nc.vector.tensor_scalar(self.index[:, t, :], ps[:, 0, t * G:(t + 1) * G], float(L), self.first_row, ALU.mult, ALU.add).then_inc(ve.step("index", t), 1)
        dve.wait_ge(self.pe.sem, self.pe.at(0, "weight"))
        nc.vector.tensor_copy(self.weight[:, :, :].rearrange("p g t -> p t g"),
                                      ps[:, 1, 0:self.sheets * G].rearrange("p (t g) -> p t g", t=self.sheets)).then_inc(ve.step("weight"), 1)

    def scalar(self, act):
        act.wait_ge(self.ve.sem, self.ve.at(0, "gap"))
        self.core.nc.scalar.activation(self.e2[:, :], self.e2[:, :], ACT.Exp).then_inc(self.ac.step("e2"), 1)

    def tensor(self, ten):
        nc, ps, G, P = self.core.nc, self.core.ps, L0Kron.G, self.P
        ten.wait_ge(self.ve.sem, self.ve.at(0, "wide", 2 * L0Kron.K - 1))
        for i, step in enumerate(("index", "weight")):
            for t in range(self.sheets):
                for c in range(NCH):
                    col = (c * self.sheets + t) * 128
                    ins = nc.tensor.transpose(ps[:, i, t * G + c * P:t * G + (c + 1) * P], self.wide[i][:, col:col + 128], self.core.ident[0:P, 0:P])
            ins.then_inc(self.pe.step(step), 1)


class L0Kron:

    name = "L0_ffn"
    E, K = 64, 2
    R = NB * T // 4
    G = R // 2
    I, F = 32, 64
    B = 8
    PASSES = G // (2 * B)
    BY_SP, BY_ACT = {"up": (6,), "dn": (2, 3, 4)}, {"up": (7,), "dn": (5, 6, 7)}

    def weights(self, a, d):
        n, E, I, F, B = self.name + "_", self.E, self.I, self.F, self.B
        self.wup = a.load(rows(d[n + "W_upT"]), 128, 8, E)
        wide = a.take(128, F * 2 * E)
        self.wdn = wide.rearrange("p (f e) -> p f e", f=F)
        self.bias_up, self.bias_dn = a.take(128, F), a.take(128, I)
        for r in range(2):
            half = slice(r * F, (r + 1) * F)
            a.loads.append((self.wdn[half, :, r * E:(r + 1) * E], d[n + "W_downP"]))
            a.loads.append((self.bias_up[half], d[n + "bias_up"].rearrange("(o p) -> o p", o=F)))
            a.loads.append((self.bias_dn[r * F:r * F + I], d[n + "bias_down"].rearrange("(o p) -> o p", o=I)))
        self.scale_up, self.scale_dn = (a.load(every(d[n + "scale_" + k], 128), 128, 1) for k in ("up", "down"))
        self.row32, self.row64 = a.load(d["row32"], 128, 1), a.load(d["row64"], 128, 1)
        self.xs = a.take(128, 2, B * I)
        self.ab = a.take(128, 2, B * 2 * F)
        self.u = a.take(128, 2, B * F)
        self.pre = a.take(128, 2, B * F)
        self.out = wide[:, 0:2 * B * I].rearrange("p (b n) -> p b n", b=2)

    def build(self, core, run):
        nc, d, ps, sb = core.nc, core.dram, core.ps, run.sbuf
        G, E, K, I, F, B, PASSES, R = self.G, self.E, self.K, self.I, self.F, self.B, self.PASSES, self.R
        x_rows, y_rows = core.scratch("x_rows", [R, 4 * D]), core.scratch("y_rows", [R, 4 * D])
        h = sb("h", [128, G, F])
        flat = h[:, :, :].rearrange("p g f -> p (g f)")
        P = G // NCH
        lg = sb("lg", [P, 2 * NCH, E])
        lgT = sb("lgT", [128, G])
        now = sb("now", [128, K, 2, B], U32)
        xn = flat[0:T, 0:U * D].rearrange("p (u d) -> p u d", u=U)
        xT = flat[:, U * D:U * D + KD * N4].rearrange("p (k n) -> p k n", k=KD)
        at = U * D + KD * N4
        up = Picked(core, run, "up", I, True, self.row32, [flat[0:P, at + i * NCH * 128:at + (i + 1) * NCH * 128] for i in range(2)])
        ab = self.ab.rearrange("p b n -> p (b n)")
        dn = Picked(core, run, "dn", F, False, self.row64, [ab[0:P, i * 2 * NCH * 128:(i + 1) * 2 * NCH * 128] for i in range(2)])
        norm, zeroed, rows_out = (core.semaphore(n) for n in ("norm", "zeroed", "rows_out"))
        back = [core.semaphore(f"back{c}") for c in range(NCH)]
        rows_in = core.semaphore("rows_in")
        table_up = [core.pool_dma_semaphore(f"table_up{b}") for b in range(2)]
        table_dn = [core.pool_dma_semaphore(f"table_dn{b}") for b in range(2)]
        by_pool = lambda part: [g for g in range(B) if g not in self.BY_SP[part] + self.BY_ACT[part]]
        others = lambda part: len(self.BY_SP[part] + self.BY_ACT[part])
        taken_up = [core.semaphore(f"taken_up{b}") for b in range(2)]
        taken_dn = [core.semaphore(f"taken_dn{b}") for b in range(2)]
        stored = [core.semaphore(f"stored{b}") for b in range(2)]
        ve = Progress(core, "vector", "xn", "kept")
        pe, ac = Progress(core, "tensor", ("xT", KD), ("lg", 1)), Progress(core, "scalar", ("xT", KD), ("lg", 1))
        by_block = lambda *names: (Progress(core, n, ("block", 2)) for n in names)
        po_up, pe_u, ve_u, pe_y, ve_y, ac_y = by_block("pool_up", "tensor_u", "vector_u", "tensor_y", "vector_y", "scalar_gelu")
        po_dn, ac_h, pe_v, ve_v, pe_z, ve_z = by_block("pool_dn", "scalar_h", "tensor_v", "vector_v", "tensor_z", "vector_z")
        pe_r, ac_r = Progress(core, "tensor_route", ("sums", 1), ("lg", 1)), Progress(core, "scalar_route", ("sums", 1))
        ve_r, ve_e = Progress(core, "vector_route", ("lg", 1)), Progress(core, "vector_end", "out", "stats")
        block = run.block
        by_group = lambda t: t.rearrange("p (g n) -> p g n", g=B)
        groups = lambda j, b: bass.ds(2 * B * j + B * b, B)

        def take_up(eng, j, b, mine):
            core.stand(eng)
            for g in mine:
                for p in range(0, 128, I):
                    at = eng.value_load(up.index[p:p + 1, 0, bass.ds(2 * B * j + B * b + g, 1)], min_val=0, max_val=(E - 1) * I)
                    eng.dma_start(self.ab[p:p + I, b, g * 2 * F:(g + 1) * 2 * F], d["L0_ffn_up"][bass.ds(at, I), :]).then_inc(taken_up[b], DMA)

        def take_dn(eng, j, b, mine):
            core.stand(eng)
            for g in mine:
                for p in range(0, 128, F):
                    at = eng.value_load(dn.index[p:p + 1, 1, bass.ds(2 * B * j + B * b + g, 1)], min_val=0, max_val=(E - 1) * F)
                    eng.dma_start(self.ab[p:p + F, b, (g * K + 1) * F:(g * K + 2) * F], d["L0_ffn_down"][bass.ds(at, F), :]).then_inc(taken_dn[b], DMA)

        def passes(eng, body):
            body(0, True)
            with eng.Fori(1, PASSES) as j:
                body(j, False)

        @block.sync
        def _(sp):
            sp.wait_ge(ve.sem, ve.at(NCH - 1, "kept", U - 1))
            sp.dma_start(x_rows.rearrange("n (q c) -> (n q) c", q=4).rearrange("(b t) c -> t b c", t=T), core.y[:, :, :]).then_inc(rows_out, DMA)
            sp.wait_ge(rows_out, DMA)

            def upward(j, first):
                src = x_rows.rearrange("(g r) (i n) -> r i g n", r=2, n=I)
                if not first:
                    sp.wait_ge(pe_y.sem, pe_y.at(j - 1, "block", 0))
                    take_up(sp, j, 0, self.BY_SP["up"])
                    sp.wait_ge(pe_u.sem, pe_u.at(j - 1, "block", 1))
                    core.stand(sp)
                for r in range(2):
                    for k in range(K):
                        p = slice((r * K + k) * I, (r * K + k + 1) * I)
                        sp.dma_start(self.xs[p, :, :].rearrange("p b (g n) -> p (b g) n", n=I), src[r][:, bass.ds(2 * B * j, 2 * B), :]).then_inc(rows_in, DMA)
                if first:
                    sp.wait_ge(up.ve.sem, up.ve.at(0, "weight"))
                    take_up(sp, j, 0, self.BY_SP["up"])
                else:
                    sp.wait_ge(pe_y.sem, pe_y.at(j - 1, "block", 1))
                take_up(sp, j, 1, self.BY_SP["up"])
            passes(sp, upward)
            sp.wait_ge(dn.ve.sem, dn.ve.at(0, "weight"))

            def store(j, b):
                dst = y_rows.rearrange("(g r) (o n) -> r o g n", r=2, n=I)
                sp.wait_ge(ve_z.sem, ve_z.at(j, "block", b))
                core.stand(sp)
                for r in range(2):
                    sp.dma_start(dst[r][:, groups(j, b), :], by_group(self.out[r * F:r * F + I, b])).then_inc(stored[b], DMA)

            def downward(j, first):
                for b in range(2):
                    if not first:
                        sp.wait_ge(pe_z.sem, pe_z.at(j - 1, "block", b))
                    take_dn(sp, j, b, self.BY_SP["dn"])
                    if not first:
                        store(j - 1, b)
            passes(sp, downward)
            for b in range(2):
                store(PASSES - 1, b)
            for b in range(2):
                sp.wait_ge(stored[b], 2 * DMA * PASSES)
            by_batch = y_rows.rearrange("n (q c) -> (n q) c", q=4).rearrange("(b t) c -> t b c", t=T)
            for c in range(NCH):
                sp.dma_start(core.y[:, U * c:U * c + U, :], by_batch[:, U * c:U * c + U, :]).then_inc(back[c], DMA)

        @block.gpsimd
        def _(pool):
            norm_pool(core, norm)
            pool.wait_ge(norm, 8)
            for r in range(2):
                nc.gpsimd.memset(self.wdn[r * F:(r + 1) * F, :, (1 - r) * E:(2 - r) * E], 0.0).then_inc(zeroed, 1)
            pool.wait_ge(zeroed, 2)
            pool.wait_ge(up.ve.sem, up.ve.at(0, "weight"))

            def fetch(picked, copied, used, source, dst, arrived):
                def body(j, first):
                    for b in range(2):
                        if not first:
                            pool.wait_ge(used.sem, used.at(j - 1, "block", b))
                            core.stand(pool)
                        nc.gpsimd.tensor_copy(now[:, 0:picked.sheets, b, :], picked.index[:, :, groups(j, b)]).then_inc(copied.step("block", b), 1)
                        pool.wait_ge(copied.sem, copied.at(j, "block", b))
                        core.stand(pool)
                        for t, g, place in dst(b):
                            at = bass.IndirectOffsetOnAxis(ap=now[:, t, b, g:g + 1], axis=0)
                            nc.gpsimd.indirect_dma_start(out=place, out_offset=None, in_=source[:, :], in_offset=at).then_inc(arrived[b], DMA)
                passes(pool, body)
            fetch(up, po_up, pe_y, d["L0_ffn_up"], lambda b: [(0, g, self.ab[:, b, g * 2 * F:(g + 1) * 2 * F]) for g in by_pool("up")], table_up)
            pool.wait_ge(dn.ve.sem, dn.ve.at(0, "weight"))
            fetch(dn, po_dn, pe_z, d["L0_ffn_down"], lambda b: [(k, g, self.ab[:, b, (g * K + k) * F:(g * K + k + 1) * F])
                                                                for k in range(K) for g in (by_pool("dn") if k else range(B))], table_dn)

        @block.vector
        def _(dve):
            norm_vector(core, dve, norm)
            dve.wait_ge(run.arrived, run.loads)
            with dve.Fori(0, NCH) as c:
                for u in range(U):
                    normed(core, xn[:, u], U * c + u).then_inc(ve.step("xn", u), 1)
                for u in range(U):
                    normed(core, core.y[:, U * c + u, :], U * c + u).then_inc(ve.step("kept", u), 1)
                dve.wait_ge(pe.sem, pe.at(c, "xT", KD - 1))
                core.stand(dve)
            dve.wait_ge(ac.sem, ac.at(NCH - 1, "lg"))
            up.vector(dve, lg)
            dve.wait_ge(up.ve.sem, up.ve.at(0, "weight"))

            def weighted(j, b, made, used, picked, inner):
                dve.wait_ge(used.sem, used.at(j, "block", b))
                n = B * picked.sheets
                view = lambda t: t.rearrange("p (g n) -> p g n", g=n)
                w = picked.weight[:, groups(j, b), :].rearrange("p g t -> p (g t)").unsqueeze(2).to_broadcast([128, n, inner])
                nc.vector.tensor_tensor(view(self.u[:, b]), view(ps[:, b, 0:B * F]), w, ALU.mult).then_inc(made.step("block", b), 1)

            def upward(j, first):
                for b in range(2):
                    weighted(j, b, ve_u, pe_u, up, F)
                    if not first:
                        dve.wait_ge(ac_y.sem, ac_y.at(j - 1, "block", b))
                    dve.wait_ge(pe_y.sem, pe_y.at(j, "block", b))
                    nc.vector.scalar_tensor_tensor(out=by_group(self.pre[:, b]), in0=by_group(ps[:, 2 + b, 0:B * F]), scalar=self.scale_up,
                                                             in1=self.bias_up.unsqueeze(1).to_broadcast([128, B, F]), op0=ALU.mult, op1=ALU.add).then_inc(ve_y.step("block", b), 1)
            passes(dve, upward)
            dve.wait_ge(pe_r.sem, pe_r.at(0, "lg"))
            nc.vector.tensor_copy(lg[:, :, :].rearrange("p c e -> p (c e)"), ps[0:P, 4, :]).then_inc(ve_r.step("lg"), 1)
            dve.wait_ge(ve_r.sem, ve_r.at(0, "lg"))
            dn.vector(dve, lg)
            dve.wait_ge(dn.ve.sem, dn.ve.at(0, "weight"))
            def downward(j, first):
                for b in range(2):
                    weighted(j, b, ve_v, pe_v, dn, I)
                    if not first:
                        dve.wait_ge(stored[b], j * 2 * DMA)
                    dve.wait_ge(pe_z.sem, pe_z.at(j, "block", b))
                    for r in range(2):
                        p = slice(r * F, r * F + I)
                        ins = nc.vector.scalar_tensor_tensor(out=by_group(self.out[p, b]), in0=by_group(ps[p, 2 + b, 0:B * I]), scalar=self.scale_dn[p],
                                                             in1=self.bias_dn[p].unsqueeze(1).to_broadcast([I, B, I]), op0=ALU.mult, op1=ALU.add)
                    ins.then_inc(ve_z.step("block", b), 1)
            passes(dve, downward)
            for c in range(NCH):
                dve.wait_ge(back[c], DMA)
                for u in range(U):
                    x = core.x[:, U * c + u, :]
                    nc.vector.tensor_tensor(x, x, core.y[:, U * c + u, :], ALU.add).then_inc(ve_e.step("out", u), 1)
                for u in range(U):
                    dve.wait_ge(ve_e.sem, ve_e.at(c, "out", u))
                    row_stats(core, dve, U * c + u).then_inc(ve_e.step("stats", u), 1)

        @block.scalar
        def _(act):
            run.prefetch(act)
            with act.Fori(0, NCH) as c:
                for k in range(KD):
                    act.wait_ge(pe.sem, pe.at(c, "xT", k))
                    nc.scalar.copy(xT[:, k], ps[:, k, 0:N4]).then_inc(ac.step("xT", k), 1)
                act.wait_ge(pe.sem, pe.at(c, "lg"))
                nc.scalar.copy(lg[:, bass.ds(2 * c, 2), :].rearrange("p c e -> p (c e)"), ps[0:P, 2, 0:2 * E]).then_inc(ac.step("lg"), 1)
            up.scalar(act)
            act.wait_ge(up.ve.sem, up.ve.at(0, "weight"))
            def gelu(j, b):
                act.wait_ge(ve_y.sem, ve_y.at(j, "block", b))
                nc.scalar.activation(h[:, groups(j, b), :].rearrange("p g f -> p (g f)"), self.pre[:, b], ACT.Gelu).then_inc(ac_y.step("block", b), 1)

            def upward(j, first):
                for b in range(2):
                    if not first:
                        act.wait_ge(pe_y.sem, pe_y.at(j - 1, "block", b))
                    take_up(act, j, b, self.BY_ACT["up"])
                    if not first:
                        gelu(j - 1, b)
            passes(act, upward)
            for b in range(2):
                gelu(PASSES - 1, b)
            act.wait_ge(pe_r.sem, pe_r.at(0, "sums"))
            nc.scalar.copy(lgT[:, :], ps[:, 6, 0:G]).then_inc(ac_r.step("sums"), 1)
            dn.scalar(act)

            act.wait_ge(dn.ve.sem, dn.ve.at(0, "weight"))

            def downward(j, first):
                for b in range(2):
                    if not first:
                        act.wait_ge(pe_v.sem, pe_v.at(j - 1, "block", b))
                    nc.scalar.copy(self.pre[:, b], h[:, groups(j, b), :].rearrange("p g f -> p (g f)")).then_inc(ac_h.step("block", b), 1)
                    if not first:
                        act.wait_ge(pe_z.sem, pe_z.at(j - 1, "block", b))
                    take_dn(act, j, b, self.BY_ACT["dn"])
            passes(act, downward)

        @block.tensor
        def _(ten):
            ten.wait_ge(run.arrived, run.loads)
            with ten.Fori(0, NCH) as c:
                for k in range(KD):
                    for u in range(U):
                        if k == 0:
                            ten.wait_ge(ve.sem, ve.at(c, "xn", u))
                        ins = nc.tensor.transpose(ps[:, k, u * T:(u + 1) * T], xn[:, u, k * 128:(k + 1) * 128], core.ident[0:T, 0:T])
                    ins.then_inc(pe.step("xT", k), 1)
                ten.wait_ge(ac.sem, ac.at(c, "xT", KD - 1))
                for r in range(2):
                    for q in range(4):
                        for k in range(KD):
                            ins = nc.tensor.matmul(ps[0:P, 2, r * E:(r + 1) * E], xT[:, k, 4 * r + q:N4:8], self.wup[:, KD * q + k, :],
                                                   start=(q == 0 and k == 0), stop=(q == 3 and k == KD - 1))
                ins.then_inc(pe.step("lg"), 1)
            up.tensor(ten)
            ten.wait_ge(up.ve.sem, up.ve.at(0, "weight"))
            with ten.Fori(0, PASSES) as j:
                for b in range(2):
                    ten.wait_ge(rows_in, (j + 1) * 2 * K * DMA)
                    ten.wait_ge(table_up[b], (j + 1) * len(by_pool("up")) * DMA)
                    core.stand(ten)
                    ten.wait_ge(taken_up[b], (j + 1) * 2 * K * others("up") * DMA)
                    core.stand(ten)
                    for g in range(B):
                        for r in range(2 * K):
                            p = slice(r * I, (r + 1) * I)
                            ins = nc.tensor.matmul(ps[p, b, g * F:(g + 1) * F], self.xs[p, b, g * I:(g + 1) * I], self.ab[p, b, g * 2 * F:g * 2 * F + F],
                                                   start=True, stop=True)
                    ins.then_inc(pe_u.step("block", b), 1)
                    ten.wait_ge(ve_u.sem, ve_u.at(j, "block", b))
                    core.stand(ten)
                    for g in range(B):
                        for r in range(2):
                            p = slice(r * F, (r + 1) * F)
                            ins = nc.tensor.matmul(ps[p, 2 + b, g * F:(g + 1) * F], self.u[p, b, g * F:(g + 1) * F],
                                                   self.ab[p, b, g * 2 * F + F:(g + 1) * 2 * F], start=True, stop=True)
                    ins.then_inc(pe_y.step("block", b), 1)
            ten.wait_ge(ac_y.sem, ac_y.at(PASSES - 1, "block", 1))
            ten.wait_ge(zeroed, 2)
            for f in range(F):
                ins = nc.tensor.matmul(ps[:, 6, 0:G], self.wdn[:, f, :], h[:, :, f], start=(f == 0), stop=(f == F - 1))
            ins.then_inc(pe_r.step("sums"), 1)
            ten.wait_ge(ac_r.sem, ac_r.at(0, "sums"))
            for c in range(NCH):
                ins = nc.tensor.transpose(ps[0:P, 4, c * 128:(c + 1) * 128], lgT[:, c * P:(c + 1) * P], core.ident[:, :])
            ins.then_inc(pe_r.step("lg"), 1)
            dn.tensor(ten)
            ten.wait_ge(dn.ve.sem, dn.ve.at(0, "weight"))
            with ten.Fori(0, PASSES) as j:
                for b in range(2):
                    ten.wait_ge(ac_h.sem, ac_h.at(j, "block", b))
                    ten.wait_ge(table_dn[b], (j + 1) * (B + len(by_pool("dn"))) * DMA)
                    core.stand(ten)
                    ten.wait_ge(taken_dn[b], (j + 1) * 2 * others("dn") * DMA)
                    core.stand(ten)
                    for g in range(B):
                        for r in range(2):
                            p = slice(r * F, (r + 1) * F)
                            a = self.ab[p, b, g * K * F:(g + 1) * K * F].rearrange("p (k n) -> p k n", k=K)[:, :, 0:I]
                            ins = nc.tensor.matmul(ps[p, b, g * F:(g + 1) * F], self.pre[p, b, g * F:(g + 1) * F], a, start=True, stop=True)
                    ins.then_inc(pe_v.step("block", b), 1)
                    ten.wait_ge(ve_v.sem, ve_v.at(j, "block", b))
                    core.stand(ten)
                    for g in range(B):
                        for r in range(2):
                            p = slice(r * F, (r + 1) * F)
                            for k in range(K):
                                n = (g * K + k) * F
                                ins = nc.tensor.matmul(ps[r * F:r * F + I, 2 + b, g * I:(g + 1) * I], self.u[p, b, (g * K + k) * I:(g * K + k + 1) * I],
                                                       self.ab[p, b, n + I:n + F], start=(k == 0), stop=(k == K - 1))
                    ins.then_inc(pe_z.step("block", b), 1)


class Mlp:

    H = 1024
    HK = H // 128

    def build(self, core, run):
        nc, ps, HK = core.nc, core.ps, self.HK
        sb = run.sbuf
        self.prepare(core, run)
        yn, yT, hT = sb("yn", [T, U, D]), sb("yT", [128, KD, N4]), sb("hT", [128, HK, N4])
        ln = Norm(core, run, "ln")
        pe_t, pe_u, pe_o = Progress(core, "tensor_yT", ("yT", KD)), Progress(core, "tensor_up", ("up", HK)), Progress(core, "tensor_out", "out")
        ac, ac_h = Progress(core, "scalar_yT", ("yT", KD)), Progress(core, "scalar_act", ("act", HK))
        ve_n, ve = Progress(core, "vector_norm", *ln.steps(), "yn"), Progress(core, "vector", "inner", "out", "stats")
        po = Progress(core, "pool", ("lnrs", 1))
        block = run.block

        @block.gpsimd
        def _(pool):
            self.prepare_pool(core, run, pool)
            with pool.Fori(0, NCH) as c:
                ln.pool(pool, ve_n, po, c)

        @block.vector
        def _(dve):
            self.prepare_vector(core, run, dve)

            def norms(c, first):
                ln.vector(dve, ve_n, c, lambda u, q: core.y[:, U * c + u, :], lambda u: None)
                dve.wait_ge(po.sem, po.at(c, "lnrs"))
                core.stand(dve)
                if not first:
                    dve.wait_ge(pe_t.sem, pe_t.at(c - 1, "yT", KD - 1))
                    core.stand(dve)
                for u in range(U):
                    ln.apply(yn[:, u], core.y[:, U * c + u, :], u).then_inc(ve_n.step("yn", u), 1)

            def outputs(c):
                for u in range(U):
                    x = core.x[:, U * c + u, :]
                    nc.vector.tensor_tensor(x, x, core.y[:, U * c + u, :], ALU.add).then_inc(ve.step("inner", u), 1)
                for u in range(U):
                    dve.wait_ge(pe_o.sem, pe_o.at(c, "out", u))
                    core.stand(dve)
                    dve.wait_ge(ve.sem, ve.at(c, "inner", u))
                    x = core.x[:, U * c + u, :]
                    nc.vector.tensor_tensor(x, x, ps[0:T, 4 + u, 0:D], ALU.add).then_inc(ve.step("out", u), 1)
                for u in range(U):
                    dve.wait_ge(ve.sem, ve.at(c, "out", u))
                    row_stats(core, dve, U * c + u).then_inc(ve.step("stats", u), 1)
            norms(0, True)
            self.prepare_vector_late(core, run, dve)
            with dve.Fori(0, NCH - 1) as c:
                norms(c + 1, False)
                outputs(c)
            outputs(NCH - 1)

        @block.scalar
        def _(act):
            self.prepare_scalar(core, run, act)

            def keep_turned(c):
                for k in range(KD):
                    act.wait_ge(pe_t.sem, pe_t.at(c, "yT", k))
                    nc.scalar.activation(yT[:, k], ps[:, k, 0:N4], ACT.Identity, bias=self.shift[:, k:k + 1],
                                                 scale=self.gain[:, k:k + 1]).then_inc(ac.step("yT", k), 1)

            def bend(c, first):
                for i in range(HK):
                    act.wait_ge(pe_u.sem, pe_u.at(c, "up", i))
                    if i == 0 and not first:
                        act.wait_ge(pe_o.sem, pe_o.at(c - 1, "out", U - 1))
                        core.stand(act)
                    nc.scalar.activation(hT[:, i], ps[:, i % 4, 0:N4], self.act, bias=self.b1[:, i:i + 1]).then_inc(ac_h.step("act", i), 1)
            keep_turned(0)
            bend(0, True)
            with act.Fori(1, NCH) as c:
                keep_turned(c)
                bend(c, False)

        @block.tensor
        def _(ten):
            ten.wait_ge(run.arrived, run.loads)
            self.prepare_tensor(core, run, ten)

            def turn(c, first):
                for k in range(KD):
                    if not first:
                        ten.wait_ge(ac_h.sem, ac_h.at(c - 1, "act", 4 + k))
                        core.stand(ten)
                    for u in range(U):
                        if k == 0:
                            ten.wait_ge(ve_n.sem, ve_n.at(c, "yn", u))
                        ins = nc.tensor.transpose(ps[:, k, u * T:(u + 1) * T], yn[:, u, k * 128:(k + 1) * 128],
                                                  core.ident[0:T, 0:T])
                    ins.then_inc(pe_t.step("yT", k), 1)

            def widen(c):
                for i in range(HK):
                    if i >= 4:
                        ten.wait_ge(ac_h.sem, ac_h.at(c, "act", i - 4))
                    for k in range(KD):
                        if i == 0:
                            ten.wait_ge(ac.sem, ac.at(c, "yT", 1 if k else 0))
                        ins = nc.tensor.matmul(ps[:, i % 4, 0:N4], self.w1[:, k, i * 128:(i + 1) * 128], yT[:, k],
                                               start=(k == 0), stop=(k == KD - 1))
                    ins.then_inc(pe_u.step("up", i), 1)

            def narrow(c, first):
                for u in range(U):
                    if not first:
                        ten.wait_ge(ve.sem, ve.at(c - 1, "out", u))
                        core.stand(ten)
                    for i in range(HK):
                        if u == 0:
                            ten.wait_ge(ac_h.sem, ac_h.at(c, "act", i))
                        nc.tensor.matmul(ps[0:T, 4 + u, 0:D], hT[:, i, u * T:(u + 1) * T], self.w2[:, i, :],
                                         start=(i == 0), stop=False)
                    nc.tensor.matmul(ps[0:T, 4 + u, 0:D], core.ones[0:1, 0:T], self.b2, start=False, stop=True).then_inc(pe_o.step("out", u), 1)
            turn(0, True)
            widen(0)
            turn(1, False)
            self.prepare_tensor_late(core, run, ten)
            narrow(0, True)
            with ten.Fori(1, NCH - 1) as c:
                widen(c)
                turn(c + 1, False)
                narrow(c, False)
            widen(NCH - 1)
            narrow(NCH - 1, False)

    def prepare(self, core, run):
        pass

    def prepare_vector(self, core, run, dve):
        pass

    def prepare_pool(self, core, run, pool):
        pass

    def prepare_scalar(self, core, run, act):
        run.prefetch(act)
        act.wait_ge(run.arrived, run.loads)

    def prepare_tensor(self, core, run, ten):
        pass

    def prepare_vector_late(self, core, run, dve):
        pass

    def prepare_tensor_late(self, core, run, ten):
        pass


class L0Mlp(Mlp):
    name = "L0_mlp"
    act = ACT.Gelu

    def weights(self, a, d):
        self.w1 = a.load(rows(d["L0_xattn_w1"]), 128, KD, self.H)
        self.w2 = a.load(rows(d["L0_xattn_w2"]), 128, self.HK, D)
        self.b1 = a.load(d["L0_xattn_b1_c"], 128, self.HK)
        self.b2 = a.load(every(d["L0_xattn_b2"], 1), 1, D)
        self.gain = a.load(d["L0_xattn_ln2_g_c"], 128, KD)
        self.shift = a.load(d["L0_xattn_ln2_b_c"], 128, KD)


class L1State:

    name = "L1_attn"
    DIST = (1, 2, 4, 8, 16, 32, 64)

    def weights(self, a, d):
        self.bw = a.load(rows(d["L1_attn_B_wT"]), 128, KD, 128)
        self.dw = a.load(rows(d["L1_attn_D_wT"]), 128, KD, D)
        self.s1 = a.load(rows(d["L1_attn_s_w1T"]), 128, KD, 128)
        self.gw = a.load(rows(d["L1_attn_g_wT"]), 128, KD, D)
        self.cw = a.load(d["L1_attn_C_wT"], 128, D)
        self.s2 = a.load(d["L1_attn_s_w2T"], 128, 128)
        self.sb1 = a.load(d["L1_attn_s_b1_c"], 128, 1)
        self.sb2 = a.load(d["L1_attn_s_b2_c"], 128, 1)
        self.bb = a.load(d["L1_attn_B_b_c"], 128, 1)
        self.cb = a.load(d["L1_attn_C_b_c"], 128, KD)
        self.db = a.load(d["L1_attn_D_b_c"], 128, KD)
        self.gb = a.load(d["L1_attn_g_b_c"], 128, KD)
        n = len(self.DIST)
        self.pow = a.take(128, n, 128)
        self.powT = a.take(128, n, 128)
        a.loads.append((self.pow[:, 0, :], d["L1_attn_A"]))
        a.loads.append((self.powT[:, 0, :], d["L1_attn_AT"]))

    def build(self, core, run):
        nc, ps, DIST = core.nc, core.ps, self.DIST
        sb = run.sbuf
        xn, xT = sb("xn", [T, U, D]), sb("xT", [128, KD, NB * T])
        s1, s2, h = sb("s1", [128, N4]), sb("s2", [128, N4]), sb("h", [128, NB, T])
        gate, z, ydb = sb("gate", [128, KD, N4]), sb("z", [128, KD, N4]), sb("ydb", [128, KD])
        norm, squared, squares = core.semaphore("norm"), core.semaphore("squared"), core.semaphore("squares")
        grown, added = core.semaphore("grown"), core.semaphore("added")
        pe = Progress(core, "tensor", ("xT", KD), ("s1", 1), ("b", 1), ("s2", 1))
        ac = Progress(core, "scalar", ("xT", KD), ("s1", 1), ("s2", 1))
        ve = Progress(core, "vector", "xn", ("u", 1))
        pe2 = Progress(core, "tensor2", ("g", KD), ("y", KD), "back")
        ac2 = Progress(core, "scalar2", ("gate", KD))
        ve2 = Progress(core, "vector2", ("z", KD), "out", "stats")
        block = run.block
        tok = lambda c: bass.ds(c * N4, N4)

        @block.gpsimd
        def _(pool):
            norm_pool(core, norm)

        @block.vector
        def _(dve):
            norm_vector(core, dve, norm)
            dve.wait_ge(run.arrived, run.loads)
            nc.vector.tensor_tensor(ydb[:, :], self.cb, self.db, ALU.add).then_inc(norm, 1)
            with dve.Fori(0, NCH) as c:
                for u in range(U):
                    normed(core, xn[:, u], U * c + u).then_inc(ve.step("xn", u), 1)
                dve.wait_ge(pe.sem, pe.at(c, "b"))
                dve.wait_ge(ac.sem, ac.at(c, "s2"))
                nc.vector.scalar_tensor_tensor(out=h[:, bass.ds(U * c, U), :].rearrange("p b t -> p (b t)"),
                                                       in0=ps[:, 4, 0:N4], scalar=self.bb, in1=s2[:, :],
                                                       op0=ALU.add, op1=ALU.mult).then_inc(ve.step("u"), 1)
            for i, dist in enumerate(DIST):
                for g in range(NCH):
                    dve.wait_ge(grown, NCH * i + g + 1)
                    hg = h[:, U * g:U * g + U, dist:T]
                    nc.vector.tensor_tensor(hg, hg, ps[:, g, 0:U * (T - dist)].rearrange("p (b t) -> p b t", b=U),
                                            ALU.add).then_inc(added, 1)
            dve.wait_ge(norm, 9)
            with dve.Fori(0, NCH) as c:
                for m in range(KD):
                    dve.wait_ge(pe2.sem, pe2.at(c, "y", m))
                    dve.wait_ge(ac2.sem, ac2.at(c, "gate", m))
                    nc.vector.scalar_tensor_tensor(out=z[:, m], in0=ps[:, 2 + m, 0:N4], scalar=ydb[:, m:m + 1],
                                                            in1=gate[:, m], op0=ALU.add, op1=ALU.mult).then_inc(ve2.step("z", m), 1)
                for u in range(U):
                    dve.wait_ge(pe2.sem, pe2.at(c, "back", u))
                    x = core.x[:, U * c + u, :]
                    nc.vector.tensor_tensor(x, x, ps[0:T, 4 + u, 0:D], ALU.add).then_inc(ve2.step("out", u), 1)
                for u in range(U):
                    dve.wait_ge(ve2.sem, ve2.at(c, "out", u))
                    row_stats(core, dve, U * c + u).then_inc(ve2.step("stats", u), 1)

        @block.scalar
        def _(act):
            run.prefetch(act)
            act.wait_ge(run.arrived, run.loads)
            with act.Fori(0, NCH) as c:
                for k in range(KD):
                    act.wait_ge(pe.sem, pe.at(c, "xT", k))
                    nc.scalar.copy(xT[:, k, tok(c)], ps[:, k, 0:N4]).then_inc(ac.step("xT", k), 1)
                act.wait_ge(pe.sem, pe.at(c, "s1"))
                nc.scalar.activation(s1[:, :], ps[:, 2, 0:N4], ACT.Silu, bias=self.sb1).then_inc(ac.step("s1"), 1)
                act.wait_ge(pe.sem, pe.at(c, "s2"))
                nc.scalar.activation(s2[:, :], ps[:, 3, 0:N4], ACT.Sigmoid, bias=self.sb2).then_inc(ac.step("s2"), 1)
            for i in range(1, len(DIST)):
                act.wait_ge(squares, i)
                nc.scalar.copy(self.pow[:, i, :], ps[:, 6, 0:128]).then_inc(squared, 1)
                nc.scalar.copy(self.powT[:, i, :], ps[:, 6, 128:256]).then_inc(squared, 1)
            with act.Fori(0, NCH) as c:
                for m in range(KD):
                    act.wait_ge(pe2.sem, pe2.at(c, "g", m))
                    nc.scalar.activation(gate[:, m], ps[:, m, 0:N4], ACT.Sigmoid, bias=self.gb[:, m:m + 1]).then_inc(ac2.step("gate", m), 1)

        @block.tensor
        def _(ten):
            ten.wait_ge(run.arrived, run.loads)
            with ten.Fori(0, NCH) as c:
                for k in range(KD):
                    for u in range(U):
                        if k == 0:
                            ten.wait_ge(ve.sem, ve.at(c, "xn", u))
                        ins = nc.tensor.transpose(ps[:, k, u * T:(u + 1) * T], xn[:, u, k * 128:(k + 1) * 128],
                                                  core.ident[0:T, 0:T])
                    ins.then_inc(pe.step("xT", k), 1)
                for k in range(KD):
                    ten.wait_ge(ac.sem, ac.at(c, "xT", k))
                    ins = nc.tensor.matmul(ps[:, 2, 0:N4], self.s1[:, k, :], xT[:, k, tok(c)], start=(k == 0), stop=(k == KD - 1))
                ins.then_inc(pe.step("s1"), 1)
                for k in range(KD):
                    ins = nc.tensor.matmul(ps[:, 4, 0:N4], self.bw[:, k, :], xT[:, k, tok(c)], start=(k == 0), stop=(k == KD - 1))
                ins.then_inc(pe.step("b"), 1)
                ten.wait_ge(ac.sem, ac.at(c, "s1"))
                nc.tensor.matmul(ps[:, 3, 0:N4], self.s2, s1[:, :], start=True, stop=True).then_inc(pe.step("s2"), 1)
            for i, dist in enumerate(DIST):
                if i:
                    ten.wait_ge(squared, 2 * i)
                if i + 1 < len(DIST):
                    nc.tensor.matmul(ps[:, 6, 0:128], self.powT[:, i, :], self.pow[:, i, :], start=True, stop=True)
                    nc.tensor.matmul(ps[:, 6, 128:256], self.pow[:, i, :], self.powT[:, i, :], start=True, stop=True).then_inc(squares, 1)
                for g in range(NCH):
                    if i == 0:
                        ten.wait_ge(ve.sem, ve.at(g, "u"))
                    else:
                        ten.wait_ge(added, NCH * (i - 1) + g + 1)
                    nc.tensor.matmul(ps[:, g, 0:U * (T - dist)], self.powT[:, i, :], h[:, U * g:U * g + U, 0:T - dist],
                                     start=True, stop=True).then_inc(grown, 1)
            ten.wait_ge(added, NCH * len(DIST))
            with ten.Fori(0, NCH) as c:
                for m in range(KD):
                    for k in range(KD):
                        ins = nc.tensor.matmul(ps[:, m, 0:N4], self.gw[:, k, m * 128:(m + 1) * 128], xT[:, k, tok(c)],
                                               start=(k == 0), stop=(k == KD - 1))
                    ins.then_inc(pe2.step("g", m), 1)
                for m in range(KD):
                    for k in range(KD):
                        nc.tensor.matmul(ps[:, 2 + m, 0:N4], self.dw[:, k, m * 128:(m + 1) * 128], xT[:, k, tok(c)],
                                         start=(k == 0), stop=False)
                    nc.tensor.matmul(ps[:, 2 + m, 0:N4], self.cw[:, m * 128:(m + 1) * 128],
                                              h[:, bass.ds(U * c, U), :].rearrange("p b t -> p (b t)"),
                                              start=False, stop=True).then_inc(pe2.step("y", m), 1)
                for u in range(U):
                    for m in range(KD):
                        ten.wait_ge(ve2.sem, ve2.at(c, "z", m))
                        ins = nc.tensor.transpose(ps[0:T, 4 + u, m * 128:(m + 1) * 128], z[:, m, u * T:(u + 1) * T], core.ident[:, :])
                    ins.then_inc(pe2.step("back", u), 1)


class L1Cross:

    name = "L1_xattn"
    W = 2

    def weights(self, a, d):
        self.wq = a.load(rows(d["L1_xattn_Wq"]), 128, KD, D)
        self.wk = a.load(rows(d["L1_xattn_Wk"]), 128, KD, D)
        self.wvT = a.load(rows(d["L1_xattn_WvT"]), 128, KD, D)
        self.wqk = a.take(128, KD, D)

    def build(self, core, run):
        nc, d, ps, W = core.nc, core.dram, core.ps, self.W
        sb = run.sbuf
        C = NB // W
        xn, xT, qT = sb("xn", [T, W, D]), sb("xT", [128, W, KD * T]), sb("qT", [128, W, KD * T])
        ctx, ctxT = sb("ctx", [SP_, W, ST, D]), sb("ctxT", [128, W, KD, S])
        mask, keep, low = sb("mask", [T, W, S], I32), sb("keep", [T, W, S]), sb("low", [T, W, S])
        e = sb("e", [T, W, S])
        pT, acT = sb("pT", [SP_, W, ST * T]), sb("acT", [128, W, KD * T])
        mx, nmx, den, rden = (sb(n, [T, W]) for n in ("mx", "nmx", "den", "rden"))
        norm, wqk_ready = core.semaphore("norm"), core.semaphore("wqk")
        ctxT_in, mask_in, ctx_in = ([core.semaphore(f"{n}{u}") for u in range(W)] for n in ("ctxT", "mask", "ctx"))
        pe, pe_o = Progress(core, "tensor", ("xT", 1), ("qT", 1), ("e", W)), Progress(core, "tensor_out", ("pT", W), ("ac", W), ("out", W))
        ac, ac_e = Progress(core, "scalar", ("xT", 1), ("qT", 1)), Progress(core, "scalar_exp", ("exp", W))
        ac_o = Progress(core, "scalar_out", ("pT", W), ("acT", 1))
        ve_x, ve = Progress(core, "vector_xn", ("xn", W)), Progress(core, "vector", ("kept", W), ("masked", W), ("max", W), ("negmax", W))
        ve_r, ve_o = Progress(core, "vector_rden", ("rden", W)), Progress(core, "vector_out", ("out", W), ("stats", W))
        po = Progress(core, "pool", ("gone", W), ("low", W), ("keep", W))
        SCALE = D ** -0.5
        block = run.block
        XT, QT, PT, AC, OUT = 2, 3, 4, 6, 7
        both = lambda t: t.rearrange("p u n -> p (u n)")

        @block.sync
        def _(sp):
            def load_scored(n, u):
                sp.dma_start(ctxT[:, u], d["ctxT"][n].rearrange("(k p) s -> p k s", p=128)).then_inc(ctxT_in[u], DMA)
                sp.dma_start(mask[:, u], d["mask"][n]).then_inc(mask_in[u], DMA)

            def load_summed(n, u):
                sp.dma_start(ctx[:, u], d["ctx"][n].rearrange("(s p) c -> p s c", p=SP_)).then_inc(ctx_in[u], DMA)
            for u in range(W):
                load_scored(u, u)
            for u in range(W):
                load_summed(u, u)
            with sp.Fori(1, C) as c:
                for u in range(W):
                    sp.wait_ge(pe.sem, pe.at(c - 1, "e", u))
                    core.stand(sp)
                    sp.wait_ge(po.sem, po.at(c - 1, "gone", u))
                    core.stand(sp)
                    load_scored(W * c + u, u)
                for u in range(W):
                    sp.wait_ge(pe_o.sem, pe_o.at(c - 1, "ac", u))
                    core.stand(sp)
                    load_summed(W * c + u, u)

        @block.gpsimd
        def _(pool):
            norm_pool(core, norm)

            def masks(c, first):
                for u in range(W):
                    pool.wait_ge(mask_in[u], (c + 1) * DMA)
                    core.stand(pool)
                    if not first:
                        pool.wait_ge(ve.sem, ve.at(c - 1, "masked", u))
                        core.stand(pool)
                    nc.gpsimd.tensor_scalar(keep[:, u], mask[:, u], 0.0, None, ALU.is_equal).then_inc(po.step("gone", u), 1)
                for u in range(W):
                    pool.wait_ge(po.sem, po.at(c, "gone", u))
                    core.stand(pool)
                    nc.gpsimd.tensor_scalar(low[:, u], keep[:, u], -1e10, None, ALU.mult).then_inc(po.step("low", u), 1)
                for u in range(W):
                    pool.wait_ge(po.sem, po.at(c, "low", u))
                    core.stand(pool)
                    nc.gpsimd.tensor_scalar(keep[:, u], keep[:, u], -1.0, 1.0, ALU.mult, ALU.add).then_inc(po.step("keep", u), 1)
            masks(0, True)
            with pool.Fori(1, C) as c:
                masks(c, False)

        @block.vector
        def _(dve):
            norm_vector(core, dve, norm)

            def normalise(c, first):
                if not first:
                    dve.wait_ge(pe.sem, pe.at(c - 1, "xT"))
                    core.stand(dve)
                for u in range(W):
                    normed(core, xn[:, u], W * c + u).then_inc(ve_x.step("xn", u), 1)

            def masked(c, first):
                for u in range(W):
                    dve.wait_ge(pe.sem, pe.at(c, "e", u))
                    core.stand(dve)
                    if not first:
                        dve.wait_ge(pe_o.sem, pe_o.at(c - 1, "pT", u))
                        core.stand(dve)
                    dve.wait_ge(po.sem, po.at(c, "keep", u))
                    nc.vector.tensor_tensor(e[:, u], ps[0:T, u, 0:S], keep[:, u], ALU.mult).then_inc(ve.step("kept", u), 1)
                for u in range(W):
                    dve.wait_ge(ve.sem, ve.at(c, "kept", u))
                    nc.vector.tensor_tensor(e[:, u], e[:, u], low[:, u], ALU.add).then_inc(ve.step("masked", u), 1)
                for u in range(W):
                    dve.wait_ge(ve.sem, ve.at(c, "masked", u))
                    nc.vector.tensor_reduce(mx[:, u:u + 1], e[:, u], AX.X, ALU.max).then_inc(ve.step("max", u), 1)
                for u in range(W):
                    dve.wait_ge(ve.sem, ve.at(c, "max", u))
                    nc.vector.tensor_scalar(nmx[:, u:u + 1], mx[:, u:u + 1], -SCALE, None, ALU.mult).then_inc(ve.step("negmax", u), 1)

            def result(c):
                for u in range(W):
                    dve.wait_ge(pe_o.sem, pe_o.at(c, "out", W - 1))
                    core.stand(dve)
                    dve.wait_ge(ve_r.sem, ve_r.at(c, "rden", u))
                    x = core.x[:, W * c + u, :]
                    nc.vector.scalar_tensor_tensor(out=x, in0=ps[0:T, OUT, u * D:(u + 1) * D], scalar=rden[:, u:u + 1],
                                                           in1=x, op0=ALU.mult, op1=ALU.add).then_inc(ve_o.step("out", u), 1)
                for u in range(W):
                    dve.wait_ge(ve_o.sem, ve_o.at(c, "out", u))
                    row_stats(core, dve, W * c + u).then_inc(ve_o.step("stats", u), 1)

            def attend(c, first=False, ahead=True):
                masked(c, first)
                if not first:
                    result(c - 1)
                for u in range(W):
                    dve.wait_ge(ac_e.sem, ac_e.at(c, "exp", u))
                    nc.vector.reciprocal(rden[:, u:u + 1], den[:, u:u + 1]).then_inc(ve_r.step("rden", u), 1)
                if ahead:
                    normalise(c + 2, False)
            normalise(0, True)
            normalise(1, False)
            attend(0, first=True)
            with dve.Fori(1, C - 2) as c:
                attend(c)
            attend(C - 2, ahead=False)
            attend(C - 1, ahead=False)
            result(C - 1)

        @block.scalar
        def _(act):
            run.prefetch(act)
            act.wait_ge(wqk_ready, 1)
            nc.scalar.copy(self.wqk, ps[:, 6:8, 0:D]).then_inc(wqk_ready, 1)

            def keep_q(c):
                act.wait_ge(pe.sem, pe.at(c, "xT"))
                nc.scalar.copy(both(xT[:, :, :]), ps[:, XT, 0:W * KD * T]).then_inc(ac.step("xT"), 1)
                act.wait_ge(pe.sem, pe.at(c, "qT"))
                nc.scalar.copy(both(qT[:, :, :]), ps[:, QT, 0:W * KD * T]).then_inc(ac.step("qT"), 1)

            def attend(c):
                for u in range(W):
                    act.wait_ge(ve.sem, ve.at(c, "negmax", u))
                    nc.scalar.activation(e[:, u], e[:, u], ACT.Exp, bias=nmx[:, u:u + 1], scale=SCALE,
                                                 accum_out=den[:, u:u + 1]).then_inc(ac_e.step("exp", u), 1)

            def keep_out(c):
                for u in range(W):
                    act.wait_ge(pe_o.sem, pe_o.at(c, "pT", u))
                    nc.scalar.copy(pT[:, u], ps[0:SP_, PT + u, 0:ST * T]).then_inc(ac_o.step("pT", u), 1)
                act.wait_ge(pe_o.sem, pe_o.at(c, "ac", W - 1))
                nc.scalar.copy(both(acT[:, :, :]), ps[:, AC, 0:W * KD * T]).then_inc(ac_o.step("acT"), 1)
            keep_q(0)
            with act.Fori(0, C - 1) as c:
                keep_q(c + 1)
                attend(c)
                keep_out(c)
            attend(C - 1)
            keep_out(C - 1)

        @block.tensor
        def _(ten):
            ten.wait_ge(run.arrived, run.loads)
            for k in range(KD):
                for h in range(KD):
                    ins = nc.tensor.matmul(ps[:, 6 + k, 0:D], self.wq[:, h, k * 128:(k + 1) * 128], self.wk[:, h, :],
                                           start=(h == 0), stop=(h == KD - 1))
            ins.then_inc(wqk_ready, 1)
            ten.wait_ge(wqk_ready, 2)

            def scores(c, first):
                for u in range(W):
                    ten.wait_ge(ve_x.sem, ve_x.at(c, "xn", u))
                    for k in range(KD):
                        o = (u * KD + k) * T
                        ins = nc.tensor.transpose(ps[:, XT, o:o + T], xn[:, u, k * 128:(k + 1) * 128], core.ident[0:T, 0:T])
                ins.then_inc(pe.step("xT"), 1)
                ten.wait_ge(ac.sem, ac.at(c, "xT"))
                for u in range(W):
                    for m in range(KD):
                        o = (u * KD + m) * T
                        for k in range(KD):
                            ins = nc.tensor.matmul(ps[:, QT, o:o + T], self.wqk[:, k, m * 128:(m + 1) * 128],
                                                   xT[:, u, k * T:(k + 1) * T], start=(k == 0), stop=(k == KD - 1))
                ins.then_inc(pe.step("qT"), 1)
                ten.wait_ge(ac.sem, ac.at(c, "qT"))
                for u in range(W):
                    ten.wait_ge(ctxT_in[u], (c + 1) * DMA)
                    if not first:
                        core.stand(ten)
                        ten.wait_ge(ve.sem, ve.at(c - 1, "kept", u))
                    for k in range(KD):
                        ins = nc.tensor.matmul(ps[0:T, u, 0:S], qT[:, u, k * T:(k + 1) * T], ctxT[:, u, k, :],
                                               start=(k == 0), stop=(k == KD - 1))
                    ins.then_inc(pe.step("e", u), 1)

            def result(c, first):
                for u in range(W):
                    ten.wait_ge(ac_e.sem, ac_e.at(c, "exp", u))
                    for s in range(ST):
                        ins = nc.tensor.transpose(ps[0:SP_, PT + u, s * T:(s + 1) * T], e[:, u, s * SP_:(s + 1) * SP_],
                                                  core.ident[0:T, 0:T])
                    ins.then_inc(pe_o.step("pT", u), 1)
                for u in range(W):
                    ten.wait_ge(ac_o.sem, ac_o.at(c, "pT", u))
                    core.stand(ten)
                    ten.wait_ge(ctx_in[u], (c + 1) * DMA)
                    for m in range(KD):
                        o = (u * KD + m) * T
                        for s in range(ST):
                            ins = nc.tensor.matmul(ps[:, AC, o:o + T], ctx[:, u, s, m * 128:(m + 1) * 128],
                                                   pT[:, u, s * T:(s + 1) * T], start=(s == 0), stop=(s == ST - 1))
                    ins.then_inc(pe_o.step("ac", u), 1)
                ten.wait_ge(ac_o.sem, ac_o.at(c, "acT"))
                for u in range(W):
                    if u == 0 and not first:
                        core.stand(ten)
                        ten.wait_ge(ve_o.sem, ve_o.at(c - 1, "out", W - 1))
                    for k in range(KD):
                        ins = nc.tensor.matmul(ps[0:T, OUT, u * D:(u + 1) * D], acT[:, u, k * T:(k + 1) * T], self.wvT[:, k, :],
                                               start=(k == 0), stop=(k == KD - 1))
                    ins.then_inc(pe_o.step("out", u), 1)
            scores(0, True)
            scores(1, False)
            result(0, True)
            with ten.Fori(1, C - 1) as c:
                scores(c + 1, False)
                result(c, False)
            result(C - 1, False)


class Experts:

    K = 2

    def build(self, core, run):
        nc, d, ps, E, K, TS, HM, W, NT = core.nc, core.dram, core.ps, self.E, self.K, self.TS, self.HM, self.W, self.NT
        sb, R = run.sbuf, self.R
        slots = NT * TS
        Q = TS // 128
        J = -(-NB * T // TS)
        rows_in = core.scratch("rows_in", [slots, D + 1])
        rows_out = core.scratch("rows_out", [(K * NB * T + W * TS), D])
        xn, xT = sb("xn", [T, U, D]), sb("xT", [128, KD, N4])
        lg = sb("lg", [T, NB, R])
        top, which = sb("top", [T, NB, 8]), sb("which", [T, NB, 8], U32)
        at = sb("at", [T, K, NB])
        hot = sb("hot", [T, K + 1, NB, E])
        place = sb("place", [T, NB, E])
        tmp = sb("tmp", [T, K, NB, E])
        slot, slot_i = sb("slot", [T, K, NB]), sb("slot_i", [T, K * NB], U32)
        s, e2, rden = sb("s", [T, K, NB]), sb("e2", [T, NB]), sb("rden", [T, NB])
        more, tiles = sb("more", [E, J]), sb("tiles", [E, 1])
        tiles_w, base = sb("tiles_w", [E, 128]), sb("base", [T, E])
        ended, table_f, table = sb("ended", [E, NT]), sb("table_f", [1, NT]), sb("table", [1, NT], I32)
        xs, xsT = sb("xs", [128, W, Q, D + 1]), sb("xsT", [128, W, KD, TS])
        silu, hT = sb("silu", [128, 2, TS]), sb("hT", [128, W, HM, TS])
        empty = xs[:, :, :, :].rearrange("p w q d -> p (w q) d")
        ys, dest = sb("ys", [128, W, Q, D]), sb("dest", [128, W, Q], U32)
        sent_rows, sent_last = sb("sent_rows", [T, NB, D + 1]), sb("sent_last", [T, NCH, D + 1])
        in_y = core.y[:, :, :].rearrange("p n d -> p (n d)")[:, 0:NCH * (U - 1) * (D + 1)].rearrange("p (n d) -> p n d", d=D + 1)
        second = lambda c, u: sent_last[:, bass.ds(c, 1), :] if u == U - 1 else in_y[:, bass.ds((U - 1) * c + u, 1), :]
        norm, zeroed, cleared = (core.semaphore(n) for n in ("norm", "zeroed", "cleared"))
        sent = core.pool_dma_semaphore("sent")
        loaded = [core.semaphore(f"loaded{w}") for w in range(W)]
        stored = [core.pool_dma_semaphore(f"stored{w}") for w in range(W)]
        fetched = [core.semaphore(f"fetched{g}") for g in range(NCH)]
        pe, ac = Progress(core, "tensor", ("xT", KD), ("lg", 1)), Progress(core, "scalar", ("xT", KD), ("lg", 1))
        ve, po = Progress(core, "vector", "xn", "kept"), Progress(core, "pool", ("numbers", K + 1))
        po_k = Progress(core, "pool_kept", "kept")
        ve_p = Progress(core, "vector_place", ("top", NB), ("which", NB), ("at", 1), ("hot", K), ("either", 1), ("gap", 1), ("more", 1), ("tiles", 1),
                        ("wide", 1), ("ended", 1), ("table_f", 1), ("table", 1), ("base", 1), ("place", 1), ("tmp", K), ("slot", K), ("slot_i", 1),
                        ("den", 1), ("s1", 1), ("s2", 1))
        pe_p = Progress(core, "tensor_place", ("place", 1), ("count", 1), ("base", 1), ("end", 1), ("table", 1))
        ac_p = Progress(core, "scalar_place", ("e2", 1))
        pe_t, pe_u, pe_d = (Progress(core, "tensor_" + n, (n, c)) for n, c in (("xsT", W), ("up", W * HM), ("down", W)))
        ac_s, ac_y = (Progress(core, "scalar_" + n, (n, c)) for n, c in (("silu", W * HM), ("ys", W)))
        ve_t, ve_h = (Progress(core, "vector_" + n, (n, c)) for n, c in (("xsT", W), ("h", W * HM)))
        ve_d = Progress(core, "vector_dest", ("dest", W))
        ve_e = Progress(core, "vector_end", ("first", U), ("second", U), ("stats", U))
        block = run.block
        passes, LAG = NT // W, self.LAG
        ve_a = Progress(core, "vector_xT", ("xTa", KD))

        @block.sync
        def _(sp):
            sp.wait_ge(cleared, 1)
            for r in range(W * Q):
                sp.dma_start(rows_in.rearrange("(j r p) c -> r p j c", p=128, r=W * Q)[r],
                             empty[:, r, :].unsqueeze(1).to_broadcast([128, passes, D + 1])).then_inc(zeroed, DMA)
            sp.wait_ge(ve_p.sem, ve_p.at(0, "table"))

            def weights(j, w):
                i = W * j + w
                e = sp.value_load(table[0:1, bass.ds(i, 1)], min_val=0, max_val=E - 1)
                for dst, src in self.of_expert(w, d, e):
                    sp.dma_start(dst, src).then_inc(loaded[w], DMA)

            def tile(j, w):
                i = W * j + w
                sp.dma_start(xs[:, w], rows_in[bass.ds(i * TS, TS), :].rearrange("(q p) c -> p q c", p=128)).then_inc(loaded[w], DMA)
            for w in range(W):
                weights(0, w)
            sp.wait_ge(sent, DMA * K * NB)
            for w in range(W):
                tile(0, w)
            with sp.Fori(1, passes) as j:
                for w in range(W):
                    sp.wait_ge(pe_d.sem, pe_d.at(j - 1, "down", w))
                    core.stand(sp)
                    sp.wait_ge(ve_d.sem, ve_d.at(j - 1, "dest", w))
                    core.stand(sp)
                    weights(j, w)
                    tile(j, w)
            for w in range(W):
                sp.wait_ge(stored[w], Q * DMA * passes)
            for g in range(NCH):
                for k in range(K):
                    src = rows_out[(k * NB + g * U) * T:(k * NB + (g + 1) * U) * T, :].rearrange("(u t) c -> t u c", t=T)
                    sp.dma_start((sent_rows if k else core.y)[:, g * U:(g + 1) * U, 0:D], src).then_inc(fetched[g], DMA)

        LOADS = DMA * (self.PARTS + 1)

        @block.gpsimd
        def _(pool):
            nc.gpsimd.memset(empty[:, :, 0:D], 0.0)
            pool.wait_ge(run.arrived, run.loads)
            nc.gpsimd.tensor_copy(empty[:, :, D], self.nowhere).then_inc(cleared, 1)
            norm_pool(core, norm)
            nc.gpsimd.tensor_scalar(sent_rows[:, :, D], self.token, 0.0, None, ALU.add).then_inc(po.step("numbers", 0), 1)
            by_chunk = self.token.rearrange("p (c u) -> p c u", u=U)
            nc.gpsimd.tensor_scalar(in_y[:, :, D].rearrange("p (c u) -> p c u", u=U - 1), by_chunk[:, :, 0:U - 1], float(NB * T), None, ALU.add).then_inc(po.step("numbers", 1), 1)
            nc.gpsimd.tensor_scalar(sent_last[:, :, D], by_chunk[:, :, U - 1], float(NB * T), None, ALU.add).then_inc(po.step("numbers", 2), 1)
            with pool.Fori(0, NCH) as c:
                for u in range(U):
                    pool.wait_ge(ve.sem, ve.at(c, "kept", u))
                    core.stand(pool)
                    nc.gpsimd.tensor_copy(second(c, u)[:, :, 0:D], sent_rows[:, bass.ds(U * c + u, 1), 0:D]).then_inc(po_k.step("kept", u), 1)
            pool.wait_ge(zeroed, W * Q * DMA)
            pool.wait_ge(ve_p.sem, ve_p.at(0, "slot_i"))
            pool.wait_ge(po.sem, po.at(0, "numbers", K))
            pool.wait_ge(po_k.sem, po_k.at(NCH - 1, "kept", U - 1))
            for k in range(K):
                for n in range(NB):
                    nc.gpsimd.indirect_dma_start(out=rows_in[:, :], out_offset=bass.IndirectOffsetOnAxis(ap=slot_i[:, k * NB + n:k * NB + n + 1], axis=0),
                                                 in_=second(n // U, n % U)[:, 0, :] if k else sent_rows[:, n, :], in_offset=None).then_inc(sent, DMA)
            with pool.Fori(0, passes) as j:
                for w in range(W):
                    pool.wait_ge(ve_d.sem, ve_d.at(j, "dest", w))
                    core.stand(pool)
                    pool.wait_ge(ac_y.sem, ac_y.at(j, "ys", w))
                    core.stand(pool)
                    for q in range(Q):
                        nc.gpsimd.indirect_dma_start(out=rows_out[:, :], out_offset=bass.IndirectOffsetOnAxis(ap=dest[:, w, q:q + 1], axis=0),
                                                     in_=ys[:, w, q, :], in_offset=None).then_inc(stored[w], DMA)

        @block.vector
        def _(dve):
            norm_vector(core, dve, norm)
            dve.wait_ge(run.arrived, run.loads)
            with dve.Fori(0, NCH) as c:
                for u in range(U):
                    normed(core, xn[:, u], U * c + u).then_inc(ve.step("xn", u), 1)
                for u in range(U):
                    normed(core, sent_rows[:, U * c + u, 0:D], U * c + u).then_inc(ve.step("kept", u), 1)
                if self.shared:
                    for k in range(KD):
                        dve.wait_ge(ac.sem, ac.at(c, "xT", k))
                        nc.vector.tensor_copy(self.xTa[:, k, bass.ds(c * N4, N4)], xT[:, k]).then_inc(ve_a.step("xTa", k), 1)
                dve.wait_ge(pe.sem, pe.at(c, "xT", KD - 1))
                core.stand(dve)
            dve.wait_ge(ac.sem, ac.at(NCH - 1, "lg"))
            for n in range(NB):
                nc.vector.max(top[:, n, :], lg[:, n, 0:E]).then_inc(ve_p.step("top", n), 1)
            for n in range(NB):
                dve.wait_ge(ve_p.sem, ve_p.at(0, "top", n))
                nc.vector.max_index(which[:, n, :], top[:, n, :], lg[:, n, 0:E]).then_inc(ve_p.step("which", n), 1)
            dve.wait_ge(ve_p.sem, ve_p.at(0, "which", NB - 1))
            nc.vector.tensor_copy(at[:, :, :].rearrange("p k n -> p n k"), which[:, :, 0:K]).then_inc(ve_p.step("at"), 1)
            dve.wait_ge(ve_p.sem, ve_p.at(0, "at"))
            for k in range(K):
                nc.vector.tensor_tensor(hot[:, k], self.iota[0:T, 0:E].unsqueeze(1).to_broadcast([T, NB, E]),
                                                  at[:, k, :].unsqueeze(2).to_broadcast([T, NB, E]), ALU.is_equal).then_inc(ve_p.step("hot", k), 1)
            dve.wait_ge(ve_p.sem, ve_p.at(0, "hot", K - 1))
            nc.vector.tensor_tensor(hot[:, K], hot[:, 0], hot[:, 1], ALU.add).then_inc(ve_p.step("either"), 1)
            nc.vector.tensor_tensor(e2[:, :], top[:, :, 1], top[:, :, 0], ALU.subtract).then_inc(ve_p.step("gap"), 1)
            dve.wait_ge(pe_p.sem, pe_p.at(0, "count"))
            nc.vector.tensor_scalar(more[:, :], self.steps, ps[0:E, 3, 0:1], None, ALU.is_lt).then_inc(ve_p.step("more"), 1)
            dve.wait_ge(ve_p.sem, ve_p.at(0, "more"))
            nc.vector.tensor_reduce(tiles[:, :], more[:, :], AX.X, ALU.add).then_inc(ve_p.step("tiles"), 1)
            dve.wait_ge(ve_p.sem, ve_p.at(0, "tiles"))
            nc.vector.tensor_scalar(tiles_w[:, :], core.ones[0:E, :], tiles[:, 0:1], None, ALU.mult).then_inc(ve_p.step("wide"), 1)
            dve.wait_ge(pe_p.sem, pe_p.at(0, "end"))
            nc.vector.tensor_scalar(ended[:, :], self.iota[0:E, 0:NT], ps[0:E, 5, 0:1], None, ALU.is_ge).then_inc(ve_p.step("ended"), 1)
            dve.wait_ge(pe_p.sem, pe_p.at(0, "table"))
            nc.vector.tensor_scalar(table_f[:, :], ps[0:1, 6, 0:NT], float(E - 1), None, ALU.min).then_inc(ve_p.step("table_f"), 1)
            dve.wait_ge(ve_p.sem, ve_p.at(0, "table_f"))
            nc.vector.tensor_copy(table[:, :], table_f[:, :]).then_inc(ve_p.step("table"), 1)
            nc.vector.tensor_scalar(base[:, :], ps[0:T, 4, 0:E], float(TS), None, ALU.mult).then_inc(ve_p.step("base"), 1)
            dve.wait_ge(ve_p.sem, ve_p.at(0, "base"))
            nc.vector.tensor_tensor(place[:, :, :], ps[0:T, 2, 0:NB * E].rearrange("p (n e) -> p n e", n=NB),
                                              base[:, :].unsqueeze(1).to_broadcast([T, NB, E]), ALU.add).then_inc(ve_p.step("place"), 1)
            dve.wait_ge(ve_p.sem, ve_p.at(0, "place"))
            for k in range(K):
                nc.vector.tensor_tensor(tmp[:, k], hot[:, k], place[:, :, :], ALU.mult).then_inc(ve_p.step("tmp", k), 1)
            for k in range(K):
                dve.wait_ge(ve_p.sem, ve_p.at(0, "tmp", k))
                nc.vector.tensor_reduce(slot[:, k, :], tmp[:, k], AX.X, ALU.add).then_inc(ve_p.step("slot", k), 1)
            dve.wait_ge(ve_p.sem, ve_p.at(0, "slot", K - 1))
            nc.vector.tensor_copy(slot_i[:, :], slot[:, :, :].rearrange("p k n -> p (k n)")).then_inc(ve_p.step("slot_i"), 1)
            dve.wait_ge(ac_p.sem, ac_p.at(0, "e2"))
            nc.vector.tensor_scalar(rden[:, :], e2[:, :], 1.0, None, ALU.add).then_inc(ve_p.step("den"), 1)
            dve.wait_ge(ve_p.sem, ve_p.at(0, "den"))
            nc.vector.reciprocal(s[:, 0, :], rden[:, :]).then_inc(ve_p.step("s1"), 1)
            dve.wait_ge(ve_p.sem, ve_p.at(0, "s1"))
            nc.vector.tensor_tensor(s[:, 1, :], s[:, 0, :], e2[:, :], ALU.mult).then_inc(ve_p.step("s2"), 1)
            if self.shared:
                self.shared_vector(core, dve)

            def tiles_of(j, first):
                def turned(w):
                    dve.wait_ge(pe_t.sem, pe_t.at(j, "xsT", w))
                    nc.vector.tensor_copy(xsT[:, w].rearrange("p k s -> p (k s)"), ps[:, w % 2, 0:KD * TS]).then_inc(ve_t.step("xsT", w), 1)
                turned(0)
                for w in range(W):
                    for m in range(HM):
                        i = w * HM + m
                        dve.wait_ge(ac_s.sem, ac_s.at(j, "silu", i))
                        up = ps[:, 2 + i % 4, TS:2 * TS]
                        h = hT[:, w, m]
                        if self.biased:
                            ins = nc.vector.scalar_tensor_tensor(out=h, in0=up, scalar=self.bias(w, HM + m), in1=silu[:, i % 2], op0=ALU.add, op1=ALU.mult)
                        else:
                            ins = nc.vector.tensor_tensor(h, up, silu[:, i % 2], ALU.mult)
                        ins.then_inc(ve_h.step("h", i), 1)
                    if w + 1 < W:
                        turned(w + 1)
                    if not first:
                        dve.wait_ge(stored[w], j * Q * DMA)
                        core.stand(dve)
                    nc.vector.tensor_copy(dest[:, w, :], xs[:, w, :, D]).then_inc(ve_d.step("dest", w), 1)
            tiles_of(0, True)
            with dve.Fori(1, passes) as j:
                tiles_of(j, False)
            dve.wait_ge(ve_p.sem, ve_p.at(0, "s2"))
            for g in range(NCH):
                dve.wait_ge(fetched[g], DMA * K)
                for k in range(K):
                    for u in range(U):
                        n = U * g + u
                        if k:
                            dve.wait_ge(ve_e.sem, ve_e.at(g, "first", u))
                        x = core.x[:, n, :]
                        ins = nc.vector.scalar_tensor_tensor(out=x, in0=(sent_rows if k else core.y)[:, n, 0:D], scalar=s[:, k, n:n + 1], in1=x, op0=ALU.mult, op1=ALU.add)
                        ins.then_inc(ve_e.step("second" if k else "first", u), 1)
                for u in range(U):
                    dve.wait_ge(ve_e.sem, ve_e.at(g, "second", u))
                    row_stats(core, dve, U * g + u).then_inc(ve_e.step("stats", u), 1)

        @block.scalar
        def _(act):
            run.prefetch(act)
            act.wait_ge(run.arrived, run.loads)
            with act.Fori(0, NCH) as c:
                for k in range(KD):
                    act.wait_ge(pe.sem, pe.at(c, "xT", k))
                    nc.scalar.copy(xT[:, k], ps[:, k, 0:N4]).then_inc(ac.step("xT", k), 1)
                act.wait_ge(pe.sem, pe.at(c, "lg"))
                nc.scalar.copy(lg[:, bass.ds(U * c, U), :], ps[0:T, 2, 0:U * R].rearrange("p (u r) -> p u r", u=U)).then_inc(ac.step("lg"), 1)
            act.wait_ge(ve_p.sem, ve_p.at(0, "gap"))
            nc.scalar.activation(e2[:, :], e2[:, :], ACT.Exp).then_inc(ac_p.step("e2"), 1)
            if self.shared:
                self.shared_scalar(core, act, lg)
            def body(j, first):
                def hidden(w):
                    for m in range(HM):
                        i = w * HM + m
                        if i >= 2:
                            act.wait_ge(ve_h.sem, ve_h.at(j, "h", i - 2))
                        act.wait_ge(pe_u.sem, pe_u.at(j, "up", i))
                        src = ps[:, 2 + i % 4, 0:TS]
                        if self.biased:
                            ins = nc.scalar.activation(silu[:, i % 2], src, ACT.Silu, bias=self.bias(w, m))
                        else:
                            ins = nc.scalar.activation(silu[:, i % 2], src, ACT.Silu)
                        ins.then_inc(ac_s.step("silu", i), 1)

                def result(w):
                    if not first:
                        act.wait_ge(stored[w], j * Q * DMA)
                    act.wait_ge(pe_d.sem, pe_d.at(j, "down", w))
                    nc.scalar.copy(ys[:, w].rearrange("p q c -> p (q c)"), ps[:, 6 + w % 2, 0:Q * D]).then_inc(ac_y.step("ys", w), 1)
                for w in range(W + LAG):
                    if w < W:
                        hidden(w)
                    if w >= LAG:
                        result(w - LAG)
            body(0, True)
            with act.Fori(1, passes) as j:
                body(j, False)

        @block.tensor
        def _(ten):
            ten.wait_ge(run.arrived, run.loads)
            with ten.Fori(0, NCH) as c:
                for k in range(KD):
                    for u in range(U):
                        if k == 0:
                            ten.wait_ge(ve.sem, ve.at(c, "xn", u))
                        ins = nc.tensor.transpose(ps[:, k, u * T:(u + 1) * T], xn[:, u, k * 128:(k + 1) * 128], core.ident[0:T, 0:T])
                    ins.then_inc(pe.step("xT", k), 1)
                for u in range(U):
                    for k in range(KD):
                        if u == 0:
                            ten.wait_ge(ac.sem, ac.at(c, "xT", k))
                        ins = nc.tensor.matmul(ps[0:T, 2, u * R:(u + 1) * R], xT[:, k, u * T:(u + 1) * T], self.wr[:, k, :],
                                               start=(k == 0), stop=(k == KD - 1 and not self.biased))
                    if self.biased:
                        ins = nc.tensor.matmul(ps[0:T, 2, u * R:(u + 1) * R], core.ones[0:1, 0:T], self.br, start=False, stop=True)
                ins.then_inc(pe.step("lg"), 1)
            ten.wait_ge(ve_p.sem, ve_p.at(0, "either"))
            ten.wait_ge(ac.sem, ac.at(NCH - 1, "lg"))
            either = hot[:, K]
            by_batch = ps[0:T, 2, 0:NB * E].rearrange("p (n e) -> p n e", n=NB)
            nc.tensor.matmul(by_batch, self.before[0:T, 0:T], either, start=True, stop=False)
            for n in range(NB - 1):
                ins = nc.tensor.matmul(by_batch[:, n + 1:NB, :], core.ones[0:T, 0:T], either[:, n:n + 1, :].to_broadcast([T, NB - 1 - n, E]),
                                       start=False, stop=(n == NB - 2))
            ins.then_inc(pe_p.step("place"), 1)
            for n in range(NB):
                ins = nc.tensor.matmul(ps[0:E, 3, 0:1], either[:, n, :], core.ones[0:T, 0:1], start=(n == 0), stop=(n == NB - 1))
            ins.then_inc(pe_p.step("count"), 1)
            ten.wait_ge(ve_p.sem, ve_p.at(0, "wide"))
            nc.tensor.matmul(ps[0:T, 4, 0:E], tiles_w[:, 0:T], self.before[0:E, 0:E], start=True, stop=True).then_inc(pe_p.step("base"), 1)
            nc.tensor.matmul(ps[0:E, 5, 0:1], self.upto[0:E, 0:E], tiles[:, 0:1], start=True, stop=True).then_inc(pe_p.step("end"), 1)
            ten.wait_ge(ve_p.sem, ve_p.at(0, "ended"))
            nc.tensor.matmul(ps[0:1, 6, 0:NT], core.ones[0:E, 0:1], ended[:, :], start=True, stop=True).then_inc(pe_p.step("table"), 1)
            ten.wait_ge(ve_p.sem, ve_p.at(0, "place"))
            if self.shared:
                self.shared_tensor(core, ten)
            with ten.Fori(0, passes) as j:
                def turn(w):
                    if w >= 2:
                        ten.wait_ge(ve_t.sem, ve_t.at(j, "xsT", w - 2))
                    ten.wait_ge(loaded[w], (j + 1) * LOADS)
                    for q in range(Q):
                        for k in range(KD):
                            ins = nc.tensor.transpose(ps[:, w % 2, k * TS + q * 128:k * TS + (q + 1) * 128], xs[:, w, q, k * 128:(k + 1) * 128], core.ident[:, :])
                    ins.then_inc(pe_t.step("xsT", w), 1)

                def hidden(w):
                    ten.wait_ge(ve_t.sem, ve_t.at(j, "xsT", w))
                    for m in range(HM):
                        i = w * HM + m
                        if i >= 4:
                            ten.wait_ge(ve_h.sem, ve_h.at(j, "h", i - 4))
                        for b in range(2):
                            for k in range(KD):
                                ins = nc.tensor.matmul(ps[:, 2 + i % 4, b * TS:(b + 1) * TS], self.up(w, k, b * HM + m), xsT[:, w, k],
                                                       start=(k == 0), stop=(k == KD - 1))
                        ins.then_inc(pe_u.step("up", i), 1)

                def result(w):
                    if w >= 2:
                        ten.wait_ge(ac_y.sem, ac_y.at(j, "ys", w - 2))
                    for q in range(Q):
                        for m in range(HM):
                            if q == 0:
                                ten.wait_ge(ve_h.sem, ve_h.at(j, "h", w * HM + m))
                            ins = nc.tensor.matmul(ps[:, 6 + w % 2, q * D:(q + 1) * D], hT[:, w, m, q * 128:(q + 1) * 128], self.down(w, m),
                                                   start=(m == 0), stop=(m == HM - 1 and not self.biased))
                        if self.biased:
                            ins = nc.tensor.matmul(ps[:, 6 + w % 2, q * D:(q + 1) * D], core.ones[0:1, 0:128], self.bias_down(w), start=False, stop=True)
                    ins.then_inc(pe_d.step("down", w), 1)
                turn(0)
                for w in range(W + LAG):
                    if w < W:
                        hidden(w)
                    if w + 1 < W:
                        turn(w + 1)
                    if w >= LAG:
                        result(w - LAG)


def tiles_for_any(experts, size, w):
    return -(-((Experts.K * NB * T + experts * (size - 1)) // size) // w) * w


class L1Experts(Experts):

    name = "L1_ffn"
    E, TS, W = 16, 128, 4
    HM = 1
    R = E + 1
    NT = tiles_for_any(E, TS, W)
    LAG = 1
    shared, biased = True, False
    PARTS = 1
    UP, DOWN = KD * 2 * 128, D
    SM = 512 // 128

    def weights(self, a, d):
        n = self.name + "_"
        self.packed = a.take(128, self.W, self.UP + self.DOWN)
        self.xTa = a.take(128, KD, NB * T)
        self.wr = a.load(rows(d[n + "routerT"]), 128, KD, self.R)
        self.sg, self.su = (a.load(rows(d[n + k + "T"]), 128, KD, 128 * self.SM) for k in ("Ws_gate", "Ws_up"))
        self.sd = a.load(rows(d[n + "Ws_downT"]), 128, self.SM, D)
        self.iota = a.load(every(d["iota"], 128), 128, 64)
        self.token, self.nowhere = a.load(d["token"], T, NB), a.load(d[self.name + "_nowhere"], 128, self.W * self.TS // 128)
        self.before = a.load(d["before"], 128, 128)
        self.upto = a.load(d["upto"][0:self.E, 0:self.E], self.E, self.E)
        self.steps = a.load(every(d["L1_ffn_steps"], self.E), self.E, -(-NB * T // self.TS))

    @staticmethod
    def pack(np, a):
        part = lambda m: m.swapaxes(-1, -2).reshape(m.shape[0], -1, 128, m.shape[1]).swapaxes(1, 2)
        up = np.concatenate([part(a.pop("L1_ffn_We_gate")), part(a.pop("L1_ffn_We_up"))], axis=3)
        down = part(a.pop("L1_ffn_We_down"))
        return np.concatenate([m.reshape(m.shape[0], 128, -1) for m in (up, down)], axis=2)

    def of_expert(self, w, d, e):
        yield self.packed[:, w, :], d["L1_ffn_packed"][bass.ds(e, 1)].rearrange("a p n -> p (a n)")

    def up(self, w, k, m):
        return self.packed[:, w, k * 256 + m * 128:k * 256 + (m + 1) * 128]

    def down(self, w, m):
        return self.packed[:, w, self.UP:self.UP + D]

    def build(self, core, run):
        sb, SM = run.sbuf, self.SM
        self.gate = sb("gate", [T, NB])
        self.ssilu, self.sh = sb("ssilu", [128, 2, N4]), sb("sh", [128, SM, N4])
        self.pe_s = Progress(core, "tensor_shared", ("up", SM), "down")
        self.ac_g = Progress(core, "scalar_gate", ("gate", 1))
        self.ac_sh, self.ve_sh = Progress(core, "scalar_shared", ("silu", SM)), Progress(core, "vector_shared", ("h", SM), "add")
        super().build(core, run)

    def shared_vector(self, core, dve):
        nc, ps, SM = core.nc, core.ps, self.SM
        dve.wait_ge(self.ac_g.sem, self.ac_g.at(0, "gate"))
        with dve.Fori(0, NCH) as c:
            for m in range(SM):
                dve.wait_ge(self.ac_sh.sem, self.ac_sh.at(c, "silu", m))
                nc.vector.tensor_tensor(self.sh[:, m], ps[:, 2 + m % 2, 0:N4], self.ssilu[:, m % 2], ALU.mult).then_inc(self.ve_sh.step("h", m), 1)
            for u in range(U):
                dve.wait_ge(self.pe_s.sem, self.pe_s.at(c, "down", u))
                x = core.x[:, U * c + u, :]
                nc.vector.scalar_tensor_tensor(out=x, in0=ps[0:T, 4 + u, 0:D], scalar=self.gate[:, bass.ds(U * c + u, 1)], in1=x,
                                                               op0=ALU.mult, op1=ALU.add).then_inc(self.ve_sh.step("add", u), 1)
        dve.wait_ge(self.ve_sh.sem, self.ve_sh.at(NCH - 1, "add", U - 1))

    def shared_scalar(self, core, act, lg):
        nc, ps, SM = core.nc, core.ps, self.SM
        nc.scalar.activation(self.gate[:, :], lg[:, :, self.E], ACT.Sigmoid).then_inc(self.ac_g.step("gate"), 1)
        with act.Fori(0, NCH) as c:
            for m in range(SM):
                if m >= 2:
                    act.wait_ge(self.ve_sh.sem, self.ve_sh.at(c, "h", m - 2))
                act.wait_ge(self.pe_s.sem, self.pe_s.at(c, "up", m))
                nc.scalar.activation(self.ssilu[:, m % 2], ps[:, m % 2, 0:N4], ACT.Silu).then_inc(self.ac_sh.step("silu", m), 1)

    def shared_tensor(self, core, ten):
        nc, ps, SM = core.nc, core.ps, self.SM
        with ten.Fori(0, NCH) as c:
            for m in range(SM):
                if m >= 2:
                    ten.wait_ge(self.ve_sh.sem, self.ve_sh.at(c, "h", m - 2))
                for b, w in enumerate((self.sg, self.su)):
                    for k in range(KD):
                        ins = nc.tensor.matmul(ps[:, 2 * b + m % 2, 0:N4], w[:, k, m * 128:(m + 1) * 128], self.xTa[:, k, bass.ds(c * N4, N4)],
                                               start=(k == 0), stop=(k == KD - 1))
                ins.then_inc(self.pe_s.step("up", m), 1)
            for u in range(U):
                for m in range(SM):
                    if u == 0:
                        ten.wait_ge(self.ve_sh.sem, self.ve_sh.at(c, "h", m))
                    ins = nc.tensor.matmul(ps[0:T, 4 + u, 0:D], self.sh[:, m, u * T:(u + 1) * T], self.sd[:, m, :], start=(m == 0), stop=(m == SM - 1))
                ins.then_inc(self.pe_s.step("down", u), 1)


class L2Experts(Experts):

    name = "L2_ffn"
    E, TS, W = 8, 256, 2
    HM = 1024 // 128
    R = E
    NT = tiles_for_any(E, TS, W)
    LAG = 0
    shared, biased = False, True
    PARTS = 2
    UP, DOWN = KD * 2 * 1024, HM * D

    def weights(self, a, d):
        self.packed = a.take(128, self.W, self.UP + self.DOWN + 2 * self.HM)
        self.wr = a.load(rows(d["L2_ffn_router_wT"]), 128, KD, self.E)
        self.br = a.load(every(d["L2_ffn_router_b"], 1), 1, self.E)
        self.iota = a.load(every(d["iota"], 128), 128, 64)
        self.token, self.nowhere = a.load(d["token"], T, NB), a.load(d[self.name + "_nowhere"], 128, self.W * self.TS // 128)
        self.before = a.load(d["before"], 128, 128)
        self.upto = a.load(d["upto"][0:self.E, 0:self.E], self.E, self.E)
        self.steps = a.load(every(d["L2_ffn_steps"], self.E), self.E, -(-NB * T // self.TS))

    @staticmethod
    def pack(np, a):
        part = lambda m: m.swapaxes(-1, -2).reshape(m.shape[0], -1, 128, m.shape[1]).swapaxes(1, 2).reshape(m.shape[0], 128, -1)
        return np.concatenate([part(a.pop("L2_ffn_w1")), part(a.pop("L2_ffn_w2")),
                               a.pop("L2_ffn_b1").reshape(8, -1, 128).swapaxes(1, 2)], axis=2)

    def of_expert(self, w, d, e):
        yield self.packed[:, w, :], d["L2_ffn_packed"][bass.ds(e, 1)].rearrange("a p n -> p (a n)")
        yield self.bdown[:, w, :], d["L2_ffn_b2"][bass.ds(e, 1), :]

    def build(self, core, run):
        self.bdown = run.sbuf("bdown", [1, self.W, D])
        super().build(core, run)

    def up(self, w, k, m):
        return self.packed[:, w, k * 2048 + m * 128:k * 2048 + (m + 1) * 128]

    def down(self, w, m):
        return self.packed[:, w, self.UP + m * D:self.UP + (m + 1) * D]

    def bias(self, w, m):
        return self.packed[:, w, self.UP + self.DOWN + m:self.UP + self.DOWN + m + 1]

    def bias_down(self, w):
        return self.bdown[:, w, :]


class L2Graph:

    name = "L2_attn"
    H = 8
    HD = D // H
    HQ = 128 // HD
    W = 2

    def weights(self, a, d):
        self.wl = a.load(rows(d["L2_attn_WlT"]), 128, KD, D)
        self.wr = a.load(rows(d["L2_attn_WrT"]), 128, KD, D)
        self.wf = a.load(rows(d["L2_attn_WfT"]), 128, KD, D)
        self.gam = a.load(every(d["L2_attn_ln_gamma"], T), T, D)
        self.bet = a.load(every(d["L2_attn_ln_beta"], T), T, D)
        self.att = a.take(128, 2)
        for q in range(self.HQ):
            for i, k in enumerate(("att_l", "att_r")):
                a.loads.append((self.att[q * self.HD:(q + 1) * self.HD, i:i + 1],
                                d["L2_attn_" + k].rearrange("a d -> d a")))
        self.attl = a.take(128, T)
        self.attr = a.take(128, T)

    def build(self, core, run):
        nc, ps, H, HD, HQ, W = core.nc, core.ps, self.H, self.HD, self.HQ, self.W
        sb = run.sbuf
        C = NB // W
        xn, xT = sb("xn", [T, W, D]), sb("xT", [128, W, KD * T])
        f, lk = sb("f", [128, W, 2 * KD * T]), sb("lk", [128, W, 2 * KD * T])
        fr = sb("fr", [T, W, D])
        p, pT = sb("p", [T, W, H * T]), sb("pT", [T, W, H * T])
        ctxT = sb("ctxT", [128, W, KD * T])
        mx, den, rden = sb("mx", [T, W, H]), sb("den", [T, W, H]), sb("rden", [T, W, H])
        y = sb("y", [T, W, D])
        norm, spread = core.semaphore("norm"), core.semaphore("spread")
        ln = Norm(core, run, "ln", units=W)
        pe_f, pe_e = Progress(core, "tensor_f", ("xT", 1), ("f", W)), Progress(core, "tensor_e", ("e", 1))
        pe_o, pe_r = Progress(core, "tensor_out", ("pT", 2 * W), ("ctx", 1), ("out", 1)), Progress(core, "tensor_fr", ("fr", 1))
        ac_f, ac_e = Progress(core, "scalar_f", ("xT", 1), ("f", W)), Progress(core, "scalar_exp", ("exp", W))
        ac_o, ac_r = Progress(core, "scalar_out", ("pT", 2 * W), ("ctx", 1)), Progress(core, "scalar_fr", ("fr", 1))
        ve_x, ve_l = Progress(core, "vector_xn", ("xn", W), ("kept", W)), Progress(core, "vector_leaky", ("leaky", W))
        ve_m = Progress(core, "vector_max", ("max", W), ("sub", W))
        ve_p = Progress(core, "vector_p", ("den", W), ("rden", W), ("p", W))
        ve_y = Progress(core, "vector_y", ("y", 1), *ln.steps(), ("yn", W), ("gain", W), ("shift", W), ("out", W), ("stats", W))
        po = Progress(core, "pool", ("lnrs", 1))
        block = run.block
        heads = lambda v: v.rearrange("p (h s) -> p h s", s=T)
        HB = H // 2 * T
        XT, F_, FR, CTX, OUT, PT = 4, 5, 7, 4, 5, 4

        def scores(u):
            return ps[0:T, 0:HQ, u * KD * T:(u + 1) * KD * T].rearrange("p q (b s) -> p q b s", b=KD)

        @block.gpsimd
        def _(pool):
            norm_pool(core, norm)
            with pool.Fori(0, C) as c:
                ln.pool(pool, ve_y, po, c)

        @block.vector
        def _(dve):
            dve.wait_ge(run.arrived, run.loads)
            nc.vector.tensor_scalar(self.attl, core.ones[:, 0:T], self.att[:, 0:1], None, ALU.mult).then_inc(spread, 1)
            nc.vector.tensor_scalar(self.attr, core.ones[:, 0:T], self.att[:, 1:2], None, ALU.mult).then_inc(spread, 1)
            norm_vector(core, dve, norm)

            def normalise(c, first):
                if not first:
                    dve.wait_ge(pe_f.sem, pe_f.at(c - 1, "xT"))
                    core.stand(dve)
                for u in range(W):
                    normed(core, xn[:, u], W * c + u).then_inc(ve_x.step("xn", u), 1)
                for u in range(W):
                    normed(core, core.y[:, W * c + u, :], W * c + u).then_inc(ve_x.step("kept", u), 1)

            def leaky(c):
                for u in range(W):
                    dve.wait_ge(ac_f.sem, ac_f.at(c, "f", u))
                    nc.vector.scalar_tensor_tensor(out=lk[:, u], in0=f[:, u], scalar=0.01, in1=f[:, u],
                                                           op0=ALU.mult, op1=ALU.max).then_inc(ve_l.step("leaky", u), 1)

            def less_max(c, first):
                dve.wait_ge(pe_e.sem, pe_e.at(c, "e"))
                for u in range(W):
                    nc.vector.tensor_reduce(mx[:, u], scores(u), AX.X, ALU.max).then_inc(ve_m.step("max", u), 1)
                if not first:
                    dve.wait_ge(pe_o.sem, pe_o.at(c - 1, "pT", 2 * W - 1))
                for u in range(W):
                    dve.wait_ge(ve_m.sem, ve_m.at(c, "max", u))
                    nc.vector.tensor_tensor(p[:, u].rearrange("p (q b s) -> p q b s", q=HQ, b=KD), scores(u),
                                                    mx[:, u].rearrange("p (q b) -> p q b", q=HQ).unsqueeze(3).to_broadcast([T, HQ, KD, T]),
                                                    ALU.subtract).then_inc(ve_m.step("sub", u), 1)

            def divide(c):
                for u in range(W):
                    dve.wait_ge(ac_e.sem, ac_e.at(c, "exp", u))
                    nc.vector.tensor_reduce(den[:, u, :], heads(p[:, u]), AX.X, ALU.add).then_inc(ve_p.step("den", u), 1)
                for u in range(W):
                    dve.wait_ge(ve_p.sem, ve_p.at(c, "den", u))
                    nc.vector.reciprocal(rden[:, u, :], den[:, u, :]).then_inc(ve_p.step("rden", u), 1)
                for u in range(W):
                    dve.wait_ge(ve_p.sem, ve_p.at(c, "rden", u))
                    nc.vector.tensor_tensor(heads(p[:, u]), heads(p[:, u]),
                                                    rden[:, u, :].unsqueeze(2).to_broadcast([T, H, T]), ALU.mult).then_inc(ve_p.step("p", u), 1)

            def result_stats(c):
                dve.wait_ge(pe_o.sem, pe_o.at(c, "out"))
                core.stand(dve)
                dve.wait_ge(ve_x.sem, ve_x.at(c, "kept", W - 1))
                core.stand(dve)
                nc.vector.tensor_tensor(y[:, :, :], core.y[:, bass.ds(W * c, W), :], ps[0:T, OUT, :].rearrange("p (u d) -> p u d", u=W),
                                        ALU.add).then_inc(ve_y.step("y"), 1)
                ln.vector(dve, ve_y, c, lambda u, q: y[:, u], lambda u: dve.wait_ge(ve_y.sem, ve_y.at(c, "y")))

            def result(c):
                dve.wait_ge(po.sem, po.at(c, "lnrs"))
                core.stand(dve)
                for u in range(W):
                    ln.apply(y[:, u], y[:, u], u).then_inc(ve_y.step("yn", u), 1)
                for u in range(W):
                    dve.wait_ge(ve_y.sem, ve_y.at(c, "yn", u))
                    nc.vector.tensor_tensor(y[:, u], y[:, u], self.gam, ALU.mult).then_inc(ve_y.step("gain", u), 1)
                for u in range(W):
                    dve.wait_ge(ve_y.sem, ve_y.at(c, "gain", u))
                    nc.vector.tensor_tensor(y[:, u], y[:, u], self.bet, ALU.add).then_inc(ve_y.step("shift", u), 1)
                for u in range(W):
                    dve.wait_ge(ve_y.sem, ve_y.at(c, "shift", u))
                    x = core.x[:, W * c + u, :]
                    nc.vector.tensor_tensor(x, x, y[:, u], ALU.add).then_inc(ve_y.step("out", u), 1)
                for u in range(W):
                    dve.wait_ge(ve_y.sem, ve_y.at(c, "out", u))
                    row_stats(core, dve, W * c + u).then_inc(ve_y.step("stats", u), 1)

            def attend(c, first=False, ahead=2):
                less_max(c, first)
                if not first:
                    result_stats(c - 1)
                if ahead > 0:
                    leaky(c + 1)
                if not first:
                    result(c - 1)
                divide(c)
                if ahead > 1:
                    normalise(c + 2, False)
            normalise(0, True)
            leaky(0)
            normalise(1, False)
            attend(0, first=True)
            with dve.Fori(1, C - 2) as c:
                attend(c)
            attend(C - 2, ahead=1)
            attend(C - 1, ahead=0)
            result_stats(C - 1)
            result(C - 1)

        @block.scalar
        def _(act):
            run.prefetch(act)

            def keep_xT(c):
                act.wait_ge(pe_f.sem, pe_f.at(c, "xT"))
                nc.scalar.copy(xT[:, :, :].rearrange("p u n -> p (u n)"), ps[:, XT, 0:W * KD * T]).then_inc(ac_f.step("xT"), 1)

            def keep_f(c):
                for u in range(W):
                    act.wait_ge(pe_f.sem, pe_f.at(c, "f", u))
                    nc.scalar.copy(f[:, u], ps[:, F_ + u, 0:2 * KD * T]).then_inc(ac_f.step("f", u), 1)

            def keep_fr(c):
                act.wait_ge(pe_r.sem, pe_r.at(c, "fr"))
                nc.scalar.copy(fr[:, :, :].rearrange("p u d -> p (u d)"), ps[0:T, FR, :]).then_inc(ac_r.step("fr"), 1)

            def exp(c):
                for u in range(W):
                    act.wait_ge(ve_m.sem, ve_m.at(c, "sub", u))
                    nc.scalar.activation(p[:, u], p[:, u], ACT.Exp).then_inc(ac_e.step("exp", u), 1)

            def keep_context(c):
                for i in range(2 * W):
                    act.wait_ge(pe_o.sem, pe_o.at(c, "pT", i))
                    nc.scalar.copy(pT[:, i // 2, i % 2 * HB:(i % 2 + 1) * HB], ps[0:T, PT + i, 0:HB]).then_inc(ac_o.step("pT", i), 1)
                act.wait_ge(pe_o.sem, pe_o.at(c, "ctx"))
                nc.scalar.copy(ctxT[:, :, :].rearrange("p u n -> p (u n)"), ps[:, CTX, 0:W * KD * T]).then_inc(ac_o.step("ctx"), 1)
            keep_xT(0)
            keep_f(0)
            keep_fr(0)
            with act.Fori(0, C - 1) as c:
                keep_xT(c + 1)
                exp(c)
                keep_f(c + 1)
                keep_context(c)
                keep_fr(c + 1)
            exp(C - 1)
            keep_context(C - 1)

        @block.tensor
        def _(ten):
            ten.wait_ge(run.arrived, run.loads)
            ten.wait_ge(spread, 2)

            def make_f(c, after):
                for u in range(W):
                    ten.wait_ge(ve_x.sem, ve_x.at(c, "xn", u))
                    for k in range(KD):
                        o = (u * KD + k) * T
                        ins = nc.tensor.transpose(ps[:, XT, o:o + T], xn[:, u, k * 128:(k + 1) * 128], core.ident[0:T, 0:T])
                ins.then_inc(pe_f.step("xT"), 1)
                if after is not None:
                    ten.wait_ge(ve_y.sem, ve_y.at(after, "y"))
                    core.stand(ten)
                ten.wait_ge(ac_f.sem, ac_f.at(c, "xT"))
                for u in range(W):
                    for i, w in enumerate((self.wl, self.wr)):
                        for m in range(KD):
                            o = (i * KD + m) * T
                            for k in range(KD):
                                ins = nc.tensor.matmul(ps[:, F_ + u, o:o + T], w[:, k, m * 128:(m + 1) * 128],
                                                       xT[:, u, k * T:(k + 1) * T], start=(k == 0), stop=(k == KD - 1))
                    ins.then_inc(pe_f.step("f", u), 1)

            def make_fr(c):
                for u in range(W):
                    for k in range(KD):
                        ins = nc.tensor.matmul(ps[0:T, FR, u * D:(u + 1) * D], xT[:, u, k * T:(k + 1) * T], self.wr[:, k, :],
                                               start=(k == 0), stop=(k == KD - 1))
                ins.then_inc(pe_r.step("fr"), 1)

            def make_scores(c, first):
                if not first:
                    ten.wait_ge(ve_m.sem, ve_m.at(c - 1, "sub", W - 1))
                    core.stand(ten)
                for u in range(W):
                    ten.wait_ge(ve_l.sem, ve_l.at(c, "leaky", u))
                    core.stand(ten)
                    for b in range(KD):
                        for q in range(HQ):
                            r = slice(q * HD, (q + 1) * HD)
                            lr = lambda i: lk[r, u, (i * KD + b) * T:(i * KD + b + 1) * T]
                            o = scores(u)[:, q, b, :]
                            nc.tensor.matmul(o, self.attr[r, :], lr(1), start=True, stop=False)
                            ins = nc.tensor.matmul(o, lr(0), self.attl[r, :], start=False, stop=True)
                ins.then_inc(pe_e.step("e"), 1)

            def make_context(c):
                ten.wait_ge(ac_r.sem, ac_r.at(c, "fr"))
                core.stand(ten)
                for u in range(W):
                    ten.wait_ge(ve_p.sem, ve_p.at(c, "p", u))
                    core.stand(ten)
                    for b in range(2):
                        for q in range(HQ):
                            ins = nc.tensor.transpose(ps[0:T, PT + 2 * u + b, q * T:(q + 1) * T],
                                                      p[:, u, (q * KD + b) * T:(q * KD + b + 1) * T], core.ident[0:T, 0:T])
                        ins.then_inc(pe_o.step("pT", 2 * u + b), 1)
                for u in range(W):
                    ten.wait_ge(ac_o.sem, ac_o.at(c, "pT", 2 * u + 1))
                    core.stand(ten)
                    for b in range(KD):
                        for q in range(HQ):
                            h = HQ * b + q
                            o = (u * KD + b) * T
                            ins = nc.tensor.matmul(ps[q * HD:(q + 1) * HD, CTX, o:o + T], fr[:, u, h * HD:(h + 1) * HD],
                                                   pT[:, u, h * T:(h + 1) * T], start=True, stop=True)
                ins.then_inc(pe_o.step("ctx"), 1)
                ten.wait_ge(ac_o.sem, ac_o.at(c, "ctx"))
                for u in range(W):
                    for k in range(KD):
                        ins = nc.tensor.matmul(ps[0:T, OUT, u * D:(u + 1) * D], ctxT[:, u, k * T:(k + 1) * T], self.wf[:, k, :],
                                               start=(k == 0), stop=(k == KD - 1))
                ins.then_inc(pe_o.step("out"), 1)
            make_f(0, None)
            make_scores(0, True)
            make_fr(0)

            def attend(c, first):
                make_f(c + 1, None if first else c - 1)
                make_scores(c + 1, False)
                make_context(c)
                make_fr(c + 1)
            attend(0, True)
            with ten.Fori(1, C - 1) as c:
                attend(c, False)
            make_context(C - 1)


class Cross:

    H = 16
    HD = D // H
    HK = H // KD
    HU = H * U

    def build(self, core, run):
        nc, d, ps, H, HD, HK, HU = core.nc, core.dram, core.ps, self.H, self.HD, self.HK, self.HU
        full, sb = self.full, run.sbuf
        xn, xT = sb("xn", [T, U, D]), sb("xT", [128, U, KD * T])
        ctxT = sb("ctxT", [128, U, KD * S])
        q = sb("q", [128, U, KD * T])
        mq = sb("mq", [128, 2, HK * T])
        kT, v = ctxT if full else sb("kT", [128, U, KD * S]), sb("v", [SP_, U, ST * D])
        p, pT = sb("p", [T, 4, S]), sb("pT", [SP_, 2, ST * T])
        mx, den = (sb(n, [T, HU]) for n in ("mx", "den"))
        o, oT = xn, xT
        norm, gains = core.semaphore("norm"), core.semaphore("gains")
        loaded = [core.semaphore(f"ctx{u}") for u in range(U)]
        block = run.block
        G = U * ST
        if full:
            mask = sb("mask", [T, U, S], I32)
            es = core.y[:, :, :].rearrange("p b c -> p (b c)")[:, 0:8 * S].rearrange("p (a i s) -> p a i s", a=2, i=4)
            kn, qn = self.kn, xn
            lnq = Norm(core, run, "lnq", eps=1e-6)
            lnk, lnv = ([Norm(core, run, f"ln{k}{u}_", rows_=SP_, eps=1e-6, units=ST) for u in range(U)] for k in "kv")
            kv = lambda w, g: v[:, g // ST, (g % ST) * D:(g % ST + 1) * D] if w else kn[:, g]
            pe = Progress(core, "tensor", "xT", "qp", ("kv0", ST), ("kv1", ST), "qT", ("kv2", ST), ("kT0", KD), ("kT1", KD), ("kv3", ST), ("kT2", KD), ("kT3", KD))
            ac = Progress(core, "scalar", "xT", "qp", *((f"kT{u}", KD) for u in range(U)))
            normed_kv = [((f"add{u}", 2 * ST), *lnk[u].steps(), *lnv[u].steps(), (f"kn{u}", ST), (f"vn{u}", ST)) for u in range(U)]
            ve = Progress(core, "vector", "xn", *lnq.steps(), "qn", *normed_kv[0], *normed_kv[1], "q", *normed_kv[2], *normed_kv[3])
            po = Progress(core, "pool", ("lnqrs", 1), *((f"ln{k}{u}_rs", 1) for u in range(U) for k in "kv"))
            po_f = Progress(core, "pool_fill", "fill")
            ve_k = Progress(core, "vector_kept", ("kept", HU))
            ve_o = Progress(core, "vector_o", "mul", "gain", "o")
        else:
            pe = Progress(core, "tensor", "xT", "qT", *((f"kT{u}", KD) for u in range(U)), ("v", 2 * U))
            ac = Progress(core, "scalar", "xT", *((f"kT{u}", KD) for u in range(U)), ("v", 2 * U))
            ve = Progress(core, "vector", "xn", "q")
            ve_o = Progress(core, "vector_o", "mul", "o")
        pe_e, pe_t, pe_o = (Progress(core, "tensor_" + n, (n, HU)) for n in ("e", "pT", "pv"))
        pe2 = Progress(core, "tensor2", "oT", "out")
        ac_p, ac2 = Progress(core, "scalar_p", ("exp", HU)), Progress(core, "scalar2", "oT")
        ve_m, ve_n = Progress(core, "vector_max", ("max", HU)), Progress(core, "vector_neg", ("neg", HU))
        turned = Progress(core, "pT", ("pT", HU))
        po_m = Progress(core, "pool_mq", ("mq", KD * U))
        ve_r, ve2 = Progress(core, "vector_rden", "rden"), Progress(core, "vector2", "out", "stats")
        LAG = 3
        LOADS = (2 if full else 1) * DMA
        @block.sync
        def _(sp):
            def load(n, u):
                sp.dma_start(ctxT[:, u].rearrange("p (k s) -> p k s", k=KD), d["ctxT"][n].rearrange("(k p) s -> p k s", p=128)).then_inc(loaded[u], DMA)
                if full:
                    sp.dma_start(mask[:, u], d["mask"][n]).then_inc(loaded[u], DMA)
            for u in range(U):
                load(u, u)
            with sp.Fori(1, NCH) as c:
                for u in range(U):
                    if full:
                        sp.wait_ge(pe_e.sem, pe_e.at(c - 1, "e", H * u + H - 1))
                        core.stand(sp)
                        sp.wait_ge(ve_k.sem, ve_k.at(c - 1, "kept", H * u + H - 1))
                    else:
                        sp.wait_ge(pe.sem, pe.at(c - 1, "v", 2 * u + 1))
                    core.stand(sp)
                    load(U * c + u, u)

        @block.gpsimd
        def _(pool):
            norm_pool(core, norm)
            pool.wait_ge(run.arrived, run.loads)
            with pool.Fori(0, NCH) as c:
                def roots(u):
                    for ln in (lnk[u], lnv[u]):
                        ln.pool(pool, ve, po, c)

                def masked(u):
                    if full:
                        if u >= 2:
                            pool.wait_ge(ac_p.sem, ac_p.at(c, "exp", H * (u - 1) - 1))
                            core.stand(pool)
                        nc.gpsimd.memset(es[:, u % 2], -1e9).then_inc(po_f.step("fill", u), 1)
                    for b in range(KD):
                        g = KD * u + b
                        pool.wait_ge(ve.sem, ve.at(c, "q", u))
                        if g >= 2:
                            pool.wait_ge(pe_e.sem, pe_e.at(c, "e", HK * (g - 1) - 1))
                        nc.gpsimd.tensor_tensor(mq[:, g % 2].rearrange("p (h t) -> p h t", h=HK),
                                                          q[:, u, b * T:(b + 1) * T].unsqueeze(1).to_broadcast([128, HK, T]),
                                                          self.heads.unsqueeze(2).to_broadcast([128, HK, T]), ALU.mult).then_inc(po_m.step("mq", g), 1)
                if full:
                    lnq.pool(pool, ve, po, c)
                    roots(0)
                    roots(1)
                masked(0)
                if full:
                    roots(2)
                    roots(3)
                for u in range(1, U):
                    masked(u)

        @block.vector
        def _(dve):
            norm_vector(core, dve, norm)
            dve.wait_ge(run.arrived, run.loads)
            if full:
                nc.vector.tensor_scalar(self.gain_q, self.gain_q, HD ** -0.5, None, ALU.mult).then_inc(gains, 1)
                nc.vector.tensor_scalar(self.shift_q, self.shift_q, HD ** -0.5, None, ALU.mult).then_inc(gains, 1)
                dve.wait_ge(gains, 2)

            def scores(c, n):
                u, i = n // H, n % H
                src = ps[0:T, i % 4, 0:S]
                if full:
                    if i == 0:
                        dve.wait_ge(po_f.sem, po_f.at(c, "fill", u))
                        core.stand(dve)
                        dve.wait_ge(loaded[u], (c + 1) * LOADS)
                        core.stand(dve)
                    if i >= 4:
                        dve.wait_ge(ac_p.sem, ac_p.at(c, "exp", n - 4))
                        core.stand(dve)
                    dve.wait_ge(pe_e.sem, pe_e.at(c, "e", n))
                    core.stand(dve)
                    nc.vector.copy_predicated(es[:, u % 2, i % 4], mask[:, u], src).then_inc(ve_k.step("kept", n), 1)
                    src = es[:, u % 2, i % 4]
                    dve.wait_ge(ve_k.sem, ve_k.at(c, "kept", n))
                else:
                    dve.wait_ge(pe_e.sem, pe_e.at(c, "e", n))
                nc.vector.tensor_reduce(mx[:, n:n + 1], src, AX.X, ALU.max).then_inc(ve_m.step("max", n), 1)
                dve.wait_ge(ve_m.sem, ve_m.at(c, "max", n))
                nc.vector.tensor_scalar(mx[:, n:n + 1], mx[:, n:n + 1], -1.0, None, ALU.mult).then_inc(ve_n.step("neg", n), 1)

            def turn(c, n):
                if n >= 2:
                    dve.wait_ge(pe_o.sem, pe_o.at(c, "pv", n - 2))
                dve.wait_ge(pe_t.sem, pe_t.at(c, "pT", n))
                nc.vector.tensor_copy(pT[:, n % 2], ps[0:SP_, 4 + n % 2, 0:ST * T]).then_inc(turned.step("pT", n), 1)

            def divide(c, u):
                h = slice(H * u, H * u + H)
                dve.wait_ge(ac_p.sem, ac_p.at(c, "exp", H * u + H - 1))
                nc.vector.reciprocal(den[:, h], den[:, h]).then_inc(ve_r.step("rden", u), 1)
                dve.wait_ge(ve_r.sem, ve_r.at(c, "rden", u))
                core.stand(dve)
                dve.wait_ge(pe_o.sem, pe_o.at(c, "pv", H * u + H - 1))
                heads = lambda t: t.rearrange("p (h e) -> p h e", h=H)
                ins = nc.vector.tensor_tensor(heads(o[:, u]), heads(ps[0:T, 6 + u % 2, 0:D]),
                                              den[:, h].unsqueeze(2).to_broadcast([T, H, HD]), ALU.mult)
                ins.then_inc(ve_o.step("mul", u), 1)

            with dve.Fori(0, NCH) as c:
                for u in range(U):
                    normed(core, xn[:, u], U * c + u).then_inc(ve.step("xn", u), 1)
                if full:
                    lnq.vector(dve, ve, c, lambda u, q: qn[:, u], lambda u: dve.wait_ge(ac.sem, ac.at(c, "qp", u)))
                    dve.wait_ge(po.sem, po.at(c, "lnqrs"))
                    for u in range(U):
                        lnq.apply(qn[:, u], qn[:, u], u).then_inc(ve.step("qn", u), 1)

                def norm_kv(u):
                    tile = lambda s: ST * u + s
                    for s in range(ST):
                        dve.wait_ge(pe.sem, pe.at(c, f"kv{u}", s))
                        for w in range(2):
                            cols = slice(w * D, (w + 1) * D)
                            nc.vector.tensor_tensor(kv(w, tile(s)), ps[0:SP_, tile(s) % 4, cols], self.bkv[:, cols], ALU.add).then_inc(ve.step(f"add{u}", 2 * s + w), 1)
                    lnk[u].vector(dve, ve, c, lambda s, q: kv(0, tile(s)), lambda s: dve.wait_ge(ve.sem, ve.at(c, f"add{u}", 2 * s)))
                    lnv[u].vector(dve, ve, c, lambda s, q: kv(1, tile(s)), lambda s: dve.wait_ge(ve.sem, ve.at(c, f"add{u}", 2 * s + 1)))
                    for w, (ln, step) in enumerate(((lnk[u], f"kn{u}"), (lnv[u], f"vn{u}"))):
                        dve.wait_ge(po.sem, po.at(c, ln.tag + "rs"))
                        for s in range(ST):
                            ln.apply(kv(w, tile(s)), kv(w, tile(s)), s).then_inc(ve.step(step, s), 1)
                if full:
                    norm_kv(0)
                    norm_kv(1)
                for u in range(U):
                    dve.wait_ge(pe.sem, pe.at(c, "qT", u))
                    for m in range(KD):
                        t = slice(m * T, (m + 1) * T)
                        if full:
                            ins = nc.vector.tensor_scalar(q[:, u, t], ps[:, 4 + u, t], self.gain_q[:, m:m + 1],
                                                          self.shift_q[:, m:m + 1], ALU.mult, ALU.add)
                        else:
                            ins = nc.vector.tensor_scalar(q[:, u, t], ps[:, 4 + u, t], self.bq[:, m:m + 1], HD ** -0.5, ALU.add, ALU.mult)
                    ins.then_inc(ve.step("q", u), 1)
                if full:
                    norm_kv(2)
                    norm_kv(3)
                for n in range(HU):
                    scores(c, n)
                    if not full and n >= LAG:
                        turn(c, n - LAG)
                    if n >= H and n % H == 6:
                        divide(c, n // H - 1)
                if not full:
                    for n in range(HU - LAG, HU):
                        turn(c, n)
                divide(c, U - 1)
                if full:
                    for u in range(U):
                        dve.wait_ge(ve_o.sem, ve_o.at(c, "mul", u))
                        nc.vector.tensor_tensor(o[:, u], o[:, u], self.gain_v, ALU.mult).then_inc(ve_o.step("gain", u), 1)
                for u in range(U):
                    dve.wait_ge(ve_o.sem, ve_o.at(c, "gain" if full else "mul", u))
                    nc.vector.tensor_tensor(o[:, u], o[:, u], self.shift_v, ALU.add).then_inc(ve_o.step("o", u), 1)
                for u in range(U):
                    dve.wait_ge(pe2.sem, pe2.at(c, "out", u))
                    x = core.x[:, U * c + u, :]
                    nc.vector.tensor_tensor(x, x, ps[0:T, 4 + u, 0:D], ALU.add).then_inc(ve2.step("out", u), 1)
                for u in range(U):
                    dve.wait_ge(ve2.sem, ve2.at(c, "out", u))
                    row_stats(core, dve, U * c + u).then_inc(ve2.step("stats", u), 1)

        @block.scalar
        def _(act):
            run.prefetch(act)
            act.wait_ge(run.arrived, run.loads)

            def turn(c, n):
                if n >= 2:
                    act.wait_ge(pe_o.sem, pe_o.at(c, "pv", n - 2))
                act.wait_ge(pe_t.sem, pe_t.at(c, "pT", n))
                nc.scalar.copy(pT[:, n % 2], ps[0:SP_, 4 + n % 2, 0:ST * T]).then_inc(turned.step("pT", n), 1)

            with act.Fori(0, NCH) as c:
                for u in range(U):
                    act.wait_ge(pe.sem, pe.at(c, "xT", u))
                    nc.scalar.copy(xT[:, u], ps[:, u, 0:KD * T]).then_inc(ac.step("xT", u), 1)
                if full:
                    for u in range(U):
                        act.wait_ge(pe.sem, pe.at(c, "qp", u))
                        nc.scalar.copy(qn[:, u], ps[0:T, 4 + u, 0:D]).then_inc(ac.step("qp", u), 1)

                def keep_kT(u):
                    for m in range(KD):
                        act.wait_ge(pe.sem, pe.at(c, f"kT{u}", m))
                        k = kT[:, u, m * S:(m + 1) * S]
                        src = ps[:, 4 + (KD * u + m) % 4, 0:S]
                        if full:
                            ins = nc.scalar.activation(k, src, ACT.Identity, bias=self.shift_k[:, m:m + 1], scale=self.gain_k[:, m:m + 1])
                        else:
                            ins = nc.scalar.activation(k, src, ACT.Identity, bias=self.bk[:, m:m + 1])
                        ins.then_inc(ac.step(f"kT{u}", m), 1)
                for u in range(U):
                    keep_kT(u)
                if not full:
                    for u in range(U):
                        for i in range(2):
                            w = (2 - i) * D
                            act.wait_ge(pe.sem, pe.at(c, "v", 2 * u + i))
                            nc.scalar.copy(v[:, u, 2 * i * D:2 * i * D + w], ps[0:SP_, (2 * u + i) % 4, 0:w]).then_inc(ac.step("v", 2 * u + i), 1)
                for n in range(HU):
                    u, i = n // H, n % H
                    if full and n >= LAG:
                        turn(c, n - LAG)
                    if n >= 4:
                        act.wait_ge(pe_t.sem, pe_t.at(c, "pT", n - 4))
                    act.wait_ge(ve_n.sem, ve_n.at(c, "neg", n))
                    nc.scalar.activation(p[:, n % 4], es[:, u % 2, i % 4] if full else ps[0:T, i % 4, 0:S], ACT.Exp,
                                                   bias=mx[:, n:n + 1], accum_out=den[:, n:n + 1]).then_inc(ac_p.step("exp", n), 1)
                if full:
                    for n in range(HU - LAG, HU):
                        turn(c, n)
                for u in range(U):
                    act.wait_ge(pe2.sem, pe2.at(c, "oT", u))
                    nc.scalar.copy(oT[:, u], ps[:, u, 0:KD * T]).then_inc(ac2.step("oT", u), 1)

        @block.tensor
        def _(ten):
            ten.wait_ge(run.arrived, run.loads)

            def qk(c, n):
                u, i = n // H, n % H
                b = i // HK
                if n >= 4:
                    if full:
                        ten.wait_ge(ve_k.sem, ve_k.at(c, "kept", n - 4))
                    else:
                        ten.wait_ge(ac_p.sem, ac_p.at(c, "exp", n - 4))
                if i % HK == 0:
                    ten.wait_ge(po_m.sem, po_m.at(c, "mq", KD * u + b))
                nc.tensor.matmul(ps[0:T, i % 4, 0:S], mq[:, b, i % HK * T:(i % HK + 1) * T], kT[:, u, b * S:(b + 1) * S],
                                           start=True, stop=True).then_inc(pe_e.step("e", n), 1)

            def turn(c, n):
                ten.wait_ge(ac_p.sem, ac_p.at(c, "exp", n))
                if n >= 2:
                    ten.wait_ge(turned.sem, turned.at(c, "pT", n - 2))
                for s in range(ST):
                    ins = nc.tensor.transpose(ps[0:SP_, 4 + n % 2, s * T:(s + 1) * T], p[:, n % 4, s * SP_:(s + 1) * SP_],
                                              core.ident[0:T, 0:T])
                ins.then_inc(pe_t.step("pT", n), 1)

            def pv(c, n):
                u, i = n // H, n % H
                if i == 0 and u >= 2:
                    ten.wait_ge(ve_o.sem, ve_o.at(c, "mul", u - 2))
                ten.wait_ge(turned.sem, turned.at(c, "pT", n))
                e = slice(i * HD, (i + 1) * HD)
                for s in range(ST):
                    ins = nc.tensor.matmul(ps[0:T, 6 + u % 2, e], pT[:, n % 2, s * T:(s + 1) * T],
                                           v[:, u, s * D + i * HD:s * D + (i + 1) * HD], start=(s == 0), stop=(s == ST - 1))
                ins.then_inc(pe_o.step("pv", n), 1)

            with ten.Fori(0, NCH) as c:
                for u in range(U):
                    ten.wait_ge(ve.sem, ve.at(c, "xn", u))
                    transposes(core, ps[:, u], xn[:, u], T, KD).then_inc(pe.step("xT", u), 1)
                if full:
                    for u in range(U):
                        ten.wait_ge(ac.sem, ac.at(c, "xT", u))
                        for k in range(KD):
                            nc.tensor.matmul(ps[0:T, 4 + u, 0:D], xT[:, u, k * T:(k + 1) * T], self.wq[:, k, :], start=(k == 0), stop=False)
                        nc.tensor.matmul(ps[0:T, 4 + u, 0:D], core.ones[0:1, 0:T], self.bq, start=False, stop=True).then_inc(pe.step("qp", u), 1)

                    def make_kv(u):
                        ten.wait_ge(loaded[u], (c + 1) * LOADS)
                        for s in range(ST):
                            g = ST * u + s
                            if g >= 4:
                                ten.wait_ge(ve.sem, ve.at(c, f"add{(g - 4) // ST}", 2 * ((g - 4) % ST) + 1))
                            for k in range(KD):
                                ins = nc.tensor.matmul(ps[0:SP_, g % 4, :], ctxT[:, u, k * S + s * SP_:k * S + (s + 1) * SP_], self.wkv[:, k, :],
                                                       start=(k == 0), stop=(k == KD - 1))
                            ins.then_inc(pe.step(f"kv{u}", s), 1)

                    def turn_k(u):
                        for m in range(KD):
                            if u >= 2:
                                ten.wait_ge(ac.sem, ac.at(c, f"kT{u - 2}", m))
                            else:
                                ten.wait_ge(ve.sem, ve.at(c, "q", U - 1))
                            for s in range(ST):
                                ten.wait_ge(ve.sem, ve.at(c, f"kn{u}", s))
                                ins = nc.tensor.transpose(ps[:, 4 + (KD * u + m) % 4, s * SP_:(s + 1) * SP_],
                                                          kn[:, ST * u + s, m * 128:(m + 1) * 128], core.ident[0:SP_, 0:SP_])
                            ins.then_inc(pe.step(f"kT{u}", m), 1)
                    make_kv(0)
                    make_kv(1)
                    for u in range(U):
                        ten.wait_ge(ve.sem, ve.at(c, "qn", u))
                        transposes(core, ps[:, 4 + u], qn[:, u], T, KD).then_inc(pe.step("qT", u), 1)
                    make_kv(2)
                    turn_k(0)
                    turn_k(1)
                    make_kv(3)
                    turn_k(2)
                    turn_k(3)
                else:
                    for u in range(U):
                        ten.wait_ge(ac.sem, ac.at(c, "xT", u))
                        for m in range(KD):
                            for k in range(KD):
                                ins = nc.tensor.matmul(ps[:, 4 + u, m * T:(m + 1) * T], self.wq[:, k, m * 128:(m + 1) * 128],
                                                       xT[:, u, k * T:(k + 1) * T], start=(k == 0), stop=(k == KD - 1))
                        ins.then_inc(pe.step("qT", u), 1)
                    for u in range(U):
                        ten.wait_ge(loaded[u], (c + 1) * LOADS)
                        for m in range(KD):
                            if u >= 2:
                                ten.wait_ge(ac.sem, ac.at(c, f"kT{u - 2}", m))
                            else:
                                ten.wait_ge(ve.sem, ve.at(c, "q", KD * u + m))
                            for k in range(KD):
                                ins = nc.tensor.matmul(ps[:, 4 + (KD * u + m) % 4, 0:S], self.wk[:, k, m * 128:(m + 1) * 128], ctxT[:, u, k * S:(k + 1) * S],
                                                       start=(k == 0), stop=(k == KD - 1))
                            ins.then_inc(pe.step(f"kT{u}", m), 1)
                    for u in range(U):
                        for i in range(2):
                            if 2 * u + i >= 4:
                                ten.wait_ge(ac.sem, ac.at(c, "v", 2 * u + i - 4))
                            for s in range(2 * i, min(2 * i + 2, ST)):
                                for k in range(KD):
                                    ins = nc.tensor.matmul(ps[0:SP_, (2 * u + i) % 4, (s % 2) * D:(s % 2 + 1) * D],
                                                           ctxT[:, u, k * S + s * SP_:k * S + (s + 1) * SP_], self.wv[:, k, :],
                                                           start=(k == 0), stop=(k == KD - 1))
                            ins.then_inc(pe.step("v", 2 * u + i), 1)
                ten.wait_ge(ac.sem, ac.at(c, *((f"kT{U - 1}", KD - 1) if full else ("v", 2 * U - 1))))
                for n in range(HU + LAG + 1):
                    if n < HU:
                        qk(c, n)
                    if LAG <= n < HU + LAG:
                        turn(c, n - LAG)
                    if n > LAG:
                        pv(c, n - LAG - 1)
                for u in range(U):
                    ten.wait_ge(ve_o.sem, ve_o.at(c, "o", u))
                    transposes(core, ps[:, u], o[:, u], T, KD).then_inc(pe2.step("oT", u), 1)
                for u in range(U):
                    ten.wait_ge(ac2.sem, ac2.at(c, "oT", u))
                    for k in range(KD):
                        nc.tensor.matmul(ps[0:T, 4 + u, 0:D], oT[:, u, k * T:(k + 1) * T], self.wo[:, k, :], start=(k == 0), stop=False)
                    nc.tensor.matmul(ps[0:T, 4 + u, 0:D], core.ones[0:1, 0:T], self.bo, start=False, stop=True).then_inc(pe2.step("out", u), 1)


class L2Cross(Cross):

    name, full = "L2_xattn", True

    def weights(self, a, d):
        n = self.name + "_"
        self.wq = a.load(rows(d[n + "Wq"]), 128, KD, D)
        self.wkv = a.take(128, KD, 2 * D)
        self.bkv = a.take(SP_, 2 * D)
        for i, k in enumerate("kv"):
            a.loads.append((self.wkv[:, :, i * D:(i + 1) * D], rows(d[n + "W" + k])))
            a.loads.append((self.bkv[:, i * D:(i + 1) * D], every(d[n + "b" + k], SP_)))
        self.wo = a.load(rows(d[n + "Wo"]), 128, KD, D)
        self.bq = a.load(every(d[n + "bq"], 1), 1, D)
        self.bo = a.load(every(d[n + "bo"], 1), 1, D)
        self.gain_q, self.shift_q = (a.load(d[n + "qn_" + k + "_c"], 128, KD) for k in ("scale", "bias"))
        self.gain_k, self.shift_k = (a.load(d[n + "kn_" + k + "_c"], 128, KD) for k in ("scale", "bias"))
        self.gain_v, self.shift_v = (a.load(every(d[n + "vn_" + k], T), T, D) for k in ("scale", "bias"))
        self.heads = a.load(d["heads"], 128, self.HK)
        self.kn = a.take(SP_, U * ST, D)


class L3Cross(Cross):
    name, full = "L3_xattn", False

    def weights(self, a, d):
        n = self.name + "_"
        self.wq, self.wk, self.wv, self.wo = (a.load(rows(d[n + "W" + k + "T"]), 128, KD, D) for k in "qkvo")
        self.bq, self.bk = (a.load(d[n + "b" + k + "_c"], 128, KD) for k in "qk")
        self.shift_v = a.load(every(d[n + "bv"], T), T, D)
        self.bo = a.load(every(d[n + "bo"], 1), 1, D)
        self.heads = a.load(d["heads"], 128, self.HK)


class Generated:

    def __init__(self, s0, s1, w, b, mix):
        self.s0, self.s1, self.w, self.b, self.mix = s0, s1, w, b, mix

    @staticmethod
    def mix_vector(core, dve, items, mixed):
        nc = core.nc
        for i in items:
            nc.vector.tensor_scalar(i.s0, i.s0, i.mix[:, 0:1], None, ALU.mult).then_inc(mixed, 1)
        for k, i in enumerate(items):
            dve.wait_ge(mixed, k + 1)
            nc.vector.scalar_tensor_tensor(out=i.s0, in0=i.s1, scalar=i.mix[:, 1:2], in1=i.s0,
                                           op0=ALU.mult, op1=ALU.add).then_inc(mixed, 1)

    @staticmethod
    def bend_scalar(core, act, items, mixed, bent):
        n = len(items)
        for k, i in enumerate(items):
            act.wait_ge(mixed, n + k + 1)
            core.nc.scalar.activation(i.s0, i.s0, ACT.Tanh).then_inc(bent, 1)

    @staticmethod
    def finish_vector(core, dve, items, mixed, bent):
        nc, n = core.nc, len(items)
        for k, i in enumerate(items):
            dve.wait_ge(bent, k + 1)
            nc.vector.tensor_tensor(i.s0, i.s0, i.w, ALU.mult).then_inc(mixed, 1)
        for k, i in enumerate(items):
            dve.wait_ge(mixed, 2 * n + k + 1)
            nc.vector.tensor_tensor(i.s0, i.s0, i.b, ALU.add).then_inc(mixed, 1)


def generated(load, d, name, pick, w, mix, late=None):
    kind = "w" if w else "b"
    turned = "T" if w else ""
    sub = d[f"{name}_sub_{kind}{turned}"]
    return Generated(load(pick(sub[0])), load(pick(sub[1])), load(pick(d[f"{name}_W_{kind}{turned}"])),
                     (late or load)(pick(d[f"{name}_B_{kind}{turned}"])), mix)


class L3Self:

    name = "L3_attn"
    H = 16
    HD = D // H
    HG = 8
    NG = U * H // HG

    def weights(self, a, d):
        n = self.name + "_"

        def flat(src, parts, k):
            cols = 1
            for s in src.shape[1:]:
                cols *= s
            v = a.take(parts, cols)
            a.loads.append((v.rearrange("p (k n) -> p k n", k=k) if k else v, src))
            return v
        mat = lambda s: flat(rows(s), 128, KD)
        row = lambda s: flat(s.rearrange("(a n) -> a n", a=1), 1, 0)
        mix = {(p, k): a.load(every(d[n + p + "_Wl_" + k], 128), 128, 2) for p in ("ca", "cp") for k in "wb"}
        self.ca = generated(mat, d, n + "ca", lambda s: s, True, mix["ca", "w"])
        self.cp = generated(mat, d, n + "cp", lambda s: s, True, mix["cp", "w"])
        col_d = {k: d[k + "_cols"] for k in (n + "ca_sub_b", n + "ca_W_b", n + "ca_B_b")}
        self.bqk = generated(lambda s: flat(s, 128, 0), col_d_named(col_d, n + "ca"), n + "ca", lambda s: s[:, 0:2 * KD], False, mix["ca", "b"])
        self.bv = generated(row, d, n + "ca", lambda s: s[2 * D:3 * D], False, mix["ca", "b"][0:1, :])
        self.bp = generated(row, d, n + "cp", lambda s: s, False, mix["cp", "b"][0:1, :])
        self.gain, self.shift = (a.load(d[n + "ln1_" + k + "_c"], 128, KD) for k in "gb")
        self.heads = a.load(d["heads"], 128, self.HG)

    def build(self, core, run):
        nc, ps, H, HD, HG, NG = core.nc, core.ps, self.H, self.HD, self.HG, self.NG
        sb = run.sbuf
        h, hT = sb("h", [T, U, D]), sb("hT", [128, KD, N4])
        qk = sb("qk", [128, 2 * KD, N4])
        v = sb("v", [T, U, H, HD + 1])
        mq = sb("mq", [128, 3, HG * T])
        p, pT = sb("p", [T, 4, HG * T]), sb("pT", [T, 2, HG * T])
        mx, rden = sb("mx", [T, NG, HG]), sb("rden", [T, U, H])
        o, oT = h, hT
        ca = self.ca.s0.rearrange("p (k n) -> p k n", k=KD)
        cp = self.cp.s0.rearrange("p (k n) -> p k n", k=KD)
        first_items, last_items = [self.ca, self.bqk, self.bv], [self.cp, self.bp]
        norm = core.semaphore("norm")
        mixed1, bent1, mixed2, bent2 = (core.semaphore(n) for n in ("mixed1", "bent1", "mixed2", "bent2"))
        quarter, filled = core.semaphore("quarter"), core.semaphore("filled")
        ln = Norm(core, run, "ln")
        pe = Progress(core, "tensor", ("hT", KD), ("qk", 2 * KD), "v")
        ac = Progress(core, "scalar", ("hT", KD), ("qk", 2 * KD), "v")
        ve = Progress(core, "vector", "xn", *ln.steps(), "hn")
        po = Progress(core, "pool", ("lnrs", 1))
        pe_e, pe_t, pe_o = Progress(core, "tensor_e", ("e", NG)), Progress(core, "tensor_pT", ("pT", 2 * NG)), Progress(core, "tensor_pv", ("pv", NG))
        po_q, po_c = Progress(core, "pool_mq", ("mq", NG)), Progress(core, "pool_causal", ("causal", NG))
        ve_m, ve_s = Progress(core, "vector_max", ("max", NG)), Progress(core, "vector_sub", ("sub", NG))
        ac_s = Progress(core, "scalar_e", ("scores", NG))
        ac_e, ac_t = Progress(core, "scalar_exp", ("exp", NG)), Progress(core, "scalar_pT", ("pT", 2 * NG))
        ve_r, ve_o = Progress(core, "vector_rden", "rden"), Progress(core, "vector_o", "o")
        ve_y = Progress(core, "vector_y", "y")
        pe2, ac2 = Progress(core, "tensor2", "oT", "out"), Progress(core, "scalar2", "oT")
        block = run.block
        by_head = lambda t: t.rearrange("p (h s) -> p h s", s=T)
        HB = HG // 2 * T

        def group(n):
            return ps[0:T, 2 * (n % 2):2 * (n % 2) + 2, 0:HB]

        @block.gpsimd
        def _(pool):
            norm_pool(core, norm)
            nc.gpsimd.memset(v[:, :, :, HD:HD + 1], 1.0).then_inc(filled, 1)
            pool.wait_ge(run.arrived, run.loads)

            def attend(c):
                def heads_of(n):
                    u, b = n // KD, n % KD
                    if n >= 3:
                        pool.wait_ge(pe_e.sem, pe_e.at(c, "e", n - 3))
                    pool.wait_ge(ac.sem, ac.at(c, "qk", b))
                    nc.gpsimd.tensor_tensor(by_head(mq[:, n % 3]), qk[:, b, u * T:(u + 1) * T].unsqueeze(1).to_broadcast([128, HG, T]),
                                                      self.heads.unsqueeze(2).to_broadcast([128, HG, T]), ALU.mult).then_inc(po_q.step("mq", n), 1)

                def causal(n):
                    pool.wait_ge(ac_s.sem, ac_s.at(c, "scores", n))
                    core.stand(pool)
                    nc.gpsimd.affine_select(p[:, n % 4], p[:, n % 4], pattern=[[0, HG], [-1, T]],
                                                      compare_op=ALU.is_ge, fill=-1e4, base=0, channel_multiplier=1).then_inc(po_c.step("causal", n), 1)
                for n in range(NG):
                    heads_of(n)
                    if n >= 1:
                        causal(n - 1)
                causal(NG - 1)
            ln.pool(pool, ve, po, 0)
            with pool.Fori(0, NCH - 1) as c:
                attend(c)
                ln.pool(pool, ve, po, c + 1)
            attend(NCH - 1)

        @block.vector
        def _(dve):
            norm_vector(core, dve, norm)
            dve.wait_ge(run.arrived, run.loads)
            Generated.mix_vector(core, dve, first_items, mixed1)
            Generated.mix_vector(core, dve, last_items, mixed2)
            Generated.finish_vector(core, dve, first_items, mixed1, bent1)
            dve.wait_ge(mixed1, 4 * len(first_items))
            nc.vector.tensor_scalar(self.bqk.s0[:, 0:KD], self.bqk.s0[:, 0:KD], HD ** -0.5, None, ALU.mult).then_inc(quarter, 1)

            def norms(c, first):
                for u in range(U):
                    normed(core, core.y[:, U * c + u, :], U * c + u).then_inc(ve.step("xn", u), 1)

                def made(u):
                    dve.wait_ge(ve.sem, ve.at(c, "xn", u))
                    core.stand(dve)
                ln.vector(dve, ve, c, lambda u, q: core.y[:, U * c + u, :], made)
                dve.wait_ge(po.sem, po.at(c, "lnrs"))
                core.stand(dve)
                if not first:
                    dve.wait_ge(pe2.sem, pe2.at(c - 1, "oT", U - 1))
                    core.stand(dve)
                for u in range(U):
                    ln.apply(h[:, u], core.y[:, U * c + u, :], u).then_inc(ve.step("hn", u), 1)

            def probabilities(c):
                def divide(u):
                    dve.wait_ge(pe_o.sem, pe_o.at(c, "pv", KD * u + KD - 1))
                    heads = ps[0:T, 6 + u % 2, 0:H * (HD + 1)].rearrange("p (h e) -> p h e", h=H)
                    nc.vector.reciprocal(rden[:, u, :], heads[:, :, HD]).then_inc(ve_r.step("rden", u), 1)
                    dve.wait_ge(ve_r.sem, ve_r.at(c, "rden", u))
                    nc.vector.tensor_tensor(o[:, u].rearrange("p (h e) -> p h e", h=H), heads[:, :, 0:HD],
                                                      rden[:, u, :].unsqueeze(2).to_broadcast([T, H, HD]), ALU.mult).then_inc(ve_o.step("o", u), 1)
                for n in range(NG):
                    dve.wait_ge(po_c.sem, po_c.at(c, "causal", n))
                    nc.vector.tensor_reduce(mx[:, n, :], by_head(p[:, n % 4]), AX.X, ALU.max).then_inc(ve_m.step("max", n), 1)
                    dve.wait_ge(ve_m.sem, ve_m.at(c, "max", n))
                    nc.vector.tensor_tensor(by_head(p[:, n % 4]), by_head(p[:, n % 4]),
                                                      mx[:, n, :].unsqueeze(2).to_broadcast([T, HG, T]), ALU.subtract).then_inc(ve_s.step("sub", n), 1)
                    if n % KD == 1 and n >= 5:
                        divide((n - 5) // KD)
                for u in range((NG - 5) // KD + 1, U):
                    divide(u)

            def outputs(c):
                for u in range(U):
                    dve.wait_ge(pe2.sem, pe2.at(c, "out", u))
                    core.stand(dve)
                    y = core.y[:, U * c + u, :]
                    nc.vector.tensor_tensor(y, y, ps[0:T, 4 + u if u < 2 else u % 2, 0:D], ALU.add).then_inc(ve_y.step("y", u), 1)
            norms(0, True)
            Generated.finish_vector(core, dve, last_items, mixed2, bent2)
            with dve.Fori(0, NCH - 1) as c:
                probabilities(c)
                norms(c + 1, False)
                outputs(c)
            probabilities(NCH - 1)
            outputs(NCH - 1)

        @block.scalar
        def _(act):
            run.prefetch(act)
            act.wait_ge(run.arrived, run.loads)
            Generated.bend_scalar(core, act, first_items, mixed1, bent1)
            Generated.bend_scalar(core, act, last_items, mixed2, bent2)
            act.wait_ge(quarter, 1)
            act.wait_ge(filled, 1)
            with act.Fori(0, NCH) as c:
                for k in range(KD):
                    act.wait_ge(pe.sem, pe.at(c, "hT", k))
                    nc.scalar.activation(hT[:, k], ps[:, 2 + k, 0:N4], ACT.Identity, bias=self.shift[:, k:k + 1],
                                                 scale=self.gain[:, k:k + 1]).then_inc(ac.step("hT", k), 1)
                for m in range(2 * KD):
                    act.wait_ge(pe.sem, pe.at(c, "qk", m))
                    nc.scalar.activation(qk[:, m], ps[:, 2 + m, 0:N4], ACT.Identity, bias=self.bqk.s0[:, m:m + 1],
                                                 scale=HD ** -0.5 if m < KD else 1.0).then_inc(ac.step("qk", m), 1)
                for u in range(U):
                    act.wait_ge(pe.sem, pe.at(c, "v", u))
                    nc.scalar.copy(v[:, u, :, 0:HD], ps[0:T, (6 + u) % 8, 0:D].rearrange("p (h e) -> p h e", h=H)).then_inc(ac.step("v", u), 1)

                def turn(n):
                    if n >= 2:
                        act.wait_ge(pe_o.sem, pe_o.at(c, "pv", n - 2))
                    for b in range(2):
                        act.wait_ge(pe_t.sem, pe_t.at(c, "pT", 2 * n + b))
                        nc.scalar.copy(pT[:, n % 2, b * HB:(b + 1) * HB], ps[0:T, 4 + b, 0:HB]).then_inc(ac_t.step("pT", 2 * n + b), 1)
                def scores(n):
                    if n >= 4:
                        act.wait_ge(pe_t.sem, pe_t.at(c, "pT", 2 * (n - 4) + 1))
                    act.wait_ge(pe_e.sem, pe_e.at(c, "e", n))
                    nc.scalar.copy(p[:, n % 4].rearrange("p (b s) -> p b s", b=2), group(n)).then_inc(ac_s.step("scores", n), 1)

                def exp(n):
                    act.wait_ge(ve_s.sem, ve_s.at(c, "sub", n))
                    nc.scalar.activation(p[:, n % 4], p[:, n % 4], ACT.Exp).then_inc(ac_e.step("exp", n), 1)
                for n in range(NG + 3):
                    if n < NG:
                        scores(n)
                    if 2 <= n < NG + 2:
                        exp(n - 2)
                    if n >= 3:
                        turn(n - 3)
                for u in range(U):
                    act.wait_ge(pe2.sem, pe2.at(c, "oT", u))
                    nc.scalar.copy(oT[:, :, u * T:(u + 1) * T], ps[:, 2 + u % 2, 0:KD * T].rearrange("p (k t) -> p k t", k=KD)).then_inc(ac2.step("oT", u), 1)

        @block.tensor
        def _(ten):
            ten.wait_ge(run.arrived, run.loads)
            ten.wait_ge(mixed1, 4 * len(first_items))

            def attend(c, first):
                for k in range(KD):
                    for u in range(U):
                        if k == 0:
                            ten.wait_ge(ve.sem, ve.at(c, "hn", u))
                        ins = nc.tensor.transpose(ps[:, 2 + k, u * T:(u + 1) * T], h[:, u, k * 128:(k + 1) * 128], core.ident[0:T, 0:T])
                    ins.then_inc(pe.step("hT", k), 1)
                ten.wait_ge(ac.sem, ac.at(c, "hT", KD - 1))
                for m in range(2 * KD):
                    if m == 2 and not first:
                        ten.wait_ge(ve_y.sem, ve_y.at(c - 1, "y", U - 1))
                        core.stand(ten)
                    for k in range(KD):
                        ins = nc.tensor.matmul(ps[:, 2 + m, 0:N4], ca[:, k, m * 128:(m + 1) * 128], hT[:, k], start=(k == 0), stop=(k == KD - 1))
                    ins.then_inc(pe.step("qk", m), 1)
                for u in range(U):
                    for k in range(KD):
                        nc.tensor.matmul(ps[0:T, (6 + u) % 8, 0:D], hT[:, k, u * T:(u + 1) * T], ca[:, k, 2 * D:3 * D], start=(k == 0), stop=False)
                    nc.tensor.matmul(ps[0:T, (6 + u) % 8, 0:D], core.ones[0:1, 0:T], self.bv.s0, start=False, stop=True).then_inc(pe.step("v", u), 1)

                def scores(n):
                    u, b = n // KD, n % KD
                    if n >= 2:
                        ten.wait_ge(ac_s.sem, ac_s.at(c, "scores", n - 2))
                    if n < 2:
                        ten.wait_ge(ac.sem, ac.at(c, "v", U - 1))
                    ten.wait_ge(po_q.sem, po_q.at(c, "mq", n))
                    for i in range(HG):
                        ins = nc.tensor.matmul(ps[0:T, 2 * (n % 2) + 2 * i // HG, i % (HG // 2) * T:(i % (HG // 2) + 1) * T], mq[:, n % 3, i * T:(i + 1) * T],
                                               qk[:, KD + b, u * T:(u + 1) * T], start=True, stop=True)
                    ins.then_inc(pe_e.step("e", n), 1)

                def turn(n):
                    ten.wait_ge(ac_e.sem, ac_e.at(c, "exp", n))
                    for b in range(2):
                        if n >= 1:
                            ten.wait_ge(ac_t.sem, ac_t.at(c, "pT", 2 * n + b - 2))
                        for i in range(HG // 2):
                            k = HG // 2 * b + i
                            ins = nc.tensor.transpose(ps[0:T, 4 + b, i * T:(i + 1) * T], p[:, n % 4, k * T:(k + 1) * T], core.ident[0:T, 0:T])
                        ins.then_inc(pe_t.step("pT", 2 * n + b), 1)

                def pv(n):
                    u, b = n // KD, n % KD
                    ten.wait_ge(ac_t.sem, ac_t.at(c, "pT", 2 * n + 1))
                    if b == 0 and u >= 2:
                        ten.wait_ge(ve_o.sem, ve_o.at(c, "o", u - 2))
                    for i in range(HG):
                        k = HG * b + i
                        ins = nc.tensor.matmul(ps[0:T, 6 + u % 2, k * (HD + 1):(k + 1) * (HD + 1)], pT[:, n % 2, i * T:(i + 1) * T], v[:, u, k, :],
                                               start=True, stop=True)
                    ins.then_inc(pe_o.step("pv", n), 1)
                for n in range(NG + 4):
                    if n < NG:
                        scores(n)
                    if 3 <= n < NG + 3:
                        turn(n - 3)
                    if n >= 4:
                        pv(n - 4)
                for u in range(U):
                    ten.wait_ge(ve_o.sem, ve_o.at(c, "o", u))
                    if u >= 2:
                        ten.wait_ge(ac2.sem, ac2.at(c, "oT", u - 2))
                    transposes(core, ps[:, 2 + u % 2], o[:, u], T, KD).then_inc(pe2.step("oT", u), 1)
                if first:
                    ten.wait_ge(mixed2, 4 * len(last_items))
                for u in range(U):
                    ten.wait_ge(ac2.sem, ac2.at(c, "oT", u))
                    bank = 4 + u if u < 2 else u % 2
                    for k in range(KD):
                        nc.tensor.matmul(ps[0:T, bank, 0:D], oT[:, k, u * T:(u + 1) * T], cp[:, k, :], start=(k == 0), stop=False)
                    nc.tensor.matmul(ps[0:T, bank, 0:D], core.ones[0:1, 0:T], self.bp.s0, start=False, stop=True).then_inc(pe2.step("out", u), 1)
            attend(0, True)
            with ten.Fori(1, NCH) as c:
                attend(c, False)


def col_d_named(arrays, name):
    return {f"{name}_sub_b": [arrays[f"{name}_sub_b"][:, i, :] for i in range(2)],
            f"{name}_W_b": arrays[f"{name}_W_b"], f"{name}_B_b": arrays[f"{name}_B_b"]}


class L3Mlp(Mlp):

    name = "L3_mlp"
    act = ACT.Gelu_apprx_tanh

    def weights(self, a, d):
        n = "L3_attn_"
        self.late = []

        def flat(src, parts, k):
            cols = 1
            for s in src.shape[1:]:
                cols *= s
            v = a.take(parts, cols)
            a.loads.append((v.rearrange("p (k n) -> p k n", k=k) if k else v, src))
            return v
        later = lambda src: self.late.append(src)
        mix = {(p, k): a.load(every(d[n + p + "_Wl_" + k], 128), 128, 2) for p in ("cf", "cm") for k in "wb"}
        self.cf = generated(lambda s: flat(rows(s), 128, KD), d, n + "cf", lambda s: s, True, mix["cf", "w"], later)
        self.cm = generated(lambda s: flat(rows(s), 128, self.HK), d, n + "cm", lambda s: s, True, mix["cm", "w"], later)
        col_d = {k: d[k + "_cols"] for k in (n + "cf_sub_b", n + "cf_W_b", n + "cf_B_b")}
        self.bf = generated(lambda s: flat(s, 128, 0), col_d_named(col_d, n + "cf"), n + "cf", lambda s: s, False, mix["cf", "b"])
        self.bm = generated(later, d, n + "cm", lambda s: s, False, mix["cm", "b"][0:1, :])
        self.gain, self.shift = (a.load(d[n + "ln2_" + k + "_c"], 128, KD) for k in "gb")

    def prepare(self, core, run):
        sb, late = run.sbuf, self.late
        self.cf.b, self.cm.b = sb("cf_b", [128, KD * self.H])[:, :], sb("cm_b", [128, self.HK * D])[:, :]
        row = sb("bm", [1, 4, D])
        self.bm.s0, self.bm.s1, self.bm.w, self.bm.b = (row[:, i, :] for i in range(4))
        self.first_items, self.last_items = [self.cf, self.bf], [self.cm, self.bm]
        self.w1 = self.cf.s0.rearrange("p (k n) -> p k n", k=KD)
        self.w2 = self.cm.s0.rearrange("p (k n) -> p k n", k=self.HK)
        self.b1, self.b2 = self.bf.s0, self.bm.s0
        self.mixed1, self.bent1, self.mixed2, self.bent2 = (core.semaphore(n) for n in ("mixed1", "bent1", "mixed2", "bent2"))
        self.rows_arrived, self.added_arrived = core.semaphore("rows_arrived"), core.semaphore("added_arrived")

        @run.block.sync
        def _(sp):
            for i in range(4):
                sp.dma_start(row[:, i, :], late[2 + i].rearrange("(a n) -> a n", a=1)).then_inc(self.rows_arrived, DMA)
            sp.dma_start(self.cf.b.rearrange("p (k n) -> p k n", k=KD), rows(late[0])).then_inc(self.added_arrived, DMA)
            sp.dma_start(self.cm.b.rearrange("p (k n) -> p k n", k=self.HK), rows(late[1])).then_inc(self.added_arrived, DMA)

    def prepare_vector(self, core, run, dve):
        dve.wait_ge(run.arrived, run.loads)
        dve.wait_ge(self.rows_arrived, 4 * DMA)
        Generated.mix_vector(core, dve, self.first_items, self.mixed1)
        Generated.mix_vector(core, dve, self.last_items, self.mixed2)
        dve.wait_ge(self.added_arrived, 2 * DMA)
        Generated.finish_vector(core, dve, self.first_items, self.mixed1, self.bent1)

    def prepare_vector_late(self, core, run, dve):
        Generated.finish_vector(core, dve, self.last_items, self.mixed2, self.bent2)

    def prepare_scalar(self, core, run, act):
        run.prefetch(act)
        Generated.bend_scalar(core, act, self.first_items, self.mixed1, self.bent1)
        Generated.bend_scalar(core, act, self.last_items, self.mixed2, self.bent2)
        act.wait_ge(self.mixed1, 4 * len(self.first_items))

    def prepare_tensor(self, core, run, ten):
        ten.wait_ge(self.mixed1, 4 * len(self.first_items))

    def prepare_tensor_late(self, core, run, ten):
        ten.wait_ge(self.mixed2, 4 * len(self.last_items))


class L3Feed:

    name = "L3_ffn"
    H = 1024
    HK = H // 128

    def weights(self, a, d):
        self.fc = a.load(rows(d["L3_ffn_W_fcT"]), 128, KD, self.H)
        self.pr = a.load(rows(d["L3_ffn_W_projT"]), 128, self.HK, D)
        self.lw = a.load(d["L3_ffn_ln_w_c"], 128, self.HK)
        self.lb = a.load(d["L3_ffn_ln_b_c"], 128, self.HK)

    def build(self, core, run):
        nc, ps, H, HK = core.nc, core.ps, self.H, self.HK
        sb = run.sbuf
        mats = [self.fc.rearrange("p k n -> p (k n)"), self.pr.rearrange("p k n -> p (k n)")]
        size = [sb(f"size{i}", [128, KD * H]) for i in range(2)]
        total, high, low = sb("total", [128, 2]), sb("high", [128, 2]), sb("low", [128, 2])
        brow = sb("brow", [1, D])
        xn, xT = sb("xn", [T, U, D]), sb("xT", [128, U, KD * T])
        h, hT = sb("h", [T, U, H]), sb("hT", [128, U, HK * T])
        norm, tern, tern_pe = core.semaphore("norm"), core.semaphore("tern"), core.semaphore("tern_pe")
        sized, written = core.semaphore("sized"), core.semaphore("written")
        W = U // 2
        lns = [Norm(core, run, f"ln{i}", parts=2, units=W) for i in range(2)]
        pe = Progress(core, "tensor", "xT", ("up", 2 * U), ("hT", 2 * U), "out")
        ac = Progress(core, "scalar", "xT", ("gelu", 2 * U), ("hT", 2 * U))
        ve_x, ve_o = Progress(core, "vector_xn", "xn"), Progress(core, "vector_out", "out")
        ve = Progress(core, "vector", *(x for i in range(2) for x in (*lns[i].steps(), (f"hn{i}", W))))
        po = Progress(core, "pool", ("ln0rs", 1), ("ln1rs", 1))
        block = run.block

        @block.sync
        def _(sp):
            with sp.Fori(0, NCH) as c:
                sp.wait_ge(ve_o.sem, ve_o.at(c, "out", U - 1))
                core.stand(sp)
                sp.dma_start(core.out[:, bass.ds(U * c, U), :], core.x[:, bass.ds(U * c, U), :]).then_inc(written, DMA)
            sp.wait_ge(written, DMA * NCH)

        @block.gpsimd
        def _(pool):
            norm_pool(core, norm)
            with pool.Fori(0, NCH) as c:
                for ln in lns:
                    ln.pool(pool, ve, po, c)

        @block.vector
        def _(dve):
            dve.wait_ge(run.arrived, run.loads)
            dve.wait_ge(tern_pe, 1)
            nc.vector.tensor_scalar(high[:, :], ps[:, 7, 0:2], 1.0 / (D * H), 1e-6, ALU.mult, ALU.add).then_inc(tern, 1)
            dve.wait_ge(tern, 1)
            nc.vector.tensor_scalar(low[:, :], high[:, :], -0.5, None, ALU.mult).then_inc(tern, 1)
            nc.vector.tensor_scalar(total[:, :], high[:, :], 0.5, None, ALU.mult).then_inc(tern, 1)
            dve.wait_ge(tern, 3)
            for i in range(2):
                nc.vector.tensor_scalar(size[i][:, :], mats[i], low[:, i:i + 1], None, ALU.is_lt).then_inc(tern, 1)
                nc.vector.tensor_scalar(mats[i], mats[i], total[:, i:i + 1], None, ALU.is_gt).then_inc(tern, 1)
                dve.wait_ge(tern, 5 + 3 * i)
                nc.vector.tensor_tensor(mats[i], mats[i], size[i][:, :], ALU.subtract).then_inc(tern, 1)
            dve.wait_ge(tern_pe, 2)
            nc.vector.tensor_copy(brow[:, :], ps[0:1, 6, 0:D]).then_inc(tern, 1)
            for i in range(HK):
                ins = nc.vector.tensor_scalar(self.pr[:, i, :], self.pr[:, i, :], self.lw[:, i:i + 1], None, ALU.mult)
                ins.then_inc(tern, 1)
            norm_vector(core, dve, norm)

            def normalise(c, first):
                if not first:
                    dve.wait_ge(pe.sem, pe.at(c - 1, "xT", U - 1))
                    core.stand(dve)
                for u in range(U):
                    normed(core, xn[:, u], U * c + u).then_inc(ve_x.step("xn", u), 1)

            def hidden_norms(c):
                for i, ln in enumerate(lns):
                    ln.vector(dve, ve, c, lambda u, q: h[:, W * i + u, q * 512:(q + 1) * 512],
                              lambda u: dve.wait_ge(ac.sem, ac.at(c, "gelu", 2 * (W * i + u) + 1)))
                    dve.wait_ge(po.sem, po.at(c, f"ln{i}rs"))
                    for u in range(W):
                        ln.apply(h[:, W * i + u], h[:, W * i + u], u).then_inc(ve.step(f"hn{i}", u), 1)

            def outputs(c):
                for u in range(U):
                    dve.wait_ge(pe.sem, pe.at(c, "out", u))
                    core.stand(dve)
                    x = core.x[:, U * c + u, :]
                    nc.vector.tensor_tensor(x, x, ps[0:T, u, 0:D], ALU.add).then_inc(ve_o.step("out", u), 1)
            normalise(0, True)
            with dve.Fori(0, NCH - 1) as c:
                hidden_norms(c)
                normalise(c + 1, False)
                outputs(c)
            hidden_norms(NCH - 1)
            outputs(NCH - 1)

        @block.scalar
        def _(act):
            run.prefetch(act)
            act.wait_ge(run.arrived, run.loads)
            for i in range(2):
                nc.scalar.activation(size[i][:, :], mats[i], ACT.Abs, accum_out=total[:, i:i + 1]).then_inc(sized, 1)
            with act.Fori(0, NCH) as c:
                for u in range(U):
                    act.wait_ge(pe.sem, pe.at(c, "xT", u))
                    nc.scalar.copy(xT[:, u], ps[:, u, 0:KD * T]).then_inc(ac.step("xT", u), 1)
                for u in range(U):
                    for q in range(2):
                        act.wait_ge(pe.sem, pe.at(c, "up", 2 * u + q))
                        nc.scalar.activation(h[:, u, q * 512:(q + 1) * 512], ps[0:T, 4 + (2 * u + q) % 4, :], ACT.Gelu).then_inc(ac.step("gelu", 2 * u + q), 1)
                for u in range(U):
                    for q in range(2):
                        act.wait_ge(pe.sem, pe.at(c, "hT", 2 * u + q))
                        w = HK // 2 * T
                        nc.scalar.copy(hT[:, u, q * w:(q + 1) * w], ps[:, 4 + (2 * u + q) % 4, 0:w]).then_inc(ac.step("hT", 2 * u + q), 1)

        @block.tensor
        def _(ten):
            ten.wait_ge(run.arrived, run.loads)
            ten.wait_ge(sized, 2)
            nc.tensor.matmul(ps[:, 7, 0:2], core.ones[:, :], total[:, :], start=True, stop=True).then_inc(tern_pe, 1)
            ten.wait_ge(tern, 9)
            for i in range(HK):
                ins = nc.tensor.matmul(ps[0:1, 6, 0:D], self.lb[:, i:i + 1], self.pr[:, i, :], start=(i == 0), stop=(i == HK - 1))
            ins.then_inc(tern_pe, 1)
            ten.wait_ge(tern, 10 + HK)

            def feed(c, first):
                for u in range(U):
                    ten.wait_ge(ve_x.sem, ve_x.at(c, "xn", u))
                    if not first:
                        core.stand(ten)
                        ten.wait_ge(ve_o.sem, ve_o.at(c - 1, "out", u))
                        core.stand(ten)
                    transposes(core, ps[:, u], xn[:, u], T, KD).then_inc(pe.step("xT", u), 1)
                for u in range(U):
                    ten.wait_ge(ac.sem, ac.at(c, "xT", u))
                    for q in range(2):
                        if u >= 2:
                            ten.wait_ge(ac.sem, ac.at(c, "gelu", 2 * u + q - 4))
                        for k in range(KD):
                            ins = nc.tensor.matmul(ps[0:T, 4 + (2 * u + q) % 4, :], xT[:, u, k * T:(k + 1) * T],
                                                   self.fc[:, k, q * 512:(q + 1) * 512], start=(k == 0), stop=(k == KD - 1))
                        ins.then_inc(pe.step("up", 2 * u + q), 1)

                def turn(u):
                    ten.wait_ge(ve.sem, ve.at(c, f"hn{u // W}", u % W))
                    for q in range(2):
                        ten.wait_ge(ac.sem, ac.at(c, "hT", 2 * u + q - 4) if u >= 2 else ac.at(c, "gelu", 2 * u + q + 4))
                        transposes(core, ps[:, 4 + (2 * u + q) % 4], h[:, u, q * 512:(q + 1) * 512], T, HK // 2).then_inc(pe.step("hT", 2 * u + q), 1)

                def down(u):
                    ten.wait_ge(ac.sem, ac.at(c, "hT", 2 * u + 1))
                    for i in range(HK):
                        nc.tensor.matmul(ps[0:T, u, 0:D], hT[:, u, i * T:(i + 1) * T], self.pr[:, i, :],
                                         start=(i == 0), stop=False)
                    return nc.tensor.matmul(ps[0:T, u, 0:D], core.ones[0:1, 0:T], brow[:, :], start=False, stop=True)
                for u in range(U):
                    turn(u)
                for u in range(U):
                    down(u).then_inc(pe.step("out", u), 1)
            feed(0, True)
            with ten.Fori(1, NCH) as c:
                feed(c, False)


class Run:

    def __init__(self, core, stack, block, own, ahead):
        self.core, self.stack, self.block, self.ahead = core, stack, block, ahead
        self.arrived, self.loads = own[0], DMA * len(own[1].loads)

    def sbuf(self, name, shape, dt=F32):
        return self.stack.enter_context(self.core.nc.sbuf_tensor(f"{self.core.stage}_{name}", shape, dt))

    def prefetch(self, eng):
        if self.ahead:
            sem, arena = self.ahead
            for dst, src in arena.loads:
                eng.dma_start(dst, src).then_inc(sem, DMA)


STAGES = [L0Banded, L0Cross, L0Mlp, L0Kron, L1State, L1Cross, L1Experts, L2Graph, L2Cross, L2Experts, L3Self, L3Mlp, L3Cross, L3Feed]


def runs(numbers):
    out = []
    for n in sorted(numbers):
        if out and out[-1][1] == n:
            out[-1][1] = n + 1
        else:
            out.append([n, n + 1])
    return out


def program(nc, d, out, stages):
    with ExitStack() as stack:
        core = Core(nc, d, stack)
        core.out = out.rearrange("b t c -> t b c")
        stages = [s() for s in stages]
        fetched = []
        for i, s in enumerate(stages):
            core.stage = s.name
            arena = Arena(core, i % 2)
            s.weights(arena, d)
            fetched.append((core.semaphore("weights"), arena))
        core.stage = "begin"
        x_in, x_stats = [core.semaphore(f"x_in{c}") for c in range(NCH)], core.semaphore("x_stats")
        first = core.semaphore("ident")
        with nc.Block() as block:
            @block.sync
            def _(sp):
                for c in range(NCH):
                    sp.dma_start(core.x[:, U * c:U * c + U, :], d["x"][U * c:U * c + U].rearrange("b t c -> t b c")).then_inc(x_in[c], DMA)
                sp.dma_start(core.ident[:, :], d["ident"]).then_inc(first, DMA)
                sem, arena = fetched[0]
                for dst, src in arena.loads:
                    sp.dma_start(dst, src).then_inc(sem, DMA)

            @block.gpsimd
            def _(pool):
                nc.gpsimd.memset(core.mhalf[:, :], -0.5)
                pool.wait_ge(first, DMA)
                nc.gpsimd.memset(core.ones[:, :], 1.0).then_inc(core.constants, 1)

            @block.vector
            def _(dve):
                for n in range(NB):
                    if n % U == 0:
                        dve.wait_ge(x_in[n // U], DMA)
                    nc.vector.bn_stats(core.stats[:, n, :], core.x[:, n, :]).then_inc(x_stats, 1)
                dve.wait_ge(x_stats, NB)
                dve.wait_ge(core.constants, 1)
        before, used = ExitStack(), []
        for i, s in enumerate(stages):
            core.stage, core.stack, core.open = s.name, ExitStack(), []
            with ExitStack() as own, nc.Block() as block:
                if used:
                    @block.gpsimd
                    def _(pool):
                        for first, stop in runs(used):
                            nc.gpsimd.sem_clear(range(first, stop))
                ahead = fetched[i + 1] if i + 1 < len(stages) else None
                s.build(core, Run(core, own, block, fetched[i], ahead))
            before.close()
            before, used = core.stack, core.open
        stack.push(before)
        if stages[-1].name == L3Feed.name:
            return
        core.stack = stack
        core.stage = "end"
        written = core.semaphore("written")
        with nc.Block() as block:
            @block.sync
            def _(sp):
                sp.dma_start(out.rearrange("b t c -> t b c"), core.x[:, :, :]).then_inc(written, DMA)
                sp.wait_ge(written, DMA)


def layout(inputs):
    import numpy as np
    i = {k: np.asarray(v) for k, v in inputs.items()}
    a = {k: v for k, v in i.items() if k not in ("ctx_1024", "mask_BxSxS2_ik0")}
    a["ctx"] = i["ctx_1024"]
    a["ctxT"] = i["ctx_1024"].transpose(0, 2, 1)
    a["mask"] = i["mask_BxSxS2_ik0"]
    a["ident"] = np.eye(128, dtype=np.float32)
    a["L1_attn_AT"] = i["L1_attn_A"].T
    a["heads"] = np.kron(np.eye(8), np.ones((16, 1))).astype(np.float32)
    for k in list(a):
        if a[k].ndim == 1 and a[k].size % 128 == 0:
            a[k + "_c"] = a[k].reshape(-1, 128).T
    bias, scales = a.pop("L0_attn_pos_bias"), a.pop("L0_attn_scale_embed")
    a["L0_attn_bias"] = bias[list(L0Banded.ROWS)].reshape(-1)
    a["L0_attn_scales"] = np.tile(scales[list(L0Banded.ROWS)].T, (L0Banded.HK, 1))
    a["iota"] = np.arange(64, dtype=np.float32)
    a["token"] = np.arange(NB * T, dtype=np.float32).reshape(NB, T).T
    a["before"] = np.triu(np.ones((128, 128), np.float32), 1)
    a["upto"] = np.triu(np.ones((128, 128), np.float32))
    a["L1_ffn_router"] = np.concatenate([a.pop("L1_ffn_Wg"), a.pop("L1_ffn_Wsg")])
    turn = lambda v: np.swapaxes(v, -1, -2)
    for k in ("up", "down"):
        a["L0_ffn_" + k] = np.concatenate([turn(a.pop(f"L0_ffn_{m}_{k}")) for m in "AB"], axis=2)
        a["L0_ffn_" + k] = a["L0_ffn_" + k].reshape(-1, a["L0_ffn_" + k].shape[2])
    a["L0_ffn_W_downP"] = a.pop("L0_ffn_W_down").reshape(L0Kron.E, L0Kron.F, L0Kron.F).transpose(1, 2, 0)
    a["row32"], a["row64"] = ((np.arange(128) % n).astype(np.float32).reshape(-1, 1) for n in (32, 64))
    for e in (L1Experts, L2Experts):
        a[e.name + "_packed"] = e.pack(np, a)
        a[e.name + "_nowhere"] = (e.K * NB * T + np.arange(e.W * e.TS, dtype=np.float32)).reshape(-1, 128).T
        a[e.name + "_steps"] = np.arange(0, NB * T, e.TS, dtype=np.float32)
    for p in ("ca", "cf"):
        for k in ("sub", "W", "B"):
            v = a[f"L3_attn_{p}_{k}_b"]
            a[f"L3_attn_{p}_{k}_b_cols"] = np.moveaxis(v.reshape(v.shape[:-1] + (-1, 128)), -1, 0)
    for k in TURNED:
        a[k + "T"] = np.swapaxes(a.pop(k), -1, -2)
    return {k: np.ascontiguousarray(v) for k, v in a.items()}


TURNED = ["L0_ffn_W_up", "L2_ffn_router_w", "L1_ffn_router", "L1_ffn_Ws_gate", "L1_ffn_Ws_up", "L1_ffn_Ws_down"] + [f"L3_attn_{p}_{k}_w" for p in ("ca", "cp", "cf", "cm") for k in ("sub", "W", "B")] + ["L1_xattn_Wv", "L3_ffn_W_fc", "L3_ffn_W_proj", "L1_attn_B_w", "L1_attn_C_w", "L1_attn_D_w", "L1_attn_s_w1",
          "L1_attn_s_w2", "L1_attn_g_w", "L2_attn_Wl", "L2_attn_Wr", "L2_attn_Wf",
          "L3_xattn_Wq", "L3_xattn_Wk", "L3_xattn_Wv", "L3_xattn_Wo"]



def kernel(**inputs):
    from concourse import bacc
    from concourse.bass_utils import run_bass_kernel_spmd
    nc = bacc.Bacc("TRN2", target_bir_lowering=False, num_devices=1)
    arrays = layout(inputs)
    dram = {k: nc.dram_tensor("in_" + k, v.shape, mybir.dt.from_np(v.dtype), kind="ExternalInput").ap()
            for k, v in arrays.items()}
    out = nc.dram_tensor("out_x", (NB, T, D), F32, kind="ExternalOutput").ap()
    program(nc, dram, out, STAGES)
    r = run_bass_kernel_spmd(nc, [{"in_" + k: v for k, v in arrays.items()}], core_ids=[0])
    return r.results[0]["out_x"]
```
